# Optimizing a Trainium2 kernel written in Bass

```python
import numpy as np
import jax
import jax.numpy as jnp

def _softmax(x, axis=-1):
    return jax.nn.softmax(x, axis=axis)

def _gelu(x):
    return jax.nn.gelu(x, approximate=True)

def _silu(x):
    return jax.nn.silu(x)

def _sigmoid(x):
    return jax.nn.sigmoid(x)

def _layernorm(x, axis=-1, eps=1e-05):
    m = jnp.mean(x, axis=axis, keepdims=True)
    v = jnp.var(x, axis=axis, keepdims=True)
    return (x - m) / jnp.sqrt(v + eps)

def _scatter_add(tgt, idx, src, axis=0):
    return tgt.at[idx].add(src)

def _segment_sum(src, seg, n):
    return jax.ops.segment_sum(src, seg, n)
kernel_name = 'mk_lm_tower_d4_tok_ids512_r4_db50ca'

def setup_inputs(seed: int=0):
    np.random.seed(seed)
    _w = jnp.asarray

    def _rec_inputs():
        import jax
        import jax.numpy as jnp
        _rk = jax.random.key(seed)
        x = jax.random.randint(jax.random.fold_in(_rk, 1), (16, 128), 0, 512, jnp.int32)
        return x
    x = _rec_inputs()

    def _L0_tok_setup():
        import jax, jax.numpy as jnp
        import numpy as np
        import math
        TYPE_STARTS = jnp.array([0, 128, 64, 128, 256], dtype=jnp.int64)
        TYPE_ENDS = jnp.array([128, 64, 128, 256, 512], dtype=jnp.int64)
        VOCAB = 512
        D_MODEL = 128
        EPS = 1e-05

        def _type_indices(x):
            matches = (x[..., None] >= TYPE_STARTS) & (x[..., None] < TYPE_ENDS)
            return jnp.argmax(matches, axis=-1)
        key = jax.random.key(seed)
        k1, k2, k3 = jax.random.split(key, 3)
        x = jax.random.randint(k1, (16, 1024), 0, VOCAB, dtype=jnp.int64)
        token_emb_table = jax.random.normal(k2, (VOCAB, D_MODEL - 8), dtype=jnp.float32) * math.sqrt(2.0 / (D_MODEL - 8))
        type_emb_table = jax.random.normal(k3, (5, 8), dtype=jnp.float32) * math.sqrt(2.0 / 8)
        ln_gamma = jnp.ones((D_MODEL,), dtype=jnp.float32)
        ln_beta = jnp.zeros((D_MODEL,), dtype=jnp.float32)
        return {'x': x, 'token_emb_table': token_emb_table, 'type_emb_table': type_emb_table, 'ln_gamma': ln_gamma, 'ln_beta': ln_beta}
    _L0_tok_all = _L0_tok_setup()
    _L0_tok_in = {k: v for k, v in _L0_tok_all.items() if k in ('token_emb_table', 'type_emb_table', 'ln_gamma', 'ln_beta')}
    del _L0_tok_all

    def _L0_attn_setup():
        import jax, jax.numpy as jnp
        import numpy as np
        B, T, D_MODEL, N_HEADS, D_FF = (2, 512, 128, 8, 512)
        D_HEAD = D_MODEL // N_HEADS
        EPS_LN = 1e-05
        DEN_MIN = 1e-06

        def layer_norm(x, g, b):
            mu = jnp.mean(x, axis=-1, keepdims=True)
            var = jnp.var(x, axis=-1, keepdims=True)
            return (x - mu) * jax.lax.rsqrt(var + EPS_LN) * g + b

        def causal_linear_attention(Q, K, V):
            KV = jnp.cumsum(K[..., :, None] * V[..., None, :], axis=2)
            z = jnp.cumsum(K, axis=2)
            num = jnp.einsum('bhtd,bhtdm->bhtm', Q, KV)
            den = jnp.maximum(jnp.einsum('bhtd,bhtd->bht', Q, z), DEN_MIN)[..., None]
            return num / den
        key = jax.random.key(seed)
        ks = jax.random.split(key, 12)

        def lin_w(k, din, dout):
            return jax.random.normal(k, (din, dout), jnp.float32) / np.sqrt(din).astype(np.float32)
        return {'x': jax.random.normal(ks[0], (B, T, D_MODEL), jnp.float32), 'ln1_g': jnp.ones((D_MODEL,), jnp.float32), 'ln1_b': jnp.zeros((D_MODEL,), jnp.float32), 'Wq': lin_w(ks[1], D_MODEL, D_MODEL), 'bq': jnp.zeros((D_MODEL,), jnp.float32), 'Wk': lin_w(ks[2], D_MODEL, D_MODEL), 'bk': jnp.zeros((D_MODEL,), jnp.float32), 'Wv': lin_w(ks[3], D_MODEL, D_MODEL), 'bv': jnp.zeros((D_MODEL,), jnp.float32), 'Wo': lin_w(ks[4], D_MODEL, D_MODEL), 'bo': jnp.zeros((D_MODEL,), jnp.float32), 'ln2_g': jnp.ones((D_MODEL,), jnp.float32), 'ln2_b': jnp.zeros((D_MODEL,), jnp.float32), 'W1': lin_w(ks[5], D_MODEL, D_FF), 'b1': jnp.zeros((D_FF,), jnp.float32), 'W2': lin_w(ks[6], D_FF, D_MODEL), 'b2': jnp.zeros((D_MODEL,), jnp.float32)}
    _L0_attn_all = _L0_attn_setup()
    _L0_attn_in = {k: v for k, v in _L0_attn_all.items() if k in ('ln1_g', 'ln1_b', 'Wq', 'bq', 'Wk', 'bk', 'Wv', 'bv', 'Wo', 'bo', 'ln2_g', 'ln2_b', 'W1', 'b1', 'W2', 'b2')}
    del _L0_attn_all

    def _L0_ffn_setup():
        import jax, jax.numpy as jnp
        import numpy as np
        B, S, D = (8, 1024, 128)
        H = 512
        O = 128
        E = 8
        TOP_K = 1
        key = jax.random.key(seed)
        ks = jax.random.split(key, 8)
        sc = 0.02
        return {'x': jax.random.normal(ks[0], (B, S, D), dtype=jnp.float32), 'Wr': jax.random.normal(ks[1], (D, E), dtype=jnp.float32) * sc, 'br': jnp.zeros((E,), dtype=jnp.float32), 'W1': jax.random.normal(ks[2], (E, D, H), dtype=jnp.float32) * sc, 'b1': jnp.zeros((E, H), dtype=jnp.float32), 'W2': jax.random.normal(ks[3], (E, H, O), dtype=jnp.float32) * sc, 'b2': jnp.zeros((E, O), dtype=jnp.float32)}
    _L0_ffn_all = _L0_ffn_setup()
    _L0_ffn_in = {k: v for k, v in _L0_ffn_all.items() if k in ('Wr', 'br', 'W1', 'b1', 'W2', 'b2')}
    del _L0_ffn_all

    def _L1_attn_setup():
        import jax, jax.numpy as jnp
        import numpy as np
        H = 8
        HKV = 8
        D = 32
        HID = 128
        G = H // HKV

        def _path_attention(x, Wq, Wk, Wv, Ww, Wbeta, bbeta, Wg, bg, Wo):
            B, T, _ = x.shape
            scale = D ** (-0.5)
            q = (x @ Wq.T).reshape(B, T, H, D)
            k = (x @ Wk.T).reshape(B, T, HKV, D)
            v = (x @ Wv.T).reshape(B, T, HKV, D)
            w = (x @ Ww.T).reshape(B, T, HKV, D)
            beta = jax.nn.sigmoid(x @ Wbeta.T + bbeta) * 2.0
            g = jax.nn.log_sigmoid(x @ Wg.T + bg)
            w = w / (jnp.linalg.norm(w, axis=-1, keepdims=True) + 1e-06)
            qs = jnp.moveaxis(q, 1, 0)
            ks_ = jnp.moveaxis(k, 1, 0)
            vs = jnp.moveaxis(v, 1, 0)
            ws = jnpp = jnp.moveaxis(w, 1, 0)
            bs = jnp.moveaxis(beta, 1, 0)
            gs = jnp.moveaxis(g, 1, 0)
            S0 = jnp.zeros((B, HKV, D, D), dtype=jnp.float32)

            def step(S, inp):
                q_t, k_t, v_t, w_t, beta_t, g_t = inp
                Sw = jnp.einsum('bhdm,bhm->bhd', S, w_t)
                S = S - beta_t[:, :, None, None] * jnp.einsum('bhd,bhm->bhdm', Sw, w_t)
                S = S + jnp.einsum('bhd,bhm->bhdm', k_t, v_t)
                q_g = q_t.reshape(B, HKV, G, D) * scale
                res = jnp.einsum('bhgd,bhdm->bhgm', q_g, S)
                res = res * jnp.exp(g_t.reshape(B, HKV, G))[..., None]
                return (S, res.reshape(B, H, D))
            _, out = jax.lax.scan(step, S0, (qs, ks_, vs, ws, bs, gs))
            out = jnp.moveaxis(out, 0, 1).reshape(B, T, H * D)
            return out @ Wo.T
        key = jax.random.key(seed)
        ks = jax.random.split(key, 10)
        B, T = (4, 1024)
        s = 1.0 / np.sqrt(HID)
        so = 1.0 / np.sqrt(H * D)
        return {'x': jax.random.normal(ks[0], (B, T, HID), dtype=jnp.float32), 'Wq': jax.random.normal(ks[1], (H * D, HID), dtype=jnp.float32) * s, 'Wk': jax.random.normal(ks[2], (HKV * D, HID), dtype=jnp.float32) * s, 'Wv': jax.random.normal(ks[3], (HKV * D, HID), dtype=jnp.float32) * s, 'Ww': jax.random.normal(ks[4], (HKV * D, HID), dtype=jnp.float32) * s, 'Wbeta': jax.random.normal(ks[5], (HKV, HID), dtype=jnp.float32) * s, 'bbeta': jax.random.normal(ks[6], (HKV,), dtype=jnp.float32) * 0.1, 'Wg': jax.random.normal(ks[7], (H, HID), dtype=jnp.float32) * s, 'bg': jax.random.normal(ks[8], (H,), dtype=jnp.float32) * 0.1, 'Wo': jax.random.normal(ks[9], (HID, H * D), dtype=jnp.float32) * so}
    _L1_attn_all = _L1_attn_setup()
    _L1_attn_in = {k: v for k, v in _L1_attn_all.items() if k in ('Wq', 'Wk', 'Wv', 'Ww', 'Wbeta', 'bbeta', 'Wg', 'bg', 'Wo')}
    del _L1_attn_all

    def _L1_ffn_setup():
        import jax, jax.numpy as jnp
        import numpy as np
        CAPACITY_FACTOR = 1.25
        TOP_K = 2

        def _moe(x, Wg, W1, b1, W2, b2):
            B, T, D = x.shape
            N = Wg.shape[1]
            K = TOP_K
            BT = B * T
            BTK = BT * K
            C = int(np.ceil(CAPACITY_FACTOR * BTK / N))
            x_flat = x.reshape(BT, D)
            probs = jax.nn.softmax(x_flat @ Wg, axis=-1)
            vals, idx = jax.lax.top_k(probs, K)
            vals = vals / jnp.clip(vals.sum(-1, keepdims=True), 1e-09)
            a = idx.reshape(BTK)
            oh = jax.nn.one_hot(a, N, dtype=jnp.int32)
            rank = jnp.cumsum(oh, axis=0) - oh
            pos = jnp.take_along_axis(rank, a[:, None], axis=1)[:, 0]
            keep = pos < C
            dest = jnp.where(keep, a * C + pos, N * C)
            token = jnp.arange(BTK) // K
            buf = jnp.zeros((N * C, D), x.dtype).at[dest].set(x_flat[token], mode='drop')
            buf = buf.reshape(N, C, D)
            h = jax.nn.relu(jnp.einsum('ncd,ndh->nch', buf, W1) + b1[:, None, :])
            o = (jnp.einsum('nch,nhd->ncd', h, W2) + b2[:, None, :]).reshape(N * C, D)
            gathered = o[jnp.minimum(dest, N * C - 1)]
            w = vals.reshape(BTK) * keep.astype(x.dtype)
            y_flat = jax.ops.segment_sum(gathered * w[:, None], token, num_segments=BT)
            contrib = jax.ops.segment_sum(w, token, num_segments=BT)
            y_flat = jnp.where(contrib[:, None] <= 1e-12, x_flat, y_flat)
            return y_flat.reshape(B, T, D)
        key = jax.random.key(seed)
        ks = jax.random.split(key, 4)
        B, T, D, H, N = (8, 2048, 128, 128, 32)
        x = jax.random.normal(ks[0], (B, T, D), jnp.float32)
        Wg = jax.random.normal(ks[1], (D, N), jnp.float32) * 0.02
        W1 = jax.random.normal(ks[2], (N, D, H), jnp.float32) * 0.02
        b1 = jnp.zeros((N, H), jnp.float32)
        W2 = jax.random.normal(ks[3], (N, H, D), jnp.float32) * 0.02
        b2 = jnp.zeros((N, D), jnp.float32)
        return {'x': x, 'Wg': Wg, 'W1': W1, 'b1': b1, 'W2': W2, 'b2': b2}
    _L1_ffn_all = _L1_ffn_setup()
    _L1_ffn_in = {k: v for k, v in _L1_ffn_all.items() if k in ('Wg', 'W1', 'b1', 'W2', 'b2')}
    del _L1_ffn_all

    def _L2_attn_setup():
        import jax, jax.numpy as jnp
        import numpy as np
        B, L, D, H = (8, 256, 128, 8)
        EPS = 1e-05
        key = jax.random.key(seed)
        ks = jax.random.split(key, 12)
        s = lambda fan_in: 1.0 / np.sqrt(fan_in)
        u = lambda k, shape, sc: jax.random.uniform(k, shape, jnp.float32, -sc, sc)
        return {'input': jax.random.normal(ks[0], (B, L, D), jnp.float32), 'wq': u(ks[1], (D, H * D), s(D)), 'bq': u(ks[2], (H * D,), s(D)), 'wk': u(ks[3], (D, H * D), s(D)), 'bk': u(ks[4], (H * D,), s(D)), 'wv': u(ks[5], (D, H * D), s(D)), 'bv': u(ks[6], (H * D,), s(D)), 'score_w': u(ks[7], (2 * D, 1), s(2 * D)), 'score_b': u(ks[8], (1,), s(2 * D)), 'fc_w': u(ks[9], (H * D, D), s(H * D)), 'fc_b': u(ks[10], (D,), s(H * D)), 'ln_g': jnp.ones((D,), jnp.float32), 'ln_b': jnp.zeros((D,), jnp.float32)}
    _L2_attn_all = _L2_attn_setup()
    _L2_attn_in = {k: v for k, v in _L2_attn_all.items() if k in ('wq', 'bq', 'wk', 'bk', 'wv', 'bv', 'score_w', 'score_b', 'fc_w', 'fc_b', 'ln_g', 'ln_b')}
    del _L2_attn_all

    def _L2_ffn_setup():
        import jax, jax.numpy as jnp
        import numpy as np
        B, S, H, E, F = (4, 512, 128, 8, 128)
        key = jax.random.key(seed)
        k = jax.random.split(key, 7)
        x = jax.random.normal(k[0], (B, S, H), dtype=jnp.float32)
        Wr = jax.random.normal(k[1], (H, E), dtype=jnp.float32) / np.sqrt(H)
        br = jnp.zeros((E,), dtype=jnp.float32)
        W1 = jax.random.normal(k[2], (E, H, F), dtype=jnp.float32) / np.sqrt(H)
        b1 = jnp.zeros((E, F), dtype=jnp.float32)
        W2 = jax.random.normal(k[3], (E, F, H), dtype=jnp.float32) / np.sqrt(F)
        b2 = jnp.zeros((E, H), dtype=jnp.float32)
        return {'x': x, 'Wr': Wr, 'br': br, 'W1': W1, 'b1': b1, 'W2': W2, 'b2': b2}
    _L2_ffn_all = _L2_ffn_setup()
    _L2_ffn_in = {k: v for k, v in _L2_ffn_all.items() if k in ('Wr', 'br', 'W1', 'b1', 'W2', 'b2')}
    del _L2_ffn_all

    def _L3_attn_setup():
        import jax, jax.numpy as jnp
        import numpy as np
        B, N, C, H = (4, 1024, 128, 16)

        def _rope(x):
            b, n, c = x.shape
            k_max = c // 2
            theta = 1.0 / 10000.0 ** (jnp.arange(k_max, dtype=jnp.float32) / k_max)
            ang = jnp.arange(n, dtype=jnp.float32)[:, None] * theta
            cos, sin = (jnp.cos(ang), jnp.sin(ang))
            xr, xi = (x[..., 0::2], x[..., 1::2])
            out = jnp.stack([xr * cos - xi * sin, xr * sin + xi * cos], axis=-1)
            return out.reshape(b, n, c)
        key = jax.random.key(seed)
        k1, k2, k3, k4 = jax.random.split(key, 4)
        x = jax.random.normal(k1, (B, N, C), jnp.float32)
        Wqk = jax.random.normal(k2, (C, 2 * C), jnp.float32) / np.sqrt(C)
        bqk = jnp.zeros((2 * C,), jnp.float32)
        lepe_w = jax.random.normal(k3, (C, 1, 3), jnp.float32) * 0.1
        lepe_b = jnp.zeros((C,), jnp.float32)
        return {'x': x, 'Wqk': Wqk, 'bqk': bqk, 'lepe_w': lepe_w, 'lepe_b': lepe_b}
    _L3_attn_all = _L3_attn_setup()
    _L3_attn_in = {k: v for k, v in _L3_attn_all.items() if k in ('Wqk', 'bqk', 'lepe_w', 'lepe_b')}
    del _L3_attn_all

    def _L3_ffn_setup():
        import jax, jax.numpy as jnp
        import numpy as np
        B, T, C = (2, 512, 128)
        E, G, TG, K = (64, 8, 4, 6)
        H, HS = (160, 128)
        key = jax.random.key(seed)
        ks = jax.random.split(key, 9)
        s = 0.02
        return {'x': jax.random.normal(ks[0], (B, T, C), dtype=jnp.float32), 'router_w': jax.random.normal(ks[1], (E, C), dtype=jnp.float32) * s, 'bias_corr': jnp.zeros((E,), dtype=jnp.float32), 'Wg': jax.random.normal(ks[2], (E, C, H), dtype=jnp.float32) * s, 'Wu': jax.random.normal(ks[3], (E, C, H), dtype=jnp.float32) * s, 'Wd': jax.random.normal(ks[4], (E, H, C), dtype=jnp.float32) * s, 'sWg': jax.random.normal(ks[5], (C, HS), dtype=jnp.float32) * s, 'sWu': jax.random.normal(ks[6], (C, HS), dtype=jnp.float32) * s, 'sWd': jax.random.normal(ks[7], (HS, C), dtype=jnp.float32) * s}
    _L3_ffn_all = _L3_ffn_setup()
    _L3_ffn_in = {k: v for k, v in _L3_ffn_all.items() if k in ('router_w', 'bias_corr', 'Wg', 'Wu', 'Wd', 'sWg', 'sWu', 'sWd')}
    del _L3_ffn_all
    return {'x': x, 'L0_tok_token_emb_table': _L0_tok_in['token_emb_table'], 'L0_tok_type_emb_table': _L0_tok_in['type_emb_table'], 'L0_tok_ln_gamma': _L0_tok_in['ln_gamma'], 'L0_tok_ln_beta': _L0_tok_in['ln_beta'], 'L0_attn_ln1_g': _L0_attn_in['ln1_g'], 'L0_attn_ln1_b': _L0_attn_in['ln1_b'], 'L0_attn_Wq': _L0_attn_in['Wq'], 'L0_attn_bq': _L0_attn_in['bq'], 'L0_attn_Wk': _L0_attn_in['Wk'], 'L0_attn_bk': _L0_attn_in['bk'], 'L0_attn_Wv': _L0_attn_in['Wv'], 'L0_attn_bv': _L0_attn_in['bv'], 'L0_attn_Wo': _L0_attn_in['Wo'], 'L0_attn_bo': _L0_attn_in['bo'], 'L0_attn_ln2_g': _L0_attn_in['ln2_g'], 'L0_attn_ln2_b': _L0_attn_in['ln2_b'], 'L0_attn_W1': _L0_attn_in['W1'], 'L0_attn_b1': _L0_attn_in['b1'], 'L0_attn_W2': _L0_attn_in['W2'], 'L0_attn_b2': _L0_attn_in['b2'], 'L0_ffn_Wr': _L0_ffn_in['Wr'], 'L0_ffn_br': _L0_ffn_in['br'], 'L0_ffn_W1': _L0_ffn_in['W1'], 'L0_ffn_b1': _L0_ffn_in['b1'], 'L0_ffn_W2': _L0_ffn_in['W2'], 'L0_ffn_b2': _L0_ffn_in['b2'], 'L1_attn_Wq': _L1_attn_in['Wq'], 'L1_attn_Wk': _L1_attn_in['Wk'], 'L1_attn_Wv': _L1_attn_in['Wv'], 'L1_attn_Ww': _L1_attn_in['Ww'], 'L1_attn_Wbeta': _L1_attn_in['Wbeta'], 'L1_attn_bbeta': _L1_attn_in['bbeta'], 'L1_attn_Wg': _L1_attn_in['Wg'], 'L1_attn_bg': _L1_attn_in['bg'], 'L1_attn_Wo': _L1_attn_in['Wo'], 'L1_ffn_Wg': _L1_ffn_in['Wg'], 'L1_ffn_W1': _L1_ffn_in['W1'], 'L1_ffn_b1': _L1_ffn_in['b1'], 'L1_ffn_W2': _L1_ffn_in['W2'], 'L1_ffn_b2': _L1_ffn_in['b2'], 'L2_attn_wq': _L2_attn_in['wq'], 'L2_attn_bq': _L2_attn_in['bq'], 'L2_attn_wk': _L2_attn_in['wk'], 'L2_attn_bk': _L2_attn_in['bk'], 'L2_attn_wv': _L2_attn_in['wv'], 'L2_attn_bv': _L2_attn_in['bv'], 'L2_attn_score_w': _L2_attn_in['score_w'], 'L2_attn_score_b': _L2_attn_in['score_b'], 'L2_attn_fc_w': _L2_attn_in['fc_w'], 'L2_attn_fc_b': _L2_attn_in['fc_b'], 'L2_attn_ln_g': _L2_attn_in['ln_g'], 'L2_attn_ln_b': _L2_attn_in['ln_b'], 'L2_ffn_Wr': _L2_ffn_in['Wr'], 'L2_ffn_br': _L2_ffn_in['br'], 'L2_ffn_W1': _L2_ffn_in['W1'], 'L2_ffn_b1': _L2_ffn_in['b1'], 'L2_ffn_W2': _L2_ffn_in['W2'], 'L2_ffn_b2': _L2_ffn_in['b2'], 'L3_attn_Wqk': _L3_attn_in['Wqk'], 'L3_attn_bqk': _L3_attn_in['bqk'], 'L3_attn_lepe_w': _L3_attn_in['lepe_w'], 'L3_attn_lepe_b': _L3_attn_in['lepe_b'], 'L3_ffn_router_w': _L3_ffn_in['router_w'], 'L3_ffn_bias_corr': _L3_ffn_in['bias_corr'], 'L3_ffn_Wg': _L3_ffn_in['Wg'], 'L3_ffn_Wu': _L3_ffn_in['Wu'], 'L3_ffn_Wd': _L3_ffn_in['Wd'], 'L3_ffn_sWg': _L3_ffn_in['sWg'], 'L3_ffn_sWu': _L3_ffn_in['sWu'], 'L3_ffn_sWd': _L3_ffn_in['sWd']}

def reference(x, L0_tok_token_emb_table, L0_tok_type_emb_table, L0_tok_ln_gamma, L0_tok_ln_beta, L0_attn_ln1_g, L0_attn_ln1_b, L0_attn_Wq, L0_attn_bq, L0_attn_Wk, L0_attn_bk, L0_attn_Wv, L0_attn_bv, L0_attn_Wo, L0_attn_bo, L0_attn_ln2_g, L0_attn_ln2_b, L0_attn_W1, L0_attn_b1, L0_attn_W2, L0_attn_b2, L0_ffn_Wr, L0_ffn_br, L0_ffn_W1, L0_ffn_b1, L0_ffn_W2, L0_ffn_b2, L1_attn_Wq, L1_attn_Wk, L1_attn_Wv, L1_attn_Ww, L1_attn_Wbeta, L1_attn_bbeta, L1_attn_Wg, L1_attn_bg, L1_attn_Wo, L1_ffn_Wg, L1_ffn_W1, L1_ffn_b1, L1_ffn_W2, L1_ffn_b2, L2_attn_wq, L2_attn_bq, L2_attn_wk, L2_attn_bk, L2_attn_wv, L2_attn_bv, L2_attn_score_w, L2_attn_score_b, L2_attn_fc_w, L2_attn_fc_b, L2_attn_ln_g, L2_attn_ln_b, L2_ffn_Wr, L2_ffn_br, L2_ffn_W1, L2_ffn_b1, L2_ffn_W2, L2_ffn_b2, L3_attn_Wqk, L3_attn_bqk, L3_attn_lepe_w, L3_attn_lepe_b, L3_ffn_router_w, L3_ffn_bias_corr, L3_ffn_Wg, L3_ffn_Wu, L3_ffn_Wd, L3_ffn_sWg, L3_ffn_sWu, L3_ffn_sWd):
    import jax
    import jax.numpy as jnp

    def _L0_tok_ref(x, token_emb_table, type_emb_table, ln_gamma, ln_beta):
        import jax, jax.numpy as jnp
        import numpy as np
        import math
        TYPE_STARTS = jnp.array([0, 128, 64, 128, 256], dtype=jnp.int64)
        TYPE_ENDS = jnp.array([128, 64, 128, 256, 512], dtype=jnp.int64)
        VOCAB = 512
        D_MODEL = 128
        EPS = 1e-05

        def _type_indices(x):
            matches = (x[..., None] >= TYPE_STARTS) & (x[..., None] < TYPE_ENDS)
            return jnp.argmax(matches, axis=-1)
        token_emb = token_emb_table[x]
        type_emb = type_emb_table[_type_indices(x)]
        combined = jnp.concatenate([token_emb, type_emb], axis=-1)
        mean = jnp.mean(combined, axis=-1, keepdims=True)
        var = jnp.var(combined, axis=-1, keepdims=True)
        normed = (combined - mean) * jax.lax.rsqrt(var + EPS) * ln_gamma + ln_beta
        return normed * jnp.asarray(math.sqrt(D_MODEL), dtype=normed.dtype)

    def _L0_attn_ref(x, ln1_g, ln1_b, Wq, bq, Wk, bk, Wv, bv, Wo, bo, ln2_g, ln2_b, W1, b1, W2, b2):
        import jax, jax.numpy as jnp
        import numpy as np
        B, T, D_MODEL, N_HEADS, D_FF = (2, 512, 128, 8, 512)
        D_HEAD = D_MODEL // N_HEADS
        EPS_LN = 1e-05
        DEN_MIN = 1e-06

        def layer_norm(x, g, b):
            mu = jnp.mean(x, axis=-1, keepdims=True)
            var = jnp.var(x, axis=-1, keepdims=True)
            return (x - mu) * jax.lax.rsqrt(var + EPS_LN) * g + b

        def causal_linear_attention(Q, K, V):
            KV = jnp.cumsum(K[..., :, None] * V[..., None, :], axis=2)
            z = jnp.cumsum(K, axis=2)
            num = jnp.einsum('bhtd,bhtdm->bhtm', Q, KV)
            den = jnp.maximum(jnp.einsum('bhtd,bhtd->bht', Q, z), DEN_MIN)[..., None]
            return num / den
        Bx, Tx, _ = x.shape
        h = layer_norm(x, ln1_g, ln1_b)

        def heads(y):
            return y.reshape(Bx, Tx, N_HEADS, D_HEAD).transpose(0, 2, 1, 3)
        Q = jax.nn.elu(heads(h @ Wq + bq)) + 1.0
        K = jax.nn.elu(heads(h @ Wk + bk)) + 1.0
        V = heads(h @ Wv + bv)
        attn = causal_linear_attention(Q, K, V)
        attn = attn.transpose(0, 2, 1, 3).reshape(Bx, Tx, D_MODEL)
        x = x + (attn @ Wo + bo)
        h2 = layer_norm(x, ln2_g, ln2_b)
        ffn = jax.nn.relu(h2 @ W1 + b1) @ W2 + b2
        return x + ffn

    def _L0_ffn_ref(x, Wr, br, W1, b1, W2, b2):
        import jax, jax.numpy as jnp
        import numpy as np
        B, S, D = (8, 1024, 128)
        H = 512
        O = 128
        E = 8
        TOP_K = 1
        b, s, d = x.shape
        xf = x.reshape(-1, d)
        router_logits = xf @ Wr + br
        topk_logits, topk_idx = jax.lax.top_k(router_logits, TOP_K)
        topk_gates = jax.nn.softmax(topk_logits, axis=1)
        out = jnp.zeros((xf.shape[0], O), dtype=x.dtype)
        for k in range(TOP_K):
            idx_k = topk_idx[:, k]
            gate_k = topk_gates[:, k:k + 1]
            for e in range(E):
                h = jax.nn.relu(xf @ W1[e] + b1[e])
                oe = h @ W2[e] + b2[e]
                mask = (idx_k == e)[:, None]
                out = out + jnp.where(mask, gate_k * oe, 0.0)
        return out.reshape(b, s, O)

    def _L1_attn_ref(x, Wq, Wk, Wv, Ww, Wbeta, bbeta, Wg, bg, Wo):
        import jax, jax.numpy as jnp
        import numpy as np
        H = 8
        HKV = 8
        D = 32
        HID = 128
        G = H // HKV

        def _path_attention(x, Wq, Wk, Wv, Ww, Wbeta, bbeta, Wg, bg, Wo):
            B, T, _ = x.shape
            scale = D ** (-0.5)
            q = (x @ Wq.T).reshape(B, T, H, D)
            k = (x @ Wk.T).reshape(B, T, HKV, D)
            v = (x @ Wv.T).reshape(B, T, HKV, D)
            w = (x @ Ww.T).reshape(B, T, HKV, D)
            beta = jax.nn.sigmoid(x @ Wbeta.T + bbeta) * 2.0
            g = jax.nn.log_sigmoid(x @ Wg.T + bg)
            w = w / (jnp.linalg.norm(w, axis=-1, keepdims=True) + 1e-06)
            qs = jnp.moveaxis(q, 1, 0)
            ks_ = jnp.moveaxis(k, 1, 0)
            vs = jnp.moveaxis(v, 1, 0)
            ws = jnpp = jnp.moveaxis(w, 1, 0)
            bs = jnp.moveaxis(beta, 1, 0)
            gs = jnp.moveaxis(g, 1, 0)
            S0 = jnp.zeros((B, HKV, D, D), dtype=jnp.float32)

            def step(S, inp):
                q_t, k_t, v_t, w_t, beta_t, g_t = inp
                Sw = jnp.einsum('bhdm,bhm->bhd', S, w_t)
                S = S - beta_t[:, :, None, None] * jnp.einsum('bhd,bhm->bhdm', Sw, w_t)
                S = S + jnp.einsum('bhd,bhm->bhdm', k_t, v_t)
                q_g = q_t.reshape(B, HKV, G, D) * scale
                res = jnp.einsum('bhgd,bhdm->bhgm', q_g, S)
                res = res * jnp.exp(g_t.reshape(B, HKV, G))[..., None]
                return (S, res.reshape(B, H, D))
            _, out = jax.lax.scan(step, S0, (qs, ks_, vs, ws, bs, gs))
            out = jnp.moveaxis(out, 0, 1).reshape(B, T, H * D)
            return out @ Wo.T
        return _path_attention(x, Wq, Wk, Wv, Ww, Wbeta, bbeta, Wg, bg, Wo)

    def _L1_ffn_ref(x, Wg, W1, b1, W2, b2):
        import jax, jax.numpy as jnp
        import numpy as np
        CAPACITY_FACTOR = 1.25
        TOP_K = 2

        def _moe(x, Wg, W1, b1, W2, b2):
            B, T, D = x.shape
            N = Wg.shape[1]
            K = TOP_K
            BT = B * T
            BTK = BT * K
            C = int(np.ceil(CAPACITY_FACTOR * BTK / N))
            x_flat = x.reshape(BT, D)
            probs = jax.nn.softmax(x_flat @ Wg, axis=-1)
            vals, idx = jax.lax.top_k(probs, K)
            vals = vals / jnp.clip(vals.sum(-1, keepdims=True), 1e-09)
            a = idx.reshape(BTK)
            oh = jax.nn.one_hot(a, N, dtype=jnp.int32)
            rank = jnp.cumsum(oh, axis=0) - oh
            pos = jnp.take_along_axis(rank, a[:, None], axis=1)[:, 0]
            keep = pos < C
            dest = jnp.where(keep, a * C + pos, N * C)
            token = jnp.arange(BTK) // K
            buf = jnp.zeros((N * C, D), x.dtype).at[dest].set(x_flat[token], mode='drop')
            buf = buf.reshape(N, C, D)
            h = jax.nn.relu(jnp.einsum('ncd,ndh->nch', buf, W1) + b1[:, None, :])
            o = (jnp.einsum('nch,nhd->ncd', h, W2) + b2[:, None, :]).reshape(N * C, D)
            gathered = o[jnp.minimum(dest, N * C - 1)]
            w = vals.reshape(BTK) * keep.astype(x.dtype)
            y_flat = jax.ops.segment_sum(gathered * w[:, None], token, num_segments=BT)
            contrib = jax.ops.segment_sum(w, token, num_segments=BT)
            y_flat = jnp.where(contrib[:, None] <= 1e-12, x_flat, y_flat)
            return y_flat.reshape(B, T, D)
        return _moe(x, Wg, W1, b1, W2, b2)

    def _L2_attn_ref(input, wq, bq, wk, bk, wv, bv, score_w, score_b, fc_w, fc_b, ln_g, ln_b):
        import jax, jax.numpy as jnp
        import numpy as np
        B, L, D, H = (8, 256, 128, 8)
        EPS = 1e-05
        x = input
        b, l, d = x.shape
        h = wq.shape[1] // d

        def proj(w, bias):
            y = (x @ w + bias).reshape(b, l, h, d)
            return y.transpose(2, 0, 1, 3).reshape(h * b, l, d)
        q = proj(wq, bq)
        k = proj(wk, bk)
        v = proj(wv, bv)
        sk = (k @ score_w[:d])[:, :, 0]
        sq = (q @ score_w[d:])[:, :, 0]
        kq = jnp.tanh(sk[:, :, None] + sq[:, None, :] + score_b[0])
        score = jax.nn.softmax(kq[..., None], axis=-1)[..., 0]
        out = jnp.einsum('nij,njd->nid', score, v)
        out = out.reshape(h, b, l, d).transpose(1, 2, 0, 3).reshape(b, l, h * d)
        out = out @ fc_w + fc_b
        y = out + x
        mu = jnp.mean(y, axis=-1, keepdims=True)
        var = jnp.var(y, axis=-1, keepdims=True)
        return (y - mu) / jnp.sqrt(var + EPS) * ln_g + ln_b

    def _L2_ffn_ref(x, Wr, br, W1, b1, W2, b2):
        import jax, jax.numpy as jnp
        import numpy as np
        B, S, H, E, F = (4, 512, 128, 8, 128)
        b, s, h = x.shape
        xt = x.reshape(-1, h)
        logits = xt @ Wr + br
        probs = jax.nn.softmax(logits, axis=-1)
        G = jnp.max(probs, axis=-1)
        idx = jnp.argmax(probs, axis=-1)
        h1 = jax.nn.relu(jnp.einsum('nh,ehf->nef', xt, W1) + b1)
        eo = jnp.einsum('nef,efh->neh', h1, W2) + b2
        Eout = jnp.take_along_axis(eo, idx[:, None, None], axis=1)[:, 0, :]
        y = G[:, None] * Eout
        return y.reshape(b, s, h)

    def _L3_attn_ref(x, Wqk, bqk, lepe_w, lepe_b):
        import jax, jax.numpy as jnp
        import numpy as np
        B, N, C, H = (4, 1024, 128, 16)

        def _rope(x):
            b, n, c = x.shape
            k_max = c // 2
            theta = 1.0 / 10000.0 ** (jnp.arange(k_max, dtype=jnp.float32) / k_max)
            ang = jnp.arange(n, dtype=jnp.float32)[:, None] * theta
            cos, sin = (jnp.cos(ang), jnp.sin(ang))
            xr, xi = (x[..., 0::2], x[..., 1::2])
            out = jnp.stack([xr * cos - xi * sin, xr * sin + xi * cos], axis=-1)
            return out.reshape(b, n, c)
        b, n, c = x.shape
        h = H
        d = c // h
        qk = x @ Wqk + bqk
        q = jax.nn.elu(qk[..., :c]) + 1.0
        k = jax.nn.elu(qk[..., c:]) + 1.0
        q_rope = _rope(q).reshape(b, n, h, d).transpose(0, 2, 1, 3)
        k_rope = _rope(k).reshape(b, n, h, d).transpose(0, 2, 1, 3)
        qh = q.reshape(b, n, h, d).transpose(0, 2, 1, 3)
        kh = k.reshape(b, n, h, d).transpose(0, 2, 1, 3)
        v = x.reshape(b, n, h, d).transpose(0, 2, 1, 3)
        kmean = kh.mean(axis=2)
        z = 1.0 / (jnp.einsum('bhnd,bhd->bhn', qh, kmean) + 1e-06)
        kv = jnp.einsum('bhnd,bhne->bhde', k_rope, v) / n
        out = jnp.einsum('bhnd,bhde->bhne', q_rope, kv) * z[..., None]
        out = out.transpose(0, 2, 1, 3).reshape(b, n, c)
        vt = x.transpose(0, 2, 1)
        lepe = jax.lax.conv_general_dilated(vt, lepe_w, window_strides=(1,), padding=((1, 1),), feature_group_count=c, dimension_numbers=('NCH', 'OIH', 'NCH'))
        lepe = lepe + lepe_b[None, :, None]
        return out + lepe.transpose(0, 2, 1)

    def _L3_ffn_ref(x, router_w, bias_corr, Wg, Wu, Wd, sWg, sWu, sWd):
        import jax, jax.numpy as jnp
        import numpy as np
        B, T, C = (2, 512, 128)
        E, G, TG, K = (64, 8, 4, 6)
        H, HS = (160, 128)
        Bx, Tx, Cx = x.shape
        S = Bx * Tx
        xf = x.reshape(S, Cx)
        shared = jax.nn.silu(xf @ sWg) * (xf @ sWu) @ sWd
        logits = xf.astype(jnp.float32) @ router_w.T
        scores = jax.nn.sigmoid(logits).astype(x.dtype)
        biased = scores + bias_corr
        epg = E // G
        group_scores = biased.reshape(S, G, epg).max(axis=-1)
        _, sel_g = jax.lax.top_k(group_scores, TG)
        rows = jnp.arange(S)[:, None]
        group_mask = jnp.zeros((S, G), dtype=x.dtype).at[rows, sel_g].set(1.0)
        expert_mask = jnp.repeat(group_mask, epg, axis=1)
        masked = jnp.where(expert_mask > 0, biased, -jnp.inf)
        _, topk_idx = jax.lax.top_k(masked, K)
        w = jnp.take_along_axis(scores, topk_idx, axis=1)
        w = w / (w.sum(axis=-1, keepdims=True) + 1e-20)
        combine = jnp.zeros((S, E), dtype=x.dtype).at[rows, topk_idx].add(w)
        g = jnp.einsum('sc,ech->seh', xf, Wg)
        u = jnp.einsum('sc,ech->seh', xf, Wu)
        h = jax.nn.silu(g) * u
        hw = combine[:, :, None] * h
        routed = jnp.einsum('seh,ehc->sc', hw, Wd)
        return (shared + routed).reshape(Bx, Tx, Cx)
    h = _L0_tok_ref(x, L0_tok_token_emb_table, L0_tok_type_emb_table, L0_tok_ln_gamma, L0_tok_ln_beta)
    h = h + _L0_attn_ref(_layernorm(h, axis=-1), L0_attn_ln1_g, L0_attn_ln1_b, L0_attn_Wq, L0_attn_bq, L0_attn_Wk, L0_attn_bk, L0_attn_Wv, L0_attn_bv, L0_attn_Wo, L0_attn_bo, L0_attn_ln2_g, L0_attn_ln2_b, L0_attn_W1, L0_attn_b1, L0_attn_W2, L0_attn_b2)
    h = h + _L0_ffn_ref(_layernorm(h, axis=-1), L0_ffn_Wr, L0_ffn_br, L0_ffn_W1, L0_ffn_b1, L0_ffn_W2, L0_ffn_b2)
    h = h + _L1_attn_ref(_layernorm(h, axis=-1), L1_attn_Wq, L1_attn_Wk, L1_attn_Wv, L1_attn_Ww, L1_attn_Wbeta, L1_attn_bbeta, L1_attn_Wg, L1_attn_bg, L1_attn_Wo)
    h = h + _L1_ffn_ref(_layernorm(h, axis=-1), L1_ffn_Wg, L1_ffn_W1, L1_ffn_b1, L1_ffn_W2, L1_ffn_b2)
    h = h + _L2_attn_ref(_layernorm(h, axis=-1), L2_attn_wq, L2_attn_bq, L2_attn_wk, L2_attn_bk, L2_attn_wv, L2_attn_bv, L2_attn_score_w, L2_attn_score_b, L2_attn_fc_w, L2_attn_fc_b, L2_attn_ln_g, L2_attn_ln_b)
    h = h + _L2_ffn_ref(_layernorm(h, axis=-1), L2_ffn_Wr, L2_ffn_br, L2_ffn_W1, L2_ffn_b1, L2_ffn_W2, L2_ffn_b2)
    h = h + _L3_attn_ref(_layernorm(h, axis=-1), L3_attn_Wqk, L3_attn_bqk, L3_attn_lepe_w, L3_attn_lepe_b)
    h = h + _L3_ffn_ref(_layernorm(h, axis=-1), L3_ffn_router_w, L3_ffn_bias_corr, L3_ffn_Wg, L3_ffn_Wu, L3_ffn_Wd, L3_ffn_sWg, L3_ffn_sWu, L3_ffn_sWd)
    return h

_drawn_inputs = setup_inputs


def setup_inputs(seed=0):
    import zlib

    import numpy as np

    out = dict(_drawn_inputs(seed))
    spreads = {'L0_tok_ln_gamma': (1.0, 0.2),
     'L0_tok_ln_beta': (0.0, 0.1),
     'L0_attn_ln1_g': (1.0, 0.6),
     'L0_attn_ln1_b': (0.0, 0.673),
     'L0_attn_bq': (0.0, 0.8),
     'L0_attn_bk': (0.0, 0.8),
     'L0_attn_bv': (0.0, 0.554),
     'L0_attn_bo': (0.0, 0.65),
     'L0_attn_ln2_g': (1.0, 0.6),
     'L0_attn_ln2_b': (0.0, 0.8),
     'L0_attn_b1': (0.0, 0.8),
     'L0_attn_b2': (0.0, 0.637),
     'L0_ffn_br': (0.0, 0.735),
     'L0_ffn_b1': (0.0, 0.8),
     'L0_ffn_b2': (0.0, 0.788),
     'L1_ffn_b1': (0.0, 0.8),
     'L1_ffn_b2': (0.0, 0.8),
     'L2_attn_ln_g': (1.0, 0.6),
     'L2_attn_ln_b': (0.0, 0.8),
     'L2_ffn_br': (0.0, 0.8),
     'L2_ffn_b1': (0.0, 0.8),
     'L2_ffn_b2': (0.0, 0.8),
     'L3_attn_bqk': (0.0, 2.0),
     'L3_attn_lepe_b': (0.0, 0.8),
     'L3_ffn_bias_corr': (0.0, 0.8)}
    factors = {'L0_attn_Wq': 7.54,
     'L0_attn_Wk': 4.043,
     'L0_ffn_Wr': 4.31,
     'L0_ffn_W1': 8.0,
     'L0_ffn_W2': 7.011,
     'L1_attn_bbeta': 3.37,
     'L1_ffn_Wg': 3.424,
     'L1_ffn_W1': 8.0,
     'L1_ffn_W2': 8.0,
     'L2_attn_bv': 2.976,
     'L2_attn_fc_b': 171.023,
     'L2_ffn_Wr': 3.689,
     'L2_ffn_W1': 4.348,
     'L2_ffn_W2': 3.628,
     'L3_attn_Wqk': 197.014,
     'L3_attn_lepe_w': 5.308,
     'L3_ffn_router_w': 8.0,
     'L3_ffn_Wg': 8.0,
     'L3_ffn_Wu': 8.0,
     'L3_ffn_Wd': 8.0,
     'L3_ffn_sWg': 8.0,
     'L3_ffn_sWu': 8.0,
     'L3_ffn_sWd': 8.0}
    for name, (base, spread) in spreads.items():
        noise = np.random.default_rng([zlib.crc32(name.encode()), seed]).standard_normal(out[name].shape)
        drawn = base * np.exp(spread * noise) if base else spread * noise
        out[name] = jnp.asarray(drawn.astype(out[name].dtype))
    for name, factor in factors.items():
        out[name] = (out[name] * factor).astype(out[name].dtype)
    return out
```

```python
import math
from contextlib import ExitStack

import concourse.bass as bass
from concourse import mybir

f32 = mybir.dt.float32
f16 = mybir.dt.float16
i32 = mybir.dt.int32
u32 = mybir.dt.uint32
ALU = mybir.AluOpType
ACT = mybir.ActivationFunctionType
AX = mybir.AxisListType

T = 128
B = 16
D = 128
EPS = 1e-5


class Own:

    def __init__(self, engine, sem, first=0):
        self.engine, self.sem, self.at = engine, sem, first

    def done(self, ins):
        self.at = self.at + 1
        ins.then_inc(self.sem, 1)
        self.engine.wait_ge(self.sem, self.at)


class Space:

    used = []

    def __init__(self, nc):
        self.nc, self.ctx, self.count = nc, ExitStack(), 0

    def sb(self, name, shape, dt=f32):
        return self.ctx.enter_context(self.nc.sbuf_tensor(name, shape, dt))

    def ps(self, name, shape, dt=f32):
        return self.ctx.enter_context(self.nc.psum_tensor(name, shape, dt))

    def sem(self, name):
        handle = self.nc.alloc_semaphore(name=name)
        Space.used.append(handle)
        return handle

    def __enter__(self):
        self.ctx.__enter__()
        return self

    def __exit__(self, *a):
        return self.ctx.__exit__(*a)


def end_of_layer(nc):
    nc.clear_and_free_semaphores(Space.used)
    Space.used = []
    nc.all_engine_barrier()


def per_row(column, width):
    return column.unsqueeze(2).to_broadcast([column.shape[0], column.shape[1], width])


def per_tile(row, tiles):
    return row.unsqueeze(1).to_broadcast([row.shape[0], tiles, row.shape[1]])


def layer_norm_block(nc, name, src, dst, gamma=None, beta=None, scale=None):
    with Space(nc) as s:
        stats = s.sb(name + "_stats", [T, B, 6])
        mean = s.sb(name + "_mean", [T, B])
        gap = s.sb(name + "_gap", [T, B])
        var = s.sb(name + "_var", [T, B])
        std = s.sb(name + "_std", [T, B])
        rstd = s.sb(name + "_rstd", [T, B])
        own = s.sem(name + "_own")
        var_ready = s.sem(name + "_var_ready")
        std_ready = s.sem(name + "_std_ready")
        with nc.Block() as block:
            @block.scalar
            def _(act):
                act.wait_ge(var_ready, 1)
                nc.scalar.activation(std[:], var[:], ACT.Sqrt).then_inc(std_ready, 1)

            @block.vector
            def _(v):
                with v.Fori(0, B) as b:
                    nc.vector.bn_stats(stats[:, b, :], src[:, b, :]).then_inc(own, 1)
                v.wait_ge(own, B)
                chain = Own(v, own, B)
                nc.vector.tensor_tensor(mean[:], stats[:, :, 1], stats[:, :, 4], ALU.add)
                nc.vector.tensor_tensor(gap[:], stats[:, :, 1], stats[:, :, 4], ALU.subtract)
                chain.done(nc.vector.tensor_tensor(var[:], stats[:, :, 2], stats[:, :, 5], ALU.add))
                nc.vector.tensor_scalar(mean[:], mean[:], 0.5, None, ALU.mult)
                nc.vector.scalar_tensor_tensor(out=gap[:], in0=gap[:], scalar=0.25, in1=gap[:], op0=ALU.mult,
                                               op1=ALU.mult)
                chain.done(nc.vector.tensor_scalar(var[:], var[:], 1.0 / D, EPS, ALU.mult, ALU.add))
                nc.vector.tensor_tensor(var[:], var[:], gap[:], ALU.add).then_inc(var_ready, 1)
                v.wait_ge(std_ready, 1)
                chain.done(nc.vector.reciprocal(rstd[:], std[:]))
                with v.Fori(0, B) as b:
                    nc.vector.tensor_scalar(dst[:, b, :], src[:, b, :], mean[:, bass.ts(b, 1)], rstd[:, bass.ts(b, 1)],
                                            ALU.subtract, ALU.mult).then_inc(own, 1)
                chain.at += B
                v.wait_ge(own, chain.at)
                if gamma is not None:
                    chain.done(nc.vector.tensor_tensor(dst[:], dst[:], per_tile(gamma[:], B), ALU.mult))
                    chain.done(nc.vector.tensor_tensor(dst[:], dst[:], per_tile(beta[:], B), ALU.add))
                if scale is not None:
                    chain.done(nc.vector.tensor_scalar(dst[:], dst[:], scale, None, ALU.mult))


def constants_and_embedding(nc, W, K):
    with Space(nc) as s:
        ids = s.sb("ids", [T, B], i32)
        idf = s.sb("idf", [T, B])
        raw = s.sb("raw", [T, B, D])
        types = s.sb("types", [T, 5, 8])
        sel = s.sb("sel", [T, 3, B])
        low = s.sb("low", [T, B])
        part = s.sb("part", [T, B, 8])
        gamma = s.sb("gamma", [T, D])
        beta = s.sb("beta", [T, D])
        ids_in = s.sem("ids_in")
        rows_in = s.sem("rows_in")
        made = s.sem("made")
        gathered = s.sem("gathered")
        own = s.sem("emb_own")
        NTOK = D - 8
        with nc.Block() as block:
            @block.sync
            def _(sp):
                sp.dma_start(ids[:], W["x_t"]).then_inc(ids_in, 16)
                sp.dma_start(types[:].rearrange("p a b -> p (a b)"),
                             W["L0_tok_type_emb_table"].rearrange("a b -> (a b)").partition_broadcast(T)
                             ).then_inc(rows_in, 16)
                sp.dma_start(gamma[:], W["L0_tok_ln_gamma"].partition_broadcast(T)).then_inc(rows_in, 16)
                sp.dma_start(beta[:], W["L0_tok_ln_beta"].partition_broadcast(T)).then_inc(rows_in, 16)

            @block.gpsimd
            def _(g):
                g.wait_ge(ids_in, 16)
                for b in range(B):
                    g.indirect_dma_start(out=raw[:, b, 0:NTOK], out_offset=None, in_=W["L0_tok_token_emb_table"],
                                         in_offset=bass.IndirectOffsetOnAxis(ap=ids[:, b:b + 1], axis=0)
                                         ).then_inc(gathered, 16)
                K.fill(g, made)

            @block.vector
            def _(v):
                chain = Own(v, own)
                v.wait_ge(ids_in, 16)
                chain.done(nc.vector.tensor_copy(idf[:], ids[:]))
                nc.vector.tensor_scalar(sel[:, 0, :], idf[:], 128.0, None, ALU.is_lt)
                nc.vector.tensor_scalar(low[:], idf[:], 256.0, None, ALU.is_lt)
                chain.done(nc.vector.tensor_scalar(sel[:, 2, :], idf[:], 256.0, None, ALU.is_ge))
                v.wait_ge(rows_in, 48)
                chain.done(nc.vector.tensor_tensor(sel[:, 1, :], low[:], sel[:, 0, :], ALU.subtract))
                emb = raw[:, :, NTOK:D]
                for n, row in enumerate((0, 3, 4)):
                    to = emb if n == 0 else part[:]
                    chain.done(nc.vector.tensor_tensor(to, per_row(sel[:, n, :], 8), per_tile(types[:, row, :], B),
                                                       ALU.mult))
                    if n:
                        chain.done(nc.vector.tensor_tensor(emb, emb, part[:], ALU.add))
                v.wait_ge(gathered, 16 * B)
        layer_norm_block(nc, "ln_emb", raw, K.h, gamma, beta, math.sqrt(D))
    end_of_layer(nc)


class Constants:

    def __init__(self, nc, s):
        self.nc = nc
        self.h = s.sb("h", [T, B, D])
        self.ident = s.sb("ident", [T, T])
        self.ones = s.sb("ones", [T, T])
        self.up_to = s.sb("up_to", [T, T])
        self.before = s.sb("before", [T, T])
        self.after = s.sb("after", [T, T])

    def fill(self, g, made):
        g.memset(self.ones[:], 1.0).then_inc(made, 1)
        g.wait_ge(made, 1)
        for m, op, base, sign in ((self.ident, ALU.is_equal, 0, 1), (self.up_to, ALU.is_ge, 0, 1),
                                  (self.before, ALU.is_gt, 0, 1), (self.after, ALU.is_gt, 0, -1)):
            g.affine_select(out=m[:], in_=self.ones[:], compare_op=op, fill=0.0, base=base,
                            pattern=[[sign, T]], channel_multiplier=-sign)


def causal_linear_attention_block(nc, W, K, xin, x2):
    HEADS, DH = 8, 16
    NG, PER = 2, 4
    with Space(nc) as s:
        h1 = s.sb("a0_h1", [T, B, D])
        g1 = s.sb("a0_g1", [T, D])
        b1 = s.sb("a0_b1", [T, D])
        wq = s.sb("a0_wq", [D, 2, NG, PER, 32])
        bq = s.sb("a0_bq", [D, 2, NG])
        wv = s.sb("a0_wv", [D, D])
        bv = s.sb("a0_bv", [T, D])
        wo = s.sb("a0_wo", [D, D])
        bo = s.sb("a0_bo", [T, D])
        loads = s.sem("a0_loads")
        own0 = s.sem("a0_own0")
        with nc.Block() as block:
            @block.gpsimd
            def _(g):
                g.memset(wq[:], 0.0).then_inc(own0, 1)
                g.memset(bq[:], 0.0).then_inc(own0, 1)

            @block.sync
            def _(sp):
                sp.dma_start(g1[:], W["L0_attn_ln1_g"].partition_broadcast(T)).then_inc(loads, 16)
                sp.dma_start(b1[:], W["L0_attn_ln1_b"].partition_broadcast(T)).then_inc(loads, 16)
                sp.dma_start(wv[:], W["L0_attn_Wv"]).then_inc(loads, 16)
                sp.dma_start(wo[:], W["L0_attn_Wo"]).then_inc(loads, 16)
                sp.dma_start(bv[:], W["L0_attn_bv"].partition_broadcast(T)).then_inc(loads, 16)
                sp.dma_start(bo[:], W["L0_attn_bo"].partition_broadcast(T)).then_inc(loads, 16)
                sp.wait_ge(own0, 2)
                for n, (w, b) in enumerate((("L0_attn_Wq", "L0_attn_bq"), ("L0_attn_Wk", "L0_attn_bk"))):
                    for g in range(NG):
                        sp.dma_start(wq[:, n, g, :, 0:DH],
                                     W[w].rearrange("c (j g d) -> c g j d", g=NG, d=DH)[:, g]).then_inc(loads, 16)
                        for j in range(PER):
                            at = (j * NG + g) * DH
                            sp.dma_start(bq[32 * j:32 * j + DH, n, g:g + 1],
                                         W[b][at:at + DH].unsqueeze(1)).then_inc(loads, 16)
                sp.wait_ge(loads, 16 * (6 + 4 + 16))
        layer_norm_block(nc, "a0_ln1", xin, h1, g1, b1)

        hs = s.sb("a0_hs", [T, 2, D])
        h1t = s.sb("a0_h1t", [D, 2, T])
        xb = s.sb("a0_xb", [D, 2, NG, 2, T])
        neg = s.sb("a0_neg", [D, 2, NG, 2, T])
        ex = s.sb("a0_ex", [D, 2, NG, 2, T])
        qk = s.sb("a0_qk", [D, 2, NG, 2, T])
        v17 = s.sb("a0_v17", [T, 2, HEADS, DH + 1])
        sm = s.sb("a0_sm", [T, 2, HEADS, T])
        den = s.sb("a0_den", [T, 2, HEADS])
        rden = s.sb("a0_rden", [T, 2, HEADS])
        at_ = s.sb("a0_at", [T, 2, D])
        att = s.sb("a0_att", [D, 2, T])
        xbo = s.sb("a0_xbo", [T, B, D])
        p_t = s.ps("a0_p_t", [T, 2, 2, T])
        p_q = s.ps("a0_p_q", [T, 2, NG, 2, T])
        p_s = s.ps("a0_p_s", [T, PER, 2, NG, T])
        p_n = s.ps("a0_p_n", [T, 512])
        num = p_n[:, 0:2 * HEADS * (DH + 1)].rearrange("t (u h e) -> t u h e", u=2, h=HEADS)
        hs_ready, t1, h1t_ready, qk_ps, v_ps, xb_ready, neg_ready, ex_ready, qk_ready, v_ready, s_ps, sm_ready, \
            n_ps, at_ready, att_ps, att_ready, o_ps, x2_ready, ones_ready, own, rd = (s.sem("a0_" + n) for n in (
                "hs_ready", "t1", "h1t_ready", "qk_ps", "v_ps", "xb_ready", "neg_ready", "ex_ready", "qk_ready",
                "v_ready", "s_ps", "sm_ready", "n_ps", "at_ready", "att_ps", "att_ready", "o_ps", "x2_ready",
                "ones_ready", "own", "rd"))
        with nc.Block() as block:
            @block.gpsimd
            def _(g):
                g.memset(v17[:, :, :, DH:DH + 1], 1.0).then_inc(ones_ready, 1)
                g.tensor_tensor(out=xbo[:], in0=xin[:], in1=per_tile(bo[:], B), op=ALU.add).then_inc(ones_ready, 1)

            @block.vector
            def _(v):
                v.sem_inc(x2_ready, 2)
                with v.Fori(0, B // 2) as i:
                    for u in range(2):
                        v.wait_ge(x2_ready, 2 * i + u + 1)
                        nc.vector.tensor_copy(hs[:, u, :], h1[:, 2 * i + u, :]).then_inc(hs_ready, 1)
                    for n in range(2):
                        v.wait_ge(xb_ready, 4 * i + 2 * n + 2)
                        nc.vector.tensor_scalar(neg[:, n], xb[:, n], 0.0, None, ALU.min).then_inc(neg_ready, 1)
                    v.wait_ge(v_ps, i + 1)
                    nc.vector.tensor_tensor(v17[:, :, :, 0:DH],
                                            p_t[:, 1].rearrange("t u (h d) -> t u h d", h=HEADS),
                                            bv[:].rearrange("t (h d) -> t h d", h=HEADS).unsqueeze(1)
                                            .to_broadcast([T, 2, HEADS, DH]), ALU.add).then_inc(v_ready, 1)
                    for n in range(2):
                        v.wait_ge(ex_ready, 2 * i + n + 1)
                        nc.vector.scalar_tensor_tensor(out=qk[:, n].rearrange("c g u t -> c (g u t)"),
                                                       in0=xb[:, n].rearrange("c g u t -> c (g u t)"), scalar=0.0,
                                                       in1=ex[:, n].rearrange("c g u t -> c (g u t)"), op0=ALU.max,
                                                       op1=ALU.add).then_inc(qk_ready, 1)
                    v.wait_ge(s_ps, 2 * i + 2)
                    for u in range(2):
                        nc.vector.tensor_tensor(sm[:, u].rearrange("t (j g) s -> t j g s", g=NG), p_s[:, :, u],
                                                K.up_to[:].unsqueeze(1).unsqueeze(1).to_broadcast([T, PER, NG, T]),
                                                ALU.mult).then_inc(sm_ready, 1)
                    chain = Own(v, own, 2 * i)
                    v.wait_ge(n_ps, 2 * i + 2)
                    chain.done(nc.vector.tensor_scalar(den[:], num[:, :, :, DH], 1e-6, None, ALU.max))
                    chain.done(nc.vector.reciprocal(rden[:], den[:]))
                    for u in range(2):
                        nc.vector.tensor_tensor(at_[:, u].rearrange("t (h d) -> t h d", h=HEADS), num[:, u, :, 0:DH],
                                                per_row(rden[:, u], DH), ALU.mult).then_inc(at_ready, 1)
                    v.wait_ge(ones_ready, 2)
                    v.wait_ge(o_ps, 2 * i + 2)
                    for u in range(2):
                        nc.vector.tensor_tensor(x2[:, 2 * i + u, :], xbo[:, 2 * i + u, :], p_q[:, 0, 0, u, :],
                                                ALU.add).then_inc(x2_ready, 1)

            @block.scalar
            def _(act):
                with act.Fori(0, B // 2) as i:
                    act.wait_ge(t1, 2 * i + 2)
                    nc.scalar.activation(h1t[:], p_t[:, 0], ACT.Copy).then_inc(h1t_ready, 1)
                    act.wait_ge(qk_ps, i + 1)
                    for n in range(2):
                        for g in range(NG):
                            nc.scalar.activation(xb[:, n, g], p_q[:, n, g], ACT.Identity,
                                                 bias=bq[:, n, g:g + 1]).then_inc(xb_ready, 1)
                    for n in range(2):
                        act.wait_ge(neg_ready, 2 * i + n + 1)
                        nc.scalar.activation(ex[:, n], neg[:, n], ACT.Exp).then_inc(ex_ready, 1)
                    act.wait_ge(att_ps, 2 * i + 2)
                    nc.scalar.activation(att[:], p_t[:, 0], ACT.Copy).then_inc(att_ready, 1)

            @block.tensor
            def _(pe):
                pe.wait_ge(ones_ready, 1)
                with pe.Fori(0, B // 2) as i:
                    for u in range(2):
                        pe.wait_ge(hs_ready, 2 * i + u + 1)
                        nc.tensor.transpose(p_t[:, 0, u], hs[:, u], K.ident[:]).then_inc(t1, 1)
                    pe.wait_ge(h1t_ready, i + 1)
                    for n in range(2):
                        for g in range(NG):
                            last = nc.tensor.matmul(p_q[:, n, g], wq[:, n, g].rearrange("c j d -> c (j d)"), h1t[:],
                                                    start=True, stop=True)
                    last.then_inc(qk_ps, 1)
                    for u in range(2):
                        last = nc.tensor.matmul(p_t[:, 1, u], h1t[:, u], wv[:], start=True, stop=True)
                    last.then_inc(v_ps, 1)
                    pe.wait_ge(qk_ready, 2 * i + 2)
                    for u in range(2):
                        for h in range(HEADS):
                            j, g = divmod(h, NG)
                            rows = slice(32 * j, 32 * j + DH)
                            last = nc.tensor.matmul(p_s[:, j, u, g], qk[rows, 1, g, u], qk[rows, 0, g, u],
                                                    start=True, stop=True)
                        last.then_inc(s_ps, 1)
                    pe.wait_ge(v_ready, i + 1)
                    for u in range(2):
                        pe.wait_ge(sm_ready, 2 * i + u + 1)
                        for h in range(HEADS):
                            last = nc.tensor.matmul(num[:, u, h], sm[:, u, h], v17[:, u, h], start=True, stop=True)
                        last.then_inc(n_ps, 1)
                    for u in range(2):
                        pe.wait_ge(at_ready, 2 * i + u + 1)
                        nc.tensor.transpose(p_t[:, 0, u], at_[:, u], K.ident[:]).then_inc(att_ps, 1)
                    pe.wait_ge(att_ready, i + 1)
                    for u in range(2):
                        nc.tensor.matmul(p_q[:, 0, 0, u], att[:, u], wo[:], start=True, stop=True).then_inc(o_ps, 1)


def dense_ffn_block(nc, W, K, x2):
    CH = 4
    with Space(nc) as s:
        h2 = s.sb("f_h2", [T, B, D])
        g2 = s.sb("f_g2", [T, D])
        be2 = s.sb("f_be2", [T, D])
        w1 = s.sb("f_w1", [D, CH, T])
        b1 = s.sb("f_b1", [T, CH])
        w2 = s.sb("f_w2", [T, CH, D])
        b2 = s.sb("f_b2", [T, D])
        loads = s.sem("f_loads")
        with nc.Block() as block:
            @block.sync
            def _(sp):
                sp.dma_start(g2[:], W["L0_attn_ln2_g"].partition_broadcast(T)).then_inc(loads, 16)
                sp.dma_start(be2[:], W["L0_attn_ln2_b"].partition_broadcast(T)).then_inc(loads, 16)
                sp.dma_start(w1[:].rearrange("c k n -> c (k n)"), W["L0_attn_W1"]).then_inc(loads, 16)
                sp.dma_start(w2[:], W["L0_attn_W2"].rearrange("(k p) n -> p k n", p=T)).then_inc(loads, 16)
                sp.dma_start(b1[:], W["L0_attn_b1_t"]).then_inc(loads, 16)
                sp.dma_start(b2[:], W["L0_attn_b2"].partition_broadcast(T)).then_inc(loads, 16)
                sp.wait_ge(loads, 96)
        layer_norm_block(nc, "f_ln2", x2, h2, g2, be2)
        hs = s.sb("f_hs", [T, 2, D])
        h2t = s.sb("f_h2t", [D, 2, T])
        hid = s.sb("f_hid", [T, CH, 2, T])
        p_t = s.ps("f_p_t", [T, 2, 2, T])
        p_h = s.ps("f_p_h", [T, CH, 2, T])
        hs_ready, t1, h2t_ready, h_ps, hid_ready, y_ps, y_done, base_ready = (s.sem("f_" + n) for n in (
            "hs_ready", "t1", "h2t_ready", "h_ps", "hid_ready", "y_ps", "y_done", "base_ready"))
        with nc.Block() as block:
            @block.gpsimd
            def _(g):
                g.tensor_tensor(out=x2[:], in0=x2[:], in1=per_tile(b2[:], B), op=ALU.add).then_inc(base_ready, 1)
                g.wait_ge(base_ready, 1)
                g.tensor_tensor(out=K.h[:], in0=K.h[:], in1=x2[:], op=ALU.add).then_inc(base_ready, 1)

            @block.vector
            def _(v):
                v.sem_inc(y_done, 2)
                with v.Fori(0, B // 2) as i:
                    for u in range(2):
                        v.wait_ge(y_done, 2 * i + u + 1)
                        nc.vector.tensor_copy(hs[:, u, :], h2[:, 2 * i + u, :]).then_inc(hs_ready, 1)
                    v.wait_ge(base_ready, 2)
                    v.wait_ge(y_ps, 2 * i + 2)
                    for u in range(2):
                        nc.vector.tensor_tensor(K.h[:, 2 * i + u, :], K.h[:, 2 * i + u, :], p_t[:, 1, u],
                                                ALU.add).then_inc(y_done, 1)

            @block.scalar
            def _(act):
                with act.Fori(0, B // 2) as i:
                    act.wait_ge(t1, 2 * i + 2)
                    nc.scalar.activation(h2t[:], p_t[:, 0], ACT.Copy).then_inc(h2t_ready, 1)
                    for c in range(CH):
                        act.wait_ge(h_ps, 2 * i + c // 2 + 1)
                        nc.scalar.activation(hid[:, c], p_h[:, c], ACT.Relu, bias=b1[:, c:c + 1]).then_inc(hid_ready, 1)

            @block.tensor
            def _(pe):
                with pe.Fori(0, B // 2) as i:
                    for u in range(2):
                        pe.wait_ge(hs_ready, 2 * i + u + 1)
                        nc.tensor.transpose(p_t[:, 0, u], hs[:, u], K.ident[:]).then_inc(t1, 1)
                    pe.wait_ge(h2t_ready, i + 1)
                    for c in range(CH):
                        last = nc.tensor.matmul(p_h[:, c], w1[:, c], h2t[:], start=True, stop=True)
                        if c % 2:
                            last.then_inc(h_ps, 1)
                    for u in range(2):
                        for c in range(CH):
                            pe.wait_ge(hid_ready, CH * i + c + 1)
                            last = nc.tensor.matmul(p_t[:, 1, u], hid[:, c, u], w2[:, c], start=c == 0, stop=c == CH - 1)
                        last.then_inc(y_ps, 1)


def layer0_attention(nc, W, K):
    with Space(nc) as s:
        xin = s.sb("xin", [T, B, D])
        x2 = s.sb("x2", [T, B, D])
        layer_norm_block(nc, "a0_ln0", K.h, xin)
        causal_linear_attention_block(nc, W, K, xin, x2)
        dense_ffn_block(nc, W, K, x2)
    end_of_layer(nc)


SLOTS = 128
NTOK = B * T


class Route:

    def __init__(self, s, name, experts, picks, tiles):
        self.experts, self.picks, self.tiles = experts, picks, tiles
        self.dest = s.sb(name + "_dest", [T, B, picks], i32)
        self.gate = s.sb(name + "_gate", [T, B, picks])
        self.who = s.sb(name + "_who", [SLOTS, tiles], i32)
        self.expert_of = s.sb(name + "_expert_of", [1, tiles], i32)


def router_logits_block(nc, name, K, xn, xn_dram, w_dram, experts, logits, bias_dram=None):
    Q = 4
    with Space(nc) as s:
        w = s.sb(name + "_wr", [D, experts])
        bias = s.sb(name + "_br", [T, experts])
        xs = s.sb(name + "_xs", [T, Q, D])
        xt = s.sb(name + "_xt", [D, Q, T])
        p_t = s.ps(name + "_p_t", [D, Q, T])
        p_l = s.ps(name + "_p_l", [T, 512])
        lg = p_l[:, 0:Q * experts].rearrange("t (q e) -> t q e", q=Q)
        stored, loads, xs_ready, t_ps, xt_ready, l_ps, l_ready = (s.sem(name + "_" + n) for n in (
            "stored", "loads", "xs_ready", "t_ps", "xt_ready", "l_ps", "l_ready"))
        n_loads = 32 if bias_dram is not None else 16
        with nc.Block() as block:
            @block.sync
            def _(sp):
                sp.dma_start(w[:], w_dram).then_inc(loads, 16)
                if bias_dram is not None:
                    sp.dma_start(bias[:], bias_dram.partition_broadcast(T)).then_inc(loads, 16)
                sp.dma_start(xn_dram.rearrange("(b t) c -> t b c", t=T), xn[:]).then_inc(stored, 16)
                sp.wait_ge(stored, 16)

            @block.vector
            def _(v):
                v.sem_inc(l_ready, 1)
                with v.Fori(0, B // Q) as i:
                    v.wait_ge(l_ready, i + 1)
                    nc.vector.tensor_copy(xs[:], xn[:, bass.ts(i, Q), :]).then_inc(xs_ready, 1)
                    v.wait_ge(loads, n_loads)
                    v.wait_ge(l_ps, i + 1)
                    if bias_dram is not None:
                        nc.vector.tensor_tensor(logits[:, bass.ts(i, Q), :], lg, per_tile(bias[:], Q),
                                                ALU.add).then_inc(l_ready, 1)
                    else:
                        nc.vector.tensor_copy(logits[:, bass.ts(i, Q), :], lg).then_inc(l_ready, 1)

            @block.scalar
            def _(act):
                with act.Fori(0, B // Q) as i:
                    act.wait_ge(t_ps, i + 1)
                    nc.scalar.activation(xt[:], p_t[:], ACT.Copy).then_inc(xt_ready, 1)

            @block.tensor
            def _(pe):
                pe.wait_ge(loads, n_loads)
                with pe.Fori(0, B // Q) as i:
                    pe.wait_ge(xs_ready, i + 1)
                    for q in range(Q):
                        last = nc.tensor.transpose(p_t[:, q], xs[:, q], K.ident[:])
                    last.then_inc(t_ps, 1)
                    pe.wait_ge(xt_ready, i + 1)
                    for q in range(Q):
                        last = nc.tensor.matmul(lg[:, q], xt[:, q], w[:], start=True, stop=True)
                    last.then_inc(l_ps, 1)


def sort_block(nc, name, K, route, index, chosen=None, capacity=None):
    E, P, NT = route.experts, route.picks, route.tiles
    COLS = B * E
    NB = max(1, COLS // 512)
    with Space(nc) as s:
        iota_e = s.sb(name + "_iota_e", [T, E])
        iota_row = s.sb(name + "_iota_row", [T, 256])
        iota_h = s.sb(name + "_iota_h", [T, 256], f16)
        token = s.sb(name + "_token", [T, B])
        hot = s.sb(name + "_hot", [T, B, E])
        mask = s.sb(name + "_mask", [T, B, E])
        mask_h = s.sb(name + "_mask_h", [T, B, E], f16)
        sums = s.sb(name + "_sums", [T, B + 1, E])
        sums_h = s.sb(name + "_sums_h", [T, B + 1, E], f16)
        before_h = s.sb(name + "_before_h", [T, T], f16)
        ones_h = s.sb(name + "_ones_h", [T, T], f16)
        pos = s.sb(name + "_pos", [T, B, E])
        prod = s.sb(name + "_prod", [T, B, E])
        prod2 = s.sb(name + "_prod2", [T, B, E])
        tiles_i = s.sb(name + "_tiles_i", [T, E], i32)
        tiles_f = s.sb(name + "_tiles_f", [T, E])
        incl = s.sb(name + "_incl", [T, E])
        base = s.sb(name + "_base", [T, E])
        col_i = s.sb(name + "_col_i", [E, 1], i32)
        col_f = s.sb(name + "_col_f", [E, 1])
        cum = s.sb(name + "_cum", [E, 1])
        passed = s.sb(name + "_passed", [E, NT])
        dest_f = s.sb(name + "_dest_f", [T, B, P])
        keep = s.sb(name + "_keep", [T, B, P])
        second = s.sb(name + "_second", [T, B, P])
        part_i = s.sb(name + "_part_i", [T, B, P], i32)
        lo = s.sb(name + "_lo", [T, B, P])
        hi = s.sb(name + "_hi", [T, B, P])
        R = 8
        low_hot = s.sb(name + "_low_hot", [T, R, SLOTS], f16)
        high_tok = s.sb(name + "_high_tok", [T, R, NT], f16)
        zeros_h = s.sb(name + "_zeros_h", [T, SLOTS], f16)
        p_rank = s.ps(name + "_p_rank", [T, NB, min(512, COLS)])
        p_cnt = s.ps(name + "_p_cnt", [T, 512])
        p_col = s.ps(name + "_p_col", [T, 512])
        p_who = s.ps(name + "_p_who", [T, 512])
        consts, mask_ready, rank_ps, cnt_ps, col_ps, col_ready, cum_ps, passed_ready, te_ps, hots, hots_used, \
            who_ps, own, filled = (s.sem(name + "_" + n) for n in (
                "consts", "mask_ready", "rank_ps", "cnt_ps", "col_ps", "col_ready", "cum_ps", "passed_ready",
                "te_ps", "hots", "hots_used", "who_ps", "own", "filled"))
        with nc.Block() as block:
            @block.gpsimd
            def _(g):
                g.iota(iota_e[:], pattern=[[1, E]], base=0, channel_multiplier=0,
                       allow_small_or_imprecise_dtypes=True)
                g.iota(iota_row[:], pattern=[[1, 256]], base=0, channel_multiplier=0,
                       allow_small_or_imprecise_dtypes=True)
                g.iota(iota_h[:], pattern=[[1, 256]], base=0, channel_multiplier=0,
                       allow_small_or_imprecise_dtypes=True)
                g.iota(token[:], pattern=[[T, B]], base=0, channel_multiplier=1,
                       allow_small_or_imprecise_dtypes=True)
                g.memset(zeros_h[:], 0.0)
                g.memset(sums[:, 0, :], 0.0)
                g.tensor_copy(before_h[:], K.before[:])
                g.tensor_copy(ones_h[:], K.ones[:]).then_inc(consts, 1)

            @block.vector
            def _(v):
                chain = Own(v, own)
                v.wait_ge(consts, 1)

                def flat(a):
                    return a[:].rearrange("t b k -> t (b k)")

                def one_hot(k, out):
                    return nc.vector.tensor_tensor(out, per_tile(iota_e[:], B), per_row(index[:, :, k], E),
                                                   ALU.is_equal)

                def picked(out, values, k_hot, tmp):
                    chain.done(nc.vector.tensor_tensor(tmp, k_hot, values, ALU.mult))
                    return nc.vector.tensor_reduce(out=out, in_=tmp, axis=AX.X, op=ALU.add)

                for k in range(P):
                    chain.done(one_hot(k, mask[:] if k == 0 else hot[:]))
                    if k:
                        chain.done(nc.vector.tensor_tensor(mask[:], mask[:], hot[:], ALU.add))
                for b in range(B):
                    chain.done(nc.vector.tensor_tensor(sums[:, b + 1, :], sums[:, b, :], mask[:, b, :], ALU.add))
                nc.vector.tensor_copy(mask_h[:], mask[:])
                nc.vector.tensor_copy(sums_h[:], sums[:]).then_inc(mask_ready, 1)
                if capacity is None:
                    v.wait_ge(cnt_ps, 1)
                    chain.done(nc.vector.tensor_scalar(tiles_i[:], p_cnt[:, 0:E], float(SLOTS - 1), None, ALU.add))
                    chain.done(nc.vector.tensor_scalar(tiles_i[:], tiles_i[:], 7, None, ALU.arith_shift_right))
                    chain.done(nc.vector.tensor_copy(tiles_f[:], tiles_i[:]))
                    chain.done(nc.vector.tensor_tensor_scan(incl[:], K.ones[:, 0:E], tiles_f[:], 0.0, ALU.mult, ALU.add))
                    chain.done(nc.vector.tensor_tensor(base[:], incl[:], tiles_f[:], ALU.subtract))
                    chain.done(nc.vector.tensor_scalar(base[:], base[:], float(SLOTS), None, ALU.mult))
                    v.wait_ge(col_ps, 1)
                    chain.done(nc.vector.tensor_scalar(col_i[:], p_col[0:E, 0:1], float(SLOTS - 1), None, ALU.add))
                    chain.done(nc.vector.tensor_scalar(col_i[:], col_i[:], 7, None, ALU.arith_shift_right))
                    nc.vector.tensor_copy(col_f[:], col_i[:]).then_inc(col_ready, 1)
                    v.wait_ge(cum_ps, 1)
                    chain.done(nc.vector.tensor_copy(cum[:], p_col[0:E, 0:1]))
                    nc.vector.tensor_scalar(passed[:], iota_row[0:E, 0:NT], cum[:, 0:1], None,
                                            ALU.is_ge).then_inc(passed_ready, 1)
                    v.wait_ge(te_ps, 1)
                    nc.vector.tensor_scalar(route.expert_of[:], p_col[0:1, 0:NT], float(E - 1), None, ALU.min)
                v.wait_ge(rank_ps, 1)
                ranks = p_rank[:].rearrange("t n (b e) -> t (n b) e", e=E)
                if capacity is None:
                    chain.done(nc.vector.tensor_tensor(pos[:], ranks, per_tile(base[:], B), ALU.add))
                else:
                    chain.done(nc.vector.tensor_copy(pos[:], ranks))
                for k in range(P):
                    chain.done(one_hot(k, hot[:]))
                    if chosen is not None:
                        chain.done(picked(route.gate[:, :, k], chosen[:], hot[:], prod2[:]))
                    chain.done(picked(dest_f[:, :, k], pos[:], hot[:], prod[:]))
                if capacity is None:
                    chain.done(nc.vector.tensor_copy(route.dest[:], dest_f[:]))
                    chain.done(nc.vector.tensor_scalar(part_i[:], route.dest[:], 7, None, ALU.arith_shift_right))
                    chain.done(nc.vector.tensor_copy(hi[:], part_i[:]))
                    chain.done(nc.vector.tensor_scalar(part_i[:], route.dest[:], SLOTS - 1, None, ALU.bitwise_and))
                    chain.done(nc.vector.tensor_copy(lo[:], part_i[:]))
                else:
                    chain.done(nc.vector.tensor_scalar(keep[:], dest_f[:], float(capacity), None, ALU.is_lt))
                    chain.done(nc.vector.tensor_tensor(route.gate[:], route.gate[:], keep[:], ALU.mult))
                    chain.done(nc.vector.tensor_scalar(second[:], dest_f[:], float(SLOTS), None, ALU.is_ge))
                    chain.done(nc.vector.scalar_tensor_tensor(out=flat(hi), in0=flat(index), scalar=2.0, in1=flat(second),
                                                              op0=ALU.mult, op1=ALU.add))
                    chain.done(nc.vector.scalar_tensor_tensor(out=flat(lo), in0=flat(second), scalar=-float(SLOTS),
                                                              in1=flat(dest_f), op0=ALU.mult, op1=ALU.add))
                    chain.done(nc.vector.tensor_scalar(hi[:], hi[:], float(-NT), None, ALU.add))
                    chain.done(nc.vector.tensor_tensor(hi[:], hi[:], keep[:], ALU.mult))
                    chain.done(nc.vector.tensor_scalar(hi[:], hi[:], float(NT), None, ALU.add))
                    chain.done(nc.vector.scalar_tensor_tensor(out=flat(dest_f), in0=flat(index), scalar=float(capacity),
                                                              in1=flat(dest_f), op0=ALU.mult, op1=ALU.add))
                    chain.done(nc.vector.tensor_tensor(dest_f[:], dest_f[:], keep[:], ALU.mult))
                    chain.done(nc.vector.tensor_copy(route.dest[:], dest_f[:]))
                lo_c, hi_c = lo[:].rearrange("t b k -> t (b k)"), hi[:].rearrange("t b k -> t (b k)")
                token_c = prod2[:].rearrange("t b e -> t (b e)")[:, 0:B * P]
                chain.done(nc.vector.tensor_copy(token_c.rearrange("t (b k) -> t b k", k=P), per_row(token[:], P)))
                v.sem_inc(hots_used, 1)
                with v.Fori(0, B * P // R) as i:
                    v.wait_ge(hots_used, i + 1)
                    for r in range(R):
                        c = i * R + r
                        nc.vector.tensor_scalar(low_hot[:, r], iota_h[:, 0:SLOTS], lo_c[:, bass.ds(c, 1)], None,
                                                ALU.is_equal)
                        nc.vector.tensor_scalar(high_tok[:, r], iota_h[:, 0:NT], hi_c[:, bass.ds(c, 1)],
                                                token_c[:, bass.ds(c, 1)], ALU.is_equal, ALU.mult).then_inc(hots, 1)
                v.wait_ge(who_ps, 1)
                nc.vector.tensor_copy(route.who[:], p_who[:, 0:NT])

            @block.tensor
            def _(pe):
                pe.wait_ge(mask_ready, 1)
                flat_m = mask_h[:].rearrange("t b e -> t (b e)")
                flat_s = sums_h[:].rearrange("t b e -> t (b e)")
                W_ = min(512, COLS)
                if capacity is None:
                    nc.tensor.matmul(p_cnt[:, 0:E], ones_h[:], sums_h[:, B, :], start=True, stop=True).then_inc(cnt_ps, 1)
                    nc.tensor.matmul(p_col[0:E, 0:1], sums_h[:, B, :], ones_h[:, 0:1], start=True,
                                     stop=True).then_inc(col_ps, 1)
                for n in range(NB):
                    cols = slice(n * W_, (n + 1) * W_)
                    nc.tensor.matmul(p_rank[:, n], before_h[:], flat_m[:, cols], start=True, stop=False)
                    last = nc.tensor.matmul(p_rank[:, n], ones_h[:], flat_s[:, cols], start=False, stop=True)
                last.then_inc(rank_ps, 1)
                if capacity is None:
                    pe.wait_ge(col_ready, 1)
                    nc.tensor.matmul(p_col[0:E, 0:1], K.up_to[0:E, 0:E], col_f[:], start=True, stop=True).then_inc(cum_ps, 1)
                    pe.wait_ge(passed_ready, 1)
                    nc.tensor.matmul(p_col[0:1, 0:NT], K.ones[0:E, 0:1], passed[:], start=True, stop=True).then_inc(te_ps, 1)
                nc.tensor.matmul(p_who[:, 0:NT], zeros_h[:], iota_h[:, 0:NT], start=True, stop=False)
                with pe.Fori(0, B * P // R) as i:
                    for r in range(R):
                        pe.wait_ge(hots, i * R + r + 1)
                        last = nc.tensor.matmul(p_who[:, 0:NT], low_hot[:, r], high_tok[:, r], start=False, stop=False)
                    last.then_inc(hots_used, 1)
                nc.tensor.matmul(p_who[:, 0:NT], zeros_h[:], iota_h[:, 0:NT], start=False, stop=True).then_inc(who_ps, 1)


def expert_tiles_block(nc, name, K, route, xn_dram, o_dram, w1, b1_t, w2, b2, chunks):
    E, NT, CH = route.experts, route.tiles, chunks
    TURNS = (NT + 1) // 2
    assert NT % 2 == 0
    with Space(nc) as s:
        who2 = s.sb(name + "_who2", [SLOTS, 2], i32)
        xg = s.sb(name + "_xg", [SLOTS, 2, D])
        xgt = s.sb(name + "_xgt", [D, 2, SLOTS])
        w1b = s.sb(name + "_w1b", [D, 2, CH * T])
        w2b = s.sb(name + "_w2b", [T, 2, CH, D])
        b1b = s.sb(name + "_b1b", [T, 2, CH])
        b2b = s.sb(name + "_b2b", [1, 2, D])
        hid = s.sb(name + "_hid", [T, 2, CH, SLOTS])
        ob = s.sb(name + "_ob", [SLOTS, 2, D])
        p_t = [s.ps(f"{name}_p_t{u}", [D, 512]) for u in range(2)]
        p_h = [s.ps(f"{name}_p_h{u}", [T, 4, SLOTS]) for u in range(2)]
        p_o = [s.ps(f"{name}_p_o{u}", [SLOTS, 512]) for u in range(2)]
        who_ready, gathered, w_in, t_ps, xgt_ready, h_ps, hid_ready, o_ps, ob_ready, stored = (
            [s.sem(f"{name}_{n}{u}") for u in range(2)] for n in (
                "who_ready", "gathered", "w_in", "t_ps", "xgt_ready", "h_ps", "hid_ready", "o_ps", "ob_ready", "stored"))
        with nc.Block() as block:
            @block.gpsimd
            def _(g):
                for u in range(2):
                    g.sem_inc(xgt_ready[u], 1)
                with g.Fori(0, TURNS) as i:
                    for u in range(2):
                        g.wait_ge(xgt_ready[u], i + 1)
                        g.tensor_copy(who2[:, u:u + 1], route.who[:, bass.ds(2 * i + u, 1)]).then_inc(who_ready[u], 1)
                        g.wait_ge(who_ready[u], i + 1)
                        g.nop(nofuse=True)
                        g.indirect_dma_start(out=xg[:, u, :], out_offset=None, in_=xn_dram,
                                             in_offset=bass.IndirectOffsetOnAxis(ap=who2[:, u:u + 1], axis=0)
                                             ).then_inc(gathered[u], 16)

            @block.sync
            def _(sp):
                for u in range(2):
                    sp.sem_inc(o_ps[u], 1)
                with sp.Fori(0, TURNS) as i:
                    for u in range(2):
                        e = sp.value_load(route.expert_of[0:1, bass.ds(2 * i + u, 1)], min_val=0, max_val=E - 1)
                        sp.wait_ge(o_ps[u], i + 1)
                        sp.dma_start(w1b[:, u, :], w1[bass.ds(e, 1), :, :].rearrange("a c n -> (a c) n")
                                     ).then_inc(w_in[u], 16)
                        sp.dma_start(w2b[:, u], w2[bass.ds(e, 1), :, :].rearrange("a (k p) n -> p (a k) n", p=T)
                                     ).then_inc(w_in[u], 16)
                        sp.dma_start(b1b[:, u, :], b1_t[bass.ds(e, 1), :, :].rearrange("a p k -> (a p) k")
                                     ).then_inc(w_in[u], 16)
                        sp.dma_start(b2b[:, u, :], b2[bass.ds(e, 1), :]).then_inc(w_in[u], 16)

            @block.tensor
            def _(pe):
                with pe.Fori(0, TURNS) as i:
                    for u in range(2):
                        pe.wait_ge(gathered[u], 16 * i + 16)
                        nc.tensor.transpose(p_t[u][:, 0:SLOTS], xg[:, u, :], K.ident[:]).then_inc(t_ps[u], 1)
                    for u in range(2):
                        pe.wait_ge(w_in[u], 64 * i + 64)
                        pe.wait_ge(xgt_ready[u], i + 2)
                        for c in range(CH):
                            last = nc.tensor.matmul(p_h[u][:, c], w1b[:, u, c * T:(c + 1) * T], xgt[:, u, :],
                                                    start=True, stop=True)
                        last.then_inc(h_ps[u], 1)
                    for u in range(2):
                        pe.wait_ge(hid_ready[u], CH * i + CH)
                        for c in range(CH):
                            nc.tensor.matmul(p_o[u][:, 0:D], hid[:, u, c], w2b[:, u, c], start=c == 0, stop=False)
                        nc.tensor.matmul(p_o[u][:, 0:D], K.ones[0:1, 0:SLOTS], b2b[:, u, :], start=False,
                                         stop=True).then_inc(o_ps[u], 1)

            @block.scalar
            def _(act):
                with act.Fori(0, TURNS) as i:
                    for u in range(2):
                        act.wait_ge(t_ps[u], i + 1)
                        nc.scalar.activation(xgt[:, u, :], p_t[u][:, 0:SLOTS], ACT.Copy).then_inc(xgt_ready[u], 1)
                    for u in range(2):
                        act.wait_ge(h_ps[u], i + 1)
                        for c in range(CH):
                            nc.scalar.activation(hid[:, u, c], p_h[u][:, c], ACT.Relu,
                                                 bias=b1b[:, u, c:c + 1]).then_inc(hid_ready[u], 1)
                    for u in range(2):
                        act.wait_ge(ob_ready[u], i + 1)
                        act.dma_start(o_dram[bass.ds((2 * i + u) * SLOTS, SLOTS), :], ob[:, u, :]).then_inc(stored[u], 16)
                for u in range(2):
                    act.wait_ge(stored[u], 16 * TURNS + 16)

            @block.vector
            def _(v):
                for u in range(2):
                    v.sem_inc(stored[u], 16)
                with v.Fori(0, TURNS) as i:
                    for u in range(2):
                        v.wait_ge(o_ps[u], i + 2)
                        v.wait_ge(stored[u], 16 * i + 16)
                        nc.vector.tensor_copy(ob[:, u, :], p_o[u][:, 0:D]).then_inc(ob_ready[u], 1)


def combine_block(nc, name, K, route, o_dram, n_seq):
    P = route.picks
    R = n_seq * P
    TURNS = B // (2 * n_seq)
    with Space(nc) as s:
        at = s.sb(name + "_at", [T, 2, R], i32)
        og = s.sb(name + "_og", [T, 2, R, D])
        at_ready = [s.sem(f"{name}_at_ready{u}") for u in range(2)]
        used = [s.sem(f"{name}_used{u}") for u in range(2)]
        got = [[s.sem(f"{name}_got{u}_{r}") for r in range(R)] for u in range(2)]
        own = s.sem(name + "_own")
        dest_c = route.dest[:].rearrange("t b k -> t (b k)")
        gate_c = route.gate[:].rearrange("t b k -> t (b k)")
        with nc.Block() as block:
            @block.gpsimd
            def _(g):
                for u in range(2):
                    g.sem_inc(used[u], 1)
                with g.Fori(0, TURNS) as i:
                    for u in range(2):
                        g.wait_ge(used[u], i + 1)
                        g.tensor_copy(at[:, u, :], dest_c[:, bass.ds((2 * i + u) * R, R)]).then_inc(at_ready[u], 1)
                        g.wait_ge(at_ready[u], i + 1)
                        g.nop(nofuse=True)
                        for r in range(R):
                            g.indirect_dma_start(out=og[:, u, r, :], out_offset=None, in_=o_dram,
                                                 in_offset=bass.IndirectOffsetOnAxis(ap=at[:, u, r:r + 1], axis=0)
                                                 ).then_inc(got[u][r], 16)

            @block.vector
            def _(v):
                with v.Fori(0, TURNS) as i:
                    for u in range(2):
                        for r in range(R):
                            n = (2 * i + u) * R + r
                            k, m = r % P, r // P
                            b = (2 * i + u) * n_seq + m
                            v.wait_ge(got[u][r], 16 * i + 16)
                            if k:
                                v.wait_ge(own, n)
                            ins = nc.vector.scalar_tensor_tensor(out=K.h[:, b, :], in0=og[:, u, r, :],
                                                                 scalar=gate_c[:, bass.ds(n, 1)], in1=K.h[:, b, :],
                                                                 op0=ALU.mult, op1=ALU.add)
                            ins.then_inc(own, 1)
                        v.wait_ge(own, (2 * i + u + 1) * R)
                        v.sem_inc(used[u], 1)


def top1_experts(nc, W, K, name, experts, chunks, soft_gate):
    NT = 2 * -(-(NTOK // SLOTS + experts - 1) // 2)
    xn_dram = nc.dram_tensor(name + "_xn_dram", (NTOK, D), f32, kind="Internal").ap()
    o_dram = nc.dram_tensor(name + "_o_dram", (NT * SLOTS, D), f32, kind="Internal").ap()
    with Space(nc) as s:
        route = Route(s, name, experts, 1, NT)
        with Space(nc) as s2:
            xn = s2.sb(name + "_xn", [T, B, D])
            logits = s2.sb(name + "_logits", [T, B, experts])
            layer_norm_block(nc, name + "_ln", K.h, xn)
            router_logits_block(nc, name + "_r", K, xn, xn_dram, W[name + "_Wr"], experts, logits, W[name + "_br"])
            index = s2.sb(name + "_index", [T, B, 1])
            top = s2.sb(name + "_top", [T, B, 8])
            which = s2.sb(name + "_which", [T, B, 8], u32)
            low = s2.sb(name + "_low", [T, B, experts])
            total = s2.sb(name + "_total", [T, B])
            own = s2.sem(name + "_own")
            low_ready = s2.sem(name + "_low_ready")
            exp_ready = s2.sem(name + "_exp_ready")
            with nc.Block() as block:
                @block.scalar
                def _(act):
                    if soft_gate:
                        act.wait_ge(low_ready, 1)
                        nc.scalar.activation(low[:], low[:], ACT.Exp).then_inc(exp_ready, 1)

                @block.vector
                def _(v):
                    chain = Own(v, own)
                    if soft_gate:
                        chain.done(nc.vector.tensor_reduce(out=total[:], in_=logits[:], axis=AX.X, op=ALU.max))
                        nc.vector.tensor_tensor(low[:], logits[:], per_row(total[:], experts),
                                                ALU.subtract).then_inc(low_ready, 1)
                        v.wait_ge(exp_ready, 1)
                        chain.done(nc.vector.tensor_reduce(out=total[:], in_=low[:], axis=AX.X, op=ALU.add))
                        nc.vector.reciprocal(route.gate[:].rearrange("t b k -> t (b k)"), total[:])
                        values = low
                    else:
                        nc.vector.memset(route.gate[:], 1.0)
                        values = logits
                    for b in range(B):
                        ins = nc.vector.max(top[:, b, :], values[:, b, :])
                    chain.done(ins)
                    for b in range(B):
                        ins = nc.vector.max_index(which[:, b, :], top[:, b, :], values[:, b, :])
                    chain.done(ins)
                    chain.done(nc.vector.tensor_copy(index[:], which[:, :, 0:1]))
            sort_block(nc, name + "_sort", K, route, index)
        expert_tiles_block(nc, name + "_x", K, route, xn_dram, o_dram, W[name + "_W1"], W[name + "_b1_t"], W[name + "_W2"],
                           W[name + "_b2"], chunks)
        combine_block(nc, name + "_c", K, route, o_dram, 4)
    end_of_layer(nc)


def householder_attention(nc, W, K):
    NH, DH, PER = 8, 32, 4
    F = NH * DH
    BK = 16
    STEPS = T // BK - 1
    with Space(nc) as s:
        xn = s.sb("a1_xn", [T, B, D])
        layer_norm_block(nc, "a1_ln", K.h, xn)
        wkv = s.sb("a1_wkv", [D, 2, F])
        wq = s.sb("a1_wq", [D, F])
        ww = s.sb("a1_ww", [D, F])
        wbg = s.sb("a1_wbg", [D, 2 * NH])
        wo = s.sb("a1_wo", [T, 2, D])
        bbg = s.sb("a1_bbg", [T, 2 * NH])
        xt = s.sb("a1_xt", [D, B, T])
        kv = s.sb("a1_kv", [T, B, 2, F])
        wn = s.sb("a1_wn", [T, B, F])
        bg = s.sb("a1_bg", [T, B, 2 * NH])
        ss = s.sb("a1_ss", [T, B, NH])
        rw = s.sb("a1_rw", [T, B, NH])
        masks = s.sb("a1_masks", [T, 2, T])
        packs = s.sb("a1_packs", [T, 5, BK])
        loads = s.sem("a1_loads")
        with Space(nc) as s2:
            xs = s2.sb("a1_xs", [T, 2, D])
            xts = s2.sb("a1_xts", [D, 2, T])
            sq = s2.sb("a1_sq", [T, 2, F])
            p_t = [s2.ps(f"a1_p_t{u}", [D, 512]) for u in range(2)]
            p_kv = [s2.ps(f"a1_p_kv{u}", [T, 2, F]) for u in range(2)]
            p_w = [s2.ps(f"a1_p_w{u}", [T, 512]) for u in range(2)]
            xs_ready, t_ps, xts_ready, kv_ps, w_ps, kv_done, w_done, sq_ready = (
                [s2.sem(f"a1_{n}{u}") for u in range(2)] for n in (
                    "xs_ready", "t_ps", "xts_ready", "kv_ps", "w_ps", "kv_done", "w_done", "sq_ready"))
            with nc.Block() as block:
                @block.sync
                def _(sp):
                    sp.dma_start(wkv[:, 0], W["L1_attn_Wk_t"]).then_inc(loads, 16)
                    sp.dma_start(wkv[:, 1], W["L1_attn_Wv_t"]).then_inc(loads, 16)
                    sp.dma_start(wq[:], W["L1_attn_Wq_t"]).then_inc(loads, 16)
                    sp.dma_start(ww[:], W["L1_attn_Ww_t"]).then_inc(loads, 16)
                    sp.dma_start(wbg[:, 0:NH], W["L1_attn_Wbeta_t"]).then_inc(loads, 16)
                    sp.dma_start(wbg[:, NH:2 * NH], W["L1_attn_Wg_t"]).then_inc(loads, 16)
                    sp.dma_start(bbg[:, 0:NH], W["L1_attn_bbeta"].partition_broadcast(T)).then_inc(loads, 16)
                    sp.dma_start(bbg[:, NH:2 * NH], W["L1_attn_bg"].partition_broadcast(T)).then_inc(loads, 16)
                    sp.dma_start(wo[:], W["L1_attn_Wo_t"].rearrange("(g p) n -> p g n", p=T)).then_inc(loads, 16)
                    sp.dma_start(masks[:], W["block_masks"]).then_inc(loads, 16)
                    sp.dma_start(packs[:], W["packed_masks"]).then_inc(loads, 16)
                    sp.wait_ge(loads, 176)

                @block.vector
                def _(v):
                    for u in range(2):
                        v.sem_inc(xts_ready[u], 1)
                    with v.Fori(0, B // 2) as i:
                        for u in range(2):
                            b = 2 * i + u
                            v.wait_ge(xts_ready[u], i + 1)
                            nc.vector.tensor_copy(xs[:, u], xn[:, b, :]).then_inc(xs_ready[u], 1)
                        for u in range(2):
                            b = 2 * i + u
                            v.wait_ge(w_ps[u], i + 1)
                            nc.vector.tensor_tensor(bg[:, b, :], p_w[u][:, F:F + 2 * NH], bbg[:], ALU.add)
                            nc.vector.tensor_copy(wn[:, b, :], p_w[u][:, 0:F]).then_inc(w_done[u], 1)
                            v.wait_ge(w_done[u], i + 1)
                            nc.vector.tensor_tensor(sq[:, u], wn[:, b, :], wn[:, b, :], ALU.mult).then_inc(sq_ready[u], 1)
                            v.wait_ge(sq_ready[u], i + 1)
                            nc.vector.tensor_reduce(out=ss[:, b, :], in_=sq[:, u].rearrange("t (h d) -> t h d", d=DH),
                                                    axis=AX.X, op=ALU.add)

                @block.scalar
                def _(act):
                    with act.Fori(0, B // 2) as i:
                        for u in range(2):
                            act.wait_ge(t_ps[u], i + 1)
                            nc.scalar.activation(xts[:, u], p_t[u][:, 0:T], ACT.Copy)
                            nc.scalar.activation(xt[:, 2 * i + u, :], p_t[u][:, 0:T], ACT.Copy).then_inc(xts_ready[u], 1)
                        for u in range(2):
                            act.wait_ge(kv_ps[u], i + 1)
                            nc.scalar.activation(kv[:, 2 * i + u], p_kv[u][:], ACT.Copy).then_inc(kv_done[u], 1)

                @block.tensor
                def _(pe):
                    pe.wait_ge(loads, 176)
                    for u in range(2):
                        pe.sem_inc(kv_done[u], 1)
                    with pe.Fori(0, B // 2) as i:
                        for u in range(2):
                            pe.wait_ge(xs_ready[u], i + 1)
                            nc.tensor.transpose(p_t[u][:, 0:T], xs[:, u], K.ident[:]).then_inc(t_ps[u], 1)
                        for u in range(2):
                            pe.wait_ge(xts_ready[u], i + 2)
                            pe.wait_ge(kv_done[u], i + 1)
                            nc.tensor.matmul(p_kv[u][:], xts[:, u], wkv[:], start=True, stop=True).then_inc(kv_ps[u], 1)
                            nc.tensor.matmul(p_w[u][:, 0:F], xts[:, u], ww[:], start=True, stop=True)
                            nc.tensor.matmul(p_w[u][:, F:F + 2 * NH], xts[:, u], wbg[:], start=True,
                                             stop=True).then_inc(w_ps[u], 1)
        own = s.sem("a1_own")
        norm_ready = s.sem("a1_norm_ready")
        exp_ready = s.sem("a1_exp_ready")
        with nc.Block() as block:
            @block.scalar
            def _(act):
                nc.scalar.activation(rw[:], ss[:], ACT.Sqrt).then_inc(norm_ready, 1)
                nc.scalar.activation(bg[:], bg[:], ACT.Exp, scale=-1.0).then_inc(exp_ready, 1)

            @block.vector
            def _(v):
                chain = Own(v, own)
                v.wait_ge(norm_ready, 1)
                chain.done(nc.vector.tensor_scalar(rw[:], rw[:], 1e-6, None, ALU.add))
                nc.vector.reciprocal(rw[:].rearrange("t b h -> t (b h)"), rw[:].rearrange("t b h -> t (b h)"))
                v.wait_ge(exp_ready, 1)
                chain.done(nc.vector.tensor_scalar(bg[:], bg[:], 1.0, None, ALU.add))
                chain.done(nc.vector.reciprocal(bg[:].rearrange("t b h -> t (b h)"), bg[:].rearrange("t b h -> t (b h)")))
                nc.vector.tensor_scalar(bg[:, :, 0:NH], bg[:, :, 0:NH], 2.0, None, ALU.mult)
                chain.done(nc.vector.tensor_scalar(bg[:, :, NH:2 * NH], bg[:, :, NH:2 * NH], DH ** -0.5, None, ALU.mult))

        ws = s.sb("a1_ws", [T, 2, F])
        wt = s.sb("a1_wt", [T, 4, T])
        qkt = s.sb("a1_qkt", [T, 4, T])
        vt = s.sb("a1_vt", [T, 2, T])
        lraw = s.sb("a1_lraw", [T, 2, PER, T])
        lbd = s.sb("a1_lbd", [T, 2, PER, T])
        bm = s.sb("a1_bm", [T, 2, PER, T])
        am = s.sb("a1_am", [T, 2, PER, T])
        cm = s.sb("a1_cm", [T, 2, PER, T])
        mt = s.sb("a1_mt", [T, 2, PER, T])
        pm = s.sb("a1_pm", [T, 2, PER, BK])
        yp = s.sb("a1_yp", [T, 2, PER, BK])
        ye = s.sb("a1_ye", [T, 2, PER, T])
        xe = s.sb("a1_xe", [T, 2, PER, T])
        r0 = s.sb("a1_r0", [T, 2, PER * DH])
        r1 = s.sb("a1_r1", [T, 2, PER * DH])
        uu = s.sb("a1_uu", [T, 2, PER * DH])
        ut = s.sb("a1_ut", [T, 2, T])
        at_ = s.sb("a1_at", [T, 2, T])
        att = s.sb("a1_att", [T, 2, T])
        p_g = s.ps("a1_p_g", [T, PER, 4, T])
        p_s = [s.ps(f"a1_p_s{g}", [T, 4, T]) for g in range(2)]
        p_b = [s.ps(f"a1_p_b{g}", [T, 4, T]) for g in range(2)]
        wt_ready, v_ps, b_ready, done, ws_ready, wt_ps, qk_ps, qk_ready, v_ready, att_ps, att_ready, h_ps = (
            s.sem("a1_" + n) for n in ("wt_ready", "v_ps", "b_ready", "done", "ws_ready", "wt_ps", "qk_ps", "qk_ready",
                                       "v_ready", "att_ps", "att_ready", "h_ps"))
        g_ps, lraw_ready, g_ready, p_ps, y_ready, pm_ready, dy_ps, ye_ready, xt_ps, xe_ready, r_ps, r_ready, r1_ps, m_ps, \
            m_ready, u_ready, it_ps, ut_ps, ut_ready, c_ps, c_ready, o_ps, o_ready, own_g = (
                [s.sem(f"a1_{n}_{g}") for g in range(2)] for n in (
                    "g_ps", "lraw_ready", "g_ready", "p_ps", "y_ready", "pm_ready", "dy_ps", "ye_ready", "xt_ps",
                    "xe_ready", "r_ps", "r_ready", "r1_ps", "m_ps", "m_ready", "u_ready", "it_ps", "ut_ps", "ut_ready",
                    "c_ps", "c_ready", "o_ps", "o_ready", "own_g"))
        LV = 4

        def heads(tile):
            return tile.rearrange("t (h d) -> t h d", d=DH)

        def over_heads(m):
            return per_tile(m, PER)

        def expanded(packed):
            return packed.unsqueeze(2).to_broadcast([T, PER, T // BK, BK])

        bd = masks[:, 0].rearrange("t (k c) -> t k c", c=BK).unsqueeze(1).to_broadcast([T, PER, T // BK, BK])
        with nc.Block() as block:
            @block.vector
            def _(v):
                v.sem_inc(done, 1)
                with v.Fori(0, B) as b:
                    v.wait_ge(done, b + 1)
                    nc.vector.tensor_tensor(heads(ws[:, 0]), heads(wn[:, b, :]), rw[:, b, :].unsqueeze(2)
                                            .to_broadcast([T, NH, DH]), ALU.mult).then_inc(ws_ready, 1)
                    v.wait_ge(ws_ready, 2 * b + 1)
                    nc.vector.tensor_tensor(heads(ws[:, 1]), heads(ws[:, 0]), bg[:, b, 0:NH].unsqueeze(2)
                                            .to_broadcast([T, NH, DH]), ALU.mult).then_inc(ws_ready, 1)
                    for g in range(2):
                        v.wait_ge(g_ps[g], b + 1)
                        nc.vector.tensor_tensor(lbd[:, g], p_g[:, :, 0], over_heads(masks[:, 0]), ALU.mult)
                        nc.vector.tensor_tensor(bm[:, g], p_g[:, :, 1], over_heads(K.before[:]), ALU.mult)
                        nc.vector.tensor_tensor(am[:, g], p_g[:, :, 2], over_heads(K.up_to[:]),
                                                ALU.mult).then_inc(g_ready[g], 1)
                    for l in range(LV):
                        for g in range(2):
                            v.wait_ge(p_ps[g], LV * b + l + 1)
                            nc.vector.tensor_tensor(pm[:, g], p_s[g][:, 0, 0:PER * BK].rearrange(
                                "t (h c) -> t h c", c=BK), over_heads(packs[:, 1 + l]), ALU.mult).then_inc(pm_ready[g], 1)
                            if l == 0:
                                v.wait_ge(pm_ready[g], LV * b + 1)
                                nc.vector.tensor_tensor(yp[:, g], over_heads(packs[:, 0]), pm[:, g],
                                                        ALU.subtract).then_inc(y_ready[g], 1)
                        for g in range(2):
                            if l:
                                v.wait_ge(dy_ps[g], (LV - 1) * b + l)
                                nc.vector.tensor_tensor(yp[:, g], yp[:, g], p_s[g][:, 1, 0:PER * BK].rearrange(
                                    "t (h c) -> t h c", c=BK), ALU.subtract).then_inc(y_ready[g], 1)
                            v.wait_ge(y_ready[g], LV * b + l + 1)
                            nc.vector.tensor_tensor(ye[:, g].rearrange("t h (k c) -> t h k c", c=BK), expanded(yp[:, g]),
                                                    bd, ALU.mult).then_inc(ye_ready[g], 1)
                    for g in range(2):
                        v.wait_ge(r1_ps[g], b + 1)
                        nc.vector.tensor_copy(r1[:, g], p_s[g][:, 3]).then_inc(own_g[g], 1)
                        v.wait_ge(m_ps[g], b + 1)
                        nc.vector.tensor_tensor(mt[:, g], p_b[g][:], over_heads(masks[:, 1]), ALU.mult).then_inc(m_ready[g], 1)
                    for k in range(STEPS):
                        for g in range(2):
                            v.wait_ge(it_ps[g], STEPS * b + k + 1)
                            if k == 0:
                                v.wait_ge(own_g[g], b + 1)
                            nc.vector.tensor_tensor(uu[:, g], r1[:, g], p_s[g][:, 2], ALU.subtract).then_inc(u_ready[g], 1)
                    for g in range(2):
                        v.wait_ge(c_ps[g], b + 1)
                        nc.vector.tensor_tensor(cm[:, g], p_g[:, :, 3], over_heads(K.up_to[:]), ALU.mult).then_inc(c_ready[g], 1)
                    for g in range(2):
                        v.wait_ge(o_ps[g], b + 1)
                        nc.vector.tensor_tensor(heads(at_[:, g]), heads(p_s[g][:, 0]),
                                                bg[:, b, NH + PER * g:NH + PER * g + PER].unsqueeze(2)
                                                .to_broadcast([T, PER, DH]), ALU.mult).then_inc(o_ready[g], 1)
                    v.wait_ge(h_ps, b + 1)
                    nc.vector.tensor_tensor(K.h[:, b, :], K.h[:, b, :], p_b[1][:, 0], ALU.add).then_inc(done, 1)

            @block.scalar
            def _(act):
                with act.Fori(0, B) as b:
                    act.wait_ge(wt_ps, b + 1)
                    nc.scalar.activation(wt[:], p_b[0][:], ACT.Copy).then_inc(wt_ready, 1)
                    act.wait_ge(qk_ps, b + 1)
                    nc.scalar.activation(qkt[:], p_b[1][:], ACT.Copy).then_inc(qk_ready, 1)
                    act.wait_ge(v_ps, b + 1)
                    nc.scalar.activation(vt[:], p_s[0][:, 0:2], ACT.Copy).then_inc(v_ready, 1)
                    for g in range(2):
                        act.wait_ge(g_ready[g], b + 1)
                        nc.scalar.activation(lraw[:, g], p_g[:, :, 0], ACT.Copy).then_inc(lraw_ready[g], 1)
                    for l in range(LV - 1):
                        for g in range(2):
                            act.wait_ge(xt_ps[g], (LV - 1) * b + l + 1)
                            nc.scalar.activation(xe[:, g], p_b[g][:], ACT.Copy).then_inc(xe_ready[g], 1)
                        if l == 0:
                            for g in range(2):
                                act.wait_ge(r_ps[g], b + 1)
                                nc.scalar.activation(r0[:, g], p_s[g][:, 2], ACT.Copy).then_inc(r_ready[g], 1)
                    for g in range(2):
                        act.wait_ge(ut_ps[g], b + 1)
                        nc.scalar.activation(ut[:, g], p_b[g][:, 0], ACT.Copy, scale=-1.0).then_inc(ut_ready[g], 1)
                    act.wait_ge(att_ps, b + 1)
                    nc.scalar.activation(att[:], p_b[0][:, 0:2], ACT.Copy).then_inc(att_ready, 1)

            @block.tensor
            def _(pe):
                with pe.Fori(0, B) as b:
                    pe.wait_ge(ws_ready, 2 * b + 2)
                    for n in range(4):
                        last = nc.tensor.transpose(p_b[0][:, n], ws[:, n // 2, (n % 2) * T:(n % 2 + 1) * T], K.ident[:])
                    last.then_inc(wt_ps, 1)
                    for n in range(4):
                        w = wq if n < 2 else wkv[:, 0]
                        last = nc.tensor.matmul(p_b[1][:, n], w[:, (n % 2) * T:(n % 2 + 1) * T], xt[:, b, :],
                                                start=True, stop=True)
                    last.then_inc(qk_ps, 1)
                    for g in range(2):
                        last = nc.tensor.matmul(p_s[0][:, g], wkv[:, 1, g * T:(g + 1) * T], xt[:, b, :],
                                                start=True, stop=True)
                    last.then_inc(v_ps, 1)
                    pe.wait_ge(wt_ready, b + 1)
                    pe.wait_ge(qk_ready, b + 1)
                    pe.wait_ge(v_ready, b + 1)
                    for g in range(2):
                        if g:
                            pe.wait_ge(lraw_ready[0], b + 1)
                        for j in range(PER):
                            r = slice(DH * j, DH * j + DH)
                            nc.tensor.matmul(p_g[:, j, 0], wt[r, 2 + g], wt[r, g], start=True, stop=True)
                            nc.tensor.matmul(p_g[:, j, 1], vt[r, g], wt[r, 2 + g], start=True, stop=True)
                            last = nc.tensor.matmul(p_g[:, j, 2], qkt[r, 2 + g], qkt[r, g], start=True, stop=True)
                        last.then_inc(g_ps[g], 1)
                    for l in range(LV):
                        for g in range(2):
                            if l == 0:
                                pe.wait_ge(g_ready[g], b + 1)
                            else:
                                pe.wait_ge(ye_ready[g], LV * b + l)
                                if l == 1:
                                    pe.wait_ge(r_ready[g], b + 1)
                            for h in range(PER):
                                y = packs[:, 0] if l == 0 else yp[:, g, h]
                                last = nc.tensor.matmul(p_s[g][:, 0, h * BK:(h + 1) * BK], lbd[:, g, h], y,
                                                        start=True, stop=True)
                            last.then_inc(p_ps[g], 1)
                        if l:
                            for g in range(2):
                                pe.wait_ge(pm_ready[g], LV * b + l + 1)
                                pe.wait_ge(xe_ready[g], (LV - 1) * b + l)
                                for h in range(PER):
                                    last = nc.tensor.matmul(p_s[g][:, 1, h * BK:(h + 1) * BK], xe[:, g, h], pm[:, g, h],
                                                            start=True, stop=True)
                                last.then_inc(dy_ps[g], 1)
                        if l < LV - 1:
                            for g in range(2):
                                pe.wait_ge(ye_ready[g], LV * b + l + 1)
                                for h in range(PER):
                                    last = nc.tensor.transpose(p_b[g][:, h], ye[:, g, h], K.ident[:])
                                last.then_inc(xt_ps[g], 1)
                        if l == 0:
                            for g in range(2):
                                for h in range(PER):
                                    last = nc.tensor.matmul(p_s[g][:, 2, h * DH:(h + 1) * DH], bm[:, g, h],
                                                            kv[:, b, 0, (PER * g + h) * DH:(PER * g + h + 1) * DH],
                                                            start=True, stop=True)
                                last.then_inc(r_ps[g], 1)
                    for g in range(2):
                        pe.wait_ge(ye_ready[g], LV * b + LV)
                        for h in range(PER):
                            last = nc.tensor.matmul(p_s[g][:, 3, h * DH:(h + 1) * DH], ye[:, g, h],
                                                    r0[:, g, h * DH:(h + 1) * DH], start=True, stop=True)
                        last.then_inc(r1_ps[g], 1)
                        pe.wait_ge(lraw_ready[g], b + 1)
                        for h in range(PER):
                            last = nc.tensor.matmul(p_b[g][:, h], lraw[:, g, h], ye[:, g, h], start=True, stop=True)
                        last.then_inc(m_ps[g], 1)
                    for k in range(STEPS):
                        for g in range(2):
                            if k == 0:
                                pe.wait_ge(m_ready[g], b + 1)
                            else:
                                pe.wait_ge(u_ready[g], STEPS * b + k)
                            for h in range(PER):
                                u_ = (r1 if k == 0 else uu)[:, g, h * DH:(h + 1) * DH]
                                last = nc.tensor.matmul(p_s[g][:, 2, h * DH:(h + 1) * DH], mt[:, g, h], u_,
                                                        start=True, stop=True)
                            last.then_inc(it_ps[g], 1)
                    for g in range(2):
                        pe.wait_ge(u_ready[g], STEPS * b + STEPS)
                        nc.tensor.transpose(p_b[g][:, 0], uu[:, g], K.ident[:]).then_inc(ut_ps[g], 1)
                    for g in range(2):
                        if g:
                            pe.wait_ge(c_ready[0], b + 1)
                        pe.wait_ge(ut_ready[g], b + 1)
                        for j in range(PER):
                            r = slice(DH * j, DH * j + DH)
                            last = nc.tensor.matmul(p_g[:, j, 3], ut[r, g], qkt[r, g], start=True, stop=True)
                        last.then_inc(c_ps[g], 1)
                    for g in range(2):
                        pe.wait_ge(c_ready[g], b + 1)
                        for h in range(PER):
                            at = (PER * g + h) * DH
                            out = p_s[g][:, 0, h * DH:(h + 1) * DH]
                            nc.tensor.matmul(out, am[:, g, h], kv[:, b, 1, at:at + DH], start=True, stop=False)
                            last = nc.tensor.matmul(out, cm[:, g, h], ws[:, 0, at:at + DH], start=False, stop=True)
                        last.then_inc(o_ps[g], 1)
                    for g in range(2):
                        pe.wait_ge(o_ready[g], b + 1)
                        last = nc.tensor.transpose(p_b[0][:, g], at_[:, g], K.ident[:])
                    last.then_inc(att_ps, 1)
                    pe.wait_ge(att_ready, b + 1)
                    for g in range(2):
                        last = nc.tensor.matmul(p_b[1][:, 0], att[:, g], wo[:, g], start=g == 0, stop=g == 1)
                    last.then_inc(h_ps, 1)
    end_of_layer(nc)


def capacity_experts(nc, W, K):
    E, P = 32, 2
    CAP = math.ceil(1.25 * NTOK * P / E)
    REST = CAP - SLOTS
    NT = 2 * E
    name = "L1_ffn"
    xn_dram = nc.dram_tensor(name + "_xn_dram", (NTOK, D), f32, kind="Internal").ap()
    o_dram = nc.dram_tensor(name + "_o_dram", (E * CAP, D), f32, kind="Internal").ap()
    with Space(nc) as s:
        route = Route(s, name, E, P, NT)
        xn = s.sb(name + "_xn", [T, B, D])
        layer_norm_block(nc, name + "_ln", K.h, xn)
        with Space(nc) as s2:
            prob = s2.sb(name + "_prob", [T, B, E])
            router_logits_block(nc, name + "_r", K, xn, xn_dram, W["L1_ffn_Wg"], E, prob)
            index = s2.sb(name + "_index", [T, B, P])
            top = s2.sb(name + "_top", [T, B, 8])
            which = s2.sb(name + "_which", [T, B, 8], u32)
            total = s2.sb(name + "_total", [T, B])
            own = s2.sem(name + "_own")
            low_ready = s2.sem(name + "_low_ready")
            exp_ready = s2.sem(name + "_exp_ready")
            with nc.Block() as block:
                @block.scalar
                def _(act):
                    act.wait_ge(low_ready, 1)
                    nc.scalar.activation(prob[:], prob[:], ACT.Exp).then_inc(exp_ready, 1)

                @block.vector
                def _(v):
                    chain = Own(v, own)
                    chain.done(nc.vector.tensor_reduce(out=total[:], in_=prob[:], axis=AX.X, op=ALU.max))
                    nc.vector.tensor_tensor(prob[:], prob[:], per_row(total[:], E), ALU.subtract).then_inc(low_ready, 1)
                    v.wait_ge(exp_ready, 1)
                    chain.done(nc.vector.tensor_reduce(out=total[:], in_=prob[:], axis=AX.X, op=ALU.add))
                    chain.done(nc.vector.reciprocal(total[:], total[:]))
                    chain.done(nc.vector.tensor_tensor(prob[:], prob[:], per_row(total[:], E), ALU.mult))
                    for b in range(B):
                        ins = nc.vector.max(top[:, b, :], prob[:, b, :])
                    chain.done(ins)
                    for b in range(B):
                        ins = nc.vector.max_index(which[:, b, :], top[:, b, :], prob[:, b, :])
                    chain.done(ins)
                    nc.vector.tensor_copy(index[:], which[:, :, 0:P])
                    chain.done(nc.vector.tensor_tensor(total[:], top[:, :, 0], top[:, :, 1], ALU.add))
                    chain.done(nc.vector.tensor_scalar(total[:], total[:], 1e-9, None, ALU.max))
                    chain.done(nc.vector.reciprocal(total[:], total[:]))
                    chain.done(nc.vector.tensor_tensor(route.gate[:], top[:, :, 0:P], per_row(total[:], P), ALU.mult))
            sort_block(nc, name + "_sort", K, route, index, capacity=CAP)
        capacity_tiles_block(nc, name + "_x", K, route, xn_dram, o_dram, W, REST)
        contrib = s.sb(name + "_contrib", [T, B])
        lost = s.sb(name + "_lost", [T, B])
        held = s.sb(name + "_held", [T, B])
        own = s.sem(name + "_own2")
        with nc.Block() as block:
            @block.vector
            def _(v):
                chain = Own(v, own)
                chain.done(nc.vector.tensor_tensor(contrib[:], route.gate[:, :, 0], route.gate[:, :, 1], ALU.add))
                nc.vector.tensor_scalar(lost[:], contrib[:], 1e-12, None, ALU.is_le)
                chain.done(nc.vector.tensor_scalar(held[:], contrib[:], 1e-12, None, ALU.is_gt))
                chain.done(nc.vector.tensor_tensor(route.gate[:], route.gate[:], per_row(held[:], P), ALU.mult))
                chain.done(nc.vector.tensor_tensor(xn[:], xn[:], per_row(lost[:], D), ALU.mult))
                chain.done(nc.vector.tensor_tensor(K.h[:], K.h[:], xn[:], ALU.add))
        combine_block(nc, name + "_c", K, route, o_dram, 2)
    end_of_layer(nc)


def capacity_tiles_block(nc, name, K, route, xn_dram, o_dram, W, rest):
    E = route.experts
    CAP = SLOTS + rest
    with Space(nc) as s:
        who2 = s.sb(name + "_who2", [SLOTS, 2, 2], i32)
        xg = s.sb(name + "_xg", [SLOTS, 2, 2, D])
        xgt = s.sb(name + "_xgt", [D, 2, CAP])
        w1b = s.sb(name + "_w1b", [D, 2, T])
        w2b = s.sb(name + "_w2b", [T, 2, D])
        b1b = s.sb(name + "_b1b", [T, E])
        b2b = s.sb(name + "_b2b", [1, 2, D])
        hid = s.sb(name + "_hid", [T, 2, CAP])
        ob = s.sb(name + "_ob", [SLOTS, 2, 2, D])
        p_t = [s.ps(f"{name}_p_t{u}", [D, 512]) for u in range(2)]
        p_h = [s.ps(f"{name}_p_h{u}", [T, 512]) for u in range(2)]
        p_o = [s.ps(f"{name}_p_o{u}", [SLOTS, 4, D]) for u in range(2)]
        b1_in = s.sem(name + "_b1_in")
        who_ready, gathered, gathered_rest, w_in, t_ps, xgt_ready, h_ps, hid_ready, o_ps, ob_ready, stored = (
            [s.sem(f"{name}_{n}{u}") for u in range(2)] for n in (
                "who_ready", "gathered", "gathered_rest", "w_in", "t_ps", "xgt_ready", "h_ps", "hid_ready", "o_ps",
                "ob_ready", "stored"))
        with nc.Block() as block:
            @block.gpsimd
            def _(g):
                for u in range(2):
                    g.sem_inc(xgt_ready[u], 1)
                with g.Fori(0, E // 2) as i:
                    for u in range(2):
                        g.wait_ge(xgt_ready[u], i + 1)
                        g.tensor_copy(who2[:, u], route.who[:, bass.ds((2 * i + u) * 2, 2)]).then_inc(who_ready[u], 1)
                        g.wait_ge(who_ready[u], i + 1)
                        g.nop(nofuse=True)
                        g.indirect_dma_start(out=xg[:, u, 0, :], out_offset=None, in_=xn_dram,
                                             in_offset=bass.IndirectOffsetOnAxis(ap=who2[:, u, 0:1], axis=0)
                                             ).then_inc(gathered[u], 16)
                        g.indirect_dma_start(out=xg[0:rest, u, 1, :], out_offset=None, in_=xn_dram,
                                             in_offset=bass.IndirectOffsetOnAxis(ap=who2[0:rest, u, 1:2], axis=0)
                                             ).then_inc(gathered_rest[u], 16)

            @block.sync
            def _(sp):
                sp.dma_start(b1b[:], W["L1_ffn_b1_t"]).then_inc(b1_in, 16)
                for u in range(2):
                    sp.sem_inc(o_ps[u], 1)
                with sp.Fori(0, E // 2) as i:
                    for u in range(2):
                        e = 2 * i + u
                        sp.wait_ge(o_ps[u], i + 1)
                        sp.dma_start(w1b[:, u, :], W["L1_ffn_W1"][bass.ds(e, 1), :, :].rearrange("a c n -> (a c) n")
                                     ).then_inc(w_in[u], 16)
                        sp.dma_start(w2b[:, u, :], W["L1_ffn_W2"][bass.ds(e, 1), :, :].rearrange("a c n -> (a c) n")
                                     ).then_inc(w_in[u], 16)
                        sp.dma_start(b2b[:, u, :], W["L1_ffn_b2"][bass.ds(e, 1), :]).then_inc(w_in[u], 16)

            @block.tensor
            def _(pe):
                with pe.Fori(0, E // 2) as i:
                    for u in range(2):
                        pe.wait_ge(gathered[u], 16 * i + 16)
                        pe.wait_ge(gathered_rest[u], 16 * i + 16)
                        nc.tensor.transpose(p_t[u][:, 0:SLOTS], xg[:, u, 0, :], K.ident[:])
                        nc.tensor.transpose(p_t[u][:, SLOTS:CAP], xg[0:rest, u, 1, :],
                                            K.ident[0:rest, 0:rest]).then_inc(t_ps[u], 1)
                    for u in range(2):
                        pe.wait_ge(w_in[u], 48 * i + 48)
                        pe.wait_ge(xgt_ready[u], i + 2)
                        nc.tensor.matmul(p_h[u][:, 0:CAP], w1b[:, u, :], xgt[:, u, :], start=True,
                                         stop=True).then_inc(h_ps[u], 1)
                    for u in range(2):
                        pe.wait_ge(hid_ready[u], i + 1)
                        for n, (at, rows) in enumerate(((0, SLOTS), (SLOTS, rest))):
                            nc.tensor.matmul(p_o[u][0:rows, n], hid[:, u, at:at + rows], w2b[:, u, :], start=True,
                                             stop=False)
                            last = nc.tensor.matmul(p_o[u][0:rows, n], K.ones[0:1, 0:rows], b2b[:, u, :], start=False,
                                                    stop=True)
                        last.then_inc(o_ps[u], 1)

            @block.scalar
            def _(act):
                act.wait_ge(b1_in, 16)
                with act.Fori(0, E // 2) as i:
                    for u in range(2):
                        act.wait_ge(t_ps[u], i + 1)
                        nc.scalar.activation(xgt[:, u, :], p_t[u][:, 0:CAP], ACT.Copy).then_inc(xgt_ready[u], 1)
                    for u in range(2):
                        act.wait_ge(h_ps[u], i + 1)
                        nc.scalar.activation(hid[:, u, :], p_h[u][:, 0:CAP], ACT.Relu,
                                             bias=b1b[:, bass.ds(2 * i + u, 1)]).then_inc(hid_ready[u], 1)
                    for u in range(2):
                        row = (2 * i + u) * CAP
                        act.wait_ge(ob_ready[u], i + 1)
                        act.dma_start(o_dram[bass.ds(row, SLOTS), :], ob[:, u, 0, :]).then_inc(stored[u], 16)
                        act.dma_start(o_dram[bass.ds(row + SLOTS, rest), :], ob[0:rest, u, 1, :]).then_inc(stored[u], 16)
                for u in range(2):
                    act.wait_ge(stored[u], 16 * E + 32)

            @block.vector
            def _(v):
                for u in range(2):
                    v.sem_inc(stored[u], 32)
                with v.Fori(0, E // 2) as i:
                    for u in range(2):
                        v.wait_ge(o_ps[u], i + 2)
                        v.wait_ge(stored[u], 32 * i + 32)
                        nc.vector.tensor_copy(ob[:, u, 0, :], p_o[u][:, 0])
                        nc.vector.tensor_copy(ob[0:rest, u, 1, :], p_o[u][0:rest, 1]).then_inc(ob_ready[u], 1)


def layer2_attention(nc, W, K):
    NH = 8
    with Space(nc) as s:
        xn = s.sb("a2_xn", [T, B, D])
        layer_norm_block(nc, "a2_ln", K.h, xn)
        wv = s.sb("a2_wv", [D, NH, D])
        bv = s.sb("a2_bv", [D, NH])
        fc = s.sb("a2_fc", [D, NH, D])
        fb = s.sb("a2_fb", [T, D])
        lg = s.sb("a2_lg", [T, D])
        lb = s.sb("a2_lb", [T, D])
        xs = s.sb("a2_xs", [D, B])
        vs = s.sb("a2_vs", [D, NH, B])
        at_ = s.sb("a2_at", [B, D])
        pick = s.sb("a2_pick", [B, B, T])
        y = s.sb("a2_y", [T, B, D])
        p_x = s.ps("a2_p_x", [T, 512])
        p_v = s.ps("a2_p_v", [T, 512])
        p_o = s.ps("a2_p_o", [T, 512])
        p_y = [s.ps(f"a2_p_y{n}", [T, 4, D]) for n in range(4)]
        loads, x_ps, xs_ready, v_ps, vs_ready, o_ps, at_ready, y_ps, pick_ready, base_ready, own = (
            s.sem("a2_" + n) for n in ("loads", "x_ps", "xs_ready", "v_ps", "vs_ready", "o_ps", "at_ready", "y_ps",
                                       "pick_ready", "base_ready", "own"))
        vals = p_v[:, 0:NH * B].rearrange("d (h b) -> d h b", h=NH)
        with nc.Block() as block:
            @block.sync
            def _(sp):
                sp.dma_start(wv[:].rearrange("c h d -> c (h d)"), W["L2_attn_wv"]).then_inc(loads, 16)
                sp.dma_start(fc[:], W["L2_attn_fc_w"].rearrange("(h d) n -> d h n", h=NH)).then_inc(loads, 16)
                sp.dma_start(bv[:], W["L2_attn_bv_t"]).then_inc(loads, 16)
                sp.dma_start(fb[:], W["L2_attn_fc_b"].partition_broadcast(T)).then_inc(loads, 16)
                sp.dma_start(lg[:], W["L2_attn_ln_g"].partition_broadcast(T)).then_inc(loads, 16)
                sp.dma_start(lb[:], W["L2_attn_ln_b"].partition_broadcast(T)).then_inc(loads, 16)

            @block.gpsimd
            def _(g):
                g.wait_ge(loads, 96)
                g.tensor_tensor(out=y[:], in0=xn[:], in1=per_tile(fb[:], B), op=ALU.add).then_inc(base_ready, 1)

            @block.vector
            def _(v):
                chain = Own(v, own)
                nc.vector.tensor_copy(pick[:], K.ident[0:B, 0:B].unsqueeze(2).to_broadcast([B, B, T])
                                      ).then_inc(pick_ready, 1)
                v.wait_ge(x_ps, 1)
                nc.vector.tensor_copy(xs[:], p_x[:, 0:B]).then_inc(xs_ready, 1)
                v.wait_ge(loads, 96)
                chain.done(nc.vector.tensor_scalar(bv[:], bv[:], float(T), None, ALU.mult))
                v.wait_ge(v_ps, 1)
                nc.vector.tensor_tensor(vs[:], vals, per_row(bv[:], B), ALU.add).then_inc(vs_ready, 1)
                v.wait_ge(o_ps, 1)
                nc.vector.tensor_copy(at_[:], p_o[0:B, 0:D]).then_inc(at_ready, 1)
                v.wait_ge(base_ready, 1)
                v.wait_ge(y_ps, 1)
                for n in range(4):
                    ins = nc.vector.tensor_tensor(y[:, 4 * n:4 * n + 4], y[:, 4 * n:4 * n + 4], p_y[n][:], ALU.add)
                chain.done(ins)

            @block.tensor
            def _(pe):
                for b in range(B):
                    last = nc.tensor.matmul(p_x[:, b:b + 1], xn[:, b], K.ones[:, 0:1], start=True, stop=True)
                last.then_inc(x_ps, 1)
                pe.wait_ge(loads, 96)
                pe.wait_ge(xs_ready, 1)
                for h in range(NH):
                    last = nc.tensor.matmul(vals[:, h], wv[:, h], xs[:], start=True, stop=True)
                last.then_inc(v_ps, 1)
                pe.wait_ge(vs_ready, 1)
                for h in range(NH):
                    last = nc.tensor.matmul(p_o[0:B, 0:D], vs[:, h], fc[:, h], start=h == 0, stop=h == NH - 1)
                last.then_inc(o_ps, 1)
                pe.wait_ge(at_ready, 1)
                pe.wait_ge(pick_ready, 1)
                for b in range(B):
                    last = nc.tensor.matmul(p_y[b // 4][:, b % 4], pick[:, b], at_[:], start=True, stop=True)
                last.then_inc(y_ps, 1)
        layer_norm_block(nc, "a2_ln2", y, y, lg, lb)
        own2 = s.sem("a2_own2")
        with nc.Block() as block:
            @block.vector
            def _(v):
                nc.vector.tensor_tensor(K.h[:], K.h[:], y[:], ALU.add).then_inc(own2, 1)
                v.wait_ge(own2, 1)
    end_of_layer(nc)


def rope_attention(nc, W, K):
    NH, DH, HALF = 16, 8, D // 2
    with Space(nc) as s:
        xn = s.sb("a3_xn", [T, B, D])
        layer_norm_block(nc, "a3_ln", K.h, xn)
        wqk = s.sb("a3_wqk", [D, 2 * D])
        bqk = s.sb("a3_bqk", [T, 2 * D])
        taps = s.sb("a3_taps", [D, 3])
        lb = s.sb("a3_lb", [T, D])
        cosn = s.sb("a3_cos", [T, D])
        sinn = s.sb("a3_sin", [T, D])
        hmask = s.sb("a3_hmask", [D, D])
        hcol = s.sb("a3_hcol", [D, NH])
        diag = s.sb("a3_diag", [D, 3, D])
        xs = s.sb("a3_xs", [T, 2, D])
        xp = s.sb("a3_xp", [D, 2, T + 2])
        xb = s.sb("a3_xb", [T, 2, 2, D])
        neg = s.sb("a3_neg", [T, 2, 2, D])
        qk = s.sb("a3_qk", [T, 2, 2, D])
        ro = s.sb("a3_ro", [T, 2, 2, D])
        sw = s.sb("a3_sw", [T, 2, 2, D])
        qt = s.sb("a3_qt", [D, 4, T])
        kvm = s.sb("a3_kvm", [D, 2, D])
        km = s.sb("a3_km", [D, 2, NH])
        z = s.sb("a3_z", [T, 2, NH])
        at_ = s.sb("a3_at", [T, 2, D])
        p_t = s.ps("a3_p_t", [D, 4, T])
        p_q = s.ps("a3_p_q", [T, 2, 2, D])
        p_kv = s.ps("a3_p_kv", [D, 2, D])
        p_km = s.ps("a3_p_km", [D, 512])
        p_o = s.ps("a3_p_o", [T, 2, D])
        p_z = s.ps("a3_p_z", [T, 512])
        p_l = s.ps("a3_p_l", [T, 2, D])
        zz = p_z[:, 0:2 * NH].rearrange("t (u h) -> t u h", u=2)
        loads, diag_ready, pads, xs_ready, xt_ps, xp_ready, qk_ps, l_ps, neg_ready, exp_ready, qk_ready, ro_ready, kv_ps, \
            kvm_ready, qt_ps, qt_ready, o_ps, done, own, base_ready = (s.sem("a3_" + n) for n in (
                "loads", "diag_ready", "pads", "xs_ready", "xt_ps", "xp_ready", "qk_ps", "l_ps", "neg_ready", "exp_ready",
                "qk_ready", "ro_ready", "kv_ps", "kvm_ready", "qt_ps", "qt_ready", "o_ps", "done", "own", "base_ready"))

        def flat(a):
            return a.rearrange("t u n d -> t (u n d)")

        def pairs(a):
            return a.rearrange("t u n (i two) -> t (u n) i two", two=2)

        with nc.Block() as block:
            @block.sync
            def _(sp):
                for to, source in ((wqk[:], W["L3_attn_Wqk"]), (bqk[:], W["L3_attn_bqk"].partition_broadcast(T)),
                                   (taps[:], W["L3_attn_lepe_w"].rearrange("c a k -> c (a k)")),
                                   (lb[:], W["L3_attn_lepe_b"].partition_broadcast(T)),
                                   (cosn[:], W["rope_cos"]), (sinn[:], W["rope_sin"]),
                                   (hmask[:], W["head_mask"]), (hcol[:], W["head_columns"])):
                    sp.dma_start(to, source).then_inc(loads, 16)

            @block.gpsimd
            def _(g):
                g.memset(xp[:], 0.0).then_inc(pads, 1)
                g.wait_ge(loads, 128)
                g.tensor_tensor(out=K.h[:], in0=K.h[:], in1=per_tile(lb[:], B), op=ALU.add).then_inc(base_ready, 1)

            @block.vector
            def _(v):
                v.wait_ge(loads, 128)
                for k in range(3):
                    ins = nc.vector.tensor_scalar(diag[:, k], K.ident[:], taps[:, k:k + 1], None, ALU.mult)
                ins.then_inc(diag_ready, 1)
                v.sem_inc(done, 1)
                with v.Fori(0, B // 2) as i:
                    v.wait_ge(done, i + 1)
                    nc.vector.tensor_copy(xs[:], xn[:, bass.ds(2 * i, 2), :]).then_inc(xs_ready, 1)
                    v.wait_ge(qk_ps, i + 1)
                    chain = Own(v, own, 8 * i)
                    chain.done(nc.vector.tensor_tensor(xb[:].rearrange("t u n d -> t u (n d)"),
                                                       p_q[:].rearrange("t u n d -> t u (n d)"), per_tile(bqk[:], 2),
                                                       ALU.add))
                    nc.vector.tensor_scalar(neg[:], xb[:], 0.0, None, ALU.min).then_inc(neg_ready, 1)
                    v.wait_ge(exp_ready, i + 1)
                    chain.done(nc.vector.scalar_tensor_tensor(out=flat(qk[:]), in0=flat(xb[:]), scalar=0.0,
                                                              in1=flat(neg[:]), op0=ALU.max, op1=ALU.add))
                    v.sem_inc(qk_ready, 1)
                    nc.vector.tensor_tensor(ro[:].rearrange("t u n d -> t (u n) d"),
                                            qk[:].rearrange("t u n d -> t (u n) d"), per_tile(cosn[:], 4), ALU.mult)
                    sin2 = sinn[:].rearrange("t (i two) -> t i two", two=2)
                    for n in range(2):
                        ins = nc.vector.tensor_tensor(pairs(sw[:])[:, :, :, n], pairs(qk[:])[:, :, :, 1 - n],
                                                      per_tile(sin2[:, :, n], 4), ALU.mult)
                    chain.done(ins)
                    nc.vector.tensor_tensor(ro[:], ro[:], sw[:], ALU.add).then_inc(ro_ready, 1)
                    v.wait_ge(kv_ps, i + 1)
                    nc.vector.scalar_tensor_tensor(out=kvm[:], in0=p_kv[:], scalar=1.0 / T, in1=per_tile(hmask[:], 2),
                                                   op0=ALU.mult, op1=ALU.mult)
                    for u in range(2):
                        ins = nc.vector.tensor_scalar(km[:, u], hcol[:], p_km[:, u:u + 1], 1.0 / T, ALU.mult, ALU.mult)
                    ins.then_inc(kvm_ready, 1)
                    v.wait_ge(o_ps, i + 1)
                    chain.done(nc.vector.tensor_scalar(z[:], zz, 1e-6, None, ALU.add))
                    chain.done(nc.vector.reciprocal(z[:].rearrange("t u h -> t (u h)"), z[:].rearrange("t u h -> t (u h)")))
                    chain.done(nc.vector.tensor_tensor(at_[:].rearrange("t u (h d) -> t (u h) d", d=DH),
                                                       p_o[:].rearrange("t u (h d) -> t (u h) d", d=DH),
                                                       z[:].rearrange("t u h -> t (u h)").unsqueeze(2)
                                                       .to_broadcast([T, 2 * NH, DH]), ALU.mult))
                    v.wait_ge(l_ps, i + 1)
                    chain.done(nc.vector.tensor_tensor(at_[:], at_[:], p_l[:], ALU.add))
                    v.wait_ge(base_ready, 1)
                    chain.done(nc.vector.tensor_tensor(K.h[:, bass.ds(2 * i, 2), :], K.h[:, bass.ds(2 * i, 2), :], at_[:],
                                                       ALU.add))
                    v.sem_inc(done, 1)

            @block.scalar
            def _(act):
                act.wait_ge(pads, 1)
                with act.Fori(0, B // 2) as i:
                    act.wait_ge(xt_ps, i + 1)
                    nc.scalar.activation(xp[:, :, 1:T + 1], p_t[:, 0:2], ACT.Copy).then_inc(xp_ready, 1)
                    act.wait_ge(neg_ready, i + 1)
                    nc.scalar.activation(neg[:], neg[:], ACT.Exp).then_inc(exp_ready, 1)
                    act.wait_ge(qt_ps, i + 1)
                    nc.scalar.activation(qt[:], p_t[:], ACT.Copy).then_inc(qt_ready, 1)

            @block.tensor
            def _(pe):
                pe.wait_ge(loads, 128)
                pe.wait_ge(diag_ready, 1)
                with pe.Fori(0, B // 2) as i:
                    pe.wait_ge(xs_ready, i + 1)
                    for u in range(2):
                        last = nc.tensor.transpose(p_t[:, u], xs[:, u], K.ident[:])
                    last.then_inc(xt_ps, 1)
                    pe.wait_ge(xp_ready, i + 1)
                    for u in range(2):
                        last = nc.tensor.matmul(p_q[:, u].rearrange("t n d -> t (n d)"), xp[:, u, 1:T + 1], wqk[:],
                                                start=True, stop=True)
                    last.then_inc(qk_ps, 1)
                    for u in range(2):
                        for k in range(3):
                            last = nc.tensor.matmul(p_l[:, u], xp[:, u, k:k + T], diag[:, k], start=k == 0, stop=k == 2)
                    last.then_inc(l_ps, 1)
                    pe.wait_ge(qk_ready, i + 1)
                    for u in range(2):
                        nc.tensor.matmul(p_km[:, u:u + 1], qk[:, u, 1], K.ones[:, 0:1], start=True, stop=True)
                    pe.wait_ge(ro_ready, i + 1)
                    for u in range(2):
                        last = nc.tensor.matmul(p_kv[:, u], ro[:, u, 1], xs[:, u], start=True, stop=True)
                    last.then_inc(kv_ps, 1)
                    for u in range(2):
                        nc.tensor.transpose(p_t[:, 2 * u], qk[:, u, 0], K.ident[:])
                        last = nc.tensor.transpose(p_t[:, 2 * u + 1], ro[:, u, 0], K.ident[:])
                    last.then_inc(qt_ps, 1)
                    pe.wait_ge(qt_ready, i + 1)
                    pe.wait_ge(kvm_ready, i + 1)
                    for u in range(2):
                        nc.tensor.matmul(p_o[:, u], qt[:, 2 * u + 1], kvm[:, u], start=True, stop=True)
                        last = nc.tensor.matmul(zz[:, u], qt[:, 2 * u], km[:, u], start=True, stop=True)
                    last.then_inc(o_ps, 1)
    end_of_layer(nc)


def shared_expert_block(nc, name, W, K, xn):
    with Space(nc) as s:
        wgu = s.sb(name + "_wgu", [D, 2, D])
        wd = s.sb(name + "_wd", [D, D])
        xs = s.sb(name + "_xs", [T, 2, 2, D])
        xt = s.sb(name + "_xt", [D, 2, 2, T])
        sg = s.sb(name + "_sg", [D, 2, 2, T])
        hid = s.sb(name + "_hid", [D, 2, 2, T])
        p_t = [s.ps(f"{name}_p_t{u}", [D, 4, T]) for u in range(2)]
        p_gu = [s.ps(f"{name}_p_gu{u}", [D, 2, 2, T]) for u in range(2)]
        p_y = [s.ps(f"{name}_p_y{u}", [T, 4, D]) for u in range(2)]
        loads = s.sem(name + "_loads")
        xs_ready, xt_ps, xt_ready, gu_ps, sg_ready, hid_ready, y_ps, done = (
            [s.sem(f"{name}_{n}{u}") for u in range(2)] for n in (
                "xs_ready", "xt_ps", "xt_ready", "gu_ps", "sg_ready", "hid_ready", "y_ps", "done"))
        TURNS = B // 4
        with nc.Block() as block:
            @block.sync
            def _(sp):
                sp.dma_start(wgu[:, 0], W["L3_ffn_sWg"]).then_inc(loads, 16)
                sp.dma_start(wgu[:, 1], W["L3_ffn_sWu"]).then_inc(loads, 16)
                sp.dma_start(wd[:], W["L3_ffn_sWd"]).then_inc(loads, 16)

            @block.vector
            def _(v):
                for u in range(2):
                    v.sem_inc(done[u], 1)
                with v.Fori(0, TURNS) as i:
                    for u in range(2):
                        b = 4 * i + 2 * u
                        v.wait_ge(done[u], i + 1)
                        nc.vector.tensor_copy(xs[:, u], xn[:, bass.ds(b, 2), :]).then_inc(xs_ready[u], 1)
                    for u in range(2):
                        v.wait_ge(sg_ready[u], i + 1)
                        nc.vector.tensor_tensor(hid[:, u], sg[:, u], p_gu[u][:, 1], ALU.mult).then_inc(hid_ready[u], 1)
                    for u in range(2):
                        b = 4 * i + 2 * u
                        v.wait_ge(y_ps[u], i + 1)
                        nc.vector.tensor_tensor(K.h[:, bass.ds(b, 2), :], K.h[:, bass.ds(b, 2), :], p_y[u][:, 0:2],
                                                ALU.add).then_inc(done[u], 1)

            @block.scalar
            def _(act):
                with act.Fori(0, TURNS) as i:
                    for u in range(2):
                        act.wait_ge(xt_ps[u], i + 1)
                        nc.scalar.activation(xt[:, u], p_t[u][:, 0:2], ACT.Copy).then_inc(xt_ready[u], 1)
                    for u in range(2):
                        act.wait_ge(gu_ps[u], i + 1)
                        nc.scalar.activation(sg[:, u], p_gu[u][:, 0], ACT.Silu).then_inc(sg_ready[u], 1)

            @block.tensor
            def _(pe):
                pe.wait_ge(loads, 48)
                with pe.Fori(0, TURNS) as i:
                    for u in range(2):
                        pe.wait_ge(xs_ready[u], i + 1)
                        for n in range(2):
                            last = nc.tensor.transpose(p_t[u][:, n], xs[:, u, n], K.ident[:])
                        last.then_inc(xt_ps[u], 1)
                    for u in range(2):
                        pe.wait_ge(xt_ready[u], i + 1)
                        for n in range(2):
                            last = nc.tensor.matmul(p_gu[u][:, n], wgu[:, n], xt[:, u], start=True, stop=True)
                        last.then_inc(gu_ps[u], 1)
                    for u in range(2):
                        pe.wait_ge(hid_ready[u], i + 1)
                        for n in range(2):
                            last = nc.tensor.matmul(p_y[u][:, n], hid[:, u, n], wd[:], start=True, stop=True)
                        last.then_inc(y_ps[u], 1)


def grouped_router_block(nc, name, W, K, xn, xn_dram, route, index, scores):
    E, P, G, KEEP = route.experts, route.picks, 8, 4
    PER = E // G
    BIG = 1e30
    with Space(nc) as s:
        corr = s.sb(name + "_corr", [T, E])
        biased = s.sb(name + "_biased", [T, B, E])
        best = s.sb(name + "_best", [T, B, G])
        top = s.sb(name + "_top", [T, B, 8])
        which = s.sb(name + "_which", [T, B, 8], u32)
        which_f = s.sb(name + "_which_f", [T, B, 8])
        iota_g = s.sb(name + "_iota_g", [T, G])
        hot = s.sb(name + "_hot", [T, B, G])
        gmask = s.sb(name + "_gmask", [T, B, G])
        corr_in, iota_ready, exp_ready, own = (s.sem(name + "_" + n) for n in ("corr_in", "iota_ready", "exp_ready", "own"))
        router_logits_block(nc, name + "_r", K, xn, xn_dram, W["L3_ffn_router_w_t"], E, scores)
        with nc.Block() as block:
            @block.sync
            def _(sp):
                sp.dma_start(corr[:], W["L3_ffn_bias_corr"].partition_broadcast(T)).then_inc(corr_in, 16)

            @block.gpsimd
            def _(g):
                g.iota(iota_g[:], pattern=[[1, G]], base=0, channel_multiplier=0,
                       allow_small_or_imprecise_dtypes=True).then_inc(iota_ready, 1)

            @block.scalar
            def _(act):
                nc.scalar.activation(scores[:], scores[:], ACT.Exp, scale=-1.0).then_inc(exp_ready, 1)

            @block.vector
            def _(v):
                chain = Own(v, own)
                v.wait_ge(exp_ready, 1)
                chain.done(nc.vector.tensor_scalar(scores[:], scores[:], 1.0, None, ALU.add))
                flat = scores[:].rearrange("t b e -> t (b e)")
                chain.done(nc.vector.reciprocal(flat, flat))
                v.wait_ge(corr_in, 16)
                chain.done(nc.vector.tensor_tensor(biased[:], scores[:], per_tile(corr[:], B), ALU.add))
                groups = biased[:].rearrange("t b (g e) -> t (b g) e", e=PER)
                chain.done(nc.vector.tensor_reduce(out=best[:].rearrange("t b g -> t (b g)"), in_=groups, axis=AX.X,
                                                   op=ALU.max))
                for b in range(B):
                    ins = nc.vector.max(top[:, b, :], best[:, b, :])
                chain.done(ins)
                for b in range(B):
                    ins = nc.vector.max_index(which[:, b, :], top[:, b, :], best[:, b, :])
                chain.done(ins)
                chain.done(nc.vector.tensor_copy(which_f[:], which[:]))
                v.wait_ge(iota_ready, 1)
                for k in range(KEEP):
                    chain.done(nc.vector.tensor_tensor(gmask[:] if k == 0 else hot[:], per_tile(iota_g[:], B),
                                                       per_row(which_f[:, :, k], G), ALU.is_equal))
                    if k:
                        chain.done(nc.vector.tensor_tensor(gmask[:], gmask[:], hot[:], ALU.add))
                chain.done(nc.vector.tensor_tensor(groups, groups, gmask[:].rearrange("t b g -> t (b g)").unsqueeze(2)
                                                   .to_broadcast([T, B * G, PER]), ALU.mult))
                chain.done(nc.vector.tensor_scalar(gmask[:], gmask[:], BIG, -BIG, ALU.mult, ALU.add))
                chain.done(nc.vector.tensor_tensor(groups, groups, gmask[:].rearrange("t b g -> t (b g)").unsqueeze(2)
                                                   .to_broadcast([T, B * G, PER]), ALU.add))
                for b in range(B):
                    ins = nc.vector.max(top[:, b, :], biased[:, b, :])
                chain.done(ins)
                for b in range(B):
                    ins = nc.vector.max_index(which[:, b, :], top[:, b, :], biased[:, b, :])
                chain.done(ins)
                chain.done(nc.vector.tensor_copy(index[:], which[:, :, 0:P]))


def gated_tiles_block(nc, name, K, route, xn_dram, o_dram, wgu, wd0, wd1, wgu_in, wd_in, H):
    E, NT = route.experts, route.tiles
    REST = H - T
    TURNS = NT // 2
    with Space(nc) as s:
        who2 = s.sb(name + "_who2", [SLOTS, 2], i32)
        xg = s.sb(name + "_xg", [SLOTS, 2, D])
        xgt = s.sb(name + "_xgt", [D, 2, SLOTS])
        sg = s.sb(name + "_sg", [SLOTS, 2, H])
        hid = s.sb(name + "_hid", [SLOTS, 2, H])
        ht = s.sb(name + "_ht", [T, 2, 2, SLOTS])
        ob = s.sb(name + "_ob", [SLOTS, 2, D])
        p_t = [s.ps(f"{name}_p_t{u}", [T, 4, SLOTS]) for u in range(2)]
        p_h = [s.ps(f"{name}_p_h{u}", [SLOTS, 512]) for u in range(2)]
        p_o = [s.ps(f"{name}_p_o{u}", [SLOTS, 512]) for u in range(2)]
        who_ready, gathered, t_ps, xgt_ready, h_ps, sg_ready, hid_ready, ht_ps, ht_ready, o_ps, ob_ready, stored = (
            [s.sem(f"{name}_{n}{u}") for u in range(2)] for n in (
                "who_ready", "gathered", "t_ps", "xgt_ready", "h_ps", "sg_ready", "hid_ready", "ht_ps", "ht_ready",
                "o_ps", "ob_ready", "stored"))
        with nc.Block() as block:
            @block.gpsimd
            def _(g):
                for u in range(2):
                    g.sem_inc(xgt_ready[u], 1)
                with g.Fori(0, TURNS) as i:
                    for u in range(2):
                        g.wait_ge(xgt_ready[u], i + 1)
                        g.tensor_copy(who2[:, u:u + 1], route.who[:, bass.ds(2 * i + u, 1)]).then_inc(who_ready[u], 1)
                        g.wait_ge(who_ready[u], i + 1)
                        g.nop(nofuse=True)
                        g.indirect_dma_start(out=xg[:, u, :], out_offset=None, in_=xn_dram,
                                             in_offset=bass.IndirectOffsetOnAxis(ap=who2[:, u:u + 1], axis=0)
                                             ).then_inc(gathered[u], 16)

            @block.tensor
            def _(pe):
                pe.wait_ge(wgu_in, 32)
                pe.wait_ge(wd_in, 32)
                with pe.Fori(0, TURNS) as i:
                    experts = [pe.value_load(route.expert_of[0:1, bass.ds(2 * i + u, 1)], min_val=0, max_val=E - 1)
                               for u in range(2)]
                    for u in range(2):
                        pe.wait_ge(gathered[u], 16 * i + 16)
                        nc.tensor.transpose(p_t[u][:, 0], xg[:, u, :], K.ident[:]).then_inc(t_ps[u], 1)
                    for u in range(2):
                        pe.wait_ge(xgt_ready[u], i + 2)
                        nc.tensor.matmul(p_h[u][:, 0:2 * H], xgt[:, u, :],
                                         wgu[:, bass.ds(experts[u], 1)].rearrange("c e n -> c (e n)"), start=True,
                                         stop=True).then_inc(h_ps[u], 1)
                    for u in range(2):
                        pe.wait_ge(hid_ready[u], i + 1)
                        nc.tensor.transpose(p_t[u][:, 1], hid[:, u, 0:T], K.ident[:])
                        nc.tensor.transpose(p_t[u][0:REST, 2], hid[:, u, T:H], K.ident[:]).then_inc(ht_ps[u], 1)
                    for u in range(2):
                        pe.wait_ge(ht_ready[u], i + 1)
                        nc.tensor.matmul(p_o[u][:, 0:D], ht[:, u, 0],
                                         wd0[:, bass.ds(experts[u], 1)].rearrange("p e n -> p (e n)"), start=True,
                                         stop=False)
                        nc.tensor.matmul(p_o[u][:, 0:D], ht[0:REST, u, 1],
                                         wd1[:, bass.ds(experts[u], 1)].rearrange("p e n -> p (e n)"), start=False,
                                         stop=True).then_inc(o_ps[u], 1)

            @block.scalar
            def _(act):
                with act.Fori(0, TURNS) as i:
                    for u in range(2):
                        act.wait_ge(t_ps[u], i + 1)
                        nc.scalar.activation(xgt[:, u, :], p_t[u][:, 0], ACT.Copy).then_inc(xgt_ready[u], 1)
                    for u in range(2):
                        act.wait_ge(h_ps[u], i + 1)
                        nc.scalar.activation(sg[:, u, :], p_h[u][:, 0:H], ACT.Silu).then_inc(sg_ready[u], 1)
                    for u in range(2):
                        act.wait_ge(ht_ps[u], i + 1)
                        nc.scalar.activation(ht[:, u, 0], p_t[u][:, 1], ACT.Copy)
                        nc.scalar.activation(ht[0:REST, u, 1], p_t[u][0:REST, 2], ACT.Copy).then_inc(ht_ready[u], 1)

            @block.vector
            def _(v):
                for u in range(2):
                    v.sem_inc(stored[u], 16)
                with v.Fori(0, TURNS) as i:
                    for u in range(2):
                        v.wait_ge(sg_ready[u], i + 1)
                        nc.vector.tensor_tensor(hid[:, u, :], sg[:, u, :], p_h[u][:, H:2 * H],
                                                ALU.mult).then_inc(hid_ready[u], 1)
                    for u in range(2):
                        v.wait_ge(o_ps[u], i + 1)
                        v.wait_ge(stored[u], 16 * i + 16)
                        nc.vector.tensor_copy(ob[:, u, :], p_o[u][:, 0:D]).then_inc(ob_ready[u], 1)

            @block.sync
            def _(sp):
                with sp.Fori(0, TURNS) as i:
                    for u in range(2):
                        sp.wait_ge(ob_ready[u], i + 1)
                        sp.dma_start(o_dram[bass.ds((2 * i + u) * SLOTS, SLOTS), :], ob[:, u, :]).then_inc(stored[u], 16)
                for u in range(2):
                    sp.wait_ge(stored[u], 16 * TURNS + 16)


def grouped_experts(nc, W, K):
    E, P, H = 64, 6, 160
    NT = 2 * -(-(NTOK * P // SLOTS + E - 1) // 2)
    name = "L3_ffn"
    xn_dram = nc.dram_tensor(name + "_xn_dram", (NTOK, D), f32, kind="Internal").ap()
    o_dram = nc.dram_tensor(name + "_o_dram", (NT * SLOTS, D), f32, kind="Internal").ap()
    with Space(nc) as s:
        route = Route(s, name, E, P, NT)
        with Space(nc) as s2:
            xn = s2.sb(name + "_xn", [T, B, D])
            layer_norm_block(nc, name + "_ln", K.h, xn)
            index = s2.sb(name + "_index", [T, B, P])
            scores = s2.sb(name + "_scores", [T, B, E])
            grouped_router_block(nc, name + "_g", W, K, xn, xn_dram, route, index, scores)
            shared_expert_block(nc, name + "_sh", W, K, xn)
            sort_block(nc, name + "_sort", K, route, index, chosen=scores)
        wgu = s.sb(name + "_wgu", [D, E, 2 * H])
        wd0 = s.sb(name + "_wd0", [T, E, D])
        wd1 = s.sb(name + "_wd1", [H - T, E, D])
        wgu_in = s.sem(name + "_wgu_in")
        wd_in = s.sem(name + "_wd_in")
        total = s.sb(name + "_total", [T, B])
        own = s.sem(name + "_own")
        with nc.Block() as block:
            @block.sync
            def _(sp):
                sp.dma_start(wgu[:, :, 0:H], W["L3_ffn_Wg"].rearrange("e c n -> c e n")).then_inc(wgu_in, 16)
                sp.dma_start(wgu[:, :, H:2 * H], W["L3_ffn_Wu"].rearrange("e c n -> c e n")).then_inc(wgu_in, 16)
                sp.dma_start(wd0[:], W["L3_ffn_Wd"][:, 0:T, :].rearrange("e p n -> p e n")).then_inc(wd_in, 16)
                sp.dma_start(wd1[:], W["L3_ffn_Wd"][:, T:H, :].rearrange("e p n -> p e n")).then_inc(wd_in, 16)

            @block.vector
            def _(v):
                chain = Own(v, own)
                chain.done(nc.vector.tensor_reduce(out=total[:], in_=route.gate[:], axis=AX.X, op=ALU.add))
                chain.done(nc.vector.tensor_scalar(total[:], total[:], 1e-20, None, ALU.add))
                chain.done(nc.vector.reciprocal(total[:], total[:]))
                chain.done(nc.vector.tensor_tensor(route.gate[:], route.gate[:], per_row(total[:], P), ALU.mult))
        gated_tiles_block(nc, name + "_x", K, route, xn_dram, o_dram, wgu, wd0, wd1, wgu_in, wd_in, H)
        combine_block(nc, name + "_c", K, route, o_dram, 1)
    end_of_layer(nc)




def tower_program(nc, W, out):
    with Space(nc) as s:
        K = Constants(nc, s)
        constants_and_embedding(nc, W, K)
        layer0_attention(nc, W, K)
        top1_experts(nc, W, K, "L0_ffn", 8, 4, False)
        householder_attention(nc, W, K)
        capacity_experts(nc, W, K)
        layer2_attention(nc, W, K)
        top1_experts(nc, W, K, "L2_ffn", 8, 1, True)
        rope_attention(nc, W, K)
        grouped_experts(nc, W, K)
        out_done = s.sem("out_done")
        with nc.Block() as block:
            @block.sync
            def _(sp):
                sp.dma_start(out.rearrange("b t c -> t b c"), K.h[:]).then_inc(out_done, 16)
                sp.wait_ge(out_done, 16)


def kernel(**inputs):
    import numpy as np
    import concourse.bacc as bacc
    from concourse.bass_utils import run_bass_kernel_spmd

    nc = bacc.Bacc("TRN2", target_bir_lowering=False, num_devices=1)
    arrays = {}
    for name, a in inputs.items():
        arrays[name] = np.ascontiguousarray(a)
    arrays["x_t"] = np.ascontiguousarray(np.asarray(inputs["x"]).T)
    arrays["L0_attn_b1_t"] = np.ascontiguousarray(np.asarray(inputs["L0_attn_b1"]).reshape(4, 128).T)
    for name, chunks in (("L0_ffn_b1", 4), ("L2_ffn_b1", 1)):
        b1 = np.asarray(inputs[name])
        arrays[name + "_t"] = np.ascontiguousarray(b1.reshape(b1.shape[0], chunks, 128).transpose(0, 2, 1))
    for name in ("Wq", "Wk", "Wv", "Ww", "Wbeta", "Wg", "Wo"):
        arrays["L1_attn_" + name + "_t"] = np.ascontiguousarray(np.asarray(inputs["L1_attn_" + name]).T)
    row, col = np.arange(128)[:, None], np.arange(128)[None, :]
    arrays["block_masks"] = np.ascontiguousarray(
        np.stack([row // 16 == col // 16, row // 16 < col // 16], 1).astype(np.float32))
    low, pcol = row % 16, np.arange(16)[None, :]
    packed = [low == pcol]
    for half in (1, 2, 4, 8):
        packed.append((low // (2 * half) == pcol // (2 * half)) & (low % (2 * half) < half) & (pcol % (2 * half) >= half))
    arrays["packed_masks"] = np.ascontiguousarray(np.stack(packed, 1).astype(np.float32))
    arrays["L1_ffn_b1_t"] = np.ascontiguousarray(np.asarray(inputs["L1_ffn_b1"]).T)
    arrays["L2_attn_bv_t"] = np.ascontiguousarray(np.asarray(inputs["L2_attn_bv"]).reshape(8, 128).T)
    theta = np.float32(1.0) / np.float32(10000.0) ** (np.arange(64, dtype=np.float32) / np.float32(64))
    angle = np.arange(128, dtype=np.float32)[:, None] * theta
    arrays["rope_cos"] = np.repeat(np.cos(angle), 2, axis=1)
    arrays["rope_sin"] = np.ascontiguousarray(np.stack([-np.sin(angle), np.sin(angle)], -1).reshape(128, 128))
    arrays["head_mask"] = (row // 8 == col // 8).astype(np.float32)
    arrays["head_columns"] = (row // 8 == np.arange(16)[None, :]).astype(np.float32)
    arrays["L3_ffn_router_w_t"] = np.ascontiguousarray(np.asarray(inputs["L3_ffn_router_w"]).T)
    W = {}
    for name, a in arrays.items():
        W[name] = nc.dram_tensor("in_" + name, a.shape, mybir.dt.from_np(a.dtype), kind="ExternalInput").ap()
    out = nc.dram_tensor("out", (B, T, D), f32, kind="ExternalOutput").ap()
    tower_program(nc, W, out)
    got = run_bass_kernel_spmd(nc, [{"in_" + n: a for n, a in arrays.items()}], core_ids=[0])
    return got.results[0]["out"]
```

```python
import math
from contextlib import ExitStack

import concourse.bass as bass
from concourse import mybir

f32 = mybir.dt.float32
f16 = mybir.dt.float16
i32 = mybir.dt.int32
u32 = mybir.dt.uint32
ALU = mybir.AluOpType
ACT = mybir.ActivationFunctionType
AX = mybir.AxisListType

T = 128
B = 16
D = 128
EPS = 1e-5


class Own:

    def __init__(self, engine, sem, first=0):
        self.engine, self.sem, self.at = engine, sem, first

    def done(self, ins):
        self.at = self.at + 1
        ins.then_inc(self.sem, 1)
        self.engine.wait_ge(self.sem, self.at)


class Space:

    used = []

    def __init__(self, nc):
        self.nc, self.ctx, self.count = nc, ExitStack(), 0

    def sb(self, name, shape, dt=f32):
        return self.ctx.enter_context(self.nc.sbuf_tensor(name, shape, dt))

    def ps(self, name, shape, dt=f32):
        return self.ctx.enter_context(self.nc.psum_tensor(name, shape, dt))

    def sem(self, name):
        handle = self.nc.alloc_semaphore(name=name)
        Space.used.append(handle)
        return handle

    def __enter__(self):
        self.ctx.__enter__()
        return self

    def __exit__(self, *a):
        return self.ctx.__exit__(*a)


def end_of_layer(nc):
    nc.clear_and_free_semaphores(Space.used)
    Space.used = []
    nc.all_engine_barrier()


def per_row(column, width):
    return column.unsqueeze(2).to_broadcast([column.shape[0], column.shape[1], width])


def per_tile(row, tiles):
    return row.unsqueeze(1).to_broadcast([row.shape[0], tiles, row.shape[1]])


def layer_norm_block(nc, name, src, dst, gamma=None, beta=None, scale=None):
    with Space(nc) as s:
        stats = s.sb(name + "_stats", [T, B, 6])
        mean = s.sb(name + "_mean", [T, B])
        gap = s.sb(name + "_gap", [T, B])
        var = s.sb(name + "_var", [T, B])
        std = s.sb(name + "_std", [T, B])
        rstd = s.sb(name + "_rstd", [T, B])
        own = s.sem(name + "_own")
        var_ready = s.sem(name + "_var_ready")
        std_ready = s.sem(name + "_std_ready")
        with nc.Block() as block:
            @block.scalar
            def _(act):
                act.wait_ge(var_ready, 1)
                nc.scalar.activation(std[:], var[:], ACT.Sqrt).then_inc(std_ready, 1)

            @block.vector
            def _(v):
                for b in range(B):
                    last = nc.vector.bn_stats(stats[:, b, :], src[:, b, :])
                last.then_inc(own, 1)
                v.wait_ge(own, 1)
                chain = Own(v, own, 1)
                nc.vector.tensor_tensor(mean[:], stats[:, :, 1], stats[:, :, 4], ALU.add)
                nc.vector.tensor_tensor(gap[:], stats[:, :, 1], stats[:, :, 4], ALU.subtract)
                chain.done(nc.vector.tensor_tensor(var[:], stats[:, :, 2], stats[:, :, 5], ALU.add))
                nc.vector.tensor_scalar(mean[:], mean[:], 0.5, None, ALU.mult)
                nc.vector.scalar_tensor_tensor(out=gap[:], in0=gap[:], scalar=0.25, in1=gap[:], op0=ALU.mult,
                                               op1=ALU.mult)
                chain.done(nc.vector.tensor_scalar(var[:], var[:], 1.0 / D, EPS, ALU.mult, ALU.add))
                nc.vector.tensor_tensor(var[:], var[:], gap[:], ALU.add).then_inc(var_ready, 1)
                chain.done(nc.vector.tensor_tensor(dst[:], src[:], per_row(mean[:], D), ALU.subtract))
                v.wait_ge(std_ready, 1)
                chain.done(nc.vector.reciprocal(rstd[:], std[:]))
                chain.done(nc.vector.tensor_tensor(dst[:], dst[:], per_row(rstd[:], D), ALU.mult))
                if gamma is not None:
                    chain.done(nc.vector.tensor_tensor(dst[:], dst[:], per_tile(gamma[:], B), ALU.mult))
                    chain.done(nc.vector.tensor_tensor(dst[:], dst[:], per_tile(beta[:], B), ALU.add))
                if scale is not None:
                    chain.done(nc.vector.tensor_scalar(dst[:], dst[:], scale, None, ALU.mult))


def constants_and_embedding(nc, W, K):
    with Space(nc) as s:
        ids = s.sb("ids", [T, B], i32)
        idf = s.sb("idf", [T, B])
        raw = s.sb("raw", [T, B, D])
        types = s.sb("types", [T, 5, 8])
        sel = s.sb("sel", [T, 3, B])
        low = s.sb("low", [T, B])
        part = s.sb("part", [T, B, 8])
        gamma = s.sb("gamma", [T, D])
        beta = s.sb("beta", [T, D])
        ids_in = s.sem("ids_in")
        rows_in = s.sem("rows_in")
        made = s.sem("made")
        gathered = s.sem("gathered")
        own = s.sem("emb_own")
        NTOK = D - 8
        with nc.Block() as block:
            @block.sync
            def _(sp):
                sp.dma_start(ids[:], W["x_t"]).then_inc(ids_in, 16)
                sp.dma_start(types[:].rearrange("p a b -> p (a b)"),
                             W["L0_tok_type_emb_table"].rearrange("a b -> (a b)").partition_broadcast(T)
                             ).then_inc(rows_in, 16)
                sp.dma_start(gamma[:], W["L0_tok_ln_gamma"].partition_broadcast(T)).then_inc(rows_in, 16)
                sp.dma_start(beta[:], W["L0_tok_ln_beta"].partition_broadcast(T)).then_inc(rows_in, 16)

            @block.gpsimd
            def _(g):
                g.wait_ge(ids_in, 16)
                for b in range(B):
                    g.indirect_dma_start(out=raw[:, b, 0:NTOK], out_offset=None, in_=W["L0_tok_token_emb_table"],
                                         in_offset=bass.IndirectOffsetOnAxis(ap=ids[:, b:b + 1], axis=0)
                                         ).then_inc(gathered, 16)
                K.fill(g, made)

            @block.vector
            def _(v):
                chain = Own(v, own)
                v.wait_ge(ids_in, 16)
                chain.done(nc.vector.tensor_copy(idf[:], ids[:]))
                nc.vector.tensor_scalar(sel[:, 0, :], idf[:], 128.0, None, ALU.is_lt)
                nc.vector.tensor_scalar(low[:], idf[:], 256.0, None, ALU.is_lt)
                chain.done(nc.vector.tensor_scalar(sel[:, 2, :], idf[:], 256.0, None, ALU.is_ge))
                v.wait_ge(rows_in, 48)
                chain.done(nc.vector.tensor_tensor(sel[:, 1, :], low[:], sel[:, 0, :], ALU.subtract))
                emb = raw[:, :, NTOK:D]
                for n, row in enumerate((0, 3, 4)):
                    to = emb if n == 0 else part[:]
                    chain.done(nc.vector.tensor_tensor(to, per_row(sel[:, n, :], 8), per_tile(types[:, row, :], B),
                                                       ALU.mult))
                    if n:
                        chain.done(nc.vector.tensor_tensor(emb, emb, part[:], ALU.add))
                v.wait_ge(gathered, 16 * B)
        layer_norm_block(nc, "ln_emb", raw, K.h, gamma, beta, math.sqrt(D))
    end_of_layer(nc)


class Constants:

    def __init__(self, nc, s):
        self.nc = nc
        self.h = s.sb("h", [T, B, D])
        self.ident = s.sb("ident", [T, T])
        self.ones = s.sb("ones", [T, T])
        self.up_to = s.sb("up_to", [T, T])
        self.before = s.sb("before", [T, T])
        self.after = s.sb("after", [T, T])

    def fill(self, g, made):
        g.memset(self.ones[:], 1.0).then_inc(made, 1)
        g.wait_ge(made, 1)
        for m, op, base, sign in ((self.ident, ALU.is_equal, 0, 1), (self.up_to, ALU.is_ge, 0, 1),
                                  (self.before, ALU.is_gt, 0, 1), (self.after, ALU.is_gt, 0, -1)):
            g.affine_select(out=m[:], in_=self.ones[:], compare_op=op, fill=0.0, base=base,
                            pattern=[[sign, T]], channel_multiplier=-sign)


def causal_linear_attention_block(nc, W, K, xin, x2):
    HEADS, DH = 8, 16
    NG, PER = 2, 4
    with Space(nc) as s:
        h1 = s.sb("a0_h1", [T, B, D])
        g1 = s.sb("a0_g1", [T, D])
        b1 = s.sb("a0_b1", [T, D])
        wq = s.sb("a0_wq", [D, 2, NG, PER, 32])
        bq = s.sb("a0_bq", [D, 2, NG])
        wv = s.sb("a0_wv", [D, D])
        bv = s.sb("a0_bv", [T, D])
        wo = s.sb("a0_wo", [D, D])
        bo = s.sb("a0_bo", [T, D])
        loads = s.sem("a0_loads")
        own0 = s.sem("a0_own0")
        with nc.Block() as block:
            @block.gpsimd
            def _(g):
                g.memset(wq[:], 0.0).then_inc(own0, 1)
                g.memset(bq[:], 0.0).then_inc(own0, 1)

            @block.sync
            def _(sp):
                sp.dma_start(g1[:], W["L0_attn_ln1_g"].partition_broadcast(T)).then_inc(loads, 16)
                sp.dma_start(b1[:], W["L0_attn_ln1_b"].partition_broadcast(T)).then_inc(loads, 16)
                sp.dma_start(wv[:], W["L0_attn_Wv"]).then_inc(loads, 16)
                sp.dma_start(wo[:], W["L0_attn_Wo"]).then_inc(loads, 16)
                sp.dma_start(bv[:], W["L0_attn_bv"].partition_broadcast(T)).then_inc(loads, 16)
                sp.dma_start(bo[:], W["L0_attn_bo"].partition_broadcast(T)).then_inc(loads, 16)
                sp.wait_ge(own0, 2)
                for n, (w, b) in enumerate((("L0_attn_Wq", "L0_attn_bq"), ("L0_attn_Wk", "L0_attn_bk"))):
                    for g in range(NG):
                        sp.dma_start(wq[:, n, g, :, 0:DH],
                                     W[w].rearrange("c (j g d) -> c g j d", g=NG, d=DH)[:, g]).then_inc(loads, 16)
                        for j in range(PER):
                            at = (j * NG + g) * DH
                            sp.dma_start(bq[32 * j:32 * j + DH, n, g:g + 1],
                                         W[b][at:at + DH].unsqueeze(1)).then_inc(loads, 16)
                sp.wait_ge(loads, 16 * (6 + 4 + 16))
        layer_norm_block(nc, "a0_ln1", xin, h1, g1, b1)

        hs = s.sb("a0_hs", [T, 2, D])
        h1t = s.sb("a0_h1t", [D, 2, T])
        xb = s.sb("a0_xb", [D, 2, NG, 2, T])
        neg = s.sb("a0_neg", [D, 2, NG, 2, T])
        ex = s.sb("a0_ex", [D, 2, NG, 2, T])
        qk = s.sb("a0_qk", [D, 2, NG, 2, T])
        v17 = s.sb("a0_v17", [T, 2, HEADS, DH + 1])
        sm = s.sb("a0_sm", [T, 2, HEADS, T])
        den = s.sb("a0_den", [T, 2, HEADS])
        rden = s.sb("a0_rden", [T, 2, HEADS])
        at_ = s.sb("a0_at", [T, 2, D])
        att = s.sb("a0_att", [D, 2, T])
        xbo = s.sb("a0_xbo", [T, B, D])
        p_t = s.ps("a0_p_t", [T, 2, 2, T])
        p_q = s.ps("a0_p_q", [T, 2, NG, 2, T])
        p_s = s.ps("a0_p_s", [T, PER, 2, NG, T])
        p_n = s.ps("a0_p_n", [T, 512])
        num = p_n[:, 0:2 * HEADS * (DH + 1)].rearrange("t (u h e) -> t u h e", u=2, h=HEADS)
        hs_ready, t1, h1t_ready, qk_ps, v_ps, xb_ready, neg_ready, ex_ready, qk_ready, v_ready, s_ps, sm_ready, \
            n_ps, at_ready, att_ps, att_ready, o_ps, x2_ready, ones_ready, own, rd = (s.sem("a0_" + n) for n in (
                "hs_ready", "t1", "h1t_ready", "qk_ps", "v_ps", "xb_ready", "neg_ready", "ex_ready", "qk_ready",
                "v_ready", "s_ps", "sm_ready", "n_ps", "at_ready", "att_ps", "att_ready", "o_ps", "x2_ready",
                "ones_ready", "own", "rd"))
        with nc.Block() as block:
            @block.gpsimd
            def _(g):
                g.memset(v17[:, :, :, DH:DH + 1], 1.0).then_inc(ones_ready, 1)
                g.tensor_tensor(out=xbo[:], in0=xin[:], in1=per_tile(bo[:], B), op=ALU.add).then_inc(ones_ready, 1)

            @block.vector
            def _(v):
                v.sem_inc(x2_ready, 2)
                with v.Fori(0, B // 2) as i:
                    for u in range(2):
                        v.wait_ge(x2_ready, 2 * i + u + 1)
                        nc.vector.tensor_copy(hs[:, u, :], h1[:, 2 * i + u, :]).then_inc(hs_ready, 1)
                    for n in range(2):
                        v.wait_ge(xb_ready, 4 * i + 2 * n + 2)
                        nc.vector.tensor_scalar(neg[:, n], xb[:, n], 0.0, None, ALU.min).then_inc(neg_ready, 1)
                    v.wait_ge(v_ps, i + 1)
                    nc.vector.tensor_tensor(v17[:, :, :, 0:DH],
                                            p_t[:, 1].rearrange("t u (h d) -> t u h d", h=HEADS),
                                            bv[:].rearrange("t (h d) -> t h d", h=HEADS).unsqueeze(1)
                                            .to_broadcast([T, 2, HEADS, DH]), ALU.add).then_inc(v_ready, 1)
                    for n in range(2):
                        v.wait_ge(ex_ready, 2 * i + n + 1)
                        nc.vector.scalar_tensor_tensor(out=qk[:, n].rearrange("c g u t -> c (g u t)"),
                                                       in0=xb[:, n].rearrange("c g u t -> c (g u t)"), scalar=0.0,
                                                       in1=ex[:, n].rearrange("c g u t -> c (g u t)"), op0=ALU.max,
                                                       op1=ALU.add).then_inc(qk_ready, 1)
                    v.wait_ge(s_ps, 2 * i + 2)
                    for u in range(2):
                        nc.vector.tensor_tensor(sm[:, u].rearrange("t (j g) s -> t j g s", g=NG), p_s[:, :, u],
                                                K.up_to[:].unsqueeze(1).unsqueeze(1).to_broadcast([T, PER, NG, T]),
                                                ALU.mult).then_inc(sm_ready, 1)
                    chain = Own(v, own, 2 * i)
                    v.wait_ge(n_ps, 2 * i + 2)
                    chain.done(nc.vector.tensor_scalar(den[:], num[:, :, :, DH], 1e-6, None, ALU.max))
                    chain.done(nc.vector.reciprocal(rden[:], den[:]))
                    for u in range(2):
                        nc.vector.tensor_tensor(at_[:, u].rearrange("t (h d) -> t h d", h=HEADS), num[:, u, :, 0:DH],
                                                per_row(rden[:, u], DH), ALU.mult).then_inc(at_ready, 1)
                    v.wait_ge(ones_ready, 2)
                    v.wait_ge(o_ps, 2 * i + 2)
                    for u in range(2):
                        nc.vector.tensor_tensor(x2[:, 2 * i + u, :], xbo[:, 2 * i + u, :], p_q[:, 0, 0, u, :],
                                                ALU.add).then_inc(x2_ready, 1)

            @block.scalar
            def _(act):
                with act.Fori(0, B // 2) as i:
                    act.wait_ge(t1, 2 * i + 2)
                    nc.scalar.activation(h1t[:], p_t[:, 0], ACT.Copy).then_inc(h1t_ready, 1)
                    act.wait_ge(qk_ps, i + 1)
                    for n in range(2):
                        for g in range(NG):
                            nc.scalar.activation(xb[:, n, g], p_q[:, n, g], ACT.Identity,
                                                 bias=bq[:, n, g:g + 1]).then_inc(xb_ready, 1)
                    for n in range(2):
                        act.wait_ge(neg_ready, 2 * i + n + 1)
                        nc.scalar.activation(ex[:, n], neg[:, n], ACT.Exp).then_inc(ex_ready, 1)
                    act.wait_ge(att_ps, 2 * i + 2)
                    nc.scalar.activation(att[:], p_t[:, 0], ACT.Copy).then_inc(att_ready, 1)

            @block.tensor
            def _(pe):
                pe.wait_ge(ones_ready, 1)
                with pe.Fori(0, B // 2) as i:
                    for u in range(2):
                        pe.wait_ge(hs_ready, 2 * i + u + 1)
                        nc.tensor.transpose(p_t[:, 0, u], hs[:, u], K.ident[:]).then_inc(t1, 1)
                    pe.wait_ge(h1t_ready, i + 1)
                    for n in range(2):
                        for g in range(NG):
                            last = nc.tensor.matmul(p_q[:, n, g], wq[:, n, g].rearrange("c j d -> c (j d)"), h1t[:],
                                                    start=True, stop=True)
                    last.then_inc(qk_ps, 1)
                    for u in range(2):
                        last = nc.tensor.matmul(p_t[:, 1, u], h1t[:, u], wv[:], start=True, stop=True)
                    last.then_inc(v_ps, 1)
                    pe.wait_ge(qk_ready, 2 * i + 2)
                    for u in range(2):
                        for h in range(HEADS):
                            j, g = divmod(h, NG)
                            rows = slice(32 * j, 32 * j + DH)
                            last = nc.tensor.matmul(p_s[:, j, u, g], qk[rows, 1, g, u], qk[rows, 0, g, u],
                                                    start=True, stop=True)
                        last.then_inc(s_ps, 1)
                    pe.wait_ge(v_ready, i + 1)
                    for u in range(2):
                        pe.wait_ge(sm_ready, 2 * i + u + 1)
                        for h in range(HEADS):
                            last = nc.tensor.matmul(num[:, u, h], sm[:, u, h], v17[:, u, h], start=True, stop=True)
                        last.then_inc(n_ps, 1)
                    for u in range(2):
                        pe.wait_ge(at_ready, 2 * i + u + 1)
                        nc.tensor.transpose(p_t[:, 0, u], at_[:, u], K.ident[:]).then_inc(att_ps, 1)
                    pe.wait_ge(att_ready, i + 1)
                    for u in range(2):
                        nc.tensor.matmul(p_q[:, 0, 0, u], att[:, u], wo[:], start=True, stop=True).then_inc(o_ps, 1)


def dense_ffn_block(nc, W, K, x2):
    CH = 4
    with Space(nc) as s:
        h2 = s.sb("f_h2", [T, B, D])
        g2 = s.sb("f_g2", [T, D])
        be2 = s.sb("f_be2", [T, D])
        w1 = s.sb("f_w1", [D, CH, T])
        b1 = s.sb("f_b1", [T, CH])
        w2 = s.sb("f_w2", [T, CH, D])
        b2 = s.sb("f_b2", [T, D])
        loads = s.sem("f_loads")
        with nc.Block() as block:
            @block.sync
            def _(sp):
                sp.dma_start(g2[:], W["L0_attn_ln2_g"].partition_broadcast(T)).then_inc(loads, 16)
                sp.dma_start(be2[:], W["L0_attn_ln2_b"].partition_broadcast(T)).then_inc(loads, 16)
                sp.dma_start(w1[:].rearrange("c k n -> c (k n)"), W["L0_attn_W1"]).then_inc(loads, 16)
                sp.dma_start(w2[:], W["L0_attn_W2"].rearrange("(k p) n -> p k n", p=T)).then_inc(loads, 16)
                sp.dma_start(b1[:], W["L0_attn_b1_t"]).then_inc(loads, 16)
                sp.dma_start(b2[:], W["L0_attn_b2"].partition_broadcast(T)).then_inc(loads, 16)
                sp.wait_ge(loads, 96)
        layer_norm_block(nc, "f_ln2", x2, h2, g2, be2)
        hs = s.sb("f_hs", [T, 2, D])
        h2t = s.sb("f_h2t", [D, 2, T])
        hid = s.sb("f_hid", [T, CH, 2, T])
        p_t = s.ps("f_p_t", [T, 2, 2, T])
        p_h = s.ps("f_p_h", [T, CH, 2, T])
        hs_ready, t1, h2t_ready, h_ps, hid_ready, y_ps, y_done, base_ready = (s.sem("f_" + n) for n in (
            "hs_ready", "t1", "h2t_ready", "h_ps", "hid_ready", "y_ps", "y_done", "base_ready"))
        with nc.Block() as block:
            @block.gpsimd
            def _(g):
                g.tensor_tensor(out=x2[:], in0=x2[:], in1=per_tile(b2[:], B), op=ALU.add).then_inc(base_ready, 1)
                g.wait_ge(base_ready, 1)
                g.tensor_tensor(out=K.h[:], in0=K.h[:], in1=x2[:], op=ALU.add).then_inc(base_ready, 1)

            @block.vector
            def _(v):
                v.sem_inc(y_done, 2)
                with v.Fori(0, B // 2) as i:
                    for u in range(2):
                        v.wait_ge(y_done, 2 * i + u + 1)
                        nc.vector.tensor_copy(hs[:, u, :], h2[:, 2 * i + u, :]).then_inc(hs_ready, 1)
                    v.wait_ge(base_ready, 2)
                    v.wait_ge(y_ps, 2 * i + 2)
                    for u in range(2):
                        nc.vector.tensor_tensor(K.h[:, 2 * i + u, :], K.h[:, 2 * i + u, :], p_t[:, 1, u],
                                                ALU.add).then_inc(y_done, 1)

            @block.scalar
            def _(act):
                with act.Fori(0, B // 2) as i:
                    act.wait_ge(t1, 2 * i + 2)
                    nc.scalar.activation(h2t[:], p_t[:, 0], ACT.Copy).then_inc(h2t_ready, 1)
                    for c in range(CH):
                        act.wait_ge(h_ps, 2 * i + c // 2 + 1)
                        nc.scalar.activation(hid[:, c], p_h[:, c], ACT.Relu, bias=b1[:, c:c + 1]).then_inc(hid_ready, 1)

            @block.tensor
            def _(pe):
                with pe.Fori(0, B // 2) as i:
                    for u in range(2):
                        pe.wait_ge(hs_ready, 2 * i + u + 1)
                        nc.tensor.transpose(p_t[:, 0, u], hs[:, u], K.ident[:]).then_inc(t1, 1)
                    pe.wait_ge(h2t_ready, i + 1)
                    for c in range(CH):
                        last = nc.tensor.matmul(p_h[:, c], w1[:, c], h2t[:], start=True, stop=True)
                        if c % 2:
                            last.then_inc(h_ps, 1)
                    for u in range(2):
                        for c in range(CH):
                            pe.wait_ge(hid_ready, CH * i + c + 1)
                            last = nc.tensor.matmul(p_t[:, 1, u], hid[:, c, u], w2[:, c], start=c == 0, stop=c == CH - 1)
                        last.then_inc(y_ps, 1)


def layer0_attention(nc, W, K):
    with Space(nc) as s:
        xin = s.sb("xin", [T, B, D])
        x2 = s.sb("x2", [T, B, D])
        layer_norm_block(nc, "a0_ln0", K.h, xin)
        causal_linear_attention_block(nc, W, K, xin, x2)
        dense_ffn_block(nc, W, K, x2)
    end_of_layer(nc)


SLOTS = 128
NTOK = B * T


class Route:

    def __init__(self, s, name, experts, picks, tiles):
        self.experts, self.picks, self.tiles = experts, picks, tiles
        self.dest = s.sb(name + "_dest", [T, B, picks], i32)
        self.gate = s.sb(name + "_gate", [T, B, picks])
        self.who = s.sb(name + "_who", [SLOTS, tiles], i32)
        self.expert_of = s.sb(name + "_expert_of", [1, tiles], i32)


def router_logits_block(nc, name, K, xn, xn_dram, w_dram, experts, logits, bias_dram=None):
    Q = 4
    with Space(nc) as s:
        w = s.sb(name + "_wr", [D, experts])
        bias = s.sb(name + "_br", [T, experts])
        xs = s.sb(name + "_xs", [T, Q, D])
        xt = s.sb(name + "_xt", [D, Q, T])
        p_t = s.ps(name + "_p_t", [D, Q, T])
        p_l = s.ps(name + "_p_l", [T, 512])
        lg = p_l[:, 0:Q * experts].rearrange("t (q e) -> t q e", q=Q)
        stored, loads, xs_ready, t_ps, xt_ready, l_ps, l_ready = (s.sem(name + "_" + n) for n in (
            "stored", "loads", "xs_ready", "t_ps", "xt_ready", "l_ps", "l_ready"))
        n_loads = 32 if bias_dram is not None else 16
        with nc.Block() as block:
            @block.sync
            def _(sp):
                sp.dma_start(w[:], w_dram).then_inc(loads, 16)
                if bias_dram is not None:
                    sp.dma_start(bias[:], bias_dram.partition_broadcast(T)).then_inc(loads, 16)
                sp.dma_start(xn_dram.rearrange("(b t) c -> t b c", t=T), xn[:]).then_inc(stored, 16)
                sp.wait_ge(stored, 16)

            @block.vector
            def _(v):
                v.sem_inc(l_ready, 1)
                with v.Fori(0, B // Q) as i:
                    v.wait_ge(l_ready, i + 1)
                    nc.vector.tensor_copy(xs[:], xn[:, bass.ts(i, Q), :]).then_inc(xs_ready, 1)
                    v.wait_ge(loads, n_loads)
                    v.wait_ge(l_ps, i + 1)
                    if bias_dram is not None:
                        nc.vector.tensor_tensor(logits[:, bass.ts(i, Q), :], lg, per_tile(bias[:], Q),
                                                ALU.add).then_inc(l_ready, 1)
                    else:
                        nc.vector.tensor_copy(logits[:, bass.ts(i, Q), :], lg).then_inc(l_ready, 1)

            @block.scalar
            def _(act):
                with act.Fori(0, B // Q) as i:
                    act.wait_ge(t_ps, i + 1)
                    nc.scalar.activation(xt[:], p_t[:], ACT.Copy).then_inc(xt_ready, 1)

            @block.tensor
            def _(pe):
                pe.wait_ge(loads, n_loads)
                with pe.Fori(0, B // Q) as i:
                    pe.wait_ge(xs_ready, i + 1)
                    for q in range(Q):
                        last = nc.tensor.transpose(p_t[:, q], xs[:, q], K.ident[:])
                    last.then_inc(t_ps, 1)
                    pe.wait_ge(xt_ready, i + 1)
                    for q in range(Q):
                        last = nc.tensor.matmul(lg[:, q], xt[:, q], w[:], start=True, stop=True)
                    last.then_inc(l_ps, 1)


def sort_block(nc, name, K, route, index, chosen=None, capacity=None):
    E, P, NT = route.experts, route.picks, route.tiles
    COLS = B * E
    NB = max(1, COLS // 512)
    with Space(nc) as s:
        iota_e = s.sb(name + "_iota_e", [T, E])
        iota_row = s.sb(name + "_iota_row", [T, 256])
        iota_h = s.sb(name + "_iota_h", [T, 256], f16)
        token = s.sb(name + "_token", [T, B])
        hot = s.sb(name + "_hot", [T, B, E])
        mask = s.sb(name + "_mask", [T, B, E])
        mask_h = s.sb(name + "_mask_h", [T, B, E], f16)
        sums = s.sb(name + "_sums", [T, B + 1, E])
        sums_h = s.sb(name + "_sums_h", [T, B + 1, E], f16)
        before_h = s.sb(name + "_before_h", [T, T], f16)
        ones_h = s.sb(name + "_ones_h", [T, T], f16)
        pos = s.sb(name + "_pos", [T, B, E])
        prod = s.sb(name + "_prod", [T, B, E])
        prod2 = s.sb(name + "_prod2", [T, B, E])
        tiles_i = s.sb(name + "_tiles_i", [T, E], i32)
        tiles_f = s.sb(name + "_tiles_f", [T, E])
        incl = s.sb(name + "_incl", [T, E])
        base = s.sb(name + "_base", [T, E])
        col_i = s.sb(name + "_col_i", [E, 1], i32)
        col_f = s.sb(name + "_col_f", [E, 1])
        cum = s.sb(name + "_cum", [E, 1])
        passed = s.sb(name + "_passed", [E, NT])
        dest_f = s.sb(name + "_dest_f", [T, B, P])
        keep = s.sb(name + "_keep", [T, B, P])
        second = s.sb(name + "_second", [T, B, P])
        part_i = s.sb(name + "_part_i", [T, B, P], i32)
        lo = s.sb(name + "_lo", [T, B, P])
        hi = s.sb(name + "_hi", [T, B, P])
        R = 8
        low_hot = s.sb(name + "_low_hot", [T, R, SLOTS], f16)
        high_tok = s.sb(name + "_high_tok", [T, R, NT], f16)
        zeros_h = s.sb(name + "_zeros_h", [T, SLOTS], f16)
        p_rank = s.ps(name + "_p_rank", [T, NB, min(512, COLS)])
        p_cnt = s.ps(name + "_p_cnt", [T, 512])
        p_col = s.ps(name + "_p_col", [T, 512])
        p_who = s.ps(name + "_p_who", [T, 512])
        consts, mask_ready, rank_ps, cnt_ps, col_ps, col_ready, cum_ps, passed_ready, te_ps, hots, hots_used, \
            who_ps, own, filled = (s.sem(name + "_" + n) for n in (
                "consts", "mask_ready", "rank_ps", "cnt_ps", "col_ps", "col_ready", "cum_ps", "passed_ready",
                "te_ps", "hots", "hots_used", "who_ps", "own", "filled"))
        with nc.Block() as block:
            @block.gpsimd
            def _(g):
                g.iota(iota_e[:], pattern=[[1, E]], base=0, channel_multiplier=0,
                       allow_small_or_imprecise_dtypes=True)
                g.iota(iota_row[:], pattern=[[1, 256]], base=0, channel_multiplier=0,
                       allow_small_or_imprecise_dtypes=True)
                g.iota(iota_h[:], pattern=[[1, 256]], base=0, channel_multiplier=0,
                       allow_small_or_imprecise_dtypes=True)
                g.iota(token[:], pattern=[[T, B]], base=0, channel_multiplier=1,
                       allow_small_or_imprecise_dtypes=True)
                g.memset(zeros_h[:], 0.0)
                g.memset(sums[:, 0, :], 0.0)
                g.tensor_copy(before_h[:], K.before[:])
                g.tensor_copy(ones_h[:], K.ones[:]).then_inc(consts, 1)

            @block.vector
            def _(v):
                chain = Own(v, own)
                v.wait_ge(consts, 1)

                def flat(a):
                    return a[:].rearrange("t b k -> t (b k)")

                def one_hot(k, out):
                    return nc.vector.tensor_tensor(out, per_tile(iota_e[:], B), per_row(index[:, :, k], E),
                                                   ALU.is_equal)

                def picked(out, values, k_hot, tmp):
                    chain.done(nc.vector.tensor_tensor(tmp, k_hot, values, ALU.mult))
                    return nc.vector.tensor_reduce(out=out, in_=tmp, axis=AX.X, op=ALU.add)

                for k in range(P):
                    chain.done(one_hot(k, mask[:] if k == 0 else hot[:]))
                    if k:
                        chain.done(nc.vector.tensor_tensor(mask[:], mask[:], hot[:], ALU.add))
                for b in range(B):
                    chain.done(nc.vector.tensor_tensor(sums[:, b + 1, :], sums[:, b, :], mask[:, b, :], ALU.add))
                nc.vector.tensor_copy(mask_h[:], mask[:])
                nc.vector.tensor_copy(sums_h[:], sums[:]).then_inc(mask_ready, 1)
                if capacity is None:
                    v.wait_ge(cnt_ps, 1)
                    chain.done(nc.vector.tensor_scalar(tiles_i[:], p_cnt[:, 0:E], float(SLOTS - 1), None, ALU.add))
                    chain.done(nc.vector.tensor_scalar(tiles_i[:], tiles_i[:], 7, None, ALU.arith_shift_right))
                    chain.done(nc.vector.tensor_copy(tiles_f[:], tiles_i[:]))
                    chain.done(nc.vector.tensor_tensor_scan(incl[:], K.ones[:, 0:E], tiles_f[:], 0.0, ALU.mult, ALU.add))
                    chain.done(nc.vector.tensor_tensor(base[:], incl[:], tiles_f[:], ALU.subtract))
                    chain.done(nc.vector.tensor_scalar(base[:], base[:], float(SLOTS), None, ALU.mult))
                    v.wait_ge(col_ps, 1)
                    chain.done(nc.vector.tensor_scalar(col_i[:], p_col[0:E, 0:1], float(SLOTS - 1), None, ALU.add))
                    chain.done(nc.vector.tensor_scalar(col_i[:], col_i[:], 7, None, ALU.arith_shift_right))
                    nc.vector.tensor_copy(col_f[:], col_i[:]).then_inc(col_ready, 1)
                    v.wait_ge(cum_ps, 1)
                    chain.done(nc.vector.tensor_copy(cum[:], p_col[0:E, 0:1]))
                    nc.vector.tensor_scalar(passed[:], iota_row[0:E, 0:NT], cum[:, 0:1], None,
                                            ALU.is_ge).then_inc(passed_ready, 1)
                    v.wait_ge(te_ps, 1)
                    nc.vector.tensor_scalar(route.expert_of[:], p_col[0:1, 0:NT], float(E - 1), None, ALU.min)
                v.wait_ge(rank_ps, 1)
                ranks = p_rank[:].rearrange("t n (b e) -> t (n b) e", e=E)
                if capacity is None:
                    chain.done(nc.vector.tensor_tensor(pos[:], ranks, per_tile(base[:], B), ALU.add))
                else:
                    chain.done(nc.vector.tensor_copy(pos[:], ranks))
                for k in range(P):
                    chain.done(one_hot(k, hot[:]))
                    if chosen is not None:
                        chain.done(picked(route.gate[:, :, k], chosen[:], hot[:], prod2[:]))
                    chain.done(picked(dest_f[:, :, k], pos[:], hot[:], prod[:]))
                if capacity is None:
                    chain.done(nc.vector.tensor_copy(route.dest[:], dest_f[:]))
                    chain.done(nc.vector.tensor_scalar(part_i[:], route.dest[:], 7, None, ALU.arith_shift_right))
                    chain.done(nc.vector.tensor_copy(hi[:], part_i[:]))
                    chain.done(nc.vector.tensor_scalar(part_i[:], route.dest[:], SLOTS - 1, None, ALU.bitwise_and))
                    chain.done(nc.vector.tensor_copy(lo[:], part_i[:]))
                else:
                    chain.done(nc.vector.tensor_scalar(keep[:], dest_f[:], float(capacity), None, ALU.is_lt))
                    chain.done(nc.vector.tensor_tensor(route.gate[:], route.gate[:], keep[:], ALU.mult))
                    chain.done(nc.vector.tensor_scalar(second[:], dest_f[:], float(SLOTS), None, ALU.is_ge))
                    chain.done(nc.vector.scalar_tensor_tensor(out=flat(hi), in0=flat(index), scalar=2.0, in1=flat(second),
                                                              op0=ALU.mult, op1=ALU.add))
                    chain.done(nc.vector.scalar_tensor_tensor(out=flat(lo), in0=flat(second), scalar=-float(SLOTS),
                                                              in1=flat(dest_f), op0=ALU.mult, op1=ALU.add))
                    chain.done(nc.vector.tensor_scalar(hi[:], hi[:], float(-NT), None, ALU.add))
                    chain.done(nc.vector.tensor_tensor(hi[:], hi[:], keep[:], ALU.mult))
                    chain.done(nc.vector.tensor_scalar(hi[:], hi[:], float(NT), None, ALU.add))
                    chain.done(nc.vector.scalar_tensor_tensor(out=flat(dest_f), in0=flat(index), scalar=float(capacity),
                                                              in1=flat(dest_f), op0=ALU.mult, op1=ALU.add))
                    chain.done(nc.vector.tensor_tensor(dest_f[:], dest_f[:], keep[:], ALU.mult))
                    chain.done(nc.vector.tensor_copy(route.dest[:], dest_f[:]))
                lo_c, hi_c = lo[:].rearrange("t b k -> t (b k)"), hi[:].rearrange("t b k -> t (b k)")
                token_c = prod2[:].rearrange("t b e -> t (b e)")[:, 0:B * P]
                chain.done(nc.vector.tensor_copy(token_c.rearrange("t (b k) -> t b k", k=P), per_row(token[:], P)))
                v.sem_inc(hots_used, 1)
                with v.Fori(0, B * P // R) as i:
                    v.wait_ge(hots_used, i + 1)
                    for r in range(R):
                        c = i * R + r
                        nc.vector.tensor_scalar(low_hot[:, r], iota_h[:, 0:SLOTS], lo_c[:, bass.ds(c, 1)], None,
                                                ALU.is_equal)
                        nc.vector.tensor_scalar(high_tok[:, r], iota_h[:, 0:NT], hi_c[:, bass.ds(c, 1)],
                                                token_c[:, bass.ds(c, 1)], ALU.is_equal, ALU.mult).then_inc(hots, 1)
                v.wait_ge(who_ps, 1)
                nc.vector.tensor_copy(route.who[:], p_who[:, 0:NT])

            @block.tensor
            def _(pe):
                pe.wait_ge(mask_ready, 1)
                flat_m = mask_h[:].rearrange("t b e -> t (b e)")
                flat_s = sums_h[:].rearrange("t b e -> t (b e)")
                W_ = min(512, COLS)
                if capacity is None:
                    nc.tensor.matmul(p_cnt[:, 0:E], ones_h[:], sums_h[:, B, :], start=True, stop=True).then_inc(cnt_ps, 1)
                    nc.tensor.matmul(p_col[0:E, 0:1], sums_h[:, B, :], ones_h[:, 0:1], start=True,
                                     stop=True).then_inc(col_ps, 1)
                for n in range(NB):
                    cols = slice(n * W_, (n + 1) * W_)
                    nc.tensor.matmul(p_rank[:, n], before_h[:], flat_m[:, cols], start=True, stop=False)
                    last = nc.tensor.matmul(p_rank[:, n], ones_h[:], flat_s[:, cols], start=False, stop=True)
                last.then_inc(rank_ps, 1)
                if capacity is None:
                    pe.wait_ge(col_ready, 1)
                    nc.tensor.matmul(p_col[0:E, 0:1], K.up_to[0:E, 0:E], col_f[:], start=True, stop=True).then_inc(cum_ps, 1)
                    pe.wait_ge(passed_ready, 1)
                    nc.tensor.matmul(p_col[0:1, 0:NT], K.ones[0:E, 0:1], passed[:], start=True, stop=True).then_inc(te_ps, 1)
                nc.tensor.matmul(p_who[:, 0:NT], zeros_h[:], iota_h[:, 0:NT], start=True, stop=False)
                with pe.Fori(0, B * P // R) as i:
                    for r in range(R):
                        pe.wait_ge(hots, i * R + r + 1)
                        last = nc.tensor.matmul(p_who[:, 0:NT], low_hot[:, r], high_tok[:, r], start=False, stop=False)
                    last.then_inc(hots_used, 1)
                nc.tensor.matmul(p_who[:, 0:NT], zeros_h[:], iota_h[:, 0:NT], start=False, stop=True).then_inc(who_ps, 1)


def expert_tiles_block(nc, name, K, route, xn_dram, o_dram, w1, b1_t, w2, b2, chunks):
    E, NT, CH = route.experts, route.tiles, chunks
    TURNS = (NT + 1) // 2
    assert NT % 2 == 0
    with Space(nc) as s:
        who2 = s.sb(name + "_who2", [SLOTS, 2], i32)
        xg = s.sb(name + "_xg", [SLOTS, 2, D])
        xgt = s.sb(name + "_xgt", [D, 2, SLOTS])
        w1b = s.sb(name + "_w1b", [D, 2, CH * T])
        w2b = s.sb(name + "_w2b", [T, 2, CH, D])
        b1b = s.sb(name + "_b1b", [T, 2, CH])
        b2b = s.sb(name + "_b2b", [1, 2, D])
        hid = s.sb(name + "_hid", [T, 2, CH, SLOTS])
        ob = s.sb(name + "_ob", [SLOTS, 2, D])
        p_t = [s.ps(f"{name}_p_t{u}", [D, 512]) for u in range(2)]
        p_h = [s.ps(f"{name}_p_h{u}", [T, 4, SLOTS]) for u in range(2)]
        p_o = [s.ps(f"{name}_p_o{u}", [SLOTS, 512]) for u in range(2)]
        who_ready, gathered, w_in, t_ps, xgt_ready, h_ps, hid_ready, o_ps, ob_ready, stored = (
            [s.sem(f"{name}_{n}{u}") for u in range(2)] for n in (
                "who_ready", "gathered", "w_in", "t_ps", "xgt_ready", "h_ps", "hid_ready", "o_ps", "ob_ready", "stored"))
        with nc.Block() as block:
            @block.gpsimd
            def _(g):
                for u in range(2):
                    g.sem_inc(xgt_ready[u], 1)
                with g.Fori(0, TURNS) as i:
                    for u in range(2):
                        g.wait_ge(xgt_ready[u], i + 1)
                        g.tensor_copy(who2[:, u:u + 1], route.who[:, bass.ds(2 * i + u, 1)]).then_inc(who_ready[u], 1)
                        g.wait_ge(who_ready[u], i + 1)
                        g.nop(nofuse=True)
                        g.indirect_dma_start(out=xg[:, u, :], out_offset=None, in_=xn_dram,
                                             in_offset=bass.IndirectOffsetOnAxis(ap=who2[:, u:u + 1], axis=0)
                                             ).then_inc(gathered[u], 16)

            @block.sync
            def _(sp):
                for u in range(2):
                    sp.sem_inc(o_ps[u], 1)
                with sp.Fori(0, TURNS) as i:
                    for u in range(2):
                        e = sp.value_load(route.expert_of[0:1, bass.ds(2 * i + u, 1)], min_val=0, max_val=E - 1)
                        sp.wait_ge(o_ps[u], i + 1)
                        sp.dma_start(w1b[:, u, :], w1[bass.ds(e, 1), :, :].rearrange("a c n -> (a c) n")
                                     ).then_inc(w_in[u], 16)
                        sp.dma_start(w2b[:, u], w2[bass.ds(e, 1), :, :].rearrange("a (k p) n -> p (a k) n", p=T)
                                     ).then_inc(w_in[u], 16)
                        sp.dma_start(b1b[:, u, :], b1_t[bass.ds(e, 1), :, :].rearrange("a p k -> (a p) k")
                                     ).then_inc(w_in[u], 16)
                        sp.dma_start(b2b[:, u, :], b2[bass.ds(e, 1), :]).then_inc(w_in[u], 16)

            @block.tensor
            def _(pe):
                with pe.Fori(0, TURNS) as i:
                    for u in range(2):
                        pe.wait_ge(gathered[u], 16 * i + 16)
                        nc.tensor.transpose(p_t[u][:, 0:SLOTS], xg[:, u, :], K.ident[:]).then_inc(t_ps[u], 1)
                    for u in range(2):
                        pe.wait_ge(w_in[u], 64 * i + 64)
                        pe.wait_ge(xgt_ready[u], i + 2)
                        for c in range(CH):
                            last = nc.tensor.matmul(p_h[u][:, c], w1b[:, u, c * T:(c + 1) * T], xgt[:, u, :],
                                                    start=True, stop=True)
                        last.then_inc(h_ps[u], 1)
                    for u in range(2):
                        pe.wait_ge(hid_ready[u], CH * i + CH)
                        for c in range(CH):
                            nc.tensor.matmul(p_o[u][:, 0:D], hid[:, u, c], w2b[:, u, c], start=c == 0, stop=False)
                        nc.tensor.matmul(p_o[u][:, 0:D], K.ones[0:1, 0:SLOTS], b2b[:, u, :], start=False,
                                         stop=True).then_inc(o_ps[u], 1)

            @block.scalar
            def _(act):
                with act.Fori(0, TURNS) as i:
                    for u in range(2):
                        act.wait_ge(t_ps[u], i + 1)
                        nc.scalar.activation(xgt[:, u, :], p_t[u][:, 0:SLOTS], ACT.Copy).then_inc(xgt_ready[u], 1)
                    for u in range(2):
                        act.wait_ge(h_ps[u], i + 1)
                        for c in range(CH):
                            nc.scalar.activation(hid[:, u, c], p_h[u][:, c], ACT.Relu,
                                                 bias=b1b[:, u, c:c + 1]).then_inc(hid_ready[u], 1)
                    for u in range(2):
                        act.wait_ge(ob_ready[u], i + 1)
                        act.dma_start(o_dram[bass.ds((2 * i + u) * SLOTS, SLOTS), :], ob[:, u, :]).then_inc(stored[u], 16)
                for u in range(2):
                    act.wait_ge(stored[u], 16 * TURNS + 16)

            @block.vector
            def _(v):
                for u in range(2):
                    v.sem_inc(stored[u], 16)
                with v.Fori(0, TURNS) as i:
                    for u in range(2):
                        v.wait_ge(o_ps[u], i + 2)
                        v.wait_ge(stored[u], 16 * i + 16)
                        nc.vector.tensor_copy(ob[:, u, :], p_o[u][:, 0:D]).then_inc(ob_ready[u], 1)


def combine_block(nc, name, K, route, o_dram, n_seq):
    P = route.picks
    R = n_seq * P
    TURNS = B // (2 * n_seq)
    with Space(nc) as s:
        at = s.sb(name + "_at", [T, 2, R], i32)
        og = s.sb(name + "_og", [T, 2, R, D])
        at_ready = [s.sem(f"{name}_at_ready{u}") for u in range(2)]
        used = [s.sem(f"{name}_used{u}") for u in range(2)]
        got = [[s.sem(f"{name}_got{u}_{r}") for r in range(R)] for u in range(2)]
        own = s.sem(name + "_own")
        dest_c = route.dest[:].rearrange("t b k -> t (b k)")
        gate_c = route.gate[:].rearrange("t b k -> t (b k)")
        with nc.Block() as block:
            @block.gpsimd
            def _(g):
                for u in range(2):
                    g.sem_inc(used[u], 1)
                with g.Fori(0, TURNS) as i:
                    for u in range(2):
                        g.wait_ge(used[u], i + 1)
                        g.tensor_copy(at[:, u, :], dest_c[:, bass.ds((2 * i + u) * R, R)]).then_inc(at_ready[u], 1)
                        g.wait_ge(at_ready[u], i + 1)
                        g.nop(nofuse=True)
                        for r in range(R):
                            g.indirect_dma_start(out=og[:, u, r, :], out_offset=None, in_=o_dram,
                                                 in_offset=bass.IndirectOffsetOnAxis(ap=at[:, u, r:r + 1], axis=0)
                                                 ).then_inc(got[u][r], 16)

            @block.vector
            def _(v):
                with v.Fori(0, TURNS) as i:
                    for u in range(2):
                        for r in range(R):
                            n = (2 * i + u) * R + r
                            k, m = r % P, r // P
                            b = (2 * i + u) * n_seq + m
                            v.wait_ge(got[u][r], 16 * i + 16)
                            if k:
                                v.wait_ge(own, n)
                            ins = nc.vector.scalar_tensor_tensor(out=K.h[:, b, :], in0=og[:, u, r, :],
                                                                 scalar=gate_c[:, bass.ds(n, 1)], in1=K.h[:, b, :],
                                                                 op0=ALU.mult, op1=ALU.add)
                            ins.then_inc(own, 1)
                        v.wait_ge(own, (2 * i + u + 1) * R)
                        v.sem_inc(used[u], 1)


def top1_experts(nc, W, K, name, experts, chunks, soft_gate):
    NT = 2 * -(-(NTOK // SLOTS + experts - 1) // 2)
    xn_dram = nc.dram_tensor(name + "_xn_dram", (NTOK, D), f32, kind="Internal").ap()
    o_dram = nc.dram_tensor(name + "_o_dram", (NT * SLOTS, D), f32, kind="Internal").ap()
    with Space(nc) as s:
        route = Route(s, name, experts, 1, NT)
        with Space(nc) as s2:
            xn = s2.sb(name + "_xn", [T, B, D])
            logits = s2.sb(name + "_logits", [T, B, experts])
            layer_norm_block(nc, name + "_ln", K.h, xn)
            router_logits_block(nc, name + "_r", K, xn, xn_dram, W[name + "_Wr"], experts, logits, W[name + "_br"])
            index = s2.sb(name + "_index", [T, B, 1])
            top = s2.sb(name + "_top", [T, B, 8])
            which = s2.sb(name + "_which", [T, B, 8], u32)
            low = s2.sb(name + "_low", [T, B, experts])
            total = s2.sb(name + "_total", [T, B])
            own = s2.sem(name + "_own")
            low_ready = s2.sem(name + "_low_ready")
            exp_ready = s2.sem(name + "_exp_ready")
            with nc.Block() as block:
                @block.scalar
                def _(act):
                    if soft_gate:
                        act.wait_ge(low_ready, 1)
                        nc.scalar.activation(low[:], low[:], ACT.Exp).then_inc(exp_ready, 1)

                @block.vector
                def _(v):
                    chain = Own(v, own)
                    if soft_gate:
                        chain.done(nc.vector.tensor_reduce(out=total[:], in_=logits[:], axis=AX.X, op=ALU.max))
                        nc.vector.tensor_tensor(low[:], logits[:], per_row(total[:], experts),
                                                ALU.subtract).then_inc(low_ready, 1)
                        v.wait_ge(exp_ready, 1)
                        chain.done(nc.vector.tensor_reduce(out=total[:], in_=low[:], axis=AX.X, op=ALU.add))
                        nc.vector.reciprocal(route.gate[:].rearrange("t b k -> t (b k)"), total[:])
                        values = low
                    else:
                        nc.vector.memset(route.gate[:], 1.0)
                        values = logits
                    for b in range(B):
                        ins = nc.vector.max(top[:, b, :], values[:, b, :])
                    chain.done(ins)
                    for b in range(B):
                        ins = nc.vector.max_index(which[:, b, :], top[:, b, :], values[:, b, :])
                    chain.done(ins)
                    chain.done(nc.vector.tensor_copy(index[:], which[:, :, 0:1]))
            sort_block(nc, name + "_sort", K, route, index)
        expert_tiles_block(nc, name + "_x", K, route, xn_dram, o_dram, W[name + "_W1"], W[name + "_b1_t"], W[name + "_W2"],
                           W[name + "_b2"], chunks)
        combine_block(nc, name + "_c", K, route, o_dram, 4)
    end_of_layer(nc)


def householder_attention(nc, W, K):
    NH, DH, PER = 8, 32, 4
    F = NH * DH
    CK = 32
    NC = T // CK
    PAIRS = B * NH
    diag_dram = nc.dram_tensor("a1_diag_dram", (PAIRS, T, CK), f32, kind="Internal").ap()
    inv_dram = nc.dram_tensor("a1_inv_dram", (PAIRS, T, CK), f32, kind="Internal").ap()

    def per_head(a):
        return a[:].rearrange("t b (h d) -> t (b h) d", d=DH)

    with Space(nc) as s:
        wkv = s.sb("a1_wkv", [D, 2, F])
        wq = s.sb("a1_wq", [D, F])
        ww = s.sb("a1_ww", [D, F])
        wbg = s.sb("a1_wbg", [D, 2 * NH])
        wo = s.sb("a1_wo", [T, 2, D])
        bbg = s.sb("a1_bbg", [T, 2 * NH])
        head_rows = s.sb("a1_head_rows", [T, PER, T])
        xt = s.sb("a1_xt", [D, B, T])
        kv = s.sb("a1_kv", [T, B, 2, F])
        wn = s.sb("a1_wn", [T, B, F])
        bg = s.sb("a1_bg", [T, B, 2 * NH])
        ss = s.sb("a1_ss", [T, B, NH])
        rw = s.sb("a1_rw", [T, B, NH])
        loads = s.sem("a1_loads")
        xn = s.sb("a1_xn", [T, B, D])
        layer_norm_block(nc, "a1_ln", K.h, xn)
        with Space(nc) as s2:
            xs = s2.sb("a1_xs", [T, 2, D])
            xts = s2.sb("a1_xts", [D, 2, T])
            sq = s2.sb("a1_sq", [T, 2, F])
            p_t = [s2.ps(f"a1_p_t{u}", [D, 512]) for u in range(2)]
            p_kv = [s2.ps(f"a1_p_kv{u}", [T, 2, F]) for u in range(2)]
            p_w = [s2.ps(f"a1_p_w{u}", [T, 512]) for u in range(2)]
            xs_ready, t_ps, xts_ready, kv_ps, w_ps, kv_done, w_done, sq_ready = (
                [s2.sem(f"a1_{n}{u}") for u in range(2)] for n in (
                    "xs_ready", "t_ps", "xts_ready", "kv_ps", "w_ps", "kv_done", "w_done", "sq_ready"))
            with nc.Block() as block:
                @block.sync
                def _(sp):
                    sp.dma_start(wkv[:, 0], W["L1_attn_Wk_t"]).then_inc(loads, 16)
                    sp.dma_start(wkv[:, 1], W["L1_attn_Wv_t"]).then_inc(loads, 16)
                    sp.dma_start(wq[:], W["L1_attn_Wq_t"]).then_inc(loads, 16)
                    sp.dma_start(ww[:], W["L1_attn_Ww_t"]).then_inc(loads, 16)
                    sp.dma_start(wbg[:, 0:NH], W["L1_attn_Wbeta_t"]).then_inc(loads, 16)
                    sp.dma_start(wbg[:, NH:2 * NH], W["L1_attn_Wg_t"]).then_inc(loads, 16)
                    sp.dma_start(bbg[:, 0:NH], W["L1_attn_bbeta"].partition_broadcast(T)).then_inc(loads, 16)
                    sp.dma_start(bbg[:, NH:2 * NH], W["L1_attn_bg"].partition_broadcast(T)).then_inc(loads, 16)
                    sp.dma_start(wo[:], W["L1_attn_Wo_t"].rearrange("(g p) n -> p g n", p=T)).then_inc(loads, 16)
                    sp.dma_start(head_rows[:], W["head_rows"]).then_inc(loads, 16)
                    sp.wait_ge(loads, 160)

                @block.vector
                def _(v):
                    for u in range(2):
                        v.sem_inc(xts_ready[u], 1)
                    with v.Fori(0, B // 2) as i:
                        for u in range(2):
                            b = 2 * i + u
                            v.wait_ge(xts_ready[u], i + 1)
                            nc.vector.tensor_copy(xs[:, u], xn[:, b, :]).then_inc(xs_ready[u], 1)
                        for u in range(2):
                            b = 2 * i + u
                            v.wait_ge(w_ps[u], i + 1)
                            nc.vector.tensor_tensor(bg[:, b, :], p_w[u][:, F:F + 2 * NH], bbg[:], ALU.add)
                            nc.vector.tensor_copy(wn[:, b, :], p_w[u][:, 0:F]).then_inc(w_done[u], 1)
                            v.wait_ge(w_done[u], i + 1)
                            nc.vector.tensor_tensor(sq[:, u], wn[:, b, :], wn[:, b, :], ALU.mult).then_inc(sq_ready[u], 1)
                            v.wait_ge(sq_ready[u], i + 1)
                            nc.vector.tensor_reduce(out=ss[:, b, :], in_=sq[:, u].rearrange("t (h d) -> t h d", d=DH),
                                                    axis=AX.X, op=ALU.add)

                @block.scalar
                def _(act):
                    with act.Fori(0, B // 2) as i:
                        for u in range(2):
                            act.wait_ge(t_ps[u], i + 1)
                            nc.scalar.activation(xts[:, u], p_t[u][:, 0:T], ACT.Copy)
                            nc.scalar.activation(xt[:, 2 * i + u, :], p_t[u][:, 0:T], ACT.Copy).then_inc(xts_ready[u], 1)
                        for u in range(2):
                            act.wait_ge(kv_ps[u], i + 1)
                            nc.scalar.activation(kv[:, 2 * i + u], p_kv[u][:], ACT.Copy).then_inc(kv_done[u], 1)

                @block.tensor
                def _(pe):
                    pe.wait_ge(loads, 160)
                    for u in range(2):
                        pe.sem_inc(kv_done[u], 1)
                    with pe.Fori(0, B // 2) as i:
                        for u in range(2):
                            pe.wait_ge(xs_ready[u], i + 1)
                            nc.tensor.transpose(p_t[u][:, 0:T], xs[:, u], K.ident[:]).then_inc(t_ps[u], 1)
                        for u in range(2):
                            pe.wait_ge(xts_ready[u], i + 2)
                            pe.wait_ge(kv_done[u], i + 1)
                            nc.tensor.matmul(p_kv[u][:], xts[:, u], wkv[:], start=True, stop=True).then_inc(kv_ps[u], 1)
                            nc.tensor.matmul(p_w[u][:, 0:F], xts[:, u], ww[:], start=True, stop=True)
                            nc.tensor.matmul(p_w[u][:, F:F + 2 * NH], xts[:, u], wbg[:], start=True,
                                             stop=True).then_inc(w_ps[u], 1)
        own = s.sem("a1_own")
        norm_ready = s.sem("a1_norm_ready")
        exp_ready = s.sem("a1_exp_ready")
        with nc.Block() as block:
            @block.scalar
            def _(act):
                nc.scalar.activation(rw[:], ss[:], ACT.Sqrt).then_inc(norm_ready, 1)
                nc.scalar.activation(bg[:], bg[:], ACT.Exp, scale=-1.0).then_inc(exp_ready, 1)

            @block.vector
            def _(v):
                chain = Own(v, own)
                v.wait_ge(norm_ready, 1)
                chain.done(nc.vector.tensor_scalar(rw[:], rw[:], 1e-6, None, ALU.add))
                nc.vector.reciprocal(rw[:].rearrange("t b h -> t (b h)"), rw[:].rearrange("t b h -> t (b h)"))
                v.wait_ge(exp_ready, 1)
                chain.done(nc.vector.tensor_scalar(bg[:], bg[:], 1.0, None, ALU.add))
                chain.done(nc.vector.reciprocal(bg[:].rearrange("t b h -> t (b h)"), bg[:].rearrange("t b h -> t (b h)")))
                chain.done(nc.vector.tensor_tensor(per_head(wn), per_head(wn), rw[:].rearrange("t b h -> t (b h)").unsqueeze(2)
                                                   .to_broadcast([T, B * NH, DH]), ALU.mult))
                nc.vector.tensor_scalar(bg[:, :, 0:NH], bg[:, :, 0:NH], 2.0, None, ALU.mult)
                chain.done(nc.vector.tensor_scalar(bg[:, :, NH:2 * NH], bg[:, :, NH:2 * NH], DH ** -0.5, None, ALU.mult))

        wt = s.sb("a1_wt", [T, B, 4, T])
        diagonal_products(nc, s, K, wn, bg, wt, diag_dram)
        invert_diagonal_blocks(nc, K, diag_dram, inv_dram)
        solve_and_attend(nc, W, K, wkv, wq, wo, head_rows, xt, kv, wn, bg, wt, inv_dram)
    end_of_layer(nc)


def diagonal_products(nc, s, K, wn, bg, wt, diag_dram):
    NH, DH, PER, CK = 8, 32, 4, 32
    NC = T // CK
    with Space(nc) as s:
        ws = s.sb("a1d_ws", [T, 2, 2, NH * DH])
        wts = s.sb("a1d_wts", [T, 2, 4, T])
        neg = s.sb("a1d_neg", [T, B // 2, 2, NH, CK])
        p_t = [s.ps(f"a1d_p_t{u}", [T, 4, T]) for u in range(2)]
        p_d = s.ps("a1d_p_d", [T, PER, 512])
        pd = p_d[:, :, 0:2 * 2 * CK].rearrange("t j (u g i) -> t j u g i", u=2, g=2)
        ws_ready, bws_ready, t_ps, wts_ready, d_ps, neg_ready, kept, stored = (s.sem("a1d_" + n) for n in (
            "ws_ready", "bws_ready", "t_ps", "wts_ready", "d_ps", "neg_ready", "kept", "stored"))
        with nc.Block() as block:
            @block.gpsimd
            def _(g):
                with g.Fori(0, B // 2) as i:
                    for u in range(2):
                        b = 2 * i + u
                        g.wait_ge(t_ps, b + 1)
                        g.tensor_copy(ws[:, u, 0], wn[:, b, :]).then_inc(ws_ready, 1)
                    for u in range(2):
                        b = 2 * i + u
                        g.wait_ge(wts_ready, b + 1)
                        g.tensor_copy(wt[:, b], wts[:, u]).then_inc(kept, 1)

            @block.vector
            def _(v):
                v.sem_inc(t_ps, 2)
                with v.Fori(0, B // 2) as i:
                    for u in range(2):
                        b = 2 * i + u
                        v.wait_ge(t_ps, b + 1)
                        nc.vector.tensor_tensor(ws[:, u, 1].rearrange("t (h d) -> t h d", d=DH),
                                                wn[:, b, :].rearrange("t (h d) -> t h d", d=DH),
                                                bg[:, b, 0:NH].unsqueeze(2).to_broadcast([T, NH, DH]),
                                                ALU.mult).then_inc(bws_ready, 1)
                    v.wait_ge(d_ps, i + 1)
                    for u in range(2):
                        nc.vector.tensor_scalar(neg[:, i, u].rearrange("t (g j) c -> t j g c", g=2), pd[:, :, u], -1.0,
                                                None, ALU.mult).then_inc(neg_ready, 1)

            @block.scalar
            def _(act):
                act.sem_inc(kept, 2)
                with act.Fori(0, B // 2) as i:
                    for u in range(2):
                        b = 2 * i + u
                        act.wait_ge(kept, b + 1)
                        act.wait_ge(t_ps, b + 3)
                        nc.scalar.activation(wts[:, u], p_t[u][:], ACT.Copy).then_inc(wts_ready, 1)

            @block.tensor
            def _(pe):
                pe.sem_inc(neg_ready, 2)
                with pe.Fori(0, B // 2) as i:
                    for u in range(2):
                        b = 2 * i + u
                        pe.wait_ge(ws_ready, b + 1)
                        pe.wait_ge(bws_ready, b + 1)
                        for n in range(4):
                            last = nc.tensor.transpose(p_t[u][:, n], ws[:, u, n // 2, (n % 2) * T:(n % 2 + 1) * T],
                                                       K.ident[:])
                        last.then_inc(t_ps, 1)
                    pe.wait_ge(neg_ready, 2 * i + 2)
                    for u in range(2):
                        pe.wait_ge(wts_ready, 2 * i + u + 1)
                        pe.nop(nofuse=True)
                        for c in range(NC):
                            t = slice(CK * c, CK * c + CK)
                            for g in range(2):
                                for j in range(PER):
                                    r = slice(DH * j, DH * j + DH)
                                    last = nc.tensor.matmul(pd[t, j, u, g], wts[r, u, 2 + g, t], wts[r, u, g, t],
                                                            start=True, stop=True)
                    last.then_inc(d_ps, 1)

            @block.sync
            def _(sp):
                with sp.Fori(0, B // 2) as i:
                    sp.wait_ge(neg_ready, 2 * i + 4)
                    sp.dma_start(diag_dram[bass.ds(i * 2 * NH, 2 * NH)].rearrange("p t c -> t p c"),
                                 neg[:, i].rearrange("t u h c -> t (u h) c")).then_inc(stored, 16)
                sp.wait_ge(stored, 16 * (B // 2))


def invert_diagonal_blocks(nc, K, diag_dram, inv_dram):
    CK = 32
    NC = T // CK
    SPLIT = 3
    with Space(nc) as s:
        low = s.sb("a1i_low", [T, NC, CK, CK])
        inv = s.sb("a1i_inv", [T, NC, CK, CK])
        terms = s.sb("a1i_terms", [T, NC, CK, CK])
        low_in, inv_made, own, stored, done = (s.sem("a1i_" + n) for n in (
            "low_in", "inv_made", "own", "stored", "done"))

        def rows(engine, chunks, sem):
            chain = Own(engine, sem)
            for i in range(1, CK):
                shape = [T, chunks.stop - chunks.start, i, i]
                chain.done(engine.tensor_tensor(out=terms[:, chunks, 0:i, 0:i], in0=inv[:, chunks, 0:i, 0:i],
                                                in1=low[:, chunks, i, 0:i].unsqueeze(2).to_broadcast(shape), op=ALU.mult))
                chain.done(nc.vector.tensor_reduce(out=inv[:, chunks, 0:i, i], in_=terms[:, chunks, 0:i, 0:i],
                                                   axis=AX.X, op=ALU.add))

        with nc.Block() as block:
            @block.sync
            def _(sp):
                sp.dma_start(low[:].rearrange("p n i j -> p (n i) j"), diag_dram).then_inc(low_in, 16)
                sp.wait_ge(done, 1)
                sp.dma_start(inv_dram, inv[:].rearrange("p n k i -> p (n k) i")).then_inc(stored, 16)
                sp.wait_ge(stored, 16)

            @block.gpsimd
            def _(g):
                for n in range(NC):
                    g.affine_select(out=inv[:, n], in_=K.ones[:, 0:1].unsqueeze(2).to_broadcast([T, CK, CK]),
                                    compare_op=ALU.is_equal, fill=0.0, base=0, pattern=[[1, CK], [-1, CK]],
                                    channel_multiplier=0).then_inc(inv_made, 1)

            @block.vector
            def _(v):
                v.wait_ge(inv_made, NC)
                v.wait_ge(low_in, 16)
                rows(nc.vector, slice(0, NC), own)
                v.sem_inc(done, 1)


def solve_and_attend(nc, W, K, wkv, wq, wo, head_rows, xt, kv, wn, bg, wt, inv_dram):
    NH, DH, PER, CK = 8, 32, 4, 32
    NC = T // CK
    ST = 2 * NC
    with Space(nc) as s:
        w_cur = s.sb("a1s_w", [T, 2, T])
        bw_bd = s.sb("a1s_bw_bd", [T, 2, PER, T])
        qkv = s.sb("a1s_qkv", [T, 2, 3, T])
        q_bd = s.sb("a1s_q_bd", [T, 2, 2, PER, T])
        lo = s.sb("a1s_lo", [T, 2, 2, PER, T])
        bm = s.sb("a1s_bm", [T, 2, 2, PER, T])
        am = s.sb("a1s_am", [T, 2, 2, PER, T])
        cm = s.sb("a1s_cm", [T, 2, PER, T])
        xs = s.sb("a1s_xs", [T, 2, NH, CK])
        k_cur = s.sb("a1s_k", [T, 2, 2, PER * DH])
        rr = s.sb("a1s_rr", [T, 2, PER * DH])
        uu = s.sb("a1s_uu", [T, 2, PER * DH])
        ut = s.sb("a1s_ut", [T, 2, T])
        at_ = s.sb("a1s_at", [T, 2, T])
        att = s.sb("a1s_att", [T, 2, T])
        p_l = s.ps("a1s_p_l", [T, PER, T])
        p_b = s.ps("a1s_p_b", [T, PER, T])
        p_a = s.ps("a1s_p_a", [T, PER, T])
        p_q = s.ps("a1s_p_q", [T, 4, T])
        p_c = [s.ps(f"a1s_p_c{g}", [T, 4, T]) for g in range(2)]
        p_o = s.ps("a1s_p_o", [T, 4, T])
        k_ready, w_ready, bw_ready, qkv_ps, qkv_ready, q_ready, l_ps, l_ready, b_ps, b_ready, a_ps, a_ready, c_ps, c_ready, \
            ch_ps, ch_done, ut_ps, ut_ready = ([s.sem(f"a1s_{n}{g}") for g in range(2)] for n in (
                "k_ready", "w_ready", "bw_ready", "qkv_ps", "qkv_ready", "q_ready", "l_ps", "l_ready", "b_ps", "b_ready", "a_ps",
                "a_ready", "c_ps", "c_ready", "ch_ps", "ch_done", "ut_ps", "ut_ready"))
        x_in = [s.sem(f"a1s_x_in{p}") for p in range(2)]
        o_ps, at_ready, att_ps, att_ready, h_ps, h_done = (s.sem("a1s_" + n) for n in (
            "o_ps", "at_ready", "att_ps", "att_ready", "h_ps", "h_done"))

        def sequences(engine, body, finish, products=None):
            if products is not None:
                products(0, 0, True)
            body(0, 0, True, False)
            with engine.Fori(0, B // 2 - 1) as i:
                body(2 * i + 1, 1, False, False)
                body(2 * i + 2, 0, False, False)
            body(B - 1, 1, False, True)
            if finish is not None:
                finish(B - 1)

        with nc.Block() as block:
            @block.sync
            def _(sp):
                def load(n, p):
                    sp.dma_start(xs[:, p], inv_dram[bass.ds(n * NH, NH)].rearrange("p t c -> t p c")).then_inc(x_in[p], 16)

                load(0, 0)
                load(1, 1)
                with sp.Fori(0, B // 2 - 1) as i:
                    for p in range(2):
                        sp.wait_ge(ch_ps[1], ST * (2 * i + p + 1))
                        load(2 * i + 2 + p, p)

            @block.gpsimd
            def _(g):
                def w_of(n, r, first):
                    if not first:
                        g.wait_ge(b_ps[r], n)
                    g.tensor_copy(w_cur[:, r], wt[:, n, r, :]).then_inc(w_ready[r], 1)
                    g.tensor_tensor(out=bw_bd[:, r], in0=wt[:, n, 2 + r, :].unsqueeze(1).to_broadcast([T, PER, T]),
                                    in1=head_rows[:], op=ALU.mult).then_inc(bw_ready[r], 1)

                def q_of(n, p, r, early):
                    g.wait_ge(qkv_ready[r], n + 1)
                    if not early:
                        g.wait_ge(c_ps[r], n - 1)
                    g.tensor_copy(k_cur[:, p, r], kv[:, n, 0, r * PER * DH:(r + 1) * PER * DH]).then_inc(k_ready[r], 1)
                    g.tensor_tensor(out=q_bd[:, p, r], in0=qkv[:, r, 0].unsqueeze(1).to_broadcast([T, PER, T]),
                                    in1=head_rows[:], op=ALU.mult).then_inc(q_ready[r], 1)

                def seq(n, p, first, early):
                    for r in range(2):
                        w_of(n, r, first)
                    for r in range(2):
                        q_of(n, p, r, early)

                seq(0, 0, True, True)
                seq(1, 1, False, True)
                with g.Fori(1, B // 2) as i:
                    for p in range(2):
                        seq(2 * i + p, p, False, False)

            @block.vector
            def _(v):
                def step(b, k):
                    c, x = divmod(k, 2)
                    t = slice(CK * c, CK * c + CK)
                    v.wait_ge(ch_ps[0], ST * b + k + 1)
                    nc.vector.tensor_copy((uu if x else rr)[t, 0], p_c[0][t, x]).then_inc(ch_done[0], 1)

                def mask(sem, n, out, product, m, ready):
                    v.wait_ge(sem, n + 1)
                    nc.vector.tensor_tensor(out, product, per_tile(m, PER), ALU.mult).then_inc(ready, 1)

                def finish(b):
                    v.wait_ge(h_ps, b + 1)
                    nc.vector.tensor_tensor(K.h[:, b, :], K.h[:, b, :], p_o[:, 0], ALU.add).then_inc(h_done, 1)

                def keys(n, p, r):
                    mask(b_ps[r], n, bm[:, p, r], p_b[:], K.before[:], b_ready[r])

                def queries(n, p, r):
                    mask(a_ps[r], n, am[:, p, r], p_a[:], K.up_to[:], a_ready[r])

                def products(n, p, first):
                    for r in range(2):
                        keys(n, p, r)
                        queries(n, p, r)

                def body(b, p, first, last):
                    n, q = b + 1, 1 - p
                    step(b, 0)
                    step(b, 1)
                    if not first:
                        finish(b - 1)
                    step(b, 2)
                    if not last:
                        keys(n, q, 0)
                    step(b, 3)
                    if not last:
                        queries(n, q, 0)
                    step(b, 4)
                    if not last:
                        keys(n, q, 1)
                    step(b, 5)
                    if not last:
                        queries(n, q, 1)
                    step(b, 6)
                    step(b, 7)
                    mask(c_ps[0], b, cm[:, 0], p_b[:], K.up_to[:], c_ready[0])
                    mask(c_ps[1], b, cm[:, 1], p_a[:], K.up_to[:], c_ready[1])
                    v.wait_ge(o_ps, b + 1)
                    nc.vector.tensor_tensor(at_[:].rearrange("t g (j d) -> t (g j) d", d=DH),
                                            p_o[:, 0:2].rearrange("t g (j d) -> t (g j) d", d=DH),
                                            bg[:, b, NH:2 * NH].unsqueeze(2).to_broadcast([T, NH, DH]),
                                            ALU.mult).then_inc(at_ready, 1)

                sequences(v, body, finish, products)

            @block.scalar
            def _(act):
                def step(b, k):
                    c, x = divmod(k, 2)
                    t = slice(CK * c, CK * c + CK)
                    act.wait_ge(ch_ps[1], ST * b + k + 1)
                    nc.scalar.activation((uu if x else rr)[t, 1], p_c[1][t, x], ACT.Copy).then_inc(ch_done[1], 1)

                def project(n, r, first):
                    if not first:
                        act.wait_ge(a_ps[r], n)
                    act.wait_ge(qkv_ps[r], n + 1)
                    nc.scalar.activation(qkv[:, r], p_q[:, 0:3], ACT.Copy).then_inc(qkv_ready[r], 1)

                def low(n, p, r):
                    act.wait_ge(l_ps[r], n + 1)
                    nc.scalar.activation(lo[:, p, r], p_l[:], ACT.Copy, scale=-1.0).then_inc(l_ready[r], 1)

                def finish(b):
                    act.wait_ge(att_ps, b + 1)
                    nc.scalar.activation(att[:], p_o[:, 2:4], ACT.Copy).then_inc(att_ready, 1)

                def products(n, p, first):
                    for r in range(2):
                        project(n, r, first)
                    for r in range(2):
                        low(n, p, r)

                def body(b, p, first, last):
                    n, q = b + 1, 1 - p
                    step(b, 0)
                    if not first:
                        finish(b - 1)
                    if not last:
                        project(n, 0, False)
                    step(b, 1)
                    if not last:
                        project(n, 1, False)
                    step(b, 2)
                    if not last:
                        low(n, q, 0)
                    step(b, 3)
                    step(b, 4)
                    if not last:
                        low(n, q, 1)
                    step(b, 5)
                    step(b, 6)
                    step(b, 7)
                    for r in range(2):
                        act.wait_ge(ut_ps[r], b + 1)
                        nc.scalar.activation(ut[:, r], p_c[r][:, 2], ACT.Copy, scale=-1.0).then_inc(ut_ready[r], 1)

                sequences(act, body, finish, products)

            @block.tensor
            def _(pe):
                def project(n, r, first):
                    if r or not first:
                        pe.wait_ge(qkv_ready[1 - r], n + r)
                    cols = slice(r * T, (r + 1) * T)
                    for k, w in enumerate((wq[:, cols], wkv[:, 0, cols], wkv[:, 1, cols])):
                        last = nc.tensor.matmul(p_q[:, k], w, xt[:, n, :], start=True, stop=True)
                    last.then_inc(qkv_ps[r], 1)

                def low(n, r, first):
                    pe.wait_ge(w_ready[r], n + 1)
                    pe.wait_ge(bw_ready[r], n + 1)
                    if r or not first:
                        pe.wait_ge(l_ready[1 - r], n + r)
                    nc.tensor.matmul(p_l[:], w_cur[:, r], bw_bd[:, r], start=True, stop=True).then_inc(l_ps[r], 1)

                def keys(n, r, early):
                    pe.wait_ge(qkv_ready[r], n + 1)
                    if r:
                        pe.wait_ge(b_ready[0], n + 1)
                    elif not early:
                        pe.wait_ge(c_ready[0], n - 1)
                    nc.tensor.matmul(p_b[:], qkv[:, r, 2], bw_bd[:, r], start=True, stop=True).then_inc(b_ps[r], 1)

                def queries(n, p, r, early):
                    pe.wait_ge(q_ready[r], n + 1)
                    if r:
                        pe.wait_ge(a_ready[0], n + 1)
                    elif not early:
                        pe.wait_ge(c_ready[1], n - 1)
                    nc.tensor.matmul(p_a[:], qkv[:, r, 1], q_bd[:, p, r], start=True, stop=True).then_inc(a_ps[r], 1)

                def products(n, p, first):
                    for r in range(2):
                        project(n, r, first)
                    for r in range(2):
                        low(n, r, first)
                        keys(n, r, True)
                        queries(n, p, r, True)

                def right_side(b, p, c, first):
                    t = slice(CK * c, CK * c + CK)
                    for r in range(2):
                        if c == 0:
                            pe.wait_ge(k_ready[r], b + 1)
                            pe.wait_ge(b_ready[r], b + 1)
                            pe.wait_ge(l_ready[r], b + 1)
                        else:
                            pe.wait_ge(ch_done[r], ST * b + 2 * c)
                        pe.nop(nofuse=True)
                        for j in range(PER):
                            out = p_c[r][t, 0, j * DH:(j + 1) * DH]
                            last = nc.tensor.matmul(out, bm[:, p, r, j, t], k_cur[:, p, r, j * DH:(j + 1) * DH],
                                                    start=j == 0, stop=c == 0 and j == PER - 1)
                            if c:
                                last = nc.tensor.matmul(out, lo[0:CK * c, p, r, j, t], uu[0:CK * c, r, j * DH:(j + 1) * DH],
                                                        start=False, stop=j == PER - 1)
                        last.then_inc(ch_ps[r], 1)

                def solve(b, p, c, loaded):
                    t = slice(CK * c, CK * c + CK)
                    for r in range(2):
                        if c == 0:
                            pe.wait_ge(x_in[p], loaded)
                        pe.wait_ge(ch_done[r], ST * b + 2 * c + 1)
                        pe.nop(nofuse=True)
                        for j in range(PER):
                            last = nc.tensor.matmul(p_c[r][t, 1, j * DH:(j + 1) * DH], xs[t, p, PER * r + j],
                                                    rr[t, r, j * DH:(j + 1) * DH], start=True, stop=True)
                        last.then_inc(ch_ps[r], 1)

                def values(b, p, r):
                    pe.wait_ge(a_ready[r], b + 1)
                    for j in range(PER):
                        h = PER * r + j
                        nc.tensor.matmul(p_o[:, r, j * DH:(j + 1) * DH], am[:, p, r, j], kv[:, b, 1, h * DH:(h + 1) * DH],
                                         start=h == 0, stop=False)

                def transpose_out(b):
                    pe.wait_ge(at_ready, b + 1)
                    for r in range(2):
                        last = nc.tensor.transpose(p_o[:, 2 + r], at_[:, r], K.ident[:])
                    last.then_inc(att_ps, 1)

                def project_out(b):
                    pe.wait_ge(att_ready, b + 1)
                    for r in range(2):
                        last = nc.tensor.matmul(p_o[:, 0], att[:, r], wo[:, r], start=r == 0, stop=r == 1)
                    last.then_inc(h_ps, 1)

                def finish(b):
                    transpose_out(b)
                    project_out(b)

                def body(b, p, first, last):
                    n, q = b + 1, 1 - p
                    loaded = 16 * (b // 2) + 16 if isinstance(b, int) else 8 * (b - p) + 16
                    right_side(b, p, 0, first)
                    if not first:
                        transpose_out(b - 1)
                    if not last:
                        project(n, 0, False)
                    solve(b, p, 0, loaded)
                    if not first:
                        project_out(b - 1)
                    if not last:
                        project(n, 1, False)
                    right_side(b, p, 1, first)
                    if not last:
                        low(n, 0, False)
                        keys(n, 0, first)
                    solve(b, p, 1, loaded)
                    if not last:
                        queries(n, q, 0, first)
                    right_side(b, p, 2, first)
                    if not last:
                        low(n, 1, False)
                        keys(n, 1, first)
                    solve(b, p, 2, loaded)
                    if not last:
                        queries(n, q, 1, first)
                    right_side(b, p, 3, first)
                    if not first:
                        pe.wait_ge(h_done, b)
                    values(b, p, 0)
                    solve(b, p, 3, loaded)
                    values(b, p, 1)
                    for r in range(2):
                        pe.wait_ge(ch_done[r], ST * b + ST)
                        nc.tensor.transpose(p_c[r][:, 2], uu[:, r], K.ident[:]).then_inc(ut_ps[r], 1)
                    for r, bank in enumerate((p_b, p_a)):
                        pe.wait_ge(ut_ready[r], b + 1)
                        if last:
                            pe.wait_ge((b_ready, a_ready)[r][1], b + 1)
                        else:
                            pe.wait_ge((b_ready, a_ready)[r][1], b + 2)
                        nc.tensor.matmul(bank[:], ut[:, r], q_bd[:, p, r], start=True, stop=True).then_inc(c_ps[r], 1)
                    for r in range(2):
                        pe.wait_ge(c_ready[r], b + 1)
                        for j in range(PER):
                            h = PER * r + j
                            last_ = nc.tensor.matmul(p_o[:, r, j * DH:(j + 1) * DH], cm[:, r, j],
                                                     wn[:, b, h * DH:(h + 1) * DH], start=False, stop=h == NH - 1)
                    last_.then_inc(o_ps, 1)

                sequences(pe, body, finish, products)


def capacity_experts(nc, W, K):
    E, P = 32, 2
    CAP = math.ceil(1.25 * NTOK * P / E)
    REST = CAP - SLOTS
    NT = 2 * E
    name = "L1_ffn"
    xn_dram = nc.dram_tensor(name + "_xn_dram", (NTOK, D), f32, kind="Internal").ap()
    o_dram = nc.dram_tensor(name + "_o_dram", (E * CAP, D), f32, kind="Internal").ap()
    with Space(nc) as s:
        route = Route(s, name, E, P, NT)
        xn = s.sb(name + "_xn", [T, B, D])
        layer_norm_block(nc, name + "_ln", K.h, xn)
        with Space(nc) as s2:
            prob = s2.sb(name + "_prob", [T, B, E])
            router_logits_block(nc, name + "_r", K, xn, xn_dram, W["L1_ffn_Wg"], E, prob)
            index = s2.sb(name + "_index", [T, B, P])
            top = s2.sb(name + "_top", [T, B, 8])
            which = s2.sb(name + "_which", [T, B, 8], u32)
            total = s2.sb(name + "_total", [T, B])
            own = s2.sem(name + "_own")
            low_ready = s2.sem(name + "_low_ready")
            exp_ready = s2.sem(name + "_exp_ready")
            with nc.Block() as block:
                @block.scalar
                def _(act):
                    act.wait_ge(low_ready, 1)
                    nc.scalar.activation(prob[:], prob[:], ACT.Exp).then_inc(exp_ready, 1)

                @block.vector
                def _(v):
                    chain = Own(v, own)
                    chain.done(nc.vector.tensor_reduce(out=total[:], in_=prob[:], axis=AX.X, op=ALU.max))
                    nc.vector.tensor_tensor(prob[:], prob[:], per_row(total[:], E), ALU.subtract).then_inc(low_ready, 1)
                    v.wait_ge(exp_ready, 1)
                    chain.done(nc.vector.tensor_reduce(out=total[:], in_=prob[:], axis=AX.X, op=ALU.add))
                    chain.done(nc.vector.reciprocal(total[:], total[:]))
                    chain.done(nc.vector.tensor_tensor(prob[:], prob[:], per_row(total[:], E), ALU.mult))
                    for b in range(B):
                        ins = nc.vector.max(top[:, b, :], prob[:, b, :])
                    chain.done(ins)
                    for b in range(B):
                        ins = nc.vector.max_index(which[:, b, :], top[:, b, :], prob[:, b, :])
                    chain.done(ins)
                    nc.vector.tensor_copy(index[:], which[:, :, 0:P])
                    chain.done(nc.vector.tensor_tensor(total[:], top[:, :, 0], top[:, :, 1], ALU.add))
                    chain.done(nc.vector.tensor_scalar(total[:], total[:], 1e-9, None, ALU.max))
                    chain.done(nc.vector.reciprocal(total[:], total[:]))
                    chain.done(nc.vector.tensor_tensor(route.gate[:], top[:, :, 0:P], per_row(total[:], P), ALU.mult))
            sort_block(nc, name + "_sort", K, route, index, capacity=CAP)
        capacity_tiles_block(nc, name + "_x", K, route, xn_dram, o_dram, W, REST)
        contrib = s.sb(name + "_contrib", [T, B])
        lost = s.sb(name + "_lost", [T, B])
        held = s.sb(name + "_held", [T, B])
        own = s.sem(name + "_own2")
        with nc.Block() as block:
            @block.vector
            def _(v):
                chain = Own(v, own)
                chain.done(nc.vector.tensor_tensor(contrib[:], route.gate[:, :, 0], route.gate[:, :, 1], ALU.add))
                nc.vector.tensor_scalar(lost[:], contrib[:], 1e-12, None, ALU.is_le)
                chain.done(nc.vector.tensor_scalar(held[:], contrib[:], 1e-12, None, ALU.is_gt))
                chain.done(nc.vector.tensor_tensor(route.gate[:], route.gate[:], per_row(held[:], P), ALU.mult))
                chain.done(nc.vector.tensor_tensor(xn[:], xn[:], per_row(lost[:], D), ALU.mult))
                chain.done(nc.vector.tensor_tensor(K.h[:], K.h[:], xn[:], ALU.add))
        combine_block(nc, name + "_c", K, route, o_dram, 2)
    end_of_layer(nc)


def capacity_tiles_block(nc, name, K, route, xn_dram, o_dram, W, rest):
    E = route.experts
    CAP = SLOTS + rest
    with Space(nc) as s:
        who2 = s.sb(name + "_who2", [SLOTS, 2, 2], i32)
        xg = s.sb(name + "_xg", [SLOTS, 2, 2, D])
        xgt = s.sb(name + "_xgt", [D, 2, CAP])
        w1b = s.sb(name + "_w1b", [D, 2, T])
        w2b = s.sb(name + "_w2b", [T, 2, D])
        b1b = s.sb(name + "_b1b", [T, E])
        b2b = s.sb(name + "_b2b", [1, 2, D])
        hid = s.sb(name + "_hid", [T, 2, CAP])
        ob = s.sb(name + "_ob", [SLOTS, 2, 2, D])
        p_t = [s.ps(f"{name}_p_t{u}", [D, 512]) for u in range(2)]
        p_h = [s.ps(f"{name}_p_h{u}", [T, 512]) for u in range(2)]
        p_o = [s.ps(f"{name}_p_o{u}", [SLOTS, 4, D]) for u in range(2)]
        b1_in = s.sem(name + "_b1_in")
        who_ready, gathered, gathered_rest, w_in, t_ps, xgt_ready, h_ps, hid_ready, o_ps, ob_ready, stored = (
            [s.sem(f"{name}_{n}{u}") for u in range(2)] for n in (
                "who_ready", "gathered", "gathered_rest", "w_in", "t_ps", "xgt_ready", "h_ps", "hid_ready", "o_ps",
                "ob_ready", "stored"))
        with nc.Block() as block:
            @block.gpsimd
            def _(g):
                for u in range(2):
                    g.sem_inc(xgt_ready[u], 1)
                with g.Fori(0, E // 2) as i:
                    for u in range(2):
                        g.wait_ge(xgt_ready[u], i + 1)
                        g.tensor_copy(who2[:, u], route.who[:, bass.ds((2 * i + u) * 2, 2)]).then_inc(who_ready[u], 1)
                        g.wait_ge(who_ready[u], i + 1)
                        g.nop(nofuse=True)
                        g.indirect_dma_start(out=xg[:, u, 0, :], out_offset=None, in_=xn_dram,
                                             in_offset=bass.IndirectOffsetOnAxis(ap=who2[:, u, 0:1], axis=0)
                                             ).then_inc(gathered[u], 16)
                        g.indirect_dma_start(out=xg[0:rest, u, 1, :], out_offset=None, in_=xn_dram,
                                             in_offset=bass.IndirectOffsetOnAxis(ap=who2[0:rest, u, 1:2], axis=0)
                                             ).then_inc(gathered_rest[u], 16)

            @block.sync
            def _(sp):
                sp.dma_start(b1b[:], W["L1_ffn_b1_t"]).then_inc(b1_in, 16)
                for u in range(2):
                    sp.sem_inc(o_ps[u], 1)
                with sp.Fori(0, E // 2) as i:
                    for u in range(2):
                        e = 2 * i + u
                        sp.wait_ge(o_ps[u], i + 1)
                        sp.dma_start(w1b[:, u, :], W["L1_ffn_W1"][bass.ds(e, 1), :, :].rearrange("a c n -> (a c) n")
                                     ).then_inc(w_in[u], 16)
                        sp.dma_start(w2b[:, u, :], W["L1_ffn_W2"][bass.ds(e, 1), :, :].rearrange("a c n -> (a c) n")
                                     ).then_inc(w_in[u], 16)
                        sp.dma_start(b2b[:, u, :], W["L1_ffn_b2"][bass.ds(e, 1), :]).then_inc(w_in[u], 16)

            @block.tensor
            def _(pe):
                with pe.Fori(0, E // 2) as i:
                    for u in range(2):
                        pe.wait_ge(gathered[u], 16 * i + 16)
                        pe.wait_ge(gathered_rest[u], 16 * i + 16)
                        nc.tensor.transpose(p_t[u][:, 0:SLOTS], xg[:, u, 0, :], K.ident[:])
                        nc.tensor.transpose(p_t[u][:, SLOTS:CAP], xg[0:rest, u, 1, :],
                                            K.ident[0:rest, 0:rest]).then_inc(t_ps[u], 1)
                    for u in range(2):
                        pe.wait_ge(w_in[u], 48 * i + 48)
                        pe.wait_ge(xgt_ready[u], i + 2)
                        nc.tensor.matmul(p_h[u][:, 0:CAP], w1b[:, u, :], xgt[:, u, :], start=True,
                                         stop=True).then_inc(h_ps[u], 1)
                    for u in range(2):
                        pe.wait_ge(hid_ready[u], i + 1)
                        for n, (at, rows) in enumerate(((0, SLOTS), (SLOTS, rest))):
                            nc.tensor.matmul(p_o[u][0:rows, n], hid[:, u, at:at + rows], w2b[:, u, :], start=True,
                                             stop=False)
                            last = nc.tensor.matmul(p_o[u][0:rows, n], K.ones[0:1, 0:rows], b2b[:, u, :], start=False,
                                                    stop=True)
                        last.then_inc(o_ps[u], 1)

            @block.scalar
            def _(act):
                act.wait_ge(b1_in, 16)
                with act.Fori(0, E // 2) as i:
                    for u in range(2):
                        act.wait_ge(t_ps[u], i + 1)
                        nc.scalar.activation(xgt[:, u, :], p_t[u][:, 0:CAP], ACT.Copy).then_inc(xgt_ready[u], 1)
                    for u in range(2):
                        act.wait_ge(h_ps[u], i + 1)
                        nc.scalar.activation(hid[:, u, :], p_h[u][:, 0:CAP], ACT.Relu,
                                             bias=b1b[:, bass.ds(2 * i + u, 1)]).then_inc(hid_ready[u], 1)
                    for u in range(2):
                        row = (2 * i + u) * CAP
                        act.wait_ge(ob_ready[u], i + 1)
                        act.dma_start(o_dram[bass.ds(row, SLOTS), :], ob[:, u, 0, :]).then_inc(stored[u], 16)
                        act.dma_start(o_dram[bass.ds(row + SLOTS, rest), :], ob[0:rest, u, 1, :]).then_inc(stored[u], 16)
                for u in range(2):
                    act.wait_ge(stored[u], 16 * E + 32)

            @block.vector
            def _(v):
                for u in range(2):
                    v.sem_inc(stored[u], 32)
                with v.Fori(0, E // 2) as i:
                    for u in range(2):
                        v.wait_ge(o_ps[u], i + 2)
                        v.wait_ge(stored[u], 32 * i + 32)
                        nc.vector.tensor_copy(ob[:, u, 0, :], p_o[u][:, 0])
                        nc.vector.tensor_copy(ob[0:rest, u, 1, :], p_o[u][0:rest, 1]).then_inc(ob_ready[u], 1)


def layer2_attention(nc, W, K):
    NH = 8
    with Space(nc) as s:
        xn = s.sb("a2_xn", [T, B, D])
        layer_norm_block(nc, "a2_ln", K.h, xn)
        wv = s.sb("a2_wv", [D, NH, D])
        bv = s.sb("a2_bv", [D, NH])
        fc = s.sb("a2_fc", [D, NH, D])
        fb = s.sb("a2_fb", [T, D])
        lg = s.sb("a2_lg", [T, D])
        lb = s.sb("a2_lb", [T, D])
        xs = s.sb("a2_xs", [D, B])
        vs = s.sb("a2_vs", [D, NH, B])
        at_ = s.sb("a2_at", [B, D])
        pick = s.sb("a2_pick", [B, B, T])
        y = s.sb("a2_y", [T, B, D])
        p_x = s.ps("a2_p_x", [T, 512])
        p_v = s.ps("a2_p_v", [T, 512])
        p_o = s.ps("a2_p_o", [T, 512])
        p_y = [s.ps(f"a2_p_y{n}", [T, 4, D]) for n in range(4)]
        loads, x_ps, xs_ready, v_ps, vs_ready, o_ps, at_ready, y_ps, pick_ready, base_ready, own = (
            s.sem("a2_" + n) for n in ("loads", "x_ps", "xs_ready", "v_ps", "vs_ready", "o_ps", "at_ready", "y_ps",
                                       "pick_ready", "base_ready", "own"))
        vals = p_v[:, 0:NH * B].rearrange("d (h b) -> d h b", h=NH)
        with nc.Block() as block:
            @block.sync
            def _(sp):
                sp.dma_start(wv[:].rearrange("c h d -> c (h d)"), W["L2_attn_wv"]).then_inc(loads, 16)
                sp.dma_start(fc[:], W["L2_attn_fc_w"].rearrange("(h d) n -> d h n", h=NH)).then_inc(loads, 16)
                sp.dma_start(bv[:], W["L2_attn_bv_t"]).then_inc(loads, 16)
                sp.dma_start(fb[:], W["L2_attn_fc_b"].partition_broadcast(T)).then_inc(loads, 16)
                sp.dma_start(lg[:], W["L2_attn_ln_g"].partition_broadcast(T)).then_inc(loads, 16)
                sp.dma_start(lb[:], W["L2_attn_ln_b"].partition_broadcast(T)).then_inc(loads, 16)

            @block.gpsimd
            def _(g):
                g.wait_ge(loads, 96)
                g.tensor_tensor(out=y[:], in0=xn[:], in1=per_tile(fb[:], B), op=ALU.add).then_inc(base_ready, 1)

            @block.vector
            def _(v):
                chain = Own(v, own)
                nc.vector.tensor_copy(pick[:], K.ident[0:B, 0:B].unsqueeze(2).to_broadcast([B, B, T])
                                      ).then_inc(pick_ready, 1)
                v.wait_ge(x_ps, 1)
                nc.vector.tensor_copy(xs[:], p_x[:, 0:B]).then_inc(xs_ready, 1)
                v.wait_ge(loads, 96)
                chain.done(nc.vector.tensor_scalar(bv[:], bv[:], float(T), None, ALU.mult))
                v.wait_ge(v_ps, 1)
                nc.vector.tensor_tensor(vs[:], vals, per_row(bv[:], B), ALU.add).then_inc(vs_ready, 1)
                v.wait_ge(o_ps, 1)
                nc.vector.tensor_copy(at_[:], p_o[0:B, 0:D]).then_inc(at_ready, 1)
                v.wait_ge(base_ready, 1)
                v.wait_ge(y_ps, 1)
                for n in range(4):
                    ins = nc.vector.tensor_tensor(y[:, 4 * n:4 * n + 4], y[:, 4 * n:4 * n + 4], p_y[n][:], ALU.add)
                chain.done(ins)

            @block.tensor
            def _(pe):
                for b in range(B):
                    last = nc.tensor.matmul(p_x[:, b:b + 1], xn[:, b], K.ones[:, 0:1], start=True, stop=True)
                last.then_inc(x_ps, 1)
                pe.wait_ge(loads, 96)
                pe.wait_ge(xs_ready, 1)
                for h in range(NH):
                    last = nc.tensor.matmul(vals[:, h], wv[:, h], xs[:], start=True, stop=True)
                last.then_inc(v_ps, 1)
                pe.wait_ge(vs_ready, 1)
                for h in range(NH):
                    last = nc.tensor.matmul(p_o[0:B, 0:D], vs[:, h], fc[:, h], start=h == 0, stop=h == NH - 1)
                last.then_inc(o_ps, 1)
                pe.wait_ge(at_ready, 1)
                pe.wait_ge(pick_ready, 1)
                for b in range(B):
                    last = nc.tensor.matmul(p_y[b // 4][:, b % 4], pick[:, b], at_[:], start=True, stop=True)
                last.then_inc(y_ps, 1)
        layer_norm_block(nc, "a2_ln2", y, y, lg, lb)
        own2 = s.sem("a2_own2")
        with nc.Block() as block:
            @block.vector
            def _(v):
                nc.vector.tensor_tensor(K.h[:], K.h[:], y[:], ALU.add).then_inc(own2, 1)
                v.wait_ge(own2, 1)
    end_of_layer(nc)


def rope_attention(nc, W, K):
    NH, DH, HALF = 16, 8, D // 2
    with Space(nc) as s:
        xn = s.sb("a3_xn", [T, B, D])
        layer_norm_block(nc, "a3_ln", K.h, xn)
        wqk = s.sb("a3_wqk", [D, 2 * D])
        bqk = s.sb("a3_bqk", [T, 2 * D])
        taps = s.sb("a3_taps", [D, 3])
        lb = s.sb("a3_lb", [T, D])
        cosn = s.sb("a3_cos", [T, D])
        sinn = s.sb("a3_sin", [T, D])
        hmask = s.sb("a3_hmask", [D, D])
        hcol = s.sb("a3_hcol", [D, NH])
        diag = s.sb("a3_diag", [D, 3, D])
        xs = s.sb("a3_xs", [T, 2, D])
        xp = s.sb("a3_xp", [D, 2, T + 2])
        xb = s.sb("a3_xb", [T, 2, 2, D])
        neg = s.sb("a3_neg", [T, 2, 2, D])
        qk = s.sb("a3_qk", [T, 2, 2, D])
        ro = s.sb("a3_ro", [T, 2, 2, D])
        sw = s.sb("a3_sw", [T, 2, 2, D])
        qt = s.sb("a3_qt", [D, 4, T])
        kvm = s.sb("a3_kvm", [D, 2, D])
        km = s.sb("a3_km", [D, 2, NH])
        z = s.sb("a3_z", [T, 2, NH])
        at_ = s.sb("a3_at", [T, 2, D])
        p_t = s.ps("a3_p_t", [D, 4, T])
        p_q = s.ps("a3_p_q", [T, 2, 2, D])
        p_kv = s.ps("a3_p_kv", [D, 2, D])
        p_km = s.ps("a3_p_km", [D, 512])
        p_o = s.ps("a3_p_o", [T, 2, D])
        p_z = s.ps("a3_p_z", [T, 512])
        p_l = s.ps("a3_p_l", [T, 2, D])
        zz = p_z[:, 0:2 * NH].rearrange("t (u h) -> t u h", u=2)
        loads, diag_ready, pads, xs_ready, xt_ps, xp_ready, qk_ps, l_ps, neg_ready, exp_ready, qk_ready, ro_ready, kv_ps, \
            kvm_ready, qt_ps, qt_ready, o_ps, done, own, base_ready = (s.sem("a3_" + n) for n in (
                "loads", "diag_ready", "pads", "xs_ready", "xt_ps", "xp_ready", "qk_ps", "l_ps", "neg_ready", "exp_ready",
                "qk_ready", "ro_ready", "kv_ps", "kvm_ready", "qt_ps", "qt_ready", "o_ps", "done", "own", "base_ready"))

        def flat(a):
            return a.rearrange("t u n d -> t (u n d)")

        def pairs(a):
            return a.rearrange("t u n (i two) -> t (u n) i two", two=2)

        with nc.Block() as block:
            @block.sync
            def _(sp):
                for to, source in ((wqk[:], W["L3_attn_Wqk"]), (bqk[:], W["L3_attn_bqk"].partition_broadcast(T)),
                                   (taps[:], W["L3_attn_lepe_w"].rearrange("c a k -> c (a k)")),
                                   (lb[:], W["L3_attn_lepe_b"].partition_broadcast(T)),
                                   (cosn[:], W["rope_cos"]), (sinn[:], W["rope_sin"]),
                                   (hmask[:], W["head_mask"]), (hcol[:], W["head_columns"])):
                    sp.dma_start(to, source).then_inc(loads, 16)

            @block.gpsimd
            def _(g):
                g.memset(xp[:], 0.0).then_inc(pads, 1)
                g.wait_ge(loads, 128)
                g.tensor_tensor(out=K.h[:], in0=K.h[:], in1=per_tile(lb[:], B), op=ALU.add).then_inc(base_ready, 1)

            @block.vector
            def _(v):
                v.wait_ge(loads, 128)
                for k in range(3):
                    ins = nc.vector.tensor_scalar(diag[:, k], K.ident[:], taps[:, k:k + 1], None, ALU.mult)
                ins.then_inc(diag_ready, 1)
                v.sem_inc(done, 1)
                with v.Fori(0, B // 2) as i:
                    v.wait_ge(done, i + 1)
                    nc.vector.tensor_copy(xs[:], xn[:, bass.ds(2 * i, 2), :]).then_inc(xs_ready, 1)
                    v.wait_ge(qk_ps, i + 1)
                    chain = Own(v, own, 8 * i)
                    chain.done(nc.vector.tensor_tensor(xb[:].rearrange("t u n d -> t u (n d)"),
                                                       p_q[:].rearrange("t u n d -> t u (n d)"), per_tile(bqk[:], 2),
                                                       ALU.add))
                    nc.vector.tensor_scalar(neg[:], xb[:], 0.0, None, ALU.min).then_inc(neg_ready, 1)
                    v.wait_ge(exp_ready, i + 1)
                    chain.done(nc.vector.scalar_tensor_tensor(out=flat(qk[:]), in0=flat(xb[:]), scalar=0.0,
                                                              in1=flat(neg[:]), op0=ALU.max, op1=ALU.add))
                    v.sem_inc(qk_ready, 1)
                    nc.vector.tensor_tensor(ro[:].rearrange("t u n d -> t (u n) d"),
                                            qk[:].rearrange("t u n d -> t (u n) d"), per_tile(cosn[:], 4), ALU.mult)
                    sin2 = sinn[:].rearrange("t (i two) -> t i two", two=2)
                    for n in range(2):
                        ins = nc.vector.tensor_tensor(pairs(sw[:])[:, :, :, n], pairs(qk[:])[:, :, :, 1 - n],
                                                      per_tile(sin2[:, :, n], 4), ALU.mult)
                    chain.done(ins)
                    nc.vector.tensor_tensor(ro[:], ro[:], sw[:], ALU.add).then_inc(ro_ready, 1)
                    v.wait_ge(kv_ps, i + 1)
                    nc.vector.scalar_tensor_tensor(out=kvm[:], in0=p_kv[:], scalar=1.0 / T, in1=per_tile(hmask[:], 2),
                                                   op0=ALU.mult, op1=ALU.mult)
                    for u in range(2):
                        ins = nc.vector.tensor_scalar(km[:, u], hcol[:], p_km[:, u:u + 1], 1.0 / T, ALU.mult, ALU.mult)
                    ins.then_inc(kvm_ready, 1)
                    v.wait_ge(o_ps, i + 1)
                    chain.done(nc.vector.tensor_scalar(z[:], zz, 1e-6, None, ALU.add))
                    chain.done(nc.vector.reciprocal(z[:].rearrange("t u h -> t (u h)"), z[:].rearrange("t u h -> t (u h)")))
                    chain.done(nc.vector.tensor_tensor(at_[:].rearrange("t u (h d) -> t (u h) d", d=DH),
                                                       p_o[:].rearrange("t u (h d) -> t (u h) d", d=DH),
                                                       z[:].rearrange("t u h -> t (u h)").unsqueeze(2)
                                                       .to_broadcast([T, 2 * NH, DH]), ALU.mult))
                    v.wait_ge(l_ps, i + 1)
                    chain.done(nc.vector.tensor_tensor(at_[:], at_[:], p_l[:], ALU.add))
                    v.wait_ge(base_ready, 1)
                    chain.done(nc.vector.tensor_tensor(K.h[:, bass.ds(2 * i, 2), :], K.h[:, bass.ds(2 * i, 2), :], at_[:],
                                                       ALU.add))
                    v.sem_inc(done, 1)

            @block.scalar
            def _(act):
                act.wait_ge(pads, 1)
                with act.Fori(0, B // 2) as i:
                    act.wait_ge(xt_ps, i + 1)
                    nc.scalar.activation(xp[:, :, 1:T + 1], p_t[:, 0:2], ACT.Copy).then_inc(xp_ready, 1)
                    act.wait_ge(neg_ready, i + 1)
                    nc.scalar.activation(neg[:], neg[:], ACT.Exp).then_inc(exp_ready, 1)
                    act.wait_ge(qt_ps, i + 1)
                    nc.scalar.activation(qt[:], p_t[:], ACT.Copy).then_inc(qt_ready, 1)

            @block.tensor
            def _(pe):
                pe.wait_ge(loads, 128)
                pe.wait_ge(diag_ready, 1)
                with pe.Fori(0, B // 2) as i:
                    pe.wait_ge(xs_ready, i + 1)
                    for u in range(2):
                        last = nc.tensor.transpose(p_t[:, u], xs[:, u], K.ident[:])
                    last.then_inc(xt_ps, 1)
                    pe.wait_ge(xp_ready, i + 1)
                    for u in range(2):
                        last = nc.tensor.matmul(p_q[:, u].rearrange("t n d -> t (n d)"), xp[:, u, 1:T + 1], wqk[:],
                                                start=True, stop=True)
                    last.then_inc(qk_ps, 1)
                    for u in range(2):
                        for k in range(3):
                            last = nc.tensor.matmul(p_l[:, u], xp[:, u, k:k + T], diag[:, k], start=k == 0, stop=k == 2)
                    last.then_inc(l_ps, 1)
                    pe.wait_ge(qk_ready, i + 1)
                    for u in range(2):
                        nc.tensor.matmul(p_km[:, u:u + 1], qk[:, u, 1], K.ones[:, 0:1], start=True, stop=True)
                    pe.wait_ge(ro_ready, i + 1)
                    for u in range(2):
                        last = nc.tensor.matmul(p_kv[:, u], ro[:, u, 1], xs[:, u], start=True, stop=True)
                    last.then_inc(kv_ps, 1)
                    for u in range(2):
                        nc.tensor.transpose(p_t[:, 2 * u], qk[:, u, 0], K.ident[:])
                        last = nc.tensor.transpose(p_t[:, 2 * u + 1], ro[:, u, 0], K.ident[:])
                    last.then_inc(qt_ps, 1)
                    pe.wait_ge(qt_ready, i + 1)
                    pe.wait_ge(kvm_ready, i + 1)
                    for u in range(2):
                        nc.tensor.matmul(p_o[:, u], qt[:, 2 * u + 1], kvm[:, u], start=True, stop=True)
                        last = nc.tensor.matmul(zz[:, u], qt[:, 2 * u], km[:, u], start=True, stop=True)
                    last.then_inc(o_ps, 1)
    end_of_layer(nc)


def shared_expert_block(nc, name, W, K, xn):
    with Space(nc) as s:
        wgu = s.sb(name + "_wgu", [D, 2, D])
        wd = s.sb(name + "_wd", [D, D])
        xs = s.sb(name + "_xs", [T, 2, 2, D])
        xt = s.sb(name + "_xt", [D, 2, 2, T])
        sg = s.sb(name + "_sg", [D, 2, 2, T])
        hid = s.sb(name + "_hid", [D, 2, 2, T])
        p_t = [s.ps(f"{name}_p_t{u}", [D, 4, T]) for u in range(2)]
        p_gu = [s.ps(f"{name}_p_gu{u}", [D, 2, 2, T]) for u in range(2)]
        p_y = [s.ps(f"{name}_p_y{u}", [T, 4, D]) for u in range(2)]
        loads = s.sem(name + "_loads")
        xs_ready, xt_ps, xt_ready, gu_ps, sg_ready, hid_ready, y_ps, done = (
            [s.sem(f"{name}_{n}{u}") for u in range(2)] for n in (
                "xs_ready", "xt_ps", "xt_ready", "gu_ps", "sg_ready", "hid_ready", "y_ps", "done"))
        TURNS = B // 4
        with nc.Block() as block:
            @block.sync
            def _(sp):
                sp.dma_start(wgu[:, 0], W["L3_ffn_sWg"]).then_inc(loads, 16)
                sp.dma_start(wgu[:, 1], W["L3_ffn_sWu"]).then_inc(loads, 16)
                sp.dma_start(wd[:], W["L3_ffn_sWd"]).then_inc(loads, 16)

            @block.vector
            def _(v):
                for u in range(2):
                    v.sem_inc(done[u], 1)
                with v.Fori(0, TURNS) as i:
                    for u in range(2):
                        b = 4 * i + 2 * u
                        v.wait_ge(done[u], i + 1)
                        nc.vector.tensor_copy(xs[:, u], xn[:, bass.ds(b, 2), :]).then_inc(xs_ready[u], 1)
                    for u in range(2):
                        v.wait_ge(sg_ready[u], i + 1)
                        nc.vector.tensor_tensor(hid[:, u], sg[:, u], p_gu[u][:, 1], ALU.mult).then_inc(hid_ready[u], 1)
                    for u in range(2):
                        b = 4 * i + 2 * u
                        v.wait_ge(y_ps[u], i + 1)
                        nc.vector.tensor_tensor(K.h[:, bass.ds(b, 2), :], K.h[:, bass.ds(b, 2), :], p_y[u][:, 0:2],
                                                ALU.add).then_inc(done[u], 1)

            @block.scalar
            def _(act):
                with act.Fori(0, TURNS) as i:
                    for u in range(2):
                        act.wait_ge(xt_ps[u], i + 1)
                        nc.scalar.activation(xt[:, u], p_t[u][:, 0:2], ACT.Copy).then_inc(xt_ready[u], 1)
                    for u in range(2):
                        act.wait_ge(gu_ps[u], i + 1)
                        nc.scalar.activation(sg[:, u], p_gu[u][:, 0], ACT.Silu).then_inc(sg_ready[u], 1)

            @block.tensor
            def _(pe):
                pe.wait_ge(loads, 48)
                with pe.Fori(0, TURNS) as i:
                    for u in range(2):
                        pe.wait_ge(xs_ready[u], i + 1)
                        for n in range(2):
                            last = nc.tensor.transpose(p_t[u][:, n], xs[:, u, n], K.ident[:])
                        last.then_inc(xt_ps[u], 1)
                    for u in range(2):
                        pe.wait_ge(xt_ready[u], i + 1)
                        for n in range(2):
                            last = nc.tensor.matmul(p_gu[u][:, n], wgu[:, n], xt[:, u], start=True, stop=True)
                        last.then_inc(gu_ps[u], 1)
                    for u in range(2):
                        pe.wait_ge(hid_ready[u], i + 1)
                        for n in range(2):
                            last = nc.tensor.matmul(p_y[u][:, n], hid[:, u, n], wd[:], start=True, stop=True)
                        last.then_inc(y_ps[u], 1)


def grouped_router_block(nc, name, W, K, xn, xn_dram, route, index, scores):
    E, P, G, KEEP = route.experts, route.picks, 8, 4
    PER = E // G
    BIG = 1e30
    with Space(nc) as s:
        corr = s.sb(name + "_corr", [T, E])
        biased = s.sb(name + "_biased", [T, B, E])
        best = s.sb(name + "_best", [T, B, G])
        top = s.sb(name + "_top", [T, B, 8])
        which = s.sb(name + "_which", [T, B, 8], u32)
        which_f = s.sb(name + "_which_f", [T, B, 8])
        iota_g = s.sb(name + "_iota_g", [T, G])
        hot = s.sb(name + "_hot", [T, B, G])
        gmask = s.sb(name + "_gmask", [T, B, G])
        corr_in, iota_ready, exp_ready, own = (s.sem(name + "_" + n) for n in ("corr_in", "iota_ready", "exp_ready", "own"))
        router_logits_block(nc, name + "_r", K, xn, xn_dram, W["L3_ffn_router_w_t"], E, scores)
        with nc.Block() as block:
            @block.sync
            def _(sp):
                sp.dma_start(corr[:], W["L3_ffn_bias_corr"].partition_broadcast(T)).then_inc(corr_in, 16)

            @block.gpsimd
            def _(g):
                g.iota(iota_g[:], pattern=[[1, G]], base=0, channel_multiplier=0,
                       allow_small_or_imprecise_dtypes=True).then_inc(iota_ready, 1)

            @block.scalar
            def _(act):
                nc.scalar.activation(scores[:], scores[:], ACT.Exp, scale=-1.0).then_inc(exp_ready, 1)

            @block.vector
            def _(v):
                chain = Own(v, own)
                v.wait_ge(exp_ready, 1)
                chain.done(nc.vector.tensor_scalar(scores[:], scores[:], 1.0, None, ALU.add))
                flat = scores[:].rearrange("t b e -> t (b e)")
                chain.done(nc.vector.reciprocal(flat, flat))
                v.wait_ge(corr_in, 16)
                chain.done(nc.vector.tensor_tensor(biased[:], scores[:], per_tile(corr[:], B), ALU.add))
                groups = biased[:].rearrange("t b (g e) -> t (b g) e", e=PER)
                chain.done(nc.vector.tensor_reduce(out=best[:].rearrange("t b g -> t (b g)"), in_=groups, axis=AX.X,
                                                   op=ALU.max))
                for b in range(B):
                    ins = nc.vector.max(top[:, b, :], best[:, b, :])
                chain.done(ins)
                for b in range(B):
                    ins = nc.vector.max_index(which[:, b, :], top[:, b, :], best[:, b, :])
                chain.done(ins)
                chain.done(nc.vector.tensor_copy(which_f[:], which[:]))
                v.wait_ge(iota_ready, 1)
                for k in range(KEEP):
                    chain.done(nc.vector.tensor_tensor(gmask[:] if k == 0 else hot[:], per_tile(iota_g[:], B),
                                                       per_row(which_f[:, :, k], G), ALU.is_equal))
                    if k:
                        chain.done(nc.vector.tensor_tensor(gmask[:], gmask[:], hot[:], ALU.add))
                chain.done(nc.vector.tensor_tensor(groups, groups, gmask[:].rearrange("t b g -> t (b g)").unsqueeze(2)
                                                   .to_broadcast([T, B * G, PER]), ALU.mult))
                chain.done(nc.vector.tensor_scalar(gmask[:], gmask[:], BIG, -BIG, ALU.mult, ALU.add))
                chain.done(nc.vector.tensor_tensor(groups, groups, gmask[:].rearrange("t b g -> t (b g)").unsqueeze(2)
                                                   .to_broadcast([T, B * G, PER]), ALU.add))
                for b in range(B):
                    ins = nc.vector.max(top[:, b, :], biased[:, b, :])
                chain.done(ins)
                for b in range(B):
                    ins = nc.vector.max_index(which[:, b, :], top[:, b, :], biased[:, b, :])
                chain.done(ins)
                chain.done(nc.vector.tensor_copy(index[:], which[:, :, 0:P]))


def gated_tiles_block(nc, name, K, route, xn_dram, o_dram, wgu, wd0, wd1, wgu_in, wd_in, H):
    E, NT = route.experts, route.tiles
    REST = H - T
    TURNS = NT // 2
    with Space(nc) as s:
        who2 = s.sb(name + "_who2", [SLOTS, 2], i32)
        xg = s.sb(name + "_xg", [SLOTS, 2, D])
        xgt = s.sb(name + "_xgt", [D, 2, SLOTS])
        sg = s.sb(name + "_sg", [SLOTS, 2, H])
        hid = s.sb(name + "_hid", [SLOTS, 2, H])
        ht = s.sb(name + "_ht", [T, 2, 2, SLOTS])
        ob = s.sb(name + "_ob", [SLOTS, 2, D])
        p_t = [s.ps(f"{name}_p_t{u}", [T, 4, SLOTS]) for u in range(2)]
        p_h = [s.ps(f"{name}_p_h{u}", [SLOTS, 512]) for u in range(2)]
        p_o = [s.ps(f"{name}_p_o{u}", [SLOTS, 512]) for u in range(2)]
        who_ready, gathered, t_ps, xgt_ready, h_ps, sg_ready, hid_ready, ht_ps, ht_ready, o_ps, ob_ready, stored = (
            [s.sem(f"{name}_{n}{u}") for u in range(2)] for n in (
                "who_ready", "gathered", "t_ps", "xgt_ready", "h_ps", "sg_ready", "hid_ready", "ht_ps", "ht_ready",
                "o_ps", "ob_ready", "stored"))
        with nc.Block() as block:
            @block.gpsimd
            def _(g):
                for u in range(2):
                    g.sem_inc(xgt_ready[u], 1)
                with g.Fori(0, TURNS) as i:
                    for u in range(2):
                        g.wait_ge(xgt_ready[u], i + 1)
                        g.tensor_copy(who2[:, u:u + 1], route.who[:, bass.ds(2 * i + u, 1)]).then_inc(who_ready[u], 1)
                        g.wait_ge(who_ready[u], i + 1)
                        g.nop(nofuse=True)
                        g.indirect_dma_start(out=xg[:, u, :], out_offset=None, in_=xn_dram,
                                             in_offset=bass.IndirectOffsetOnAxis(ap=who2[:, u:u + 1], axis=0)
                                             ).then_inc(gathered[u], 16)

            @block.tensor
            def _(pe):
                pe.wait_ge(wgu_in, 32)
                pe.wait_ge(wd_in, 32)
                with pe.Fori(0, TURNS) as i:
                    experts = [pe.value_load(route.expert_of[0:1, bass.ds(2 * i + u, 1)], min_val=0, max_val=E - 1)
                               for u in range(2)]
                    for u in range(2):
                        pe.wait_ge(gathered[u], 16 * i + 16)
                        nc.tensor.transpose(p_t[u][:, 0], xg[:, u, :], K.ident[:]).then_inc(t_ps[u], 1)
                    for u in range(2):
                        pe.wait_ge(xgt_ready[u], i + 2)
                        nc.tensor.matmul(p_h[u][:, 0:2 * H], xgt[:, u, :],
                                         wgu[:, bass.ds(experts[u], 1)].rearrange("c e n -> c (e n)"), start=True,
                                         stop=True).then_inc(h_ps[u], 1)
                    for u in range(2):
                        pe.wait_ge(hid_ready[u], i + 1)
                        nc.tensor.transpose(p_t[u][:, 1], hid[:, u, 0:T], K.ident[:])
                        nc.tensor.transpose(p_t[u][0:REST, 2], hid[:, u, T:H], K.ident[:]).then_inc(ht_ps[u], 1)
                    for u in range(2):
                        pe.wait_ge(ht_ready[u], i + 1)
                        nc.tensor.matmul(p_o[u][:, 0:D], ht[:, u, 0],
                                         wd0[:, bass.ds(experts[u], 1)].rearrange("p e n -> p (e n)"), start=True,
                                         stop=False)
                        nc.tensor.matmul(p_o[u][:, 0:D], ht[0:REST, u, 1],
                                         wd1[:, bass.ds(experts[u], 1)].rearrange("p e n -> p (e n)"), start=False,
                                         stop=True).then_inc(o_ps[u], 1)

            @block.scalar
            def _(act):
                with act.Fori(0, TURNS) as i:
                    for u in range(2):
                        act.wait_ge(t_ps[u], i + 1)
                        nc.scalar.activation(xgt[:, u, :], p_t[u][:, 0], ACT.Copy).then_inc(xgt_ready[u], 1)
                    for u in range(2):
                        act.wait_ge(h_ps[u], i + 1)
                        nc.scalar.activation(sg[:, u, :], p_h[u][:, 0:H], ACT.Silu).then_inc(sg_ready[u], 1)
                    for u in range(2):
                        act.wait_ge(ht_ps[u], i + 1)
                        nc.scalar.activation(ht[:, u, 0], p_t[u][:, 1], ACT.Copy)
                        nc.scalar.activation(ht[0:REST, u, 1], p_t[u][0:REST, 2], ACT.Copy).then_inc(ht_ready[u], 1)

            @block.vector
            def _(v):
                for u in range(2):
                    v.sem_inc(stored[u], 16)
                with v.Fori(0, TURNS) as i:
                    for u in range(2):
                        v.wait_ge(sg_ready[u], i + 1)
                        nc.vector.tensor_tensor(hid[:, u, :], sg[:, u, :], p_h[u][:, H:2 * H],
                                                ALU.mult).then_inc(hid_ready[u], 1)
                    for u in range(2):
                        v.wait_ge(o_ps[u], i + 1)
                        v.wait_ge(stored[u], 16 * i + 16)
                        nc.vector.tensor_copy(ob[:, u, :], p_o[u][:, 0:D]).then_inc(ob_ready[u], 1)

            @block.sync
            def _(sp):
                with sp.Fori(0, TURNS) as i:
                    for u in range(2):
                        sp.wait_ge(ob_ready[u], i + 1)
                        sp.dma_start(o_dram[bass.ds((2 * i + u) * SLOTS, SLOTS), :], ob[:, u, :]).then_inc(stored[u], 16)
                for u in range(2):
                    sp.wait_ge(stored[u], 16 * TURNS + 16)


def grouped_experts(nc, W, K):
    E, P, H = 64, 6, 160
    NT = 2 * -(-(NTOK * P // SLOTS + E - 1) // 2)
    name = "L3_ffn"
    xn_dram = nc.dram_tensor(name + "_xn_dram", (NTOK, D), f32, kind="Internal").ap()
    o_dram = nc.dram_tensor(name + "_o_dram", (NT * SLOTS, D), f32, kind="Internal").ap()
    with Space(nc) as s:
        route = Route(s, name, E, P, NT)
        with Space(nc) as s2:
            xn = s2.sb(name + "_xn", [T, B, D])
            layer_norm_block(nc, name + "_ln", K.h, xn)
            index = s2.sb(name + "_index", [T, B, P])
            scores = s2.sb(name + "_scores", [T, B, E])
            grouped_router_block(nc, name + "_g", W, K, xn, xn_dram, route, index, scores)
            shared_expert_block(nc, name + "_sh", W, K, xn)
            sort_block(nc, name + "_sort", K, route, index, chosen=scores)
        wgu = s.sb(name + "_wgu", [D, E, 2 * H])
        wd0 = s.sb(name + "_wd0", [T, E, D])
        wd1 = s.sb(name + "_wd1", [H - T, E, D])
        wgu_in = s.sem(name + "_wgu_in")
        wd_in = s.sem(name + "_wd_in")
        total = s.sb(name + "_total", [T, B])
        own = s.sem(name + "_own")
        with nc.Block() as block:
            @block.sync
            def _(sp):
                sp.dma_start(wgu[:, :, 0:H], W["L3_ffn_Wg"].rearrange("e c n -> c e n")).then_inc(wgu_in, 16)
                sp.dma_start(wgu[:, :, H:2 * H], W["L3_ffn_Wu"].rearrange("e c n -> c e n")).then_inc(wgu_in, 16)
                sp.dma_start(wd0[:], W["L3_ffn_Wd"][:, 0:T, :].rearrange("e p n -> p e n")).then_inc(wd_in, 16)
                sp.dma_start(wd1[:], W["L3_ffn_Wd"][:, T:H, :].rearrange("e p n -> p e n")).then_inc(wd_in, 16)

            @block.vector
            def _(v):
                chain = Own(v, own)
                chain.done(nc.vector.tensor_reduce(out=total[:], in_=route.gate[:], axis=AX.X, op=ALU.add))
                chain.done(nc.vector.tensor_scalar(total[:], total[:], 1e-20, None, ALU.add))
                chain.done(nc.vector.reciprocal(total[:], total[:]))
                chain.done(nc.vector.tensor_tensor(route.gate[:], route.gate[:], per_row(total[:], P), ALU.mult))
        gated_tiles_block(nc, name + "_x", K, route, xn_dram, o_dram, wgu, wd0, wd1, wgu_in, wd_in, H)
        combine_block(nc, name + "_c", K, route, o_dram, 1)
    end_of_layer(nc)




def tower_program(nc, W, out):
    with Space(nc) as s:
        K = Constants(nc, s)
        constants_and_embedding(nc, W, K)
        layer0_attention(nc, W, K)
        top1_experts(nc, W, K, "L0_ffn", 8, 4, False)
        householder_attention(nc, W, K)
        capacity_experts(nc, W, K)
        layer2_attention(nc, W, K)
        top1_experts(nc, W, K, "L2_ffn", 8, 1, True)
        rope_attention(nc, W, K)
        grouped_experts(nc, W, K)
        out_done = s.sem("out_done")
        with nc.Block() as block:
            @block.sync
            def _(sp):
                sp.dma_start(out.rearrange("b t c -> t b c"), K.h[:]).then_inc(out_done, 16)
                sp.wait_ge(out_done, 16)


def kernel(**inputs):
    import numpy as np
    import concourse.bacc as bacc
    from concourse.bass_utils import run_bass_kernel_spmd

    nc = bacc.Bacc("TRN2", target_bir_lowering=False, num_devices=1)
    arrays = {}
    for name, a in inputs.items():
        arrays[name] = np.ascontiguousarray(a)
    arrays["x_t"] = np.ascontiguousarray(np.asarray(inputs["x"]).T)
    arrays["L0_attn_b1_t"] = np.ascontiguousarray(np.asarray(inputs["L0_attn_b1"]).reshape(4, 128).T)
    for name, chunks in (("L0_ffn_b1", 4), ("L2_ffn_b1", 1)):
        b1 = np.asarray(inputs[name])
        arrays[name + "_t"] = np.ascontiguousarray(b1.reshape(b1.shape[0], chunks, 128).transpose(0, 2, 1))
    for name in ("Wq", "Wk", "Wv", "Ww", "Wbeta", "Wg", "Wo"):
        arrays["L1_attn_" + name + "_t"] = np.ascontiguousarray(np.asarray(inputs["L1_attn_" + name]).T)
    row, col = np.arange(128)[:, None], np.arange(128)[None, :]
    arrays["head_rows"] = np.ascontiguousarray(np.broadcast_to(
        (row // 32 == np.arange(4)[None, :])[:, :, None], (128, 4, 128)).astype(np.float32))
    arrays["L1_ffn_b1_t"] = np.ascontiguousarray(np.asarray(inputs["L1_ffn_b1"]).T)
    arrays["L2_attn_bv_t"] = np.ascontiguousarray(np.asarray(inputs["L2_attn_bv"]).reshape(8, 128).T)
    theta = np.float32(1.0) / np.float32(10000.0) ** (np.arange(64, dtype=np.float32) / np.float32(64))
    angle = np.arange(128, dtype=np.float32)[:, None] * theta
    arrays["rope_cos"] = np.repeat(np.cos(angle), 2, axis=1)
    arrays["rope_sin"] = np.ascontiguousarray(np.stack([-np.sin(angle), np.sin(angle)], -1).reshape(128, 128))
    arrays["head_mask"] = (row // 8 == col // 8).astype(np.float32)
    arrays["head_columns"] = (row // 8 == np.arange(16)[None, :]).astype(np.float32)
    arrays["L3_ffn_router_w_t"] = np.ascontiguousarray(np.asarray(inputs["L3_ffn_router_w"]).T)
    W = {}
    for name, a in arrays.items():
        W[name] = nc.dram_tensor("in_" + name, a.shape, mybir.dt.from_np(a.dtype), kind="ExternalInput").ap()
    out = nc.dram_tensor("out", (B, T, D), f32, kind="ExternalOutput").ap()
    tower_program(nc, W, out)
    got = run_bass_kernel_spmd(nc, [{"in_" + n: a for n, a in arrays.items()}], core_ids=[0])
    return got.results[0]["out"]
```

```python
import math
from contextlib import ExitStack

import concourse.bass as bass
from concourse import mybir

f32 = mybir.dt.float32
f16 = mybir.dt.float16
i32 = mybir.dt.int32
u32 = mybir.dt.uint32
ALU = mybir.AluOpType
ACT = mybir.ActivationFunctionType
AX = mybir.AxisListType

T = 128
B = 16
D = 128
EPS = 1e-5


class Own:

    def __init__(self, engine, sem, first=0):
        self.engine, self.sem, self.at = engine, sem, first

    def done(self, ins):
        self.at = self.at + 1
        ins.then_inc(self.sem, 1)
        self.engine.wait_ge(self.sem, self.at)


class Space:

    used = []

    def __init__(self, nc):
        self.nc, self.ctx, self.count = nc, ExitStack(), 0

    def sb(self, name, shape, dt=f32):
        return self.ctx.enter_context(self.nc.sbuf_tensor(name, shape, dt))

    def ps(self, name, shape, dt=f32):
        return self.ctx.enter_context(self.nc.psum_tensor(name, shape, dt))

    def sem(self, name):
        handle = self.nc.alloc_semaphore(name=name)
        Space.used.append(handle)
        return handle

    def __enter__(self):
        self.ctx.__enter__()
        return self

    def __exit__(self, *a):
        return self.ctx.__exit__(*a)


def end_of_layer(nc):
    nc.clear_and_free_semaphores(Space.used)
    Space.used = []
    nc.all_engine_barrier()


def turns(engine, count, turn):
    with engine.Fori(0, count // 2) as i:
        for p in range(2):
            turn(2 * i + p, p)


def sequences(engine, body, ahead=None, finish=None, count=B):
    if ahead is not None:
        ahead()
    body(0, 0, True, False)
    with engine.Fori(0, count // 2 - 1) as i:
        body(2 * i + 1, 1, False, False)
        body(2 * i + 2, 0, False, False)
    body(count - 1, 1, False, True)
    if finish is not None:
        finish(count - 1)


def per_row(column, width):
    return column.unsqueeze(2).to_broadcast([column.shape[0], column.shape[1], width])


def per_tile(row, tiles):
    return row.unsqueeze(1).to_broadcast([row.shape[0], tiles, row.shape[1]])


def layer_norm_block(nc, name, src, dst, gamma=None, beta=None, scale=None):
    with Space(nc) as s:
        stats = s.sb(name + "_stats", [T, B, 6])
        mean = s.sb(name + "_mean", [T, B])
        gap = s.sb(name + "_gap", [T, B])
        var = s.sb(name + "_var", [T, B])
        std = s.sb(name + "_std", [T, B])
        rstd = s.sb(name + "_rstd", [T, B])
        own = s.sem(name + "_own")
        var_ready = s.sem(name + "_var_ready")
        std_ready = s.sem(name + "_std_ready")
        with nc.Block() as block:
            @block.scalar
            def _(act):
                act.wait_ge(var_ready, 1)
                nc.scalar.activation(std[:], var[:], ACT.Sqrt).then_inc(std_ready, 1)

            @block.vector
            def _(v):
                for b in range(B):
                    last = nc.vector.bn_stats(stats[:, b, :], src[:, b, :])
                last.then_inc(own, 1)
                v.wait_ge(own, 1)
                chain = Own(v, own, 1)
                nc.vector.tensor_tensor(mean[:], stats[:, :, 1], stats[:, :, 4], ALU.add)
                nc.vector.tensor_tensor(gap[:], stats[:, :, 1], stats[:, :, 4], ALU.subtract)
                chain.done(nc.vector.tensor_tensor(var[:], stats[:, :, 2], stats[:, :, 5], ALU.add))
                nc.vector.tensor_scalar(mean[:], mean[:], 0.5, None, ALU.mult)
                nc.vector.scalar_tensor_tensor(out=gap[:], in0=gap[:], scalar=0.25, in1=gap[:], op0=ALU.mult,
                                               op1=ALU.mult)
                chain.done(nc.vector.tensor_scalar(var[:], var[:], 1.0 / D, EPS, ALU.mult, ALU.add))
                nc.vector.tensor_tensor(var[:], var[:], gap[:], ALU.add).then_inc(var_ready, 1)
                v.wait_ge(std_ready, 1)
                chain.done(nc.vector.reciprocal(rstd[:], std[:]))
                for b in range(B):
                    last = nc.vector.tensor_scalar(dst[:, b, :], src[:, b, :], mean[:, b:b + 1], rstd[:, b:b + 1],
                                                   ALU.subtract, ALU.mult)
                chain.done(last)
                if gamma is not None:
                    chain.done(nc.vector.tensor_tensor(dst[:], dst[:], per_tile(gamma[:], B), ALU.mult))
                    chain.done(nc.vector.tensor_tensor(dst[:], dst[:], per_tile(beta[:], B), ALU.add))
                if scale is not None:
                    chain.done(nc.vector.tensor_scalar(dst[:], dst[:], scale, None, ALU.mult))


def constants_and_embedding(nc, W, K):
    with Space(nc) as s:
        ids = s.sb("ids", [T, B], i32)
        idf = s.sb("idf", [T, B])
        raw = s.sb("raw", [T, B, D])
        types = s.sb("types", [T, 5, 8])
        sel = s.sb("sel", [T, 3, B])
        low = s.sb("low", [T, B])
        part = s.sb("part", [T, B, 8])
        gamma = s.sb("gamma", [T, D])
        beta = s.sb("beta", [T, D])
        ids_in = s.sem("ids_in")
        rows_in = s.sem("rows_in")
        made = s.sem("made")
        gathered = s.sem("gathered")
        own = s.sem("emb_own")
        NTOK = D - 8
        with nc.Block() as block:
            @block.sync
            def _(sp):
                sp.dma_start(ids[:], W["x_t"]).then_inc(ids_in, 16)
                sp.dma_start(types[:].rearrange("p a b -> p (a b)"),
                             W["L0_tok_type_emb_table"].rearrange("a b -> (a b)").partition_broadcast(T)
                             ).then_inc(rows_in, 16)
                sp.dma_start(gamma[:], W["L0_tok_ln_gamma"].partition_broadcast(T)).then_inc(rows_in, 16)
                sp.dma_start(beta[:], W["L0_tok_ln_beta"].partition_broadcast(T)).then_inc(rows_in, 16)

            @block.gpsimd
            def _(g):
                g.wait_ge(ids_in, 16)
                for b in range(B):
                    g.indirect_dma_start(out=raw[:, b, 0:NTOK], out_offset=None, in_=W["L0_tok_token_emb_table"],
                                         in_offset=bass.IndirectOffsetOnAxis(ap=ids[:, b:b + 1], axis=0)
                                         ).then_inc(gathered, 16)
                K.fill(g, made)

            @block.vector
            def _(v):
                chain = Own(v, own)
                v.wait_ge(ids_in, 16)
                chain.done(nc.vector.tensor_copy(idf[:], ids[:]))
                nc.vector.tensor_scalar(sel[:, 0, :], idf[:], 128.0, None, ALU.is_lt)
                nc.vector.tensor_scalar(low[:], idf[:], 256.0, None, ALU.is_lt)
                chain.done(nc.vector.tensor_scalar(sel[:, 2, :], idf[:], 256.0, None, ALU.is_ge))
                v.wait_ge(rows_in, 48)
                chain.done(nc.vector.tensor_tensor(sel[:, 1, :], low[:], sel[:, 0, :], ALU.subtract))
                emb = raw[:, :, NTOK:D]
                for n, row in enumerate((0, 3, 4)):
                    to = emb if n == 0 else part[:]
                    chain.done(nc.vector.tensor_tensor(to, per_row(sel[:, n, :], 8), per_tile(types[:, row, :], B),
                                                       ALU.mult))
                    if n:
                        chain.done(nc.vector.tensor_tensor(emb, emb, part[:], ALU.add))
                v.wait_ge(gathered, 16 * B)
        layer_norm_block(nc, "ln_emb", raw, K.h, gamma, beta, math.sqrt(D))
    end_of_layer(nc)


class Constants:

    def __init__(self, nc, s):
        self.nc = nc
        self.h = s.sb("h", [T, B, D])
        self.ident = s.sb("ident", [T, T])
        self.ones = s.sb("ones", [T, T])
        self.up_to = s.sb("up_to", [T, T])
        self.before = s.sb("before", [T, T])
        self.after = s.sb("after", [T, T])

    def fill(self, g, made):
        g.memset(self.ones[:], 1.0).then_inc(made, 1)
        g.wait_ge(made, 1)
        for m, op, base, sign in ((self.ident, ALU.is_equal, 0, 1), (self.up_to, ALU.is_ge, 0, 1),
                                  (self.before, ALU.is_gt, 0, 1), (self.after, ALU.is_gt, 0, -1)):
            g.affine_select(out=m[:], in_=self.ones[:], compare_op=op, fill=0.0, base=base,
                            pattern=[[sign, T]], channel_multiplier=-sign)


def causal_linear_attention_block(nc, W, K, xin, x2):
    HEADS, DH = 8, 16
    HALF = HEADS // 2
    with Space(nc) as s:
        h1 = s.sb("a0_h1", [T, B, D])
        g1 = s.sb("a0_g1", [T, D])
        b1 = s.sb("a0_b1", [T, D])
        wqk = s.sb("a0_wqk", [D, 2, D])
        bqk = s.sb("a0_bqk", [D, 2])
        wv = s.sb("a0_wv", [D, D])
        bv = s.sb("a0_bv", [T, D])
        wo = s.sb("a0_wo", [D, D])
        bo = s.sb("a0_bo", [T, D])
        head_of = s.sb("a0_head_of", [D, HEADS])
        loads = s.sem("a0_loads")
        with nc.Block() as block:
            @block.sync
            def _(sp):
                for to, source in ((g1[:], W["L0_attn_ln1_g"].partition_broadcast(T)),
                                   (b1[:], W["L0_attn_ln1_b"].partition_broadcast(T)),
                                   (wqk[:, 0], W["L0_attn_Wq"]), (wqk[:, 1], W["L0_attn_Wk"]),
                                   (bqk[:, 0:1], W["L0_attn_bq"].unsqueeze(1)), (bqk[:, 1:2], W["L0_attn_bk"].unsqueeze(1)),
                                   (wv[:], W["L0_attn_Wv"]), (bv[:], W["L0_attn_bv"].partition_broadcast(T)),
                                   (wo[:], W["L0_attn_Wo"]), (bo[:], W["L0_attn_bo"].partition_broadcast(T)),
                                   (head_of[:], W["head_of_16"])):
                    sp.dma_start(to, source).then_inc(loads, 16)
                sp.wait_ge(loads, 176)
        layer_norm_block(nc, "a0_ln1", xin, h1, g1, b1)

        hs = s.sb("a0_hs", [T, 2, D])
        h1t = s.sb("a0_h1t", [D, T])
        xb = s.sb("a0_xb", [D, 2, T])
        ex = s.sb("a0_ex", [D, 2, T])
        qk = s.sb("a0_qk", [D, 2, 2, T])
        q_bd = s.sb("a0_q_bd", [D, 2, HEADS, T])
        v17 = s.sb("a0_v17", [T, 2, HEADS, DH + 1])
        sm = s.sb("a0_sm", [T, HEADS, T])
        den = s.sb("a0_den", [T, HEADS])
        rden = s.sb("a0_rden", [T, HEADS])
        at_ = s.sb("a0_at", [T, D])
        att = s.sb("a0_att", [D, T])
        xbo = s.sb("a0_xbo", [T, B, D])
        p_s = [s.ps(f"a0_p_s{a}", [T, HALF, T]) for a in range(2)]
        p_t, p_qk, p_v, p_n, p_at, p_o = (s.ps("a0_p_" + n, [T, 512]) for n in ("t", "qk", "v", "n", "at", "o"))
        num = p_n[:, 0:HEADS * (DH + 1)].rearrange("t (h e) -> t h e", h=HEADS)
        hs_ready, t_ps, h1t_ready, qk_ps, v_ps, xb_ready, neg_ready, ex_ready, qk_ready, v_ready, n_ps, at_ready, \
            att_ps, att_ready, o_ps, x2_ready, ones_ready, own = (s.sem("a0_" + n) for n in (
                "hs_ready", "t_ps", "h1t_ready", "qk_ps", "v_ps", "xb_ready", "neg_ready", "ex_ready", "qk_ready",
                "v_ready", "n_ps", "at_ready", "att_ps", "att_ready", "o_ps", "x2_ready", "ones_ready", "own"))
        bd_ready, s_ps, sm_ready = ([s.sem(f"a0_{n}{a}") for a in range(2)] for n in ("bd_ready", "s_ps", "sm_ready"))

        def spread(engine, p, a):
            heads = slice(HALF * a, HALF * a + HALF)
            engine.tensor_tensor(out=q_bd[:, p, heads], in0=qk[:, p, 0].unsqueeze(1).to_broadcast([D, HALF, T]),
                                 in1=head_of[:, heads].unsqueeze(2).to_broadcast([D, HALF, T]),
                                 op=ALU.mult).then_inc(bd_ready[a], 1)

        with nc.Block() as block:
            @block.gpsimd
            def _(g):
                def tokens(n, p, early):
                    if not early:
                        g.wait_ge(t_ps, n - 1)
                    g.tensor_copy(hs[:, p], h1[:, n, :]).then_inc(hs_ready, 1)

                def queries(n, p, early):
                    g.wait_ge(qk_ready, n + 1)
                    if not early:
                        g.wait_ge(s_ps[1], n - 1)
                    spread(g, p, 1)

                g.memset(v17[:, :, :, DH:DH + 1], 1.0).then_inc(ones_ready, 1)
                tokens(0, 0, True)
                g.tensor_tensor(out=xbo[:], in0=xin[:], in1=per_tile(bo[:], B), op=ALU.add).then_inc(ones_ready, 1)
                tokens(1, 1, True)
                queries(0, 0, True)
                tokens(2, 0, False)
                queries(1, 1, True)
                with g.Fori(1, B // 2 - 1) as i:
                    tokens(2 * i + 1, 1, False)
                    queries(2 * i, 0, False)
                    tokens(2 * i + 2, 0, False)
                    queries(2 * i + 1, 1, False)
                tokens(B - 1, 1, False)
                queries(B - 2, 0, False)
                queries(B - 1, 1, False)

            @block.vector
            def _(v):
                def low(n):
                    v.wait_ge(xb_ready, n + 1)
                    nc.vector.tensor_scalar(ex[:], xb[:], 0.0, None, ALU.min).then_inc(neg_ready, 1)

                def elu(n, p):
                    v.wait_ge(ex_ready, n + 1)
                    nc.vector.scalar_tensor_tensor(out=qk[:, p].rearrange("c n t -> c (n t)"),
                                                   in0=xb[:].rearrange("c n t -> c (n t)"), scalar=0.0,
                                                   in1=ex[:].rearrange("c n t -> c (n t)"), op0=ALU.max,
                                                   op1=ALU.add).then_inc(qk_ready, 1)
                    v.wait_ge(qk_ready, n + 1)
                    spread(nc.vector, p, 0)

                def values(n, p):
                    v.wait_ge(v_ps, n + 1)
                    nc.vector.tensor_tensor(v17[:, p, :, 0:DH], p_v[:, 0:D].rearrange("t (h d) -> t h d", h=HEADS),
                                            bv[:].rearrange("t (h d) -> t h d", h=HEADS), ALU.add).then_inc(v_ready, 1)

                def mask(b, a):
                    v.wait_ge(s_ps[a], b + 1)
                    nc.vector.tensor_tensor(sm[:, HALF * a:HALF * a + HALF], p_s[a][:], per_tile(K.up_to[:], HALF),
                                            ALU.mult).then_inc(sm_ready[a], 1)

                def finish(b):
                    v.wait_ge(o_ps, b + 1)
                    nc.vector.tensor_tensor(x2[:, b, :], xbo[:, b, :], p_o[:, 0:D], ALU.add).then_inc(x2_ready, 1)

                def ahead():
                    low(0)
                    elu(0, 0)
                    values(0, 0)
                    v.wait_ge(ones_ready, 2)

                def body(b, p, first, last):
                    mask(b, 0)
                    if not last:
                        low(b + 1)
                    mask(b, 1)
                    if not last:
                        elu(b + 1, 1 - p)
                        values(b + 1, 1 - p)
                    if not first:
                        finish(b - 1)
                    v.wait_ge(n_ps, b + 1)
                    chain = Own(v, own, 2 * b)
                    chain.done(nc.vector.tensor_scalar(den[:], num[:, :, DH], 1e-6, None, ALU.max))
                    chain.done(nc.vector.reciprocal(rden[:], den[:]))
                    nc.vector.tensor_tensor(at_[:].rearrange("t (h d) -> t h d", h=HEADS), num[:, :, 0:DH],
                                            per_row(rden[:], DH), ALU.mult).then_inc(at_ready, 1)

                sequences(v, body, ahead, finish)

            @block.scalar
            def _(act):
                def transposed(n):
                    act.wait_ge(t_ps, n + 1)
                    nc.scalar.activation(h1t[:], p_t[:, 0:T], ACT.Copy).then_inc(h1t_ready, 1)

                def biased(n):
                    act.wait_ge(qk_ps, n + 1)
                    for k in range(2):
                        last = nc.scalar.activation(xb[:, k], p_qk[:, k * T:(k + 1) * T], ACT.Identity,
                                                    bias=bqk[:, k:k + 1])
                    last.then_inc(xb_ready, 1)
                    act.wait_ge(neg_ready, n + 1)
                    nc.scalar.activation(ex[:], ex[:], ACT.Exp).then_inc(ex_ready, 1)

                def finish(b):
                    act.wait_ge(att_ps, b + 1)
                    nc.scalar.activation(att[:], p_at[:, 0:T], ACT.Copy).then_inc(att_ready, 1)

                def ahead():
                    transposed(0)
                    biased(0)

                def body(b, p, first, last):
                    if not last:
                        transposed(b + 1)
                        biased(b + 1)
                    if not first:
                        finish(b - 1)

                sequences(act, body, ahead, finish)

            @block.tensor
            def _(pe):
                def transpose_in(n, p):
                    pe.wait_ge(hs_ready, n + 1)
                    nc.tensor.transpose(p_t[:, 0:T], hs[:, p], K.ident[:]).then_inc(t_ps, 1)

                def project(n):
                    pe.wait_ge(h1t_ready, n + 1)
                    for k in range(2):
                        last = nc.tensor.matmul(p_qk[:, k * T:(k + 1) * T], wqk[:, k], h1t[:], start=True, stop=True)
                    last.then_inc(qk_ps, 1)

                def values(n, first):
                    if not first:
                        pe.wait_ge(v_ready, n)
                    nc.tensor.matmul(p_v[:, 0:D], h1t[:], wv[:], start=True, stop=True).then_inc(v_ps, 1)

                def scores(b, p, a, first):
                    pe.wait_ge(bd_ready[a], b + 1)
                    if not first:
                        pe.wait_ge(sm_ready[a], b)
                    nc.tensor.matmul(p_s[a][:], qk[:, p, 1], q_bd[:, p, HALF * a:HALF * a + HALF], start=True,
                                     stop=True).then_inc(s_ps[a], 1)

                def transpose_out(b):
                    pe.wait_ge(at_ready, b + 1)
                    nc.tensor.transpose(p_at[:, 0:T], at_[:], K.ident[:]).then_inc(att_ps, 1)

                def project_out(b):
                    pe.wait_ge(att_ready, b + 1)
                    pe.wait_ge(x2_ready, b + 1)
                    nc.tensor.matmul(p_o[:, 0:D], att[:], wo[:], start=True, stop=True).then_inc(o_ps, 1)

                def ahead():
                    transpose_in(0, 0)
                    project(0)
                    values(0, True)

                def finish(b):
                    transpose_out(b)
                    project_out(b)

                def body(b, p, first, last):
                    if not last:
                        transpose_in(b + 1, 1 - p)
                    scores(b, p, 0, first)
                    if not last:
                        project(b + 1)
                    scores(b, p, 1, first)
                    if not first:
                        transpose_out(b - 1)
                    if not last:
                        values(b + 1, False)
                    if not first:
                        project_out(b - 1)
                    pe.wait_ge(v_ready, b + 1)
                    for a in range(2):
                        pe.wait_ge(sm_ready[a], b + 1)
                        for h in range(HALF * a, HALF * a + HALF):
                            last_ = nc.tensor.matmul(num[:, h], sm[:, h], v17[:, p, h], start=True, stop=True)
                    last_.then_inc(n_ps, 1)

                pe.sem_inc(x2_ready, 1)
                pe.wait_ge(ones_ready, 1)
                sequences(pe, body, ahead, finish)


def dense_ffn_block(nc, W, K, x2):
    CH = 4
    with Space(nc) as s:
        h2 = s.sb("f_h2", [T, B, D])
        g2 = s.sb("f_g2", [T, D])
        be2 = s.sb("f_be2", [T, D])
        w1 = s.sb("f_w1", [D, CH, T])
        b1 = s.sb("f_b1", [T, CH])
        w2 = s.sb("f_w2", [T, CH, D])
        b2 = s.sb("f_b2", [T, D])
        loads = s.sem("f_loads")
        with nc.Block() as block:
            @block.sync
            def _(sp):
                sp.dma_start(g2[:], W["L0_attn_ln2_g"].partition_broadcast(T)).then_inc(loads, 16)
                sp.dma_start(be2[:], W["L0_attn_ln2_b"].partition_broadcast(T)).then_inc(loads, 16)
                sp.dma_start(w1[:].rearrange("c k n -> c (k n)"), W["L0_attn_W1"]).then_inc(loads, 16)
                sp.dma_start(w2[:], W["L0_attn_W2"].rearrange("(k p) n -> p k n", p=T)).then_inc(loads, 16)
                sp.dma_start(b1[:], W["L0_attn_b1_t"]).then_inc(loads, 16)
                sp.dma_start(b2[:], W["L0_attn_b2"].partition_broadcast(T)).then_inc(loads, 16)
                sp.wait_ge(loads, 96)
        layer_norm_block(nc, "f_ln2", x2, h2, g2, be2)
        PAIRS = B // 2
        hs = s.sb("f_hs", [T, 2, 2, D])
        h2t = s.sb("f_h2t", [D, 2, 2, T])
        hid = s.sb("f_hid", [T, CH, 2, T])
        p_x = s.ps("f_p_x", [T, 4, T])
        p_y = [s.ps(f"f_p_y{p}", [T, 4, T]) for p in range(2)]
        p_h = s.ps("f_p_h", [T, CH, 2, T])
        hs_ready, t_ps, h2t_ready, h_ps, hid_ready, y_ps, y_done, base_ready = (s.sem("f_" + n) for n in (
            "hs_ready", "t_ps", "h2t_ready", "h_ps", "hid_ready", "y_ps", "y_done", "base_ready"))
        with nc.Block() as block:
            @block.gpsimd
            def _(g):
                def tokens(n, p):
                    g.wait_ge(t_ps, n + 1)
                    g.tensor_copy(hs[:, p], h2[:, bass.ds(2 * n, 2), :]).then_inc(hs_ready, 1)

                g.sem_inc(t_ps, 2)
                tokens(0, 0)
                tokens(1, 1)
                g.tensor_tensor(out=x2[:], in0=x2[:], in1=per_tile(b2[:], B), op=ALU.add).then_inc(base_ready, 1)
                with g.Fori(1, PAIRS // 2) as i:
                    for p in range(2):
                        tokens(2 * i + p, p)

            @block.vector
            def _(v):
                v.wait_ge(base_ready, 1)
                nc.vector.tensor_tensor(K.h[:], K.h[:], x2[:], ALU.add).then_inc(base_ready, 1)
                v.wait_ge(base_ready, 2)

                def turn(b, p):
                    v.wait_ge(y_ps, b + 1)
                    nc.vector.tensor_tensor(K.h[:, bass.ds(2 * b, 2), :], K.h[:, bass.ds(2 * b, 2), :], p_y[p][:, 0:2],
                                            ALU.add).then_inc(y_done, 1)

                turns(v, PAIRS, turn)

            @block.scalar
            def _(act):
                def transposed(n, p):
                    act.wait_ge(t_ps, n + 3)
                    nc.scalar.activation(h2t[:, p], p_x[:, 0:2], ACT.Copy).then_inc(h2t_ready, 1)

                def body(b, p, first, last):
                    for c in range(CH):
                        act.wait_ge(h_ps, 2 * b + c // 2 + 1)
                        nc.scalar.activation(hid[:, c], p_h[:, c], ACT.Relu, bias=b1[:, c:c + 1]).then_inc(hid_ready, 1)
                        if c == 1 and not last:
                            transposed(b + 1, 1 - p)

                sequences(act, body, lambda: transposed(0, 0), count=PAIRS)

            @block.tensor
            def _(pe):
                def transpose_in(n, p):
                    pe.wait_ge(hs_ready, n + 1)
                    for u in range(2):
                        last = nc.tensor.transpose(p_x[:, u], hs[:, p, u], K.ident[:])
                    last.then_inc(t_ps, 1)

                def body(b, p, first, last):
                    pe.wait_ge(h2t_ready, b + 1)
                    for c in range(CH):
                        last_ = nc.tensor.matmul(p_h[:, c], w1[:, c], h2t[:, p], start=True, stop=True)
                        if c % 2:
                            last_.then_inc(h_ps, 1)
                    if not last:
                        transpose_in(b + 1, 1 - p)
                    pe.wait_ge(y_done, b + 1)
                    for u in range(2):
                        for c in range(CH):
                            pe.wait_ge(hid_ready, CH * b + c + 1)
                            last_ = nc.tensor.matmul(p_y[p][:, u], hid[:, c, u], w2[:, c], start=c == 0, stop=c == CH - 1)
                    last_.then_inc(y_ps, 1)

                pe.sem_inc(y_done, 2)
                sequences(pe, body, lambda: transpose_in(0, 0), count=PAIRS)


def layer0_attention(nc, W, K):
    with Space(nc) as s:
        xin = s.sb("xin", [T, B, D])
        x2 = s.sb("x2", [T, B, D])
        layer_norm_block(nc, "a0_ln0", K.h, xin)
        causal_linear_attention_block(nc, W, K, xin, x2)
        dense_ffn_block(nc, W, K, x2)
    end_of_layer(nc)


SLOTS = 128
NTOK = B * T


class Route:

    def __init__(self, s, name, experts, picks, tiles):
        self.experts, self.picks, self.tiles = experts, picks, tiles
        self.dest = s.sb(name + "_dest", [T, B, picks], i32)
        self.gate = s.sb(name + "_gate", [T, B, picks])
        self.who = s.sb(name + "_who", [SLOTS, tiles], i32)
        self.expert_of = s.sb(name + "_expert_of", [1, tiles], i32)


def router_logits_block(nc, name, K, xn, xn_dram, w_dram, experts, logits, bias_dram=None):
    Q = 4
    with Space(nc) as s:
        w = s.sb(name + "_wr", [D, experts])
        bias = s.sb(name + "_br", [T, experts])
        xt = s.sb(name + "_xt", [D, B, T])
        p_t = [s.ps(f"{name}_p_t{k}", [D, Q, T]) for k in range(B // Q)]
        p_l = [s.ps(f"{name}_p_l{k}", [T, 512]) for k in range(B // Q)]
        stored, loads, t_ps, xt_ready, l_ps = (s.sem(name + "_" + n) for n in (
            "stored", "loads", "t_ps", "xt_ready", "l_ps"))
        n_loads = 32 if bias_dram is not None else 16
        with nc.Block() as block:
            @block.sync
            def _(sp):
                sp.dma_start(w[:], w_dram).then_inc(loads, 16)
                if bias_dram is not None:
                    sp.dma_start(bias[:], bias_dram.partition_broadcast(T)).then_inc(loads, 16)
                sp.dma_start(xn_dram.rearrange("(b t) c -> t b c", t=T), xn[:]).then_inc(stored, 16)
                sp.wait_ge(stored, 16)

            @block.tensor
            def _(pe):
                def transposes(k):
                    for q in range(Q):
                        last = nc.tensor.transpose(p_t[k][:, q], xn[:, Q * k + q, :], K.ident[:])
                    last.then_inc(t_ps, 1)

                def products(k):
                    pe.wait_ge(xt_ready, k + 1)
                    for q in range(Q):
                        last = nc.tensor.matmul(p_l[k][:, q * experts:(q + 1) * experts], xt[:, Q * k + q, :], w[:],
                                                start=True, stop=True)
                    last.then_inc(l_ps, 1)

                transposes(0)
                transposes(1)
                pe.wait_ge(loads, n_loads)
                for k in range(B // Q):
                    products(k)
                    if k + 2 < B // Q:
                        transposes(k + 2)

            @block.scalar
            def _(act):
                for k in range(B // Q):
                    act.wait_ge(t_ps, k + 1)
                    nc.scalar.activation(xt[:, Q * k:Q * k + Q, :], p_t[k][:], ACT.Copy).then_inc(xt_ready, 1)

            @block.vector
            def _(v):
                v.wait_ge(loads, n_loads)
                for k in range(B // Q):
                    v.wait_ge(l_ps, k + 1)
                    product = p_l[k][:, 0:Q * experts].rearrange("t (q e) -> t q e", q=Q)
                    to = logits[:, Q * k:Q * k + Q, :]
                    if bias_dram is not None:
                        nc.vector.tensor_tensor(to, product, per_tile(bias[:], Q), ALU.add)
                    else:
                        nc.vector.tensor_copy(to, product)


def sort_block(nc, name, K, route, index, chosen=None, capacity=None):
    E, P, NT = route.experts, route.picks, route.tiles
    COLS = B * E
    NB = max(1, COLS // 512)
    with Space(nc) as s:
        iota_e = s.sb(name + "_iota_e", [T, E])
        iota_row = s.sb(name + "_iota_row", [T, 256])
        iota_h = s.sb(name + "_iota_h", [T, 256], f16)
        token = s.sb(name + "_token", [T, B])
        hot = s.sb(name + "_hot", [T, B, E])
        mask = s.sb(name + "_mask", [T, B, E])
        mask_h = s.sb(name + "_mask_h", [T, B, E], f16)
        sums = s.sb(name + "_sums", [T, B + 1, E])
        sums_h = s.sb(name + "_sums_h", [T, B + 1, E], f16)
        before_h = s.sb(name + "_before_h", [T, T], f16)
        ones_h = s.sb(name + "_ones_h", [T, T], f16)
        pos = s.sb(name + "_pos", [T, B, E])
        prod = s.sb(name + "_prod", [T, B, E])
        prod2 = s.sb(name + "_prod2", [T, B, E])
        tiles_i = s.sb(name + "_tiles_i", [T, E], i32)
        tiles_f = s.sb(name + "_tiles_f", [T, E])
        incl = s.sb(name + "_incl", [T, E])
        base = s.sb(name + "_base", [T, E])
        col_i = s.sb(name + "_col_i", [E, 1], i32)
        col_f = s.sb(name + "_col_f", [E, 1])
        cum = s.sb(name + "_cum", [E, 1])
        passed = s.sb(name + "_passed", [E, NT])
        dest_f = s.sb(name + "_dest_f", [T, B, P])
        keep = s.sb(name + "_keep", [T, B, P])
        second = s.sb(name + "_second", [T, B, P])
        four = s.sb(name + "_four", [T, B, P])
        part_i = s.sb(name + "_part_i", [T, B, P], i32)
        lo = s.sb(name + "_lo", [T, B, P])
        hi = s.sb(name + "_hi", [T, B, P])
        R = 8
        columns = s.sb(name + "_columns", [T, 3, B * P])
        cur = s.sb(name + "_cur", [T, 2, 3, R])
        low_hot = s.sb(name + "_low_hot", [T, 2, R, SLOTS], f16)
        high_tok = s.sb(name + "_high_tok", [T, 2, R, NT], f16)
        zeros_h = s.sb(name + "_zeros_h", [T, SLOTS], f16)
        p_rank = s.ps(name + "_p_rank", [T, NB, min(512, COLS)])
        p_cnt = s.ps(name + "_p_cnt", [T, 512])
        p_col = s.ps(name + "_p_col", [T, 512])
        p_who = s.ps(name + "_p_who", [T, 512])
        consts, mask_ready, rank_ps, cnt_ps, col_ps, col_ready, cum_ps, passed_ready, te_ps, cur_ready, hots, hots_used, \
            who_ps, own, filled = (s.sem(name + "_" + n) for n in (
                "consts", "mask_ready", "rank_ps", "cnt_ps", "col_ps", "col_ready", "cum_ps", "passed_ready",
                "te_ps", "cur_ready", "hots", "hots_used", "who_ps", "own", "filled"))
        with nc.Block() as block:
            @block.gpsimd
            def _(g):
                g.iota(iota_e[:], pattern=[[1, E]], base=0, channel_multiplier=0,
                       allow_small_or_imprecise_dtypes=True)
                g.iota(iota_row[:], pattern=[[1, 256]], base=0, channel_multiplier=0,
                       allow_small_or_imprecise_dtypes=True)
                g.iota(iota_h[:], pattern=[[1, 256]], base=0, channel_multiplier=0,
                       allow_small_or_imprecise_dtypes=True)
                g.iota(token[:], pattern=[[T, B]], base=0, channel_multiplier=1,
                       allow_small_or_imprecise_dtypes=True)
                g.memset(zeros_h[:], 0.0)
                g.memset(sums[:, 0, :], 0.0)
                g.tensor_copy(before_h[:], K.before[:])
                g.tensor_copy(ones_h[:], K.ones[:]).then_inc(consts, 1)

            @block.vector
            def _(v):
                chain = Own(v, own)
                v.wait_ge(consts, 1)

                def flat(a):
                    return a[:].rearrange("t b k -> t (b k)")

                def one_hot(k, out):
                    return nc.vector.tensor_tensor(out, per_tile(iota_e[:], B), per_row(index[:, :, k], E),
                                                   ALU.is_equal)

                def picked(out, values, k_hot, tmp):
                    chain.done(nc.vector.tensor_tensor(tmp, k_hot, values, ALU.mult))
                    return nc.vector.tensor_reduce(out=out, in_=tmp, axis=AX.X, op=ALU.add)

                for k in range(P):
                    chain.done(one_hot(k, mask[:] if k == 0 else hot[:]))
                    if k:
                        chain.done(nc.vector.tensor_tensor(mask[:], mask[:], hot[:], ALU.add))
                for b in range(B):
                    chain.done(nc.vector.tensor_tensor(sums[:, b + 1, :], sums[:, b, :], mask[:, b, :], ALU.add))
                nc.vector.tensor_copy(mask_h[:], mask[:])
                nc.vector.tensor_copy(sums_h[:], sums[:]).then_inc(mask_ready, 1)
                if capacity is None:
                    v.wait_ge(cnt_ps, 1)
                    chain.done(nc.vector.tensor_scalar(tiles_i[:], p_cnt[:, 0:E], float(SLOTS - 1), None, ALU.add))
                    chain.done(nc.vector.tensor_scalar(tiles_i[:], tiles_i[:], 7, None, ALU.arith_shift_right))
                    chain.done(nc.vector.tensor_copy(tiles_f[:], tiles_i[:]))
                    chain.done(nc.vector.tensor_tensor_scan(incl[:], K.ones[:, 0:E], tiles_f[:], 0.0, ALU.mult, ALU.add))
                    chain.done(nc.vector.tensor_tensor(base[:], incl[:], tiles_f[:], ALU.subtract))
                    chain.done(nc.vector.tensor_scalar(base[:], base[:], float(SLOTS), None, ALU.mult))
                    v.wait_ge(col_ps, 1)
                    chain.done(nc.vector.tensor_scalar(col_i[:], p_col[0:E, 0:1], float(SLOTS - 1), None, ALU.add))
                    chain.done(nc.vector.tensor_scalar(col_i[:], col_i[:], 7, None, ALU.arith_shift_right))
                    nc.vector.tensor_copy(col_f[:], col_i[:]).then_inc(col_ready, 1)
                    v.wait_ge(cum_ps, 1)
                    chain.done(nc.vector.tensor_copy(cum[:], p_col[0:E, 0:1]))
                    nc.vector.tensor_scalar(passed[:], iota_row[0:E, 0:NT], cum[:, 0:1], None,
                                            ALU.is_ge).then_inc(passed_ready, 1)
                    v.wait_ge(te_ps, 1)
                    nc.vector.tensor_scalar(route.expert_of[:], p_col[0:1, 0:NT], float(E - 1), None, ALU.min)
                v.wait_ge(rank_ps, 1)
                ranks = p_rank[:].rearrange("t n (b e) -> t (n b) e", e=E)
                if capacity is None:
                    chain.done(nc.vector.tensor_tensor(pos[:], ranks, per_tile(base[:], B), ALU.add))
                else:
                    chain.done(nc.vector.tensor_copy(pos[:], ranks))
                for k in range(P):
                    chain.done(one_hot(k, hot[:]))
                    if chosen is not None:
                        chain.done(picked(route.gate[:, :, k], chosen[:], hot[:], prod2[:]))
                    chain.done(picked(dest_f[:, :, k], pos[:], hot[:], prod[:]))
                if capacity is None:
                    chain.done(nc.vector.tensor_copy(route.dest[:], dest_f[:]))
                    chain.done(nc.vector.tensor_scalar(part_i[:], route.dest[:], 7, None, ALU.arith_shift_right))
                    chain.done(nc.vector.tensor_copy(hi[:], part_i[:]))
                    chain.done(nc.vector.tensor_scalar(part_i[:], route.dest[:], SLOTS - 1, None, ALU.bitwise_and))
                    chain.done(nc.vector.tensor_copy(lo[:], part_i[:]))
                else:
                    chain.done(nc.vector.tensor_scalar(keep[:], dest_f[:], float(capacity), None, ALU.is_lt))
                    chain.done(nc.vector.tensor_tensor(route.gate[:], route.gate[:], keep[:], ALU.mult))
                    chain.done(nc.vector.tensor_scalar(second[:], dest_f[:], float(SLOTS), None, ALU.is_ge))
                    chain.done(nc.vector.tensor_copy(part_i[:], index[:]))
                    chain.done(nc.vector.tensor_scalar(part_i[:], part_i[:], 2, None, ALU.arith_shift_right))
                    chain.done(nc.vector.tensor_copy(four[:], part_i[:]))
                    chain.done(nc.vector.tensor_tensor(hi[:], four[:], index[:], ALU.subtract))
                    chain.done(nc.vector.tensor_scalar(hi[:], hi[:], float(E), None, ALU.add))
                    chain.done(nc.vector.tensor_tensor(hi[:], hi[:], second[:], ALU.mult))
                    chain.done(nc.vector.tensor_tensor(hi[:], hi[:], index[:], ALU.add))
                    chain.done(nc.vector.tensor_scalar(four[:], four[:], float(-SLOTS), float(-SLOTS), ALU.mult, ALU.add))
                    chain.done(nc.vector.scalar_tensor_tensor(out=flat(lo), in0=flat(index), scalar=float(SLOTS // 4),
                                                              in1=flat(four), op0=ALU.mult, op1=ALU.add))
                    chain.done(nc.vector.tensor_tensor(lo[:], lo[:], second[:], ALU.mult))
                    chain.done(nc.vector.tensor_tensor(lo[:], lo[:], dest_f[:], ALU.add))
                    chain.done(nc.vector.tensor_scalar(hi[:], hi[:], float(-NT), None, ALU.add))
                    chain.done(nc.vector.tensor_tensor(hi[:], hi[:], keep[:], ALU.mult))
                    chain.done(nc.vector.tensor_scalar(hi[:], hi[:], float(NT), None, ALU.add))
                    chain.done(nc.vector.scalar_tensor_tensor(out=flat(dest_f), in0=flat(index), scalar=float(capacity),
                                                              in1=flat(dest_f), op0=ALU.mult, op1=ALU.add))
                    chain.done(nc.vector.tensor_tensor(dest_f[:], dest_f[:], keep[:], ALU.mult))
                    chain.done(nc.vector.tensor_copy(route.dest[:], dest_f[:]))
                nc.vector.tensor_copy(columns[:, 0], lo[:].rearrange("t b k -> t (b k)"))
                nc.vector.tensor_copy(columns[:, 1], hi[:].rearrange("t b k -> t (b k)"))
                chain.done(nc.vector.tensor_copy(columns[:, 2].rearrange("t (b k) -> t b k", k=P), per_row(token[:], P)))
                v.sem_inc(hots_used, 2)

                def turn(i, p):
                    v.wait_ge(hots_used, i + 1)
                    nc.vector.tensor_copy(cur[:, p], columns[:, :, bass.ds(i * R, R)]).then_inc(cur_ready, 1)
                    v.wait_ge(cur_ready, i + 1)
                    for r in range(R):
                        nc.vector.tensor_scalar(low_hot[:, p, r], iota_h[:, 0:SLOTS], cur[:, p, 0, r:r + 1], None,
                                                ALU.is_equal)
                        last = nc.vector.tensor_scalar(high_tok[:, p, r], iota_h[:, 0:NT], cur[:, p, 1, r:r + 1],
                                                       cur[:, p, 2, r:r + 1], ALU.is_equal, ALU.mult)
                        if r % (R // 2) == R // 2 - 1:
                            last.then_inc(hots, 1)

                turns(v, B * P // R, turn)
                v.wait_ge(who_ps, 1)
                nc.vector.tensor_copy(route.who[:], p_who[:, 0:NT])

            @block.tensor
            def _(pe):
                pe.wait_ge(mask_ready, 1)
                flat_m = mask_h[:].rearrange("t b e -> t (b e)")
                flat_s = sums_h[:].rearrange("t b e -> t (b e)")
                W_ = min(512, COLS)
                if capacity is None:
                    nc.tensor.matmul(p_cnt[:, 0:E], ones_h[:], sums_h[:, B, :], start=True, stop=True).then_inc(cnt_ps, 1)
                    nc.tensor.matmul(p_col[0:E, 0:1], sums_h[:, B, :], ones_h[:, 0:1], start=True,
                                     stop=True).then_inc(col_ps, 1)
                for n in range(NB):
                    cols = slice(n * W_, (n + 1) * W_)
                    nc.tensor.matmul(p_rank[:, n], before_h[:], flat_m[:, cols], start=True, stop=False)
                    last = nc.tensor.matmul(p_rank[:, n], ones_h[:], flat_s[:, cols], start=False, stop=True)
                last.then_inc(rank_ps, 1)
                if capacity is None:
                    pe.wait_ge(col_ready, 1)
                    nc.tensor.matmul(p_col[0:E, 0:1], K.up_to[0:E, 0:E], col_f[:], start=True, stop=True).then_inc(cum_ps, 1)
                    pe.wait_ge(passed_ready, 1)
                    nc.tensor.matmul(p_col[0:1, 0:NT], K.ones[0:E, 0:1], passed[:], start=True, stop=True).then_inc(te_ps, 1)
                nc.tensor.matmul(p_who[:, 0:NT], zeros_h[:], iota_h[:, 0:NT], start=True, stop=False)
                def turn(i, p):
                    for r in range(R):
                        if r % (R // 2) == 0:
                            pe.wait_ge(hots, 2 * i + r // (R // 2) + 1)
                        last = nc.tensor.matmul(p_who[:, 0:NT], low_hot[:, p, r], high_tok[:, p, r], start=False,
                                                stop=False)
                    last.then_inc(hots_used, 1)

                turns(pe, B * P // R, turn)
                nc.tensor.matmul(p_who[:, 0:NT], zeros_h[:], iota_h[:, 0:NT], start=False, stop=True).then_inc(who_ps, 1)


class ExpertWeights:

    def __init__(self, s, name, experts, chunks, w1, b1_t, w2, b2):
        E, CH = experts, chunks
        self.chunks = chunks
        self.w1 = s.sb(name + "_w1a", [D, E, CH * T])
        self.w2 = s.sb(name + "_w2a", [T, E, CH * D])
        self.b1 = s.sb(name + "_b1a", [T, E, CH])
        self.b2 = s.sb(name + "_b2a", [T, E, D])
        self.loads = s.sem(name + "_loads")
        self.count = 16 * (3 + CH)
        self.sources = w1, b1_t, w2, b2

    def load(self, nc):
        w1, b1_t, w2, b2 = self.sources
        with nc.Block() as block:
            @block.sync
            def _(sp):
                sp.dma_start(self.w1[:], w1.rearrange("e c n -> c e n")).then_inc(self.loads, 16)
                sp.dma_start(self.b1[:], b1_t).then_inc(self.loads, 16)
                for k in range(self.chunks):
                    sp.dma_start(self.w2[:, :, k * D:(k + 1) * D], w2[:, k * T:(k + 1) * T, :].rearrange("e p n -> p e n")
                                 ).then_inc(self.loads, 16)
                sp.dma_start(self.b2[:].rearrange("p e n -> p (e n)"),
                             b2.rearrange("e n -> (e n)").partition_broadcast(T)).then_inc(self.loads, 16)


def expert_tiles_block(nc, name, K, route, xn_dram, o_dram, weights):
    E, NT, CH = route.experts, route.tiles, weights.chunks
    w1a, w2a, b1a, b2a = weights.w1, weights.w2, weights.b1, weights.b2
    U = 4
    TURNS = NT // U
    assert NT % (2 * U) == 0
    with Space(nc) as s:
        who2 = s.sb(name + "_who2", [SLOTS, 2, U], i32)
        xg = s.sb(name + "_xg", [SLOTS, 2, U, D])
        xgt = s.sb(name + "_xgt", [D, U, SLOTS])
        w1b = s.sb(name + "_w1b", [D, 2, U, CH * T])
        b1b = s.sb(name + "_b1b", [T, 2, U, CH])
        b2b = s.sb(name + "_b2b", [T, 2, U, D])
        hid = s.sb(name + "_hid", [T, U, CH, SLOTS])
        ob = s.sb(name + "_ob", [SLOTS, U, D])
        p_t = [s.ps(f"{name}_p_t{u}", [T, 4, SLOTS]) for u in range(U)]
        p_h = [s.ps(f"{name}_p_h{u}", [T, 4, SLOTS]) for u in range(U)]
        stored = [s.sem(f"{name}_stored{half}") for half in range(U // 2)]
        who_ready, w_ready, t_ps, xgt_ready, h_ps, hid_ready, o_ps, ob_ready = (
            [s.sem(f"{name}_{n}{u}") for u in range(U)] for n in (
                "who_ready", "w_ready", "t_ps", "xgt_ready", "h_ps", "hid_ready", "o_ps", "ob_ready"))
        gathered = [[s.sem(f"{name}_gathered{p}_{u}") for u in range(U)] for p in range(2)]
        with nc.Block() as block:
            @block.gpsimd
            def _(g):
                for u in range(U):
                    g.sem_inc(t_ps[u], 2)
                def turn(i, p):
                    for u in range(U):
                        g.wait_ge(t_ps[u], i + 1)
                        g.tensor_copy(who2[:, p, u:u + 1], route.who[:, bass.ds(U * i + u, 1)]).then_inc(who_ready[u], 1)
                        g.wait_ge(who_ready[u], i + 1)
                        g.nop(nofuse=True)
                        g.indirect_dma_start(out=xg[:, p, u, :], out_offset=None, in_=xn_dram,
                                             in_offset=bass.IndirectOffsetOnAxis(ap=who2[:, p, u:u + 1], axis=0)
                                             ).then_inc(gathered[p][u], 16)

                turns(g, TURNS, turn)

            @block.sync
            def _(sp):
                for u in range(U):
                    sp.sem_inc(ob_ready[u], 1)
                def turn(i, p):
                    for half in range(U // 2):
                        pair = slice(2 * half, 2 * half + 2)
                        for u in (2 * half, 2 * half + 1):
                            sp.wait_ge(ob_ready[u], i + 2)
                        sp.dma_start(o_dram[bass.ds((U * i + 2 * half) * SLOTS, 2 * SLOTS), :].rearrange(
                            "(u p) c -> p u c", p=SLOTS), ob[:, pair, :]).then_inc(stored[half], 16)

                turns(sp, TURNS, turn)
                for half in range(U // 2):
                    sp.wait_ge(stored[half], 16 * TURNS + 16)

            @block.tensor
            def _(pe):
                pe.wait_ge(weights.loads, weights.count)
                def turn(i, p):
                    for u in range(U):
                        pe.wait_ge(gathered[p][u], 8 * (i - p) + 16)
                        pe.wait_ge(ob_ready[u], i + 1)
                        nc.tensor.transpose(p_t[u][:, 0], xg[:, p, u, :], K.ident[:]).then_inc(t_ps[u], 1)
                    for u in range(U):
                        pe.wait_ge(w_ready[u], i + 1)
                        pe.wait_ge(xgt_ready[u], i + 1)
                        for c in range(CH):
                            last = nc.tensor.matmul(p_h[u][:, c], w1b[:, p, u, c * T:(c + 1) * T], xgt[:, u, :],
                                                    start=True, stop=True)
                        last.then_inc(h_ps[u], 1)
                    for u in range(U):
                        e = pe.value_load(route.expert_of[0:1, bass.ds(U * i + u, 1)], min_val=0, max_val=E - 1)
                        for c in range(CH):
                            pe.wait_ge(hid_ready[u], CH * i + c + 1)
                            last = nc.tensor.matmul(p_t[u][:, 3], hid[:, u, c],
                                                    w2a[:, bass.ds(e, 1), c * D:(c + 1) * D].rearrange(
                                                        "p e n -> p (e n)"), start=c == 0, stop=c == CH - 1)
                        last.then_inc(o_ps[u], 1)

                turns(pe, TURNS, turn)

            @block.scalar
            def _(act):
                def turn(i, p):
                    for u in range(U):
                        act.wait_ge(t_ps[u], i + 3)
                        nc.scalar.activation(xgt[:, u, :], p_t[u][:, 0], ACT.Copy).then_inc(xgt_ready[u], 1)
                    for u in range(U):
                        act.wait_ge(h_ps[u], i + 1)
                        for c in range(CH):
                            nc.scalar.activation(hid[:, u, c], p_h[u][:, c], ACT.Relu,
                                                 bias=b1b[:, p, u, c:c + 1]).then_inc(hid_ready[u], 1)

                turns(act, TURNS, turn)

            @block.vector
            def _(v):
                for half in range(U // 2):
                    v.sem_inc(stored[half], 16)
                v.wait_ge(weights.loads, weights.count)
                def fetch(n, p, early):
                    for u in range(U):
                        if not early:
                            v.wait_ge(ob_ready[u], n)
                        e = v.value_load(route.expert_of[0:1, bass.ds(U * n + u, 1)], min_val=0, max_val=E - 1)
                        nc.vector.tensor_copy(b1b[:, p, u, :], b1a[:, bass.ds(e, 1), :].rearrange("p e k -> p (e k)"))
                        nc.vector.tensor_copy(b2b[:, p, u, :], b2a[:, bass.ds(e, 1), :].rearrange("p e n -> p (e n)"))
                        nc.vector.tensor_copy(w1b[:, p, u, :], w1a[:, bass.ds(e, 1), :].rearrange("p e n -> p (e n)")
                                              ).then_inc(w_ready[u], 1)

                def body(b, p, first, last):
                    if not last:
                        fetch(b + 1, 1 - p, first)
                    for u in range(U):
                        v.wait_ge(o_ps[u], b + 1)
                        v.wait_ge(stored[u // 2], 16 * b + 16)
                        nc.vector.tensor_tensor(ob[:, u, :], p_t[u][:, 3], b2b[:, p, u, :], ALU.add).then_inc(ob_ready[u], 1)

                sequences(v, body, lambda: fetch(0, 0, True), count=TURNS)


def combine_block(nc, name, K, route, o_dram, n_seq, beside=None):
    P = route.picks
    R = n_seq * P
    TURNS = B // (2 * n_seq)
    with Space(nc) as s:
        at = s.sb(name + "_at", [T, 2, R], i32)
        og = s.sb(name + "_og", [T, 2, R, D])
        at_ready = [s.sem(f"{name}_at_ready{u}") for u in range(2)]
        used = [s.sem(f"{name}_used{u}") for u in range(2)]
        got = [[s.sem(f"{name}_got{u}_{r}") for r in range(R)] for u in range(2)]
        own = s.sem(name + "_own")
        dest_c = route.dest[:].rearrange("t b k -> t (b k)")
        gate_c = route.gate[:].rearrange("t b k -> t (b k)")
        with nc.Block() as block:
            @block.gpsimd
            def _(g):
                for u in range(2):
                    g.sem_inc(used[u], 1)
                with g.Fori(0, TURNS) as i:
                    for u in range(2):
                        g.wait_ge(used[u], i + 1)
                        g.tensor_copy(at[:, u, :], dest_c[:, bass.ds((2 * i + u) * R, R)]).then_inc(at_ready[u], 1)
                        g.wait_ge(at_ready[u], i + 1)
                        g.nop(nofuse=True)
                        for r in range(R):
                            g.indirect_dma_start(out=og[:, u, r, :], out_offset=None, in_=o_dram,
                                                 in_offset=bass.IndirectOffsetOnAxis(ap=at[:, u, r:r + 1], axis=0)
                                                 ).then_inc(got[u][r], 16)

            if beside is not None:
                block.sync(beside.sync)
                block.scalar(beside.scalar)
                block.tensor(beside.tensor)

            @block.vector
            def _(v):
                if beside is not None:
                    beside.start(v)
                with v.Fori(0, TURNS) as i:
                    for u in range(2):
                        if beside is not None:
                            beside.step(v, i, u)
                        for r in range(R):
                            n = (2 * i + u) * R + r
                            k, m = r % P, r // P
                            b = (2 * i + u) * n_seq + m
                            v.wait_ge(got[u][r], 16 * i + 16)
                            if k:
                                v.wait_ge(own, n)
                            ins = nc.vector.scalar_tensor_tensor(out=K.h[:, b, :], in0=og[:, u, r, :],
                                                                 scalar=gate_c[:, bass.ds(n, 1)], in1=K.h[:, b, :],
                                                                 op0=ALU.mult, op1=ALU.add)
                            ins.then_inc(own, 1)
                        v.wait_ge(own, (2 * i + u + 1) * R)
                        v.sem_inc(used[u], 1)
                    if beside is not None:
                        beside.step(v, i, 2)


def top1_experts(nc, W, K, name, experts, chunks, soft_gate):
    NT = 8 * -(-(NTOK // SLOTS + experts - 1) // 8)
    xn_dram = nc.dram_tensor(name + "_xn_dram", (NTOK, D), f32, kind="Internal").ap()
    o_dram = nc.dram_tensor(name + "_o_dram", (NT * SLOTS, D), f32, kind="Internal").ap()
    with Space(nc) as s:
        route = Route(s, name, experts, 1, NT)
        weights = ExpertWeights(s, name, experts, chunks, W[name + "_W1"], W[name + "_b1_t"], W[name + "_W2"],
                                W[name + "_b2"])
        with Space(nc) as s2:
            xn = s2.sb(name + "_xn", [T, B, D])
            logits = s2.sb(name + "_logits", [T, B, experts])
            layer_norm_block(nc, name + "_ln", K.h, xn)
            router_logits_block(nc, name + "_r", K, xn, xn_dram, W[name + "_Wr"], experts, logits, W[name + "_br"])
            index = s2.sb(name + "_index", [T, B, 1])
            top = s2.sb(name + "_top", [T, B, 8])
            which = s2.sb(name + "_which", [T, B, 8], u32)
            low = s2.sb(name + "_low", [T, B, experts])
            total = s2.sb(name + "_total", [T, B])
            own = s2.sem(name + "_own")
            low_ready = s2.sem(name + "_low_ready")
            exp_ready = s2.sem(name + "_exp_ready")
            with nc.Block() as block:
                @block.scalar
                def _(act):
                    if soft_gate:
                        act.wait_ge(low_ready, 1)
                        nc.scalar.activation(low[:], low[:], ACT.Exp).then_inc(exp_ready, 1)

                @block.vector
                def _(v):
                    chain = Own(v, own)
                    if soft_gate:
                        chain.done(nc.vector.tensor_reduce(out=total[:], in_=logits[:], axis=AX.X, op=ALU.max))
                        nc.vector.tensor_tensor(low[:], logits[:], per_row(total[:], experts),
                                                ALU.subtract).then_inc(low_ready, 1)
                        v.wait_ge(exp_ready, 1)
                        chain.done(nc.vector.tensor_reduce(out=total[:], in_=low[:], axis=AX.X, op=ALU.add))
                        nc.vector.reciprocal(route.gate[:].rearrange("t b k -> t (b k)"), total[:])
                        values = low
                    else:
                        nc.vector.memset(route.gate[:], 1.0)
                        values = logits
                    for b in range(B):
                        ins = nc.vector.max(top[:, b, :], values[:, b, :])
                    chain.done(ins)
                    for b in range(B):
                        ins = nc.vector.max_index(which[:, b, :], top[:, b, :], values[:, b, :])
                    chain.done(ins)
                    chain.done(nc.vector.tensor_copy(index[:], which[:, :, 0:1]))
            weights.load(nc)
            sort_block(nc, name + "_sort", K, route, index)
        expert_tiles_block(nc, name + "_x", K, route, xn_dram, o_dram, weights)
        combine_block(nc, name + "_c", K, route, o_dram, 4)
    end_of_layer(nc)


def householder_attention(nc, W, K):
    NH, DH, PER = 8, 32, 4
    F = NH * DH
    CK = 32
    NC = T // CK
    PAIRS = B * NH
    diag_dram = nc.dram_tensor("a1_diag_dram", (PAIRS, T, CK), f32, kind="Internal").ap()
    inv_dram = nc.dram_tensor("a1_inv_dram", (PAIRS, T, CK), f32, kind="Internal").ap()

    def per_head(a):
        return a[:].rearrange("t b (h d) -> t (b h) d", d=DH)

    with Space(nc) as s:
        wkv = s.sb("a1_wkv", [D, 2, F])
        wq = s.sb("a1_wq", [D, F])
        ww = s.sb("a1_ww", [D, F])
        wbg = s.sb("a1_wbg", [D, 2 * NH])
        wo = s.sb("a1_wo", [T, 2, D])
        bbg = s.sb("a1_bbg", [T, 2 * NH])
        head_rows = s.sb("a1_head_rows", [T, PER, T])
        xt = s.sb("a1_xt", [D, B, T])
        kv = s.sb("a1_kv", [T, B, 2, F])
        wn = s.sb("a1_wn", [T, B, F])
        bg = s.sb("a1_bg", [T, B, 2 * NH])
        ss = s.sb("a1_ss", [T, B, NH])
        rw = s.sb("a1_rw", [T, B, NH])
        loads = s.sem("a1_loads")
        xn = s.sb("a1_xn", [T, B, D])
        layer_norm_block(nc, "a1_ln", K.h, xn)
        with Space(nc) as s2:
            xs = s2.sb("a1_xs", [T, 2, D])
            xts = s2.sb("a1_xts", [D, 2, T])
            p_t = [s2.ps(f"a1_p_t{u}", [D, 512]) for u in range(2)]
            p_kv = [s2.ps(f"a1_p_kv{u}", [T, 2, F]) for u in range(2)]
            p_w = [s2.ps(f"a1_p_w{u}", [T, 512]) for u in range(2)]
            xs_ready, t_ps, xts_ready, kv_ps, w_ps, kv_done, w_done = (s2.sem("a1_" + n) for n in (
                "xs_ready", "t_ps", "xts_ready", "kv_ps", "w_ps", "kv_done", "w_done"))
            with nc.Block() as block:
                @block.sync
                def _(sp):
                    sp.dma_start(wkv[:, 0], W["L1_attn_Wk_t"]).then_inc(loads, 16)
                    sp.dma_start(wkv[:, 1], W["L1_attn_Wv_t"]).then_inc(loads, 16)
                    sp.dma_start(wq[:], W["L1_attn_Wq_t"]).then_inc(loads, 16)
                    sp.dma_start(ww[:], W["L1_attn_Ww_t"]).then_inc(loads, 16)
                    sp.dma_start(wbg[:, 0:NH], W["L1_attn_Wbeta_t"]).then_inc(loads, 16)
                    sp.dma_start(wbg[:, NH:2 * NH], W["L1_attn_Wg_t"]).then_inc(loads, 16)
                    sp.dma_start(bbg[:, 0:NH], W["L1_attn_bbeta"].partition_broadcast(T)).then_inc(loads, 16)
                    sp.dma_start(bbg[:, NH:2 * NH], W["L1_attn_bg"].partition_broadcast(T)).then_inc(loads, 16)
                    sp.dma_start(wo[:], W["L1_attn_Wo_t"].rearrange("(g p) n -> p g n", p=T)).then_inc(loads, 16)
                    sp.dma_start(head_rows[:], W["head_rows"]).then_inc(loads, 16)
                    sp.wait_ge(loads, 160)

                @block.gpsimd
                def _(g):
                    g.sem_inc(t_ps, 2)
                    with g.Fori(0, B // 2) as i:
                        for p in range(2):
                            g.wait_ge(t_ps, 2 * i + p + 1)
                            g.tensor_copy(xs[:, p], xn[:, 2 * i + p, :]).then_inc(xs_ready, 1)

                @block.vector
                def _(v):
                    with v.Fori(0, B // 2) as i:
                        for p in range(2):
                            b = 2 * i + p
                            v.wait_ge(w_ps, b + 1)
                            nc.vector.tensor_tensor(bg[:, b, :], p_w[p][:, F:F + 2 * NH], bbg[:], ALU.add)
                            nc.vector.tensor_copy(wn[:, b, :], p_w[p][:, 0:F]).then_inc(w_done, 1)

                @block.scalar
                def _(act):
                    def transposed(n, p):
                        act.wait_ge(t_ps, n + 3)
                        nc.scalar.activation(xts[:, p], p_t[p][:, 0:T], ACT.Copy)
                        nc.scalar.activation(xt[:, n, :], p_t[p][:, 0:T], ACT.Copy).then_inc(xts_ready, 1)

                    def body(b, p, first, last):
                        if not last:
                            transposed(b + 1, 1 - p)
                        act.wait_ge(kv_ps, b + 1)
                        nc.scalar.activation(kv[:, b], p_kv[p][:], ACT.Copy).then_inc(kv_done, 1)

                    sequences(act, body, lambda: transposed(0, 0))

                @block.tensor
                def _(pe):
                    def transpose_in(n, p):
                        pe.wait_ge(xs_ready, n + 1)
                        nc.tensor.transpose(p_t[p][:, 0:T], xs[:, p], K.ident[:]).then_inc(t_ps, 1)

                    def body(b, p, first, last):
                        if not last:
                            transpose_in(b + 1, 1 - p)
                        pe.wait_ge(xts_ready, b + 1)
                        pe.wait_ge(kv_done, b + 1)
                        nc.tensor.matmul(p_kv[p][:], xts[:, p], wkv[:], start=True, stop=True).then_inc(kv_ps, 1)
                        pe.wait_ge(w_done, b + 1)
                        nc.tensor.matmul(p_w[p][:, 0:F], xts[:, p], ww[:], start=True, stop=True)
                        nc.tensor.matmul(p_w[p][:, F:F + 2 * NH], xts[:, p], wbg[:], start=True,
                                         stop=True).then_inc(w_ps, 1)

                    pe.wait_ge(loads, 160)
                    pe.sem_inc(kv_done, 2)
                    pe.sem_inc(w_done, 2)
                    sequences(pe, body, lambda: transpose_in(0, 0))
        squared = s.sem("a1_squared")
        with Space(nc) as s2:
            sq = s2.sb("a1_sq", [T, B, F])
            with nc.Block() as block:
                @block.gpsimd
                def _(g):
                    half = slice(B // 2, B)
                    g.tensor_tensor(out=sq[:, half], in0=wn[:, half], in1=wn[:, half], op=ALU.mult).then_inc(squared, 1)

                @block.vector
                def _(v):
                    half = slice(0, B // 2)
                    nc.vector.tensor_tensor(sq[:, half], wn[:, half], wn[:, half], ALU.mult).then_inc(squared, 1)
                    v.wait_ge(squared, 2)
                    nc.vector.tensor_reduce(out=ss[:].rearrange("t b h -> t (b h)"), in_=per_head(sq), axis=AX.X, op=ALU.add)
        own = s.sem("a1_own")
        norm_ready = s.sem("a1_norm_ready")
        exp_ready = s.sem("a1_exp_ready")
        with nc.Block() as block:
            @block.scalar
            def _(act):
                nc.scalar.activation(rw[:], ss[:], ACT.Sqrt).then_inc(norm_ready, 1)
                nc.scalar.activation(bg[:], bg[:], ACT.Exp, scale=-1.0).then_inc(exp_ready, 1)

            @block.vector
            def _(v):
                chain = Own(v, own)
                v.wait_ge(norm_ready, 1)
                chain.done(nc.vector.tensor_scalar(rw[:], rw[:], 1e-6, None, ALU.add))
                nc.vector.reciprocal(rw[:].rearrange("t b h -> t (b h)"), rw[:].rearrange("t b h -> t (b h)"))
                v.wait_ge(exp_ready, 1)
                chain.done(nc.vector.tensor_scalar(bg[:], bg[:], 1.0, None, ALU.add))
                chain.done(nc.vector.reciprocal(bg[:].rearrange("t b h -> t (b h)"), bg[:].rearrange("t b h -> t (b h)")))
                chain.done(nc.vector.tensor_tensor(per_head(wn), per_head(wn), rw[:].rearrange("t b h -> t (b h)").unsqueeze(2)
                                                   .to_broadcast([T, B * NH, DH]), ALU.mult))
                nc.vector.tensor_scalar(bg[:, :, 0:NH], bg[:, :, 0:NH], 2.0, None, ALU.mult)
                chain.done(nc.vector.tensor_scalar(bg[:, :, NH:2 * NH], bg[:, :, NH:2 * NH], DH ** -0.5, None, ALU.mult))

        wt = s.sb("a1_wt", [T, B, 4, T])
        diagonal_products(nc, s, K, wn, bg, wt, diag_dram)
        invert_diagonal_blocks(nc, K, diag_dram, inv_dram)
        solve_and_attend(nc, W, K, wkv, wq, wo, head_rows, xt, kv, wn, bg, wt, inv_dram)
    end_of_layer(nc)


def diagonal_products(nc, s, K, wn, bg, wt, diag_dram):
    NH, DH, PER, CK = 8, 32, 4, 32
    NC = T // CK
    with Space(nc) as s:
        ws = s.sb("a1d_ws", [T, 2, 2, NH * DH])
        wts = s.sb("a1d_wts", [T, 2, 4, T])
        neg = s.sb("a1d_neg", [T, B, NH, CK])
        p_t = [s.ps(f"a1d_p_t{u}", [T, 4, T]) for u in range(2)]
        p_d = s.ps("a1d_p_d", [T, PER, 512])
        pd = p_d[:, :, 0:2 * CK].rearrange("t j (g i) -> t j g i", g=2)
        ws_ready, bws_ready, t_ps, wts_ready, d_ps, neg_ready, kept, stored = (s.sem("a1d_" + n) for n in (
            "ws_ready", "bws_ready", "t_ps", "wts_ready", "d_ps", "neg_ready", "kept", "stored"))
        with nc.Block() as block:
            @block.gpsimd
            def _(g):
                with g.Fori(0, B // 2) as i:
                    for p in range(2):
                        n = 2 * i + p
                        g.wait_ge(t_ps, n + 1)
                        g.tensor_copy(ws[:, p, 0], wn[:, n, :]).then_inc(ws_ready, 1)

            @block.vector
            def _(v):
                def tokens(n, p):
                    v.wait_ge(t_ps, n + 1)
                    nc.vector.tensor_tensor(ws[:, p, 1].rearrange("t (h d) -> t h d", d=DH),
                                            wn[:, n, :].rearrange("t (h d) -> t h d", d=DH),
                                            bg[:, n, 0:NH].unsqueeze(2).to_broadcast([T, NH, DH]),
                                            ALU.mult).then_inc(bws_ready, 1)

                def negate(b):
                    v.wait_ge(d_ps, b + 1)
                    nc.vector.tensor_scalar(neg[:, b].rearrange("t (g j) c -> t j g c", g=2), pd, -1.0, None,
                                            ALU.mult).then_inc(neg_ready, 1)

                v.sem_inc(t_ps, 2)
                for p in range(2):
                    tokens(p, p)
                with v.Fori(0, B // 2 - 1) as i:
                    for p in range(2):
                        tokens(2 * i + p + 2, p)
                        negate(2 * i + p)
                for b in (B - 2, B - 1):
                    negate(b)

            @block.scalar
            def _(act):
                with act.Fori(0, B // 2) as i:
                    for p in range(2):
                        b = 2 * i + p
                        act.wait_ge(t_ps, b + 3)
                        act.wait_ge(neg_ready, b + 1)
                        nc.scalar.activation(wts[:, p], p_t[p][:], ACT.Copy).then_inc(wts_ready, 1)
                        nc.scalar.activation(wt[:, b], p_t[p][:], ACT.Copy).then_inc(kept, 1)

            @block.tensor
            def _(pe):
                def transposes(n, p):
                    pe.wait_ge(kept, n + 1)
                    pe.wait_ge(ws_ready, n + 1)
                    pe.wait_ge(bws_ready, n + 1)
                    for k in range(4):
                        last = nc.tensor.transpose(p_t[p][:, k], ws[:, p, k // 2, (k % 2) * T:(k % 2 + 1) * T], K.ident[:])
                    last.then_inc(t_ps, 1)

                def body(b, p, first, last):
                    if not last:
                        transposes(b + 1, 1 - p)
                    pe.wait_ge(neg_ready, b + 2)
                    pe.wait_ge(wts_ready, b + 1)
                    pe.nop(nofuse=True)
                    for c in range(NC):
                        t = slice(CK * c, CK * c + CK)
                        for g in range(2):
                            for j in range(PER):
                                r = slice(DH * j, DH * j + DH)
                                last_ = nc.tensor.matmul(pd[t, j, g], wts[r, p, 2 + g, t], wts[r, p, g, t], start=True,
                                                         stop=True)
                    last_.then_inc(d_ps, 1)

                pe.sem_inc(neg_ready, 2)
                pe.sem_inc(kept, 2)
                sequences(pe, body, lambda: transposes(0, 0))

            @block.sync
            def _(sp):
                with sp.Fori(0, B // 2) as i:
                    sp.wait_ge(neg_ready, 2 * i + 4)
                    sp.dma_start(diag_dram[bass.ds(i * 2 * NH, 2 * NH)].rearrange("p t c -> t p c"),
                                 neg[:, bass.ds(2 * i, 2)].rearrange("t u h c -> t (u h) c")).then_inc(stored, 16)
                sp.wait_ge(stored, 16 * (B // 2))


def invert_diagonal_blocks(nc, K, diag_dram, inv_dram):
    CK = 32
    NC = T // CK
    HALF = CK // 2
    with Space(nc) as s:
        low = s.sb("a1i_low", [T, NC, CK, CK])
        inv = s.sb("a1i_inv", [T, NC, CK, CK])
        terms = s.sb("a1i_terms", [T, NC, CK, CK])
        low_in, inv_made, own, stored, done = (s.sem("a1i_" + n) for n in (
            "low_in", "inv_made", "own", "stored", "done"))

        def sums(i, first, last):
            shape = [T, NC, last - first, i - first]
            return (nc.vector.tensor_tensor(out=terms[:, :, first:last, first:i], in0=inv[:, :, first:last, first:i],
                                            in1=low[:, :, i, first:i].unsqueeze(2).to_broadcast(shape), op=ALU.mult),
                    lambda: nc.vector.tensor_reduce(out=inv[:, :, first:last, i], in_=terms[:, :, first:last, first:i],
                                                    axis=AX.X, op=ALU.add))

        with nc.Block() as block:
            @block.sync
            def _(sp):
                sp.dma_start(low[:].rearrange("p n i j -> p (n i) j"), diag_dram).then_inc(low_in, 16)
                sp.wait_ge(done, 1)
                sp.dma_start(inv_dram, inv[:].rearrange("p n k i -> p (n k) i")).then_inc(stored, 16)
                sp.wait_ge(stored, 16)

            @block.gpsimd
            def _(g):
                for n in range(NC):
                    g.affine_select(out=inv[:, n], in_=K.ones[:, 0:1].unsqueeze(2).to_broadcast([T, CK, CK]),
                                    compare_op=ALU.is_equal, fill=0.0, base=0, pattern=[[1, CK], [-1, CK]],
                                    channel_multiplier=0).then_inc(inv_made, 1)

            @block.vector
            def _(v):
                v.wait_ge(inv_made, NC)
                v.wait_ge(low_in, 16)
                chain = Own(v, own)
                for i in range(1, CK):
                    parts = [sums(i, first, min(i, first + HALF)) for first in range(0, i, HALF)]
                    chain.done(parts[-1][0])
                    for _, reduced in parts:
                        last = reduced()
                    chain.done(last)
                v.sem_inc(done, 1)


def solve_and_attend(nc, W, K, wkv, wq, wo, head_rows, xt, kv, wn, bg, wt, inv_dram):
    NH, DH, PER, CK = 8, 32, 4, 32
    NC = T // CK
    ST = 2 * NC
    with Space(nc) as s:
        w_cur = s.sb("a1s_w", [T, 2, T])
        bw_bd = s.sb("a1s_bw_bd", [T, 2, PER, T])
        qkv = s.sb("a1s_qkv", [T, 2, 3, T])
        q_bd = s.sb("a1s_q_bd", [T, 2, 2, PER, T])
        lo = s.sb("a1s_lo", [T, 2, 2, PER, T])
        bm = s.sb("a1s_bm", [T, 2, 2, PER, T])
        am = s.sb("a1s_am", [T, 2, 2, PER, T])
        cm = s.sb("a1s_cm", [T, 2, PER, T])
        xs = s.sb("a1s_xs", [T, 2, NH, CK])
        k_cur = s.sb("a1s_k", [T, 2, 2, PER * DH])
        rr = s.sb("a1s_rr", [T, 2, PER * DH])
        uu = s.sb("a1s_uu", [T, 2, PER * DH])
        ut = s.sb("a1s_ut", [T, 2, T])
        at_ = s.sb("a1s_at", [T, 2, T])
        att = s.sb("a1s_att", [T, 2, T])
        p_l = s.ps("a1s_p_l", [T, PER, T])
        p_b = s.ps("a1s_p_b", [T, PER, T])
        p_a = s.ps("a1s_p_a", [T, PER, T])
        p_q = s.ps("a1s_p_q", [T, 4, T])
        p_c = [s.ps(f"a1s_p_c{g}", [T, 4, T]) for g in range(2)]
        p_o = s.ps("a1s_p_o", [T, 4, T])
        k_ready, w_ready, bw_ready, qkv_ps, qkv_ready, q_ready, l_ps, l_ready, b_ps, b_ready, a_ps, a_ready, c_ps, c_ready, \
            ch_ps, ch_done, ut_ps, ut_ready = ([s.sem(f"a1s_{n}{g}") for g in range(2)] for n in (
                "k_ready", "w_ready", "bw_ready", "qkv_ps", "qkv_ready", "q_ready", "l_ps", "l_ready", "b_ps", "b_ready", "a_ps",
                "a_ready", "c_ps", "c_ready", "ch_ps", "ch_done", "ut_ps", "ut_ready"))
        x_in = [s.sem(f"a1s_x_in{p}") for p in range(2)]
        o_ps, at_ready, att_ps, att_ready, h_ps, h_done = (s.sem("a1s_" + n) for n in (
            "o_ps", "at_ready", "att_ps", "att_ready", "h_ps", "h_done"))

        with nc.Block() as block:
            @block.sync
            def _(sp):
                def load(n, p):
                    sp.dma_start(xs[:, p], inv_dram[bass.ds(n * NH, NH)].rearrange("p t c -> t p c")).then_inc(x_in[p], 16)

                load(0, 0)
                load(1, 1)
                with sp.Fori(0, B // 2 - 1) as i:
                    for p in range(2):
                        sp.wait_ge(ch_ps[1], ST * (2 * i + p + 1))
                        load(2 * i + 2 + p, p)

            @block.gpsimd
            def _(g):
                def w_of(n, r, first):
                    if not first:
                        g.wait_ge(b_ps[r], n)
                    g.tensor_copy(w_cur[:, r], wt[:, n, r, :]).then_inc(w_ready[r], 1)
                    g.tensor_tensor(out=bw_bd[:, r], in0=wt[:, n, 2 + r, :].unsqueeze(1).to_broadcast([T, PER, T]),
                                    in1=head_rows[:], op=ALU.mult).then_inc(bw_ready[r], 1)

                def q_of(n, p, r, early):
                    g.wait_ge(qkv_ready[r], n + 1)
                    if not early:
                        g.wait_ge(c_ps[r], n - 1)
                    g.tensor_copy(k_cur[:, p, r], kv[:, n, 0, r * PER * DH:(r + 1) * PER * DH]).then_inc(k_ready[r], 1)
                    g.tensor_tensor(out=q_bd[:, p, r], in0=qkv[:, r, 0].unsqueeze(1).to_broadcast([T, PER, T]),
                                    in1=head_rows[:], op=ALU.mult).then_inc(q_ready[r], 1)

                def seq(n, p, first, early):
                    for r in range(2):
                        w_of(n, r, first)
                    for r in range(2):
                        q_of(n, p, r, early)

                seq(0, 0, True, True)
                seq(1, 1, False, True)
                with g.Fori(1, B // 2) as i:
                    for p in range(2):
                        seq(2 * i + p, p, False, False)

            @block.vector
            def _(v):
                def step(b, k):
                    c, x = divmod(k, 2)
                    t = slice(CK * c, CK * c + CK)
                    v.wait_ge(ch_ps[0], ST * b + k + 1)
                    nc.vector.tensor_copy((uu if x else rr)[t, 0], p_c[0][t, x]).then_inc(ch_done[0], 1)

                def mask(sem, n, out, product, m, ready):
                    v.wait_ge(sem, n + 1)
                    nc.vector.tensor_tensor(out, product, per_tile(m, PER), ALU.mult).then_inc(ready, 1)

                def finish(b):
                    v.wait_ge(h_ps, b + 1)
                    nc.vector.tensor_tensor(K.h[:, b, :], K.h[:, b, :], p_o[:, 0], ALU.add).then_inc(h_done, 1)

                def keys(n, p, r):
                    mask(b_ps[r], n, bm[:, p, r], p_b[:], K.before[:], b_ready[r])

                def queries(n, p, r):
                    mask(a_ps[r], n, am[:, p, r], p_a[:], K.up_to[:], a_ready[r])

                def products(n, p, first):
                    for r in range(2):
                        keys(n, p, r)
                        queries(n, p, r)

                def body(b, p, first, last):
                    n, q = b + 1, 1 - p
                    step(b, 0)
                    step(b, 1)
                    if not first:
                        finish(b - 1)
                    step(b, 2)
                    if not last:
                        keys(n, q, 0)
                    step(b, 3)
                    if not last:
                        queries(n, q, 0)
                    step(b, 4)
                    if not last:
                        keys(n, q, 1)
                    step(b, 5)
                    if not last:
                        queries(n, q, 1)
                    step(b, 6)
                    step(b, 7)
                    mask(c_ps[0], b, cm[:, 0], p_b[:], K.up_to[:], c_ready[0])
                    mask(c_ps[1], b, cm[:, 1], p_a[:], K.up_to[:], c_ready[1])
                    v.wait_ge(o_ps, b + 1)
                    nc.vector.tensor_tensor(at_[:].rearrange("t g (j d) -> t (g j) d", d=DH),
                                            p_o[:, 0:2].rearrange("t g (j d) -> t (g j) d", d=DH),
                                            bg[:, b, NH:2 * NH].unsqueeze(2).to_broadcast([T, NH, DH]),
                                            ALU.mult).then_inc(at_ready, 1)

                sequences(v, body, lambda: products(0, 0, True), finish)

            @block.scalar
            def _(act):
                def step(b, k):
                    c, x = divmod(k, 2)
                    t = slice(CK * c, CK * c + CK)
                    act.wait_ge(ch_ps[1], ST * b + k + 1)
                    nc.scalar.activation((uu if x else rr)[t, 1], p_c[1][t, x], ACT.Copy).then_inc(ch_done[1], 1)

                def project(n, r, first):
                    if not first:
                        act.wait_ge(a_ps[r], n)
                    act.wait_ge(qkv_ps[r], n + 1)
                    nc.scalar.activation(qkv[:, r], p_q[:, 0:3], ACT.Copy).then_inc(qkv_ready[r], 1)

                def low(n, p, r):
                    act.wait_ge(l_ps[r], n + 1)
                    nc.scalar.activation(lo[:, p, r, :, CK:T], p_l[:, :, CK:T], ACT.Copy, scale=-1.0).then_inc(l_ready[r], 1)

                def finish(b):
                    act.wait_ge(att_ps, b + 1)
                    nc.scalar.activation(att[:], p_o[:, 2:4], ACT.Copy).then_inc(att_ready, 1)

                def products(n, p, first):
                    for r in range(2):
                        project(n, r, first)
                    for r in range(2):
                        low(n, p, r)

                def body(b, p, first, last):
                    n, q = b + 1, 1 - p
                    step(b, 0)
                    if not first:
                        finish(b - 1)
                    if not last:
                        project(n, 0, False)
                    step(b, 1)
                    if not last:
                        project(n, 1, False)
                    step(b, 2)
                    if not last:
                        low(n, q, 0)
                    step(b, 3)
                    step(b, 4)
                    if not last:
                        low(n, q, 1)
                    step(b, 5)
                    step(b, 6)
                    step(b, 7)
                    for r in range(2):
                        act.wait_ge(ut_ps[r], b + 1)
                        nc.scalar.activation(ut[:, r], p_c[r][:, 2], ACT.Copy, scale=-1.0).then_inc(ut_ready[r], 1)

                sequences(act, body, lambda: products(0, 0, True), finish)

            @block.tensor
            def _(pe):
                def project(n, r, first):
                    if r or not first:
                        pe.wait_ge(qkv_ready[1 - r], n + r)
                    cols = slice(r * T, (r + 1) * T)
                    for k, w in enumerate((wq[:, cols], wkv[:, 0, cols], wkv[:, 1, cols])):
                        last = nc.tensor.matmul(p_q[:, k], w, xt[:, n, :], start=True, stop=True)
                    last.then_inc(qkv_ps[r], 1)

                def low(n, r, first):
                    pe.wait_ge(w_ready[r], n + 1)
                    pe.wait_ge(bw_ready[r], n + 1)
                    if r or not first:
                        pe.wait_ge(l_ready[1 - r], n + r)
                    nc.tensor.matmul(p_l[:, :, CK:T], w_cur[:, r], bw_bd[:, r, :, CK:T], start=True, stop=True).then_inc(l_ps[r], 1)

                def keys(n, r, early):
                    pe.wait_ge(qkv_ready[r], n + 1)
                    if r:
                        pe.wait_ge(b_ready[0], n + 1)
                    elif not early:
                        pe.wait_ge(c_ready[0], n - 1)
                    nc.tensor.matmul(p_b[:], qkv[:, r, 2], bw_bd[:, r], start=True, stop=True).then_inc(b_ps[r], 1)

                def queries(n, p, r, early):
                    pe.wait_ge(q_ready[r], n + 1)
                    if r:
                        pe.wait_ge(a_ready[0], n + 1)
                    elif not early:
                        pe.wait_ge(c_ready[1], n - 1)
                    nc.tensor.matmul(p_a[:], qkv[:, r, 1], q_bd[:, p, r], start=True, stop=True).then_inc(a_ps[r], 1)

                def products(n, p, first):
                    for r in range(2):
                        project(n, r, first)
                    for r in range(2):
                        low(n, r, first)
                        keys(n, r, True)
                        queries(n, p, r, True)

                def right_side(b, p, c):
                    t = slice(CK * c, CK * c + CK)
                    for r in range(2):
                        if c == 0:
                            pe.wait_ge(k_ready[r], b + 1)
                            pe.wait_ge(b_ready[r], b + 1)
                            pe.wait_ge(l_ready[r], b + 1)
                        else:
                            pe.wait_ge(ch_done[r], ST * b + 2 * c)
                        pe.nop(nofuse=True)
                        for j in range(PER):
                            out = p_c[r][t, 0, j * DH:(j + 1) * DH]
                            last = nc.tensor.matmul(out, bm[:, p, r, j, t], k_cur[:, p, r, j * DH:(j + 1) * DH],
                                                    start=j == 0, stop=c == 0 and j == PER - 1)
                            if c:
                                last = nc.tensor.matmul(out, lo[0:CK * c, p, r, j, t], uu[0:CK * c, r, j * DH:(j + 1) * DH],
                                                        start=False, stop=j == PER - 1)
                        last.then_inc(ch_ps[r], 1)

                def solve(b, p, c, loaded):
                    t = slice(CK * c, CK * c + CK)
                    for r in range(2):
                        if c == 0:
                            pe.wait_ge(x_in[p], loaded)
                        pe.wait_ge(ch_done[r], ST * b + 2 * c + 1)
                        pe.nop(nofuse=True)
                        for j in range(PER):
                            last = nc.tensor.matmul(p_c[r][t, 1, j * DH:(j + 1) * DH], xs[t, p, PER * r + j],
                                                    rr[t, r, j * DH:(j + 1) * DH], start=True, stop=True)
                        last.then_inc(ch_ps[r], 1)

                def values(b, p, r, of=range(PER)):
                    pe.wait_ge(a_ready[r], b + 1)
                    for j in of:
                        h = PER * r + j
                        nc.tensor.matmul(p_o[:, r, j * DH:(j + 1) * DH], am[:, p, r, j], kv[:, b, 1, h * DH:(h + 1) * DH],
                                         start=h == 0, stop=False)

                def transpose_out(b):
                    pe.wait_ge(at_ready, b + 1)
                    for r in range(2):
                        last = nc.tensor.transpose(p_o[:, 2 + r], at_[:, r], K.ident[:])
                    last.then_inc(att_ps, 1)

                def project_out(b):
                    pe.wait_ge(att_ready, b + 1)
                    for r in range(2):
                        last = nc.tensor.matmul(p_o[:, 0], att[:, r], wo[:, r], start=r == 0, stop=r == 1)
                    last.then_inc(h_ps, 1)

                def finish(b):
                    transpose_out(b)
                    project_out(b)

                def body(b, p, first, last):
                    n, q = b + 1, 1 - p
                    loaded = 16 * (b // 2) + 16 if isinstance(b, int) else 8 * (b - p) + 16
                    right_side(b, p, 0)
                    if not first:
                        transpose_out(b - 1)
                    if not last:
                        project(n, 0, False)
                    solve(b, p, 0, loaded)
                    if not first:
                        project_out(b - 1)
                    if not last:
                        project(n, 1, False)
                    right_side(b, p, 1)
                    if not last:
                        low(n, 0, False)
                        keys(n, 0, first)
                    solve(b, p, 1, loaded)
                    if not last:
                        queries(n, q, 0, first)
                    right_side(b, p, 2)
                    if not last:
                        low(n, 1, False)
                        keys(n, 1, first)
                    solve(b, p, 2, loaded)
                    if not last:
                        queries(n, q, 1, first)
                    right_side(b, p, 3)
                    if not first:
                        pe.wait_ge(h_done, b)
                    values(b, p, 0)
                    solve(b, p, 3, loaded)
                    values(b, p, 1, range(PER // 2))
                    for r in range(2):
                        pe.wait_ge(ch_done[r], ST * b + ST)
                        nc.tensor.transpose(p_c[r][:, 2], uu[:, r], K.ident[:]).then_inc(ut_ps[r], 1)
                    values(b, p, 1, range(PER // 2, PER))
                    for r, bank in enumerate((p_b, p_a)):
                        pe.wait_ge(ut_ready[r], b + 1)
                        if last:
                            pe.wait_ge((b_ready, a_ready)[r][1], b + 1)
                        else:
                            pe.wait_ge((b_ready, a_ready)[r][1], b + 2)
                        nc.tensor.matmul(bank[:], ut[:, r], q_bd[:, p, r], start=True, stop=True).then_inc(c_ps[r], 1)
                    for r in range(2):
                        pe.wait_ge(c_ready[r], b + 1)
                        for j in range(PER):
                            h = PER * r + j
                            last_ = nc.tensor.matmul(p_o[:, r, j * DH:(j + 1) * DH], cm[:, r, j],
                                                     wn[:, b, h * DH:(h + 1) * DH], start=False, stop=h == NH - 1)
                    last_.then_inc(o_ps, 1)

                sequences(pe, body, lambda: products(0, 0, True), finish)


def capacity_experts(nc, W, K):
    E, P = 32, 2
    CAP = math.ceil(1.25 * NTOK * P / E)
    REST = CAP - SLOTS
    assert 4 * REST == SLOTS
    NT = E + E // 4
    name = "L1_ffn"
    xn_dram = nc.dram_tensor(name + "_xn_dram", (NTOK, D), f32, kind="Internal").ap()
    o_dram = nc.dram_tensor(name + "_o_dram", (E * CAP, D), f32, kind="Internal").ap()
    with Space(nc) as s:
        route = Route(s, name, E, P, NT)
        weights = ExpertWeights(s, name, E, 1, W["L1_ffn_W1"], W["L1_ffn_b1_t"], W["L1_ffn_W2"], W["L1_ffn_b2"])
        xn = s.sb(name + "_xn", [T, B, D])
        layer_norm_block(nc, name + "_ln", K.h, xn)
        with Space(nc) as s2:
            prob = s2.sb(name + "_prob", [T, B, E])
            router_logits_block(nc, name + "_r", K, xn, xn_dram, W["L1_ffn_Wg"], E, prob)
            index = s2.sb(name + "_index", [T, B, P])
            top = s2.sb(name + "_top", [T, B, 8])
            which = s2.sb(name + "_which", [T, B, 8], u32)
            total = s2.sb(name + "_total", [T, B])
            own = s2.sem(name + "_own")
            low_ready = s2.sem(name + "_low_ready")
            exp_ready = s2.sem(name + "_exp_ready")
            with nc.Block() as block:
                @block.scalar
                def _(act):
                    act.wait_ge(low_ready, 1)
                    nc.scalar.activation(prob[:], prob[:], ACT.Exp).then_inc(exp_ready, 1)

                @block.vector
                def _(v):
                    chain = Own(v, own)
                    chain.done(nc.vector.tensor_reduce(out=total[:], in_=prob[:], axis=AX.X, op=ALU.max))
                    nc.vector.tensor_tensor(prob[:], prob[:], per_row(total[:], E), ALU.subtract).then_inc(low_ready, 1)
                    v.wait_ge(exp_ready, 1)
                    chain.done(nc.vector.tensor_reduce(out=total[:], in_=prob[:], axis=AX.X, op=ALU.add))
                    chain.done(nc.vector.reciprocal(total[:], total[:]))
                    chain.done(nc.vector.tensor_tensor(prob[:], prob[:], per_row(total[:], E), ALU.mult))
                    for b in range(B):
                        ins = nc.vector.max(top[:, b, :], prob[:, b, :])
                    chain.done(ins)
                    for b in range(B):
                        ins = nc.vector.max_index(which[:, b, :], top[:, b, :], prob[:, b, :])
                    chain.done(ins)
                    nc.vector.tensor_copy(index[:], which[:, :, 0:P])
                    chain.done(nc.vector.tensor_tensor(total[:], top[:, :, 0], top[:, :, 1], ALU.add))
                    chain.done(nc.vector.tensor_scalar(total[:], total[:], 1e-9, None, ALU.max))
                    chain.done(nc.vector.reciprocal(total[:], total[:]))
                    chain.done(nc.vector.tensor_tensor(route.gate[:], top[:, :, 0:P], per_row(total[:], P), ALU.mult))
            weights.load(nc)
            sort_block(nc, name + "_sort", K, route, index, capacity=CAP)
        capacity_tiles_block(nc, name + "_x", K, route, xn_dram, o_dram, weights, REST)
        contrib = s.sb(name + "_contrib", [T, B])
        lost = s.sb(name + "_lost", [T, B])
        held = s.sb(name + "_held", [T, B])
        own = s.sem(name + "_own2")
        with nc.Block() as block:
            @block.vector
            def _(v):
                chain = Own(v, own)
                chain.done(nc.vector.tensor_tensor(contrib[:], route.gate[:, :, 0], route.gate[:, :, 1], ALU.add))
                nc.vector.tensor_scalar(lost[:], contrib[:], 1e-12, None, ALU.is_le)
                chain.done(nc.vector.tensor_scalar(held[:], contrib[:], 1e-12, None, ALU.is_gt))
                chain.done(nc.vector.tensor_tensor(route.gate[:], route.gate[:], per_row(held[:], P), ALU.mult))
                chain.done(nc.vector.tensor_tensor(xn[:], xn[:], per_row(lost[:], D), ALU.mult))
                chain.done(nc.vector.tensor_tensor(K.h[:], K.h[:], xn[:], ALU.add))
        combine_block(nc, name + "_c", K, route, o_dram, 2)
    end_of_layer(nc)


def capacity_tiles_block(nc, name, K, route, xn_dram, o_dram, weights, rest):
    E = route.experts
    w1a, w2a, b1a, b2a = weights.w1, weights.w2, weights.b1, weights.b2
    CAP = SLOTS + rest
    U = 4
    TURNS = E // U
    with Space(nc) as s:
        who2 = s.sb(name + "_who2", [SLOTS, 2, U + 1], i32)
        xg = s.sb(name + "_xg", [SLOTS, 2, U + 1, D])
        xgt = s.sb(name + "_xgt", [D, U, CAP])
        w1b = s.sb(name + "_w1b", [D, 2, U, T])
        hid = s.sb(name + "_hid", [T, U, CAP])
        ob = s.sb(name + "_ob", [SLOTS, U, 2, D])
        p_t = [s.ps(f"{name}_p_t{u}", [D, 512]) for u in range(U)]
        p_o = [s.ps(f"{name}_p_o{u}", [SLOTS, 4, D]) for u in range(U)]
        who_ready, w_ready, t_ps, xgt_ready, h_ps, hid_ready, o_ps, ob_ready, stored = (
            [s.sem(f"{name}_{n}{u}") for u in range(U)] for n in (
                "who_ready", "w_ready", "t_ps", "xgt_ready", "h_ps", "hid_ready", "o_ps",
                "ob_ready", "stored"))
        gathered = [[s.sem(f"{name}_gathered{p}_{u}") for u in range(U + 1)] for p in range(2)]
        rest_who_ready, rest_ready = (s.sem(name + "_" + n) for n in ("rest_who_ready", "rest_ready"))
        with nc.Block() as block:
            @block.gpsimd
            def _(g):
                for u in range(U):
                    g.sem_inc(t_ps[u], 2)
                def turn(i, p):
                    def gather(u, tile, which):
                        g.tensor_copy(who2[:, p, u:u + 1], route.who[:, bass.ds(tile, 1)]).then_inc(which, 1)
                        g.wait_ge(which, i + 1)
                        g.nop(nofuse=True)
                        g.indirect_dma_start(out=xg[:, p, u, :], out_offset=None, in_=xn_dram,
                                             in_offset=bass.IndirectOffsetOnAxis(ap=who2[:, p, u:u + 1], axis=0)
                                             ).then_inc(gathered[p][u], 16)

                    for u in range(U):
                        g.wait_ge(t_ps[u], i + 1)
                        if u == 0:
                            gather(U, E + i, rest_who_ready)
                        gather(u, U * i + u, who_ready[u])

                turns(g, TURNS, turn)

            @block.sync
            def _(sp):
                def turn(i, p):
                    for u in range(U):
                        row = (U * i + u) * CAP
                        sp.wait_ge(ob_ready[u], i + 2)
                        sp.dma_start(o_dram[bass.ds(row, SLOTS), :], ob[:, u, 0, :]).then_inc(stored[u], 16)
                        sp.dma_start(o_dram[bass.ds(row + SLOTS, rest), :], ob[0:rest, u, 1, :]).then_inc(stored[u], 16)

                turns(sp, TURNS, turn)
                for u in range(U):
                    sp.wait_ge(stored[u], 32 * TURNS + 32)

            @block.tensor
            def _(pe):
                for u in range(U):
                    pe.sem_inc(ob_ready[u], 1)
                pe.wait_ge(weights.loads, weights.count)
                def turn(i, p):
                    pe.wait_ge(gathered[p][U], 8 * (i - p) + 16)
                    nc.tensor.transpose(p_t[0][:, SLOTS:2 * SLOTS], xg[:, p, U, :], K.ident[:])
                    for u in range(U):
                        pe.wait_ge(gathered[p][u], 8 * (i - p) + 16)
                        nc.tensor.transpose(p_t[u][:, 0:SLOTS], xg[:, p, u, :], K.ident[:]).then_inc(t_ps[u], 1)
                    for u in range(U):
                        pe.wait_ge(w_ready[u], i + 1)
                        pe.wait_ge(xgt_ready[u], i + 1)
                        pe.wait_ge(rest_ready, i + 1)
                        nc.tensor.matmul(p_t[u][:, 256:256 + CAP], w1b[:, p, u, :], xgt[:, u, :], start=True,
                                         stop=True).then_inc(h_ps[u], 1)
                    for u in range(U):
                        pe.wait_ge(hid_ready[u], i + 1)
                        pe.wait_ge(ob_ready[u], i + 1)
                        w2 = w2a[:, bass.ds(U * i + u, 1), :].rearrange("p e n -> p (e n)")
                        nc.tensor.matmul(p_o[u][0:SLOTS, 0], hid[:, u, 0:SLOTS], w2, start=True, stop=True)
                        nc.tensor.matmul(p_o[u][0:rest, 1], hid[:, u, SLOTS:CAP], w2, start=True,
                                         stop=True).then_inc(o_ps[u], 1)

                turns(pe, TURNS, turn)

            @block.scalar
            def _(act):
                act.wait_ge(weights.loads, weights.count)
                def turn(i, p):
                    for u in range(U):
                        act.wait_ge(t_ps[u], i + 3)
                        nc.scalar.activation(xgt[:, u, 0:SLOTS], p_t[u][:, 0:SLOTS], ACT.Copy).then_inc(xgt_ready[u], 1)
                        if u == 0:
                            nc.scalar.activation(xgt[:, :, SLOTS:CAP], p_t[0][:, SLOTS:2 * SLOTS].rearrange(
                                "c (u r) -> c u r", u=U), ACT.Copy).then_inc(rest_ready, 1)
                    for u in range(U):
                        act.wait_ge(h_ps[u], i + 1)
                        nc.scalar.activation(hid[:, u, :], p_t[u][:, 256:256 + CAP], ACT.Relu,
                                             bias=b1a[:, bass.ds(U * i + u, 1), 0]).then_inc(hid_ready[u], 1)

                turns(act, TURNS, turn)

            @block.vector
            def _(v):
                for u in range(U):
                    v.sem_inc(stored[u], 32)
                v.wait_ge(weights.loads, weights.count)
                def fetch(n, p):
                    for u in range(U):
                        nc.vector.tensor_copy(w1b[:, p, u, :], w1a[:, bass.ds(U * n + u, 1), :].rearrange("p e n -> p (e n)")
                                              ).then_inc(w_ready[u], 1)

                def body(b, p, first, last):
                    if not last:
                        fetch(b + 1, 1 - p)
                    for u in range(U):
                        v.wait_ge(o_ps[u], b + 1)
                        v.wait_ge(stored[u], 32 * b + 32)
                        b2 = b2a[:, bass.ds(U * b + u, 1), :].rearrange("p e n -> p (e n)")
                        nc.vector.tensor_tensor(ob[:, u, 0, :], p_o[u][:, 0], b2, ALU.add)
                        nc.vector.tensor_tensor(ob[0:rest, u, 1, :], p_o[u][0:rest, 1], b2a[0:rest, bass.ds(U * b + u, 1), :]
                                                .rearrange("p e n -> p (e n)"), ALU.add).then_inc(ob_ready[u], 1)

                sequences(v, body, lambda: fetch(0, 0), count=TURNS)


def layer2_attention(nc, W, K):
    NH = 8
    with Space(nc) as s:
        xn = s.sb("a2_xn", [T, B, D])
        layer_norm_block(nc, "a2_ln", K.h, xn)
        wv = s.sb("a2_wv", [D, NH, D])
        bv = s.sb("a2_bv", [D, NH])
        fc = s.sb("a2_fc", [D, NH, D])
        fb = s.sb("a2_fb", [T, D])
        lg = s.sb("a2_lg", [T, D])
        lb = s.sb("a2_lb", [T, D])
        xs = s.sb("a2_xs", [D, B])
        vs = s.sb("a2_vs", [D, NH, B])
        at_ = s.sb("a2_at", [B, D])
        pick = s.sb("a2_pick", [B, B, T])
        y = s.sb("a2_y", [T, B, D])
        p_x = s.ps("a2_p_x", [T, 512])
        p_v = s.ps("a2_p_v", [T, 512])
        p_o = s.ps("a2_p_o", [T, 512])
        p_y = [s.ps(f"a2_p_y{n}", [T, 4, D]) for n in range(4)]
        loads, x_ps, xs_ready, v_ps, vs_ready, o_ps, at_ready, y_ps, pick_ready, base_ready, own = (
            s.sem("a2_" + n) for n in ("loads", "x_ps", "xs_ready", "v_ps", "vs_ready", "o_ps", "at_ready", "y_ps",
                                       "pick_ready", "base_ready", "own"))
        vals = p_v[:, 0:NH * B].rearrange("d (h b) -> d h b", h=NH)
        with nc.Block() as block:
            @block.sync
            def _(sp):
                sp.dma_start(wv[:].rearrange("c h d -> c (h d)"), W["L2_attn_wv"]).then_inc(loads, 16)
                sp.dma_start(fc[:], W["L2_attn_fc_w"].rearrange("(h d) n -> d h n", h=NH)).then_inc(loads, 16)
                sp.dma_start(bv[:], W["L2_attn_bv_t"]).then_inc(loads, 16)
                sp.dma_start(fb[:], W["L2_attn_fc_b"].partition_broadcast(T)).then_inc(loads, 16)
                sp.dma_start(lg[:], W["L2_attn_ln_g"].partition_broadcast(T)).then_inc(loads, 16)
                sp.dma_start(lb[:], W["L2_attn_ln_b"].partition_broadcast(T)).then_inc(loads, 16)

            @block.gpsimd
            def _(g):
                g.wait_ge(loads, 96)
                g.tensor_tensor(out=y[:], in0=xn[:], in1=per_tile(fb[:], B), op=ALU.add).then_inc(base_ready, 1)

            @block.vector
            def _(v):
                chain = Own(v, own)
                nc.vector.tensor_copy(pick[:], K.ident[0:B, 0:B].unsqueeze(2).to_broadcast([B, B, T])
                                      ).then_inc(pick_ready, 1)
                v.wait_ge(x_ps, 1)
                nc.vector.tensor_copy(xs[:], p_x[:, 0:B]).then_inc(xs_ready, 1)
                v.wait_ge(loads, 96)
                chain.done(nc.vector.tensor_scalar(bv[:], bv[:], float(T), None, ALU.mult))
                v.wait_ge(v_ps, 1)
                nc.vector.tensor_tensor(vs[:], vals, per_row(bv[:], B), ALU.add).then_inc(vs_ready, 1)
                v.wait_ge(o_ps, 1)
                nc.vector.tensor_copy(at_[:], p_o[0:B, 0:D]).then_inc(at_ready, 1)
                v.wait_ge(base_ready, 1)
                v.wait_ge(y_ps, 1)
                for n in range(4):
                    ins = nc.vector.tensor_tensor(y[:, 4 * n:4 * n + 4], y[:, 4 * n:4 * n + 4], p_y[n][:], ALU.add)
                chain.done(ins)

            @block.tensor
            def _(pe):
                for b in range(B):
                    last = nc.tensor.matmul(p_x[:, b:b + 1], xn[:, b], K.ones[:, 0:1], start=True, stop=True)
                last.then_inc(x_ps, 1)
                pe.wait_ge(loads, 96)
                pe.wait_ge(xs_ready, 1)
                for h in range(NH):
                    last = nc.tensor.matmul(vals[:, h], wv[:, h], xs[:], start=True, stop=True)
                last.then_inc(v_ps, 1)
                pe.wait_ge(vs_ready, 1)
                for h in range(NH):
                    last = nc.tensor.matmul(p_o[0:B, 0:D], vs[:, h], fc[:, h], start=h == 0, stop=h == NH - 1)
                last.then_inc(o_ps, 1)
                pe.wait_ge(at_ready, 1)
                pe.wait_ge(pick_ready, 1)
                for b in range(B):
                    last = nc.tensor.matmul(p_y[b // 4][:, b % 4], pick[:, b], at_[:], start=True, stop=True)
                last.then_inc(y_ps, 1)
        layer_norm_block(nc, "a2_ln2", y, y, lg, lb)
        own2 = s.sem("a2_own2")
        with nc.Block() as block:
            @block.vector
            def _(v):
                nc.vector.tensor_tensor(K.h[:], K.h[:], y[:], ALU.add).then_inc(own2, 1)
                v.wait_ge(own2, 1)
    end_of_layer(nc)


def rope_attention(nc, W, K):
    NH, DH = 16, 8
    PAIRS = B // 2
    with Space(nc) as s:
        xn = s.sb("a3_xn", [T, B, D])
        layer_norm_block(nc, "a3_ln", K.h, xn)
        wqk = s.sb("a3_wqk", [D, 2 * D])
        bqk = s.sb("a3_bqk", [T, 2 * D])
        taps = s.sb("a3_taps", [D, 3])
        lb = s.sb("a3_lb", [T, D])
        cosn = s.sb("a3_cos", [T, D])
        sinn = s.sb("a3_sin", [T, D])
        hmask = s.sb("a3_hmask", [D, D])
        hcol = s.sb("a3_hcol", [D, NH])
        diag = s.sb("a3_diag", [D, 3, D])
        xs = s.sb("a3_xs", [T, 2, 2, D])
        xp = s.sb("a3_xp", [D, 2, 2, T + 2])
        xb = s.sb("a3_xb", [T, 2, 2, D])
        neg = s.sb("a3_neg", [T, 2, 2, D])
        qk = s.sb("a3_qk", [T, 2, 2, 2, D])
        ro = s.sb("a3_ro", [T, 2, 2, 2, D])
        sw = s.sb("a3_sw", [T, 2, 2, D])
        qt = s.sb("a3_qt", [D, 4, T])
        kvm = s.sb("a3_kvm", [D, 2, D])
        km = s.sb("a3_km", [D, 2, NH])
        z = s.sb("a3_z", [T, 2, NH])
        at_ = s.sb("a3_at", [T, 2, D])
        p_x = s.ps("a3_p_x", [D, 4, T])
        p_t = s.ps("a3_p_t", [D, 4, T])
        p_q = s.ps("a3_p_q", [T, 2, 2, D])
        p_kv = s.ps("a3_p_kv", [D, 2, D])
        p_km = s.ps("a3_p_km", [D, 512])
        p_o = s.ps("a3_p_o", [T, 2, D])
        p_z = s.ps("a3_p_z", [T, 512])
        p_l = s.ps("a3_p_l", [T, 2, D])
        zz = p_z[:, 0:2 * NH].rearrange("t (u h) -> t u h", u=2)
        loads, diag_ready, pads, xs_ready, xt_ps, xp_ready, qk_ps, neg_ready, exp_ready, qk_ready, ro_ready, kv_ps, \
            kvm_ready, qt_ps, qt_ready, o_ps, done, own_a, own_b, base_ready = (s.sem("a3_" + n) for n in (
                "loads", "diag_ready", "pads", "xs_ready", "xt_ps", "xp_ready", "qk_ps", "neg_ready", "exp_ready",
                "qk_ready", "ro_ready", "kv_ps", "kvm_ready", "qt_ps", "qt_ready", "o_ps", "done", "own_a",
                "own_b", "base_ready"))

        def flat(a):
            return a.rearrange("t u n d -> t (u n d)")

        def pairs(a):
            return a.rearrange("t u n (i two) -> t (u n) i two", two=2)

        with nc.Block() as block:
            @block.sync
            def _(sp):
                for to, source in ((wqk[:], W["L3_attn_Wqk"]), (bqk[:], W["L3_attn_bqk"].partition_broadcast(T)),
                                   (taps[:], W["L3_attn_lepe_w"].rearrange("c a k -> c (a k)")),
                                   (lb[:], W["L3_attn_lepe_b"].partition_broadcast(T)),
                                   (cosn[:], W["rope_cos"]), (sinn[:], W["rope_sin"]),
                                   (hmask[:], W["head_mask"]), (hcol[:], W["head_columns"])):
                    sp.dma_start(to, source).then_inc(loads, 16)

            @block.gpsimd
            def _(g):
                def tokens(n, p, early):
                    if not early:
                        g.wait_ge(kv_ps, n - 1)
                    g.tensor_copy(xs[:, p], xn[:, bass.ds(2 * n, 2), :]).then_inc(xs_ready, 1)

                g.memset(xp[:], 0.0).then_inc(pads, 1)
                tokens(0, 0, True)
                tokens(1, 1, True)
                g.wait_ge(loads, 128)
                g.tensor_tensor(out=K.h[:], in0=K.h[:], in1=per_tile(lb[:], B), op=ALU.add).then_inc(base_ready, 1)
                with g.Fori(1, PAIRS // 2) as i:
                    for p in range(2):
                        tokens(2 * i + p, p, False)

            @block.vector
            def _(v):
                sin2 = sinn[:].rearrange("t (i two) -> t i two", two=2)

                def biased(n):
                    v.wait_ge(qk_ps, n + 1)
                    chain = Own(v, own_a, 3 * n)
                    chain.done(nc.vector.tensor_tensor(xb[:].rearrange("t u n d -> t u (n d)"),
                                                       p_q[:].rearrange("t u n d -> t u (n d)"), per_tile(bqk[:], 2),
                                                       ALU.add))
                    nc.vector.tensor_scalar(neg[:], xb[:], 0.0, None, ALU.min).then_inc(neg_ready, 1)

                def rotated(n, p):
                    chain = Own(v, own_a, 3 * n + 1)
                    v.wait_ge(exp_ready, n + 1)
                    nc.vector.scalar_tensor_tensor(out=flat(qk[:, p]), in0=flat(xb[:]), scalar=0.0, in1=flat(neg[:]),
                                                   op0=ALU.max, op1=ALU.add).then_inc(qk_ready, 1)
                    v.wait_ge(qk_ready, n + 1)
                    nc.vector.tensor_tensor(ro[:, p].rearrange("t u n d -> t (u n) d"),
                                            qk[:, p].rearrange("t u n d -> t (u n) d"), per_tile(cosn[:], 4), ALU.mult)
                    nc.vector.tensor_tensor(pairs(sw[:])[:, :, :, 0], pairs(qk[:, p])[:, :, :, 1], per_tile(sin2[:, :, 0], 4),
                                            ALU.mult)
                    chain.done(nc.vector.tensor_tensor(pairs(sw[:])[:, :, :, 1], pairs(qk[:, p])[:, :, :, 0],
                                                       per_tile(sin2[:, :, 1], 4), ALU.mult))
                    chain.done(nc.vector.tensor_tensor(ro[:, p], ro[:, p], sw[:], ALU.add))
                    v.sem_inc(ro_ready, 1)

                def ahead():
                    biased(0)
                    rotated(0, 0)

                def body(b, p, first, last):
                    v.wait_ge(kv_ps, b + 1)
                    nc.vector.scalar_tensor_tensor(out=kvm[:], in0=p_kv[:], scalar=1.0 / T, in1=per_tile(hmask[:], 2),
                                                   op0=ALU.mult, op1=ALU.mult)
                    for u in range(2):
                        ins = nc.vector.tensor_scalar(km[:, u], hcol[:], p_km[:, u:u + 1], 1.0 / T, ALU.mult, ALU.mult)
                    ins.then_inc(kvm_ready, 1)
                    if not last:
                        biased(b + 1)
                    chain = Own(v, own_b, 4 * b)
                    v.wait_ge(o_ps, b + 1)
                    chain.done(nc.vector.tensor_scalar(z[:], zz, 1e-6, None, ALU.add))
                    chain.done(nc.vector.reciprocal(z[:].rearrange("t u h -> t (u h)"), z[:].rearrange("t u h -> t (u h)")))
                    chain.done(nc.vector.tensor_tensor(at_[:].rearrange("t u (h d) -> t (u h) d", d=DH),
                                                       p_o[:].rearrange("t u (h d) -> t (u h) d", d=DH),
                                                       z[:].rearrange("t u h -> t (u h)").unsqueeze(2)
                                                       .to_broadcast([T, 2 * NH, DH]), ALU.mult))
                    chain.done(nc.vector.tensor_tensor(at_[:], at_[:], p_l[:], ALU.add))
                    nc.vector.tensor_tensor(K.h[:, bass.ds(2 * b, 2), :], K.h[:, bass.ds(2 * b, 2), :], at_[:],
                                            ALU.add).then_inc(done, 1)
                    if not last:
                        rotated(b + 1, 1 - p)

                v.wait_ge(loads, 128)
                for k in range(3):
                    ins = nc.vector.tensor_scalar(diag[:, k], K.ident[:], taps[:, k:k + 1], None, ALU.mult)
                ins.then_inc(diag_ready, 1)
                v.wait_ge(base_ready, 1)
                sequences(v, body, ahead, count=PAIRS)

            @block.scalar
            def _(act):
                def transposed(n, p):
                    act.wait_ge(xt_ps, n + 1)
                    nc.scalar.activation(xp[:, p, :, 1:T + 1], p_x[:, 0:2], ACT.Copy).then_inc(xp_ready, 1)

                def exponential(n):
                    act.wait_ge(neg_ready, n + 1)
                    nc.scalar.activation(neg[:], neg[:], ACT.Exp).then_inc(exp_ready, 1)

                def ahead():
                    transposed(0, 0)
                    exponential(0)

                def body(b, p, first, last):
                    if not last:
                        transposed(b + 1, 1 - p)
                    act.wait_ge(qt_ps, b + 1)
                    nc.scalar.activation(qt[:], p_t[:], ACT.Copy).then_inc(qt_ready, 1)
                    if not last:
                        exponential(b + 1)

                act.wait_ge(pads, 1)
                sequences(act, body, ahead, count=PAIRS)

            @block.tensor
            def _(pe):
                def transpose_in(n, p):
                    pe.wait_ge(xs_ready, n + 1)
                    for u in range(2):
                        last = nc.tensor.transpose(p_x[:, u], xs[:, p, u], K.ident[:])
                    last.then_inc(xt_ps, 1)

                def project(n, p):
                    pe.wait_ge(xp_ready, n + 1)
                    for u in range(2):
                        last = nc.tensor.matmul(p_q[:, u].rearrange("t n d -> t (n d)"), xp[:, p, u, 1:T + 1], wqk[:],
                                                start=True, stop=True)
                    last.then_inc(qk_ps, 1)

                def ahead():
                    transpose_in(0, 0)
                    project(0, 0)

                def body(b, p, first, last):
                    if not last:
                        transpose_in(b + 1, 1 - p)
                    pe.wait_ge(qk_ready, b + 1)
                    for u in range(2):
                        nc.tensor.matmul(p_km[:, u:u + 1], qk[:, p, u, 1], K.ones[:, 0:1], start=True, stop=True)
                    pe.wait_ge(ro_ready, b + 1)
                    for u in range(2):
                        last_ = nc.tensor.matmul(p_kv[:, u], ro[:, p, u, 1], xs[:, p, u], start=True, stop=True)
                    last_.then_inc(kv_ps, 1)
                    for u in range(2):
                        nc.tensor.transpose(p_t[:, 2 * u], qk[:, p, u, 0], K.ident[:])
                        last_ = nc.tensor.transpose(p_t[:, 2 * u + 1], ro[:, p, u, 0], K.ident[:])
                    last_.then_inc(qt_ps, 1)
                    if not last:
                        project(b + 1, 1 - p)
                    pe.wait_ge(done, b + 1)
                    for u in range(2):
                        for k in range(3):
                            nc.tensor.matmul(p_l[:, u], xp[:, p, u, k:k + T], diag[:, k], start=k == 0, stop=k == 2)
                    pe.wait_ge(qt_ready, b + 1)
                    pe.wait_ge(kvm_ready, b + 1)
                    for u in range(2):
                        nc.tensor.matmul(p_o[:, u], qt[:, 2 * u + 1], kvm[:, u], start=True, stop=True)
                        last_ = nc.tensor.matmul(zz[:, u], qt[:, 2 * u], km[:, u], start=True, stop=True)
                    last_.then_inc(o_ps, 1)

                pe.sem_inc(done, 1)
                pe.wait_ge(loads, 128)
                pe.wait_ge(diag_ready, 1)
                sequences(pe, body, ahead, count=PAIRS)
    end_of_layer(nc)




class SharedExpert:

    TURNS = B // 2

    def __init__(self, nc, s, name, W, K, xn):
        self.nc, self.W, self.K, self.xn = nc, W, K, xn
        self.wgu = s.sb(name + "_wgu", [D, 2, D])
        self.wd = s.sb(name + "_wd", [D, D])
        self.xs = s.sb(name + "_xs", [T, 2, D])
        self.xt = s.sb(name + "_xt", [D, 2, T])
        self.sg = s.sb(name + "_sg", [D, 2, T])
        self.hid = s.sb(name + "_hid", [D, 2, T])
        self.p_t = s.ps(name + "_p_t", [D, 4, T])
        self.p_gu = s.ps(name + "_p_gu", [D, 2, 2, T])
        self.p_y = s.ps(name + "_p_y", [T, 4, D])
        self.loads, self.xs_ready, self.xt_ps, self.xt_ready, self.gu_ps, self.sg_ready, self.hid_ready, self.y_ps, \
            self.done = (s.sem(name + "_" + n) for n in ("loads", "xs_ready", "xt_ps", "xt_ready", "gu_ps", "sg_ready",
                                                         "hid_ready", "y_ps", "done"))

    def sync(self, sp):
        sp.dma_start(self.wgu[:, 0], self.W["L3_ffn_sWg"]).then_inc(self.loads, 16)
        sp.dma_start(self.wgu[:, 1], self.W["L3_ffn_sWu"]).then_inc(self.loads, 16)
        sp.dma_start(self.wd[:], self.W["L3_ffn_sWd"]).then_inc(self.loads, 16)

    def start(self, v):
        v.sem_inc(self.done, 1)

    def step(self, v, i, k):
        nc, h = self.nc, self.K.h
        if k == 0:
            v.wait_ge(self.done, i + 1)
            nc.vector.tensor_copy(self.xs[:], self.xn[:, bass.ds(2 * i, 2), :]).then_inc(self.xs_ready, 1)
        elif k == 1:
            v.wait_ge(self.sg_ready, i + 1)
            nc.vector.tensor_tensor(self.hid[:], self.sg[:], self.p_gu[:, 1], ALU.mult).then_inc(self.hid_ready, 1)
        else:
            v.wait_ge(self.y_ps, i + 1)
            nc.vector.tensor_tensor(h[:, bass.ds(2 * i, 2), :], h[:, bass.ds(2 * i, 2), :], self.p_y[:, 0:2],
                                    ALU.add).then_inc(self.done, 1)

    def scalar(self, act):
        nc = self.nc
        with act.Fori(0, self.TURNS) as i:
            act.wait_ge(self.xt_ps, i + 1)
            nc.scalar.activation(self.xt[:], self.p_t[:, 0:2], ACT.Copy).then_inc(self.xt_ready, 1)
            act.wait_ge(self.gu_ps, i + 1)
            nc.scalar.activation(self.sg[:], self.p_gu[:, 0], ACT.Silu).then_inc(self.sg_ready, 1)

    def tensor(self, pe):
        nc = self.nc
        pe.wait_ge(self.loads, 48)
        with pe.Fori(0, self.TURNS) as i:
            pe.wait_ge(self.xs_ready, i + 1)
            for n in range(2):
                last = nc.tensor.transpose(self.p_t[:, n], self.xs[:, n], self.K.ident[:])
            last.then_inc(self.xt_ps, 1)
            pe.wait_ge(self.xt_ready, i + 1)
            for n in range(2):
                last = nc.tensor.matmul(self.p_gu[:, n], self.wgu[:, n], self.xt[:], start=True, stop=True)
            last.then_inc(self.gu_ps, 1)
            pe.wait_ge(self.hid_ready, i + 1)
            for n in range(2):
                last = nc.tensor.matmul(self.p_y[:, n], self.hid[:, n], self.wd[:], start=True, stop=True)
            last.then_inc(self.y_ps, 1)


def grouped_router_block(nc, name, W, K, xn, xn_dram, route, index, scores):
    E, P, G, KEEP = route.experts, route.picks, 8, 4
    PER = E // G
    BIG = 1e30
    with Space(nc) as s:
        corr = s.sb(name + "_corr", [T, E])
        biased = s.sb(name + "_biased", [T, B, E])
        best = s.sb(name + "_best", [T, B, G])
        top = s.sb(name + "_top", [T, B, 8])
        which = s.sb(name + "_which", [T, B, 8], u32)
        which_f = s.sb(name + "_which_f", [T, B, 8])
        iota_g = s.sb(name + "_iota_g", [T, G])
        hot = s.sb(name + "_hot", [T, B, G])
        gmask = s.sb(name + "_gmask", [T, B, G])
        corr_in, iota_ready, exp_ready, own = (s.sem(name + "_" + n) for n in ("corr_in", "iota_ready", "exp_ready", "own"))
        router_logits_block(nc, name + "_r", K, xn, xn_dram, W["L3_ffn_router_w_t"], E, scores)
        with nc.Block() as block:
            @block.sync
            def _(sp):
                sp.dma_start(corr[:], W["L3_ffn_bias_corr"].partition_broadcast(T)).then_inc(corr_in, 16)

            @block.gpsimd
            def _(g):
                g.iota(iota_g[:], pattern=[[1, G]], base=0, channel_multiplier=0,
                       allow_small_or_imprecise_dtypes=True).then_inc(iota_ready, 1)

            @block.scalar
            def _(act):
                nc.scalar.activation(scores[:], scores[:], ACT.Exp, scale=-1.0).then_inc(exp_ready, 1)

            @block.vector
            def _(v):
                chain = Own(v, own)
                v.wait_ge(exp_ready, 1)
                chain.done(nc.vector.tensor_scalar(scores[:], scores[:], 1.0, None, ALU.add))
                flat = scores[:].rearrange("t b e -> t (b e)")
                chain.done(nc.vector.reciprocal(flat, flat))
                v.wait_ge(corr_in, 16)
                chain.done(nc.vector.tensor_tensor(biased[:], scores[:], per_tile(corr[:], B), ALU.add))
                groups = biased[:].rearrange("t b (g e) -> t (b g) e", e=PER)
                chain.done(nc.vector.tensor_reduce(out=best[:].rearrange("t b g -> t (b g)"), in_=groups, axis=AX.X,
                                                   op=ALU.max))
                for b in range(B):
                    ins = nc.vector.max(top[:, b, :], best[:, b, :])
                chain.done(ins)
                for b in range(B):
                    ins = nc.vector.max_index(which[:, b, :], top[:, b, :], best[:, b, :])
                chain.done(ins)
                chain.done(nc.vector.tensor_copy(which_f[:], which[:]))
                v.wait_ge(iota_ready, 1)
                for k in range(KEEP):
                    chain.done(nc.vector.tensor_tensor(gmask[:] if k == 0 else hot[:], per_tile(iota_g[:], B),
                                                       per_row(which_f[:, :, k], G), ALU.is_equal))
                    if k:
                        chain.done(nc.vector.tensor_tensor(gmask[:], gmask[:], hot[:], ALU.add))
                chain.done(nc.vector.tensor_tensor(groups, groups, gmask[:].rearrange("t b g -> t (b g)").unsqueeze(2)
                                                   .to_broadcast([T, B * G, PER]), ALU.mult))
                chain.done(nc.vector.tensor_scalar(gmask[:], gmask[:], BIG, -BIG, ALU.mult, ALU.add))
                chain.done(nc.vector.tensor_tensor(groups, groups, gmask[:].rearrange("t b g -> t (b g)").unsqueeze(2)
                                                   .to_broadcast([T, B * G, PER]), ALU.add))
                for b in range(B):
                    ins = nc.vector.max(top[:, b, :], biased[:, b, :])
                chain.done(ins)
                for b in range(B):
                    ins = nc.vector.max_index(which[:, b, :], top[:, b, :], biased[:, b, :])
                chain.done(ins)
                chain.done(nc.vector.tensor_copy(index[:], which[:, :, 0:P]))


def gated_tiles_block(nc, name, K, route, xn_dram, o_dram, wgu, wd0, wd1, wgu_in, wd_in, H):
    E, NT = route.experts, route.tiles
    REST = H - T
    U = 4
    TURNS = NT // U
    assert NT % (2 * U) == 0
    with Space(nc) as s:
        who2 = s.sb(name + "_who2", [SLOTS, 2, U], i32)
        xg = s.sb(name + "_xg", [SLOTS, 2, U, D])
        xgt = s.sb(name + "_xgt", [D, U, SLOTS])
        sg = s.sb(name + "_sg", [SLOTS, U, H])
        hid = s.sb(name + "_hid", [SLOTS, U, H])
        ht = s.sb(name + "_ht", [T, U, 2, SLOTS])
        ob = s.sb(name + "_ob", [SLOTS, U, D])
        p_t = [s.ps(f"{name}_p_t{u}", [T, 4, SLOTS]) for u in range(U)]
        p_h = [s.ps(f"{name}_p_h{u}", [SLOTS, 512]) for u in range(U)]
        stored = [s.sem(f"{name}_stored{v}") for v in range(U // 2)]
        who_ready, t_ps, xgt_ready, h_ps, sg_ready, hid_ready, ht_ps, ht_ready, o_ps, ob_ready = (
            [s.sem(f"{name}_{n}{u}") for u in range(U)] for n in (
                "who_ready", "t_ps", "xgt_ready", "h_ps", "sg_ready", "hid_ready", "ht_ps", "ht_ready",
                "o_ps", "ob_ready"))
        gathered = [[s.sem(f"{name}_gathered{p}_{u}") for u in range(U)] for p in range(2)]
        with nc.Block() as block:
            @block.gpsimd
            def _(g):
                for u in range(U):
                    g.sem_inc(t_ps[u], 2)
                def turn(i, p):
                    for u in range(U):
                        g.wait_ge(t_ps[u], i + 1)
                        g.tensor_copy(who2[:, p, u:u + 1], route.who[:, bass.ds(U * i + u, 1)]).then_inc(who_ready[u], 1)
                        g.wait_ge(who_ready[u], i + 1)
                        g.nop(nofuse=True)
                        g.indirect_dma_start(out=xg[:, p, u, :], out_offset=None, in_=xn_dram,
                                             in_offset=bass.IndirectOffsetOnAxis(ap=who2[:, p, u:u + 1], axis=0)
                                             ).then_inc(gathered[p][u], 16)

                turns(g, TURNS, turn)

            @block.tensor
            def _(pe):
                pe.wait_ge(wgu_in, 32)
                pe.wait_ge(wd_in, 32)
                def turn(i, p):
                    experts = []

                    def read_expert():
                        at = route.expert_of[0:1, bass.ds(U * i + len(experts), 1)]
                        experts.append(pe.value_load(at, min_val=0, max_val=E - 1))

                    read_expert()
                    for u in range(U):
                        pe.wait_ge(gathered[p][u], 8 * (i - p) + 16)
                        pe.wait_ge(ob_ready[u], i + 1)
                        nc.tensor.transpose(p_t[u][:, 0], xg[:, p, u, :], K.ident[:]).then_inc(t_ps[u], 1)
                    for u in range(U):
                        pe.wait_ge(xgt_ready[u], i + 1)
                        nc.tensor.matmul(p_h[u][:, 0:2 * H], xgt[:, u, :],
                                         wgu[:, bass.ds(experts[u], 1)].rearrange("c e n -> c (e n)"), start=True,
                                         stop=True).then_inc(h_ps[u], 1)
                        if u < U - 1:
                            read_expert()
                    for u in range(U):
                        pe.wait_ge(hid_ready[u], i + 1)
                        nc.tensor.transpose(p_t[u][:, 1], hid[:, u, 0:T], K.ident[:])
                        nc.tensor.transpose(p_t[u][0:REST, 2], hid[:, u, T:H], K.ident[:]).then_inc(ht_ps[u], 1)
                    for u in range(U):
                        pe.wait_ge(ht_ready[u], i + 1)
                        nc.tensor.matmul(p_t[u][:, 3], ht[:, u, 0],
                                         wd0[:, bass.ds(experts[u], 1)].rearrange("p e n -> p (e n)"), start=True,
                                         stop=False)
                        nc.tensor.matmul(p_t[u][:, 3], ht[0:REST, u, 1],
                                         wd1[:, bass.ds(experts[u], 1)].rearrange("p e n -> p (e n)"), start=False,
                                         stop=True).then_inc(o_ps[u], 1)

                turns(pe, TURNS, turn)

            @block.scalar
            def _(act):
                def turn(i, p):
                    for u in range(U):
                        act.wait_ge(t_ps[u], i + 3)
                        nc.scalar.activation(xgt[:, u, :], p_t[u][:, 0], ACT.Copy).then_inc(xgt_ready[u], 1)
                    for u in range(U):
                        act.wait_ge(h_ps[u], i + 1)
                        nc.scalar.activation(sg[:, u, :], p_h[u][:, 0:H], ACT.Silu).then_inc(sg_ready[u], 1)
                    for u in range(U):
                        act.wait_ge(ht_ps[u], i + 1)
                        nc.scalar.activation(ht[:, u, 0], p_t[u][:, 1], ACT.Copy)
                        nc.scalar.activation(ht[0:REST, u, 1], p_t[u][0:REST, 2], ACT.Copy).then_inc(ht_ready[u], 1)

                turns(act, TURNS, turn)

            @block.vector
            def _(v):
                for half in range(U // 2):
                    v.sem_inc(stored[half], 16)
                for u in range(U):
                    v.sem_inc(ob_ready[u], 1)
                def turn(i, p):
                    for u in range(U):
                        v.wait_ge(sg_ready[u], i + 1)
                        nc.vector.tensor_tensor(hid[:, u, :], sg[:, u, :], p_h[u][:, H:2 * H],
                                                ALU.mult).then_inc(hid_ready[u], 1)
                    for u in range(U):
                        v.wait_ge(o_ps[u], i + 1)
                        v.wait_ge(stored[u // 2], 16 * i + 16)
                        nc.vector.tensor_copy(ob[:, u, :], p_t[u][:, 3]).then_inc(ob_ready[u], 1)

                turns(v, TURNS, turn)

            @block.sync
            def _(sp):
                def turn(i, p):
                    for half in range(U // 2):
                        pair = slice(2 * half, 2 * half + 2)
                        for u in (2 * half, 2 * half + 1):
                            sp.wait_ge(ob_ready[u], i + 2)
                        sp.dma_start(o_dram[bass.ds((U * i + 2 * half) * SLOTS, 2 * SLOTS), :].rearrange(
                            "(u p) c -> p u c", p=SLOTS), ob[:, pair, :]).then_inc(stored[half], 16)

                turns(sp, TURNS, turn)
                for half in range(U // 2):
                    sp.wait_ge(stored[half], 16 * TURNS + 16)


def grouped_experts(nc, W, K):
    E, P, H = 64, 6, 160
    NT = 8 * -(-(NTOK * P // SLOTS + E - 1) // 8)
    name = "L3_ffn"
    xn_dram = nc.dram_tensor(name + "_xn_dram", (NTOK, D), f32, kind="Internal").ap()
    o_dram = nc.dram_tensor(name + "_o_dram", (NT * SLOTS, D), f32, kind="Internal").ap()
    with Space(nc) as s:
        route = Route(s, name, E, P, NT)
        wgu = s.sb(name + "_wgu", [D, E, 2 * H])
        wd0 = s.sb(name + "_wd0", [T, E, D])
        wgu_in = s.sem(name + "_wgu_in")
        wd_in = s.sem(name + "_wd_in")
        xn = s.sb(name + "_xn", [T, B, D])
        with Space(nc) as s2:
            layer_norm_block(nc, name + "_ln", K.h, xn)
            index = s2.sb(name + "_index", [T, B, P])
            scores = s2.sb(name + "_scores", [T, B, E])
            grouped_router_block(nc, name + "_g", W, K, xn, xn_dram, route, index, scores)
            with nc.Block() as block:
                @block.sync
                def _(sp):
                    sp.dma_start(wgu[:, :, 0:H], W["L3_ffn_Wg"].rearrange("e c n -> c e n")).then_inc(wgu_in, 16)
                    sp.dma_start(wgu[:, :, H:2 * H], W["L3_ffn_Wu"].rearrange("e c n -> c e n")).then_inc(wgu_in, 16)
                    sp.dma_start(wd0[:], W["L3_ffn_Wd"][:, 0:T, :].rearrange("e p n -> p e n")).then_inc(wd_in, 16)
            sort_block(nc, name + "_sort", K, route, index, chosen=scores)
        wd1 = s.sb(name + "_wd1", [H - T, E, D])
        total = s.sb(name + "_total", [T, B])
        own = s.sem(name + "_own")
        with nc.Block() as block:
            @block.sync
            def _(sp):
                sp.dma_start(wd1[:], W["L3_ffn_Wd"][:, T:H, :].rearrange("e p n -> p e n")).then_inc(wd_in, 16)

            @block.vector
            def _(v):
                chain = Own(v, own)
                chain.done(nc.vector.tensor_reduce(out=total[:], in_=route.gate[:], axis=AX.X, op=ALU.add))
                chain.done(nc.vector.tensor_scalar(total[:], total[:], 1e-20, None, ALU.add))
                chain.done(nc.vector.reciprocal(total[:], total[:]))
                chain.done(nc.vector.tensor_tensor(route.gate[:], route.gate[:], per_row(total[:], P), ALU.mult))
        gated_tiles_block(nc, name + "_x", K, route, xn_dram, o_dram, wgu, wd0, wd1, wgu_in, wd_in, H)
        with Space(nc) as s3:
            combine_block(nc, name + "_c", K, route, o_dram, 1, SharedExpert(nc, s3, name + "_sh", W, K, xn))
    end_of_layer(nc)




def tower_program(nc, W, out):
    with Space(nc) as s:
        K = Constants(nc, s)
        constants_and_embedding(nc, W, K)
        layer0_attention(nc, W, K)
        top1_experts(nc, W, K, "L0_ffn", 8, 4, False)
        householder_attention(nc, W, K)
        capacity_experts(nc, W, K)
        layer2_attention(nc, W, K)
        top1_experts(nc, W, K, "L2_ffn", 8, 1, True)
        rope_attention(nc, W, K)
        grouped_experts(nc, W, K)
        out_done = s.sem("out_done")
        with nc.Block() as block:
            @block.sync
            def _(sp):
                sp.dma_start(out.rearrange("b t c -> t b c"), K.h[:]).then_inc(out_done, 16)
                sp.wait_ge(out_done, 16)


def kernel(**inputs):
    import numpy as np
    import concourse.bacc as bacc
    from concourse.bass_utils import run_bass_kernel_spmd

    nc = bacc.Bacc("TRN2", target_bir_lowering=False, num_devices=1)
    arrays = {}
    for name, a in inputs.items():
        arrays[name] = np.ascontiguousarray(a)
    arrays["x_t"] = np.ascontiguousarray(np.asarray(inputs["x"]).T)
    arrays["L0_attn_b1_t"] = np.ascontiguousarray(np.asarray(inputs["L0_attn_b1"]).reshape(4, 128).T)
    for name, chunks in (("L0_ffn_b1", 4), ("L2_ffn_b1", 1)):
        b1 = np.asarray(inputs[name])
        arrays[name + "_t"] = np.ascontiguousarray(b1.reshape(b1.shape[0], chunks, 128).transpose(2, 0, 1))
    for name in ("Wq", "Wk", "Wv", "Ww", "Wbeta", "Wg", "Wo"):
        arrays["L1_attn_" + name + "_t"] = np.ascontiguousarray(np.asarray(inputs["L1_attn_" + name]).T)
    row, col = np.arange(128)[:, None], np.arange(128)[None, :]
    arrays["head_rows"] = np.ascontiguousarray(np.broadcast_to(
        (row // 32 == np.arange(4)[None, :])[:, :, None], (128, 4, 128)).astype(np.float32))
    arrays["head_of_16"] = (row // 16 == np.arange(8)[None, :]).astype(np.float32)
    arrays["L1_ffn_b1_t"] = np.ascontiguousarray(np.asarray(inputs["L1_ffn_b1"]).T[:, :, None])
    arrays["L2_attn_bv_t"] = np.ascontiguousarray(np.asarray(inputs["L2_attn_bv"]).reshape(8, 128).T)
    theta = np.float32(1.0) / np.float32(10000.0) ** (np.arange(64, dtype=np.float32) / np.float32(64))
    angle = np.arange(128, dtype=np.float32)[:, None] * theta
    arrays["rope_cos"] = np.repeat(np.cos(angle), 2, axis=1)
    arrays["rope_sin"] = np.ascontiguousarray(np.stack([-np.sin(angle), np.sin(angle)], -1).reshape(128, 128))
    arrays["head_mask"] = (row // 8 == col // 8).astype(np.float32)
    arrays["head_columns"] = (row // 8 == np.arange(16)[None, :]).astype(np.float32)
    arrays["L3_ffn_router_w_t"] = np.ascontiguousarray(np.asarray(inputs["L3_ffn_router_w"]).T)
    W = {}
    for name, a in arrays.items():
        W[name] = nc.dram_tensor("in_" + name, a.shape, mybir.dt.from_np(a.dtype), kind="ExternalInput").ap()
    out = nc.dram_tensor("out", (B, T, D), f32, kind="ExternalOutput").ap()
    tower_program(nc, W, out)
    got = run_bass_kernel_spmd(nc, [{"in_" + n: a for n, a in arrays.items()}], core_ids=[0])
    return got.results[0]["out"]
```
